# Optimizing a Trainium2 kernel written in Bass

```python
import numpy as np
import jax
import jax.numpy as jnp

def _softmax(x, axis=-1):
    return jax.nn.softmax(x, axis=axis)

def _gelu(x):
    return jax.nn.gelu(x, approximate=True)

def _silu(x):
    return jax.nn.silu(x)

def _sigmoid(x):
    return jax.nn.sigmoid(x)

def _layernorm(x, axis=-1, eps=1e-05):
    m = jnp.mean(x, axis=axis, keepdims=True)
    v = jnp.var(x, axis=axis, keepdims=True)
    return (x - m) / jnp.sqrt(v + eps)

def _scatter_add(tgt, idx, src, axis=0):
    return tgt.at[idx].add(src)

def _segment_sum(src, seg, n):
    return jax.ops.segment_sum(src, seg, n)
kernel_name = 'mk_macaron_d4_jaxref_r8_e13a2c'

def setup_inputs(seed: int=0):
    np.random.seed(seed)
    _w = jnp.asarray

    def _L0_attn_setup():
        import jax, jax.numpy as jnp
        import numpy as np
        import math
        INPUT_WIDTH = 128
        KEY_WIDTH = 64
        VALUE_WIDTH = 64
        NUM_HEADS = 16
        key = jax.random.key(seed)
        k_x, k_q, k_k, k_v, k_p = jax.random.split(key, 5)
        n, s = (2, 256)
        scale = 1.0 / math.sqrt(INPUT_WIDTH)
        X = jax.random.normal(k_x, (n, s, INPUT_WIDTH), dtype=jnp.float32)
        Wq = jax.random.uniform(k_q, (INPUT_WIDTH, NUM_HEADS * KEY_WIDTH), jnp.float32, -scale, scale)
        Wk = jax.random.uniform(k_k, (INPUT_WIDTH, NUM_HEADS * KEY_WIDTH), jnp.float32, -scale, scale)
        Wv = jax.random.uniform(k_v, (INPUT_WIDTH, NUM_HEADS * VALUE_WIDTH), jnp.float32, -scale, scale)
        p_scale = 1.0 / math.sqrt(NUM_HEADS * VALUE_WIDTH)
        Wpost = jax.random.uniform(k_p, (NUM_HEADS * VALUE_WIDTH, INPUT_WIDTH), jnp.float32, -p_scale, p_scale)
        return {'X': X, 'Wq': Wq, 'Wk': Wk, 'Wv': Wv, 'Wpost': Wpost}
    _L0_attn_in = _L0_attn_setup()

    def _L0_ffn_setup():
        import jax, jax.numpy as jnp
        import numpy as np
        B, S, H, E, DFF = (4, 512, 128, 8, 512)
        key = jax.random.key(seed)
        k0, k1, k2, k3 = jax.random.split(key, 4)
        hidden_states = jax.random.normal(k0, (B, S, H), dtype=jnp.float32)
        gate_w = jax.random.normal(k1, (E, H), dtype=jnp.float32) * 0.02
        w1 = jax.random.normal(k2, (E, H, DFF), dtype=jnp.float32) * 0.02
        b1 = jnp.zeros((E, DFF), dtype=jnp.float32)
        w2 = jax.random.normal(k3, (E, DFF, H), dtype=jnp.float32) * 0.02
        b2 = jnp.zeros((E, H), dtype=jnp.float32)
        return {'hidden_states': hidden_states, 'gate_w': gate_w, 'w1': w1, 'b1': b1, 'w2': w2, 'b2': b2}
    _L0_ffn_in = _L0_ffn_setup()

    def _L1_attn_setup():
        import math
        import jax, jax.numpy as jnp
        import numpy as np
        LN_EPS = 1e-05

        def _relative_sinusoidal(t, hd, dtype):
            pos = jnp.arange(-(t - 1), t, dtype=dtype)[:, None]
            div = jnp.exp(jnp.arange(0, hd, 2, dtype=dtype) * (-math.log(10000.0) / hd))
            pe = jnp.zeros((2 * t - 1, hd), dtype=dtype)
            pe = pe.at[:, 0::2].set(jnp.sin(pos * div))
            pe = pe.at[:, 1::2].set(jnp.cos(pos * div))
            return pe
        key = jax.random.key(seed)
        ks = jax.random.split(key, 4)
        b, t, dim, H = (2, 256, 128, 16)
        hd = dim // H
        s = 0.02
        return {'x': jax.random.normal(ks[0], (b, t, dim), jnp.float32), 'ln_g': jnp.ones((dim,), jnp.float32), 'ln_b': jnp.zeros((dim,), jnp.float32), 'w_qkv': jax.random.normal(ks[1], (dim, 3 * dim), jnp.float32) * s, 'b_qkv': jnp.zeros((3 * dim,), jnp.float32), 'w_rel': jax.random.normal(ks[2], (hd, H), jnp.float32) * s, 'w_out': jax.random.normal(ks[3], (dim, dim), jnp.float32) * s, 'b_out': jnp.zeros((dim,), jnp.float32)}
    _L1_attn_in = _L1_attn_setup()

    def _L1_ffn_setup():
        import jax, jax.numpy as jnp
        import numpy as np
        DIM = 128
        DEPTH = 2
        HEADS = 8
        DIM_HEAD = 64
        WINDOW = 64
        INNER = HEADS * DIM_HEAD
        HID = int(DIM * 4 * 2 / 3)
        B, N = (2, 1024)
        QK_SCALE = 8.0

        def shift_token(t):
            t1, t2 = jnp.split(t, 2, axis=-1)
            t2 = jnp.pad(t2, ((0, 0), (1, 0), (0, 0)))[:, :-1]
            return jnp.concatenate([t1, t2], axis=-1)

        def l2norm(t):
            return t / jnp.clip(jnp.linalg.norm(t, axis=-1, keepdims=True), 1e-12)

        def rotate_half(x):
            x1, x2 = jnp.split(x, 2, axis=-1)
            return jnp.concatenate([-x2, x1], axis=-1)

        def rotary_xpos(q, k):
            n = q.shape[-2]
            half_idx = jnp.arange(0, DIM_HEAD, 2, dtype=jnp.float32)
            inv_freq = 1.0 / 10000.0 ** (half_idx / DIM_HEAD)
            t = jnp.arange(n, dtype=jnp.float32)
            freqs = t[:, None] * inv_freq[None, :]
            freqs = jnp.concatenate([freqs, freqs], axis=-1)
            base = (half_idx + 0.4 * DIM_HEAD) / (1.4 * DIM_HEAD)
            power = (t - n // 2) / float(WINDOW // 2)
            scale = base[None, :] ** power[:, None]
            scale = jnp.concatenate([scale, scale], axis=-1)
            cos, sin = (jnp.cos(freqs), jnp.sin(freqs))
            q = q * cos * scale + rotate_half(q) * sin * scale
            k = k * cos / scale + rotate_half(k) * sin / scale
            return (q, k)

        def local_attention(q, k, v):
            b, h, n, d = q.shape
            w = n // WINDOW
            bq = q.reshape(b, h, w, WINDOW, d) * QK_SCALE
            bk = k.reshape(b, h, w, WINDOW, d)
            bv = v.reshape(b, h, w, WINDOW, d)

            def look_around(t):
                p = jnp.pad(t, ((0, 0), (0, 0), (1, 0), (0, 0), (0, 0)))
                return jnp.concatenate([p[:, :, :w], p[:, :, 1:]], axis=3)
            bk, bv = (look_around(bk), look_around(bv))
            bt = jnp.arange(n).reshape(w, WINDOW)
            btp = jnp.pad(bt, ((1, 0), (0, 0)), constant_values=-1)
            btk = jnp.concatenate([btp[:w], btp[1:]], axis=1)
            sim = jnp.einsum('bhwid,bhwjd->bhwij', bq, bk)
            i = bt[:, :, None]
            j = btk[:, None, :]
            mask = (i < j) | (i > j + WINDOW) | (j == -1)
            sim = jnp.where(mask, -jnp.finfo(sim.dtype).max, sim)
            attn = jax.nn.softmax(sim, axis=-1)
            out = jnp.einsum('bhwij,bhwjd->bhwid', attn, bv)
            return out.reshape(b, h, n, d)

        def _layer(x, wqkv, qs, ksc, wo, lg, lb, w1, b1, w2, b2):
            b, n, _ = x.shape
            h = shift_token(x)
            qkv = h @ wqkv
            q, k, v = jnp.split(qkv, 3, axis=-1)
            to_heads = lambda t: t.reshape(b, n, HEADS, DIM_HEAD).transpose(0, 2, 1, 3)
            q, k, v = (to_heads(q), to_heads(k), to_heads(v))
            q = l2norm(q) * qs
            k = l2norm(k) * ksc
            q, k = rotary_xpos(q, k)
            o = local_attention(q, k, v)
            o = o.transpose(0, 2, 1, 3).reshape(b, n, INNER)
            x = x + o @ wo
            h = shift_token(x)
            mu = h.mean(-1, keepdims=True)
            var = h.var(-1, keepdims=True)
            h = (h - mu) / jnp.sqrt(var + 1e-05) * lg + lb
            h = h @ w1 + b1
            a, g = jnp.split(h, 2, axis=-1)
            h = a * jax.nn.gelu(g, approximate=False)
            x = x + h @ w2 + b2
            return x
        key = jax.random.key(seed)
        ks = jax.random.split(key, 6)
        return {'x': jax.random.normal(ks[0], (B, N, DIM), jnp.float32), 'wqkv': jax.random.normal(ks[1], (DEPTH, DIM, 3 * INNER), jnp.float32) * 0.02, 'q_scale': jnp.ones((DEPTH, DIM_HEAD), jnp.float32), 'k_scale': jnp.ones((DEPTH, DIM_HEAD), jnp.float32), 'wo': jax.random.normal(ks[2], (DEPTH, INNER, DIM), jnp.float32) * 0.02, 'ln_g': jnp.ones((DEPTH, DIM), jnp.float32), 'ln_b': jnp.zeros((DEPTH, DIM), jnp.float32), 'w1': jax.random.normal(ks[3], (DEPTH, DIM, 2 * HID), jnp.float32) * 0.02, 'b1': jnp.zeros((DEPTH, 2 * HID), jnp.float32), 'w2': jax.random.normal(ks[4], (DEPTH, HID, DIM), jnp.float32) * 0.02, 'b2': jnp.zeros((DEPTH, DIM), jnp.float32)}
    _L1_ffn_in = _L1_ffn_setup()

    def _L2_attn_setup():
        import jax, jax.numpy as jnp
        import numpy as np
        import math
        B, L, D, N2 = (8, 512, 128, 32)

        def s4d_kernel(log_dt, log_A_real, A_imag, C_real, C_imag, length):
            dt = jnp.exp(log_dt)[:, None]
            A = -jnp.exp(log_A_real) + 1j * A_imag
            dtA = A * dt
            C = (C_real + 1j * C_imag) * (jnp.exp(dtA) - 1.0) / A
            t = jnp.arange(length, dtype=jnp.float32)
            vand = jnp.exp(dtA[:, :, None] * t)
            K = 2.0 * jnp.einsum('dn,dnl->dl', C, vand).real
            return K
        key = jax.random.key(seed)
        ks = jax.random.split(key, 6)
        x = jax.random.normal(ks[0], (B, L, D), dtype=jnp.float32)
        log_dt = jax.random.uniform(ks[1], (D,), minval=math.log(0.001), maxval=math.log(0.1)).astype(jnp.float32)
        log_A_real = jnp.log(0.5 * jnp.ones((D, N2), jnp.float32))
        A_imag = math.pi * jnp.broadcast_to(jnp.arange(N2, dtype=jnp.float32), (D, N2))
        C_real = jax.random.normal(ks[2], (D, N2), dtype=jnp.float32)
        C_imag = jax.random.normal(ks[3], (D, N2), dtype=jnp.float32)
        W = jax.random.normal(ks[4], (D, D), dtype=jnp.float32) / jnp.sqrt(jnp.float32(D))
        b = jax.random.normal(ks[5], (D,), dtype=jnp.float32) * 0.01
        return dict(x=x, log_dt=log_dt, log_A_real=log_A_real, A_imag=A_imag, C_real=C_real, C_imag=C_imag, W=W, b=b)
    _L2_attn_in = _L2_attn_setup()

    def _L2_ffn_setup():
        import jax, jax.numpy as jnp
        import numpy as np
        EPS = float(jnp.finfo(jnp.float32).eps)
        TOP_K = 2

        def rmsnorm(x, w):
            return x * jax.lax.rsqrt(jnp.mean(x * x, axis=-1, keepdims=True) + EPS) * w
        B, T, D_IN, D_MODEL, D_FF, D_OUT, E = (8, 128, 128, 128, 512, 128, 8)
        STD = 0.02
        key = jax.random.key(seed)
        ks = jax.random.split(key, 8)
        return {'s': jax.random.normal(ks[0], (B, T, D_IN), dtype=jnp.float32), 'W_in': STD * jax.random.normal(ks[1], (D_MODEL, D_IN), dtype=jnp.float32), 'in_norm_w': jnp.ones((D_MODEL,), dtype=jnp.float32), 'Wr': STD * jax.random.normal(ks[2], (E, D_MODEL), dtype=jnp.float32), 'expert_bias': jnp.zeros((E,), dtype=jnp.float32), 'Wg': STD * jax.random.normal(ks[3], (E, D_FF, D_MODEL), dtype=jnp.float32), 'Wu': STD * jax.random.normal(ks[4], (E, D_FF, D_MODEL), dtype=jnp.float32), 'Wd': STD * jax.random.normal(ks[5], (E, D_MODEL, D_FF), dtype=jnp.float32), 'enorm_w': jnp.ones((E, D_MODEL), dtype=jnp.float32), 'out_norm_w': jnp.ones((D_MODEL,), dtype=jnp.float32), 'W_out': STD * jax.random.normal(ks[6], (D_OUT, D_MODEL), dtype=jnp.float32)}
    _L2_ffn_in = _L2_ffn_setup()

    def _L3_attn_setup():
        import jax, jax.numpy as jnp
        import numpy as np
        import math
        D_MODEL = 128
        NUM_HEADS = 16
        D_HEAD = D_MODEL // NUM_HEADS
        BATCH = 4
        SEQ = 256

        def _trunc_normal(key, shape, sd):
            return sd * jax.random.truncated_normal(key, -3.0, 3.0, shape, dtype=jnp.float32)
        key = jax.random.key(seed)
        kx, kq, kk, kv, ko = jax.random.split(key, 5)
        sd = (2.0 / (NUM_HEADS * D_HEAD + D_MODEL)) ** 0.5
        x = jax.random.normal(kx, (BATCH, SEQ, D_MODEL), dtype=jnp.float32)
        WQ = _trunc_normal(kq, (NUM_HEADS, D_HEAD, D_MODEL), sd)
        WK = _trunc_normal(kk, (NUM_HEADS, D_HEAD, D_MODEL), sd)
        WV = _trunc_normal(kv, (NUM_HEADS, D_HEAD, D_MODEL), sd)
        WO = _trunc_normal(ko, (NUM_HEADS, D_MODEL, D_HEAD), sd)
        return {'x': x, 'WQ': WQ, 'WK': WK, 'WV': WV, 'WO': WO}
    _L3_attn_in = _L3_attn_setup()

    def _L3_ffn_setup():
        import jax, jax.numpy as jnp
        import numpy as np
        E = 32
        K = 4
        H = 128
        I = 64
        B, S = (2, 256)
        T = B * S
        C = 128
        ROUTED_SCALE = 1.0

        def _silu_and_mul(gu):
            g, u = jnp.split(gu, 2, axis=-1)
            return jax.nn.silu(g) * u
        key = jax.random.key(seed)
        ks = jax.random.split(key, 6)
        s = 0.02
        return {'hidden_states': jax.random.normal(ks[0], (B, S, H), jnp.float32), 'gate_w': jax.random.normal(ks[1], (E, H), jnp.float32) * s, 'w_gate_up': jax.random.normal(ks[2], (E, H, 2 * I), jnp.float32) * s, 'w_down': jax.random.normal(ks[3], (E, I, H), jnp.float32) * s, 'shared_w_gate_up': jax.random.normal(ks[4], (H, 2 * I), jnp.float32) * s, 'shared_w_down': jax.random.normal(ks[5], (I, H), jnp.float32) * s}
    _L3_ffn_in = _L3_ffn_setup()
    _d = {'L0_attn_X': _L0_attn_in['X'], 'L0_attn_Wq': _L0_attn_in['Wq'], 'L0_attn_Wk': _L0_attn_in['Wk'], 'L0_attn_Wv': _L0_attn_in['Wv'], 'L0_attn_Wpost': _L0_attn_in['Wpost'], 'L0_ffn_gate_w': _L0_ffn_in['gate_w'], 'L0_ffn_w1': _L0_ffn_in['w1'], 'L0_ffn_b1': _L0_ffn_in['b1'], 'L0_ffn_w2': _L0_ffn_in['w2'], 'L0_ffn_b2': _L0_ffn_in['b2'], 'L1_attn_ln_g': _L1_attn_in['ln_g'], 'L1_attn_ln_b': _L1_attn_in['ln_b'], 'L1_attn_w_qkv': _L1_attn_in['w_qkv'], 'L1_attn_b_qkv': _L1_attn_in['b_qkv'], 'L1_attn_w_rel': _L1_attn_in['w_rel'], 'L1_attn_w_out': _L1_attn_in['w_out'], 'L1_attn_b_out': _L1_attn_in['b_out'], 'L1_ffn_wqkv': _L1_ffn_in['wqkv'], 'L1_ffn_q_scale': _L1_ffn_in['q_scale'], 'L1_ffn_k_scale': _L1_ffn_in['k_scale'], 'L1_ffn_wo': _L1_ffn_in['wo'], 'L1_ffn_ln_g': _L1_ffn_in['ln_g'], 'L1_ffn_ln_b': _L1_ffn_in['ln_b'], 'L1_ffn_w1': _L1_ffn_in['w1'], 'L1_ffn_b1': _L1_ffn_in['b1'], 'L1_ffn_w2': _L1_ffn_in['w2'], 'L1_ffn_b2': _L1_ffn_in['b2'], 'L2_attn_log_dt': _L2_attn_in['log_dt'], 'L2_attn_log_A_real': _L2_attn_in['log_A_real'], 'L2_attn_A_imag': _L2_attn_in['A_imag'], 'L2_attn_C_real': _L2_attn_in['C_real'], 'L2_attn_C_imag': _L2_attn_in['C_imag'], 'L2_attn_W': _L2_attn_in['W'], 'L2_attn_b': _L2_attn_in['b'], 'L2_ffn_W_in': _L2_ffn_in['W_in'], 'L2_ffn_in_norm_w': _L2_ffn_in['in_norm_w'], 'L2_ffn_Wr': _L2_ffn_in['Wr'], 'L2_ffn_expert_bias': _L2_ffn_in['expert_bias'], 'L2_ffn_Wg': _L2_ffn_in['Wg'], 'L2_ffn_Wu': _L2_ffn_in['Wu'], 'L2_ffn_Wd': _L2_ffn_in['Wd'], 'L2_ffn_enorm_w': _L2_ffn_in['enorm_w'], 'L2_ffn_out_norm_w': _L2_ffn_in['out_norm_w'], 'L2_ffn_W_out': _L2_ffn_in['W_out'], 'L3_attn_WQ': _L3_attn_in['WQ'], 'L3_attn_WK': _L3_attn_in['WK'], 'L3_attn_WV': _L3_attn_in['WV'], 'L3_attn_WO': _L3_attn_in['WO'], 'L3_ffn_gate_w': _L3_ffn_in['gate_w'], 'L3_ffn_w_gate_up': _L3_ffn_in['w_gate_up'], 'L3_ffn_w_down': _L3_ffn_in['w_down'], 'L3_ffn_shared_w_gate_up': _L3_ffn_in['shared_w_gate_up'], 'L3_ffn_shared_w_down': _L3_ffn_in['shared_w_down']}
    _x0 = _d['L0_attn_X']
    _d['L0_attn_X'] = jax.random.normal(jax.random.fold_in(jax.random.key(seed), 1), (4, 512, 128), dtype=_x0.dtype)
    del _x0
    return _d

def reference(L0_attn_X, L0_attn_Wq, L0_attn_Wk, L0_attn_Wv, L0_attn_Wpost, L0_ffn_gate_w, L0_ffn_w1, L0_ffn_b1, L0_ffn_w2, L0_ffn_b2, L1_attn_ln_g, L1_attn_ln_b, L1_attn_w_qkv, L1_attn_b_qkv, L1_attn_w_rel, L1_attn_w_out, L1_attn_b_out, L1_ffn_wqkv, L1_ffn_q_scale, L1_ffn_k_scale, L1_ffn_wo, L1_ffn_ln_g, L1_ffn_ln_b, L1_ffn_w1, L1_ffn_b1, L1_ffn_w2, L1_ffn_b2, L2_attn_log_dt, L2_attn_log_A_real, L2_attn_A_imag, L2_attn_C_real, L2_attn_C_imag, L2_attn_W, L2_attn_b, L2_ffn_W_in, L2_ffn_in_norm_w, L2_ffn_Wr, L2_ffn_expert_bias, L2_ffn_Wg, L2_ffn_Wu, L2_ffn_Wd, L2_ffn_enorm_w, L2_ffn_out_norm_w, L2_ffn_W_out, L3_attn_WQ, L3_attn_WK, L3_attn_WV, L3_attn_WO, L3_ffn_gate_w, L3_ffn_w_gate_up, L3_ffn_w_down, L3_ffn_shared_w_gate_up, L3_ffn_shared_w_down):

    def _L0_attn_ref(X, Wq, Wk, Wv, Wpost):
        import jax, jax.numpy as jnp
        import numpy as np
        import math
        INPUT_WIDTH = 128
        KEY_WIDTH = 64
        VALUE_WIDTH = 64
        NUM_HEADS = 16
        n, s, _ = X.shape
        Q = (X @ Wq).reshape(n, s, NUM_HEADS, KEY_WIDTH)
        K = (X @ Wk).reshape(n, s, NUM_HEADS, KEY_WIDTH)
        V = (X @ Wv).reshape(n, s, NUM_HEADS, VALUE_WIDTH)
        inv_sqrt_d = 1.0 / math.sqrt(KEY_WIDTH)
        raw_attn = jnp.einsum('bshe,bthe->bsth', Q, K * inv_sqrt_d)
        attn = jax.nn.softmax(raw_attn, axis=2)
        A = jnp.einsum('bsth,bthe->bshe', attn, V).reshape(n, s, NUM_HEADS * VALUE_WIDTH)
        A = jax.nn.gelu(A, approximate=False)
        P = A @ Wpost
        return X + P

    def _L0_ffn_ref(hidden_states, gate_w, w1, b1, w2, b2):
        import jax, jax.numpy as jnp
        import numpy as np
        B, S, H, E, DFF = (4, 512, 128, 8, 512)
        b, s, h = hidden_states.shape
        x = hidden_states.reshape(-1, h)
        gate_logits = x @ gate_w.T
        gate_probs = jax.nn.softmax(gate_logits, axis=-1)
        expert_idx = jnp.argmax(gate_probs, axis=-1)
        expert_w = jnp.take_along_axis(gate_probs, expert_idx[:, None], axis=1)[:, 0]
        out = jnp.zeros_like(x)
        n_experts = w1.shape[0]
        for e in range(n_experts):
            ye = jax.nn.relu(x @ w1[e] + b1[e]) @ w2[e] + b2[e]
            sel = (expert_idx == e)[:, None]
            out = out + jnp.where(sel, ye * expert_w[:, None], 0.0)
        return out.reshape(b, s, h)

    def _L1_attn_ref(x, ln_g, ln_b, w_qkv, b_qkv, w_rel, w_out, b_out):
        import math
        import jax, jax.numpy as jnp
        import numpy as np
        LN_EPS = 1e-05

        def _relative_sinusoidal(t, hd, dtype):
            pos = jnp.arange(-(t - 1), t, dtype=dtype)[:, None]
            div = jnp.exp(jnp.arange(0, hd, 2, dtype=dtype) * (-math.log(10000.0) / hd))
            pe = jnp.zeros((2 * t - 1, hd), dtype=dtype)
            pe = pe.at[:, 0::2].set(jnp.sin(pos * div))
            pe = pe.at[:, 1::2].set(jnp.cos(pos * div))
            return pe
        b, t, dim = x.shape
        hd, H = w_rel.shape
        scale = hd ** (-0.5)
        mu = jnp.mean(x, axis=-1, keepdims=True)
        var = jnp.mean(jnp.square(x - mu), axis=-1, keepdims=True)
        xn = (x - mu) * jax.lax.rsqrt(var + LN_EPS) * ln_g + ln_b
        qkv = (xn @ w_qkv + b_qkv).reshape(b, t, 3, H, hd)
        qkv = jnp.transpose(qkv, (2, 0, 3, 1, 4))
        q, k, v = (qkv[0], qkv[1], qkv[2])
        scores = jnp.einsum('bhqd,bhkd->bhqk', q, k) * scale
        rel_pe = _relative_sinusoidal(t, hd, scores.dtype)
        rel_bias = rel_pe @ w_rel
        idx = jnp.arange(t)[:, None] - jnp.arange(t)[None, :] + (t - 1)
        bias = jnp.transpose(rel_bias[idx], (2, 0, 1))[None]
        attn = jax.nn.softmax(scores + bias, axis=-1)
        out = jnp.einsum('bhqk,bhkd->bhqd', attn, v)
        out = jnp.transpose(out, (0, 2, 1, 3)).reshape(b, t, dim)
        return out @ w_out + b_out

    def _L1_ffn_ref(x, wqkv, q_scale, k_scale, wo, ln_g, ln_b, w1, b1, w2, b2):
        import jax, jax.numpy as jnp
        import numpy as np
        DIM = 128
        DEPTH = 2
        HEADS = 8
        DIM_HEAD = 64
        WINDOW = 64
        INNER = HEADS * DIM_HEAD
        HID = int(DIM * 4 * 2 / 3)
        B, N = (2, 1024)
        QK_SCALE = 8.0

        def shift_token(t):
            t1, t2 = jnp.split(t, 2, axis=-1)
            t2 = jnp.pad(t2, ((0, 0), (1, 0), (0, 0)))[:, :-1]
            return jnp.concatenate([t1, t2], axis=-1)

        def l2norm(t):
            return t / jnp.clip(jnp.linalg.norm(t, axis=-1, keepdims=True), 1e-12)

        def rotate_half(x):
            x1, x2 = jnp.split(x, 2, axis=-1)
            return jnp.concatenate([-x2, x1], axis=-1)

        def rotary_xpos(q, k):
            n = q.shape[-2]
            half_idx = jnp.arange(0, DIM_HEAD, 2, dtype=jnp.float32)
            inv_freq = 1.0 / 10000.0 ** (half_idx / DIM_HEAD)
            t = jnp.arange(n, dtype=jnp.float32)
            freqs = t[:, None] * inv_freq[None, :]
            freqs = jnp.concatenate([freqs, freqs], axis=-1)
            base = (half_idx + 0.4 * DIM_HEAD) / (1.4 * DIM_HEAD)
            power = (t - n // 2) / float(WINDOW // 2)
            scale = base[None, :] ** power[:, None]
            scale = jnp.concatenate([scale, scale], axis=-1)
            cos, sin = (jnp.cos(freqs), jnp.sin(freqs))
            q = q * cos * scale + rotate_half(q) * sin * scale
            k = k * cos / scale + rotate_half(k) * sin / scale
            return (q, k)

        def local_attention(q, k, v):
            b, h, n, d = q.shape
            w = n // WINDOW
            bq = q.reshape(b, h, w, WINDOW, d) * QK_SCALE
            bk = k.reshape(b, h, w, WINDOW, d)
            bv = v.reshape(b, h, w, WINDOW, d)

            def look_around(t):
                p = jnp.pad(t, ((0, 0), (0, 0), (1, 0), (0, 0), (0, 0)))
                return jnp.concatenate([p[:, :, :w], p[:, :, 1:]], axis=3)
            bk, bv = (look_around(bk), look_around(bv))
            bt = jnp.arange(n).reshape(w, WINDOW)
            btp = jnp.pad(bt, ((1, 0), (0, 0)), constant_values=-1)
            btk = jnp.concatenate([btp[:w], btp[1:]], axis=1)
            sim = jnp.einsum('bhwid,bhwjd->bhwij', bq, bk)
            i = bt[:, :, None]
            j = btk[:, None, :]
            mask = (i < j) | (i > j + WINDOW) | (j == -1)
            sim = jnp.where(mask, -jnp.finfo(sim.dtype).max, sim)
            attn = jax.nn.softmax(sim, axis=-1)
            out = jnp.einsum('bhwij,bhwjd->bhwid', attn, bv)
            return out.reshape(b, h, n, d)

        def _layer(x, wqkv, qs, ksc, wo, lg, lb, w1, b1, w2, b2):
            b, n, _ = x.shape
            h = shift_token(x)
            qkv = h @ wqkv
            q, k, v = jnp.split(qkv, 3, axis=-1)
            to_heads = lambda t: t.reshape(b, n, HEADS, DIM_HEAD).transpose(0, 2, 1, 3)
            q, k, v = (to_heads(q), to_heads(k), to_heads(v))
            q = l2norm(q) * qs
            k = l2norm(k) * ksc
            q, k = rotary_xpos(q, k)
            o = local_attention(q, k, v)
            o = o.transpose(0, 2, 1, 3).reshape(b, n, INNER)
            x = x + o @ wo
            h = shift_token(x)
            mu = h.mean(-1, keepdims=True)
            var = h.var(-1, keepdims=True)
            h = (h - mu) / jnp.sqrt(var + 1e-05) * lg + lb
            h = h @ w1 + b1
            a, g = jnp.split(h, 2, axis=-1)
            h = a * jax.nn.gelu(g, approximate=False)
            x = x + h @ w2 + b2
            return x
        for l in range(DEPTH):
            x = _layer(x, wqkv[l], q_scale[l], k_scale[l], wo[l], ln_g[l], ln_b[l], w1[l], b1[l], w2[l], b2[l])
        return x

    def _L2_attn_ref(x, log_dt, log_A_real, A_imag, C_real, C_imag, W, b):
        import jax, jax.numpy as jnp
        import numpy as np
        import math
        B, L, D, N2 = (8, 512, 128, 32)

        def s4d_kernel(log_dt, log_A_real, A_imag, C_real, C_imag, length):
            dt = jnp.exp(log_dt)[:, None]
            A = -jnp.exp(log_A_real) + 1j * A_imag
            dtA = A * dt
            C = (C_real + 1j * C_imag) * (jnp.exp(dtA) - 1.0) / A
            t = jnp.arange(length, dtype=jnp.float32)
            vand = jnp.exp(dtA[:, :, None] * t)
            K = 2.0 * jnp.einsum('dn,dnl->dl', C, vand).real
            return K
        Bb, Ll, Dd = x.shape
        K = s4d_kernel(log_dt, log_A_real, A_imag, C_real, C_imag, Ll)
        n_fft = 2 * Ll
        x_t = jnp.transpose(x, (0, 2, 1))
        k_f = jnp.fft.rfft(K, n=n_fft)
        x_f = jnp.fft.rfft(x_t, n=n_fft)
        y = jnp.fft.irfft(x_f * k_f[None], n=n_fft)[:, :, :Ll]
        y = jnp.transpose(y, (0, 2, 1))
        y = jax.nn.gelu(y, approximate=False)
        return y @ W.T + b

    def _L2_ffn_ref(s, W_in, in_norm_w, Wr, expert_bias, Wg, Wu, Wd, enorm_w, out_norm_w, W_out):
        import jax, jax.numpy as jnp
        import numpy as np
        EPS = float(jnp.finfo(jnp.float32).eps)
        TOP_K = 2

        def rmsnorm(x, w):
            return x * jax.lax.rsqrt(jnp.mean(x * x, axis=-1, keepdims=True) + EPS) * w
        B, T, _ = s.shape
        x = s.reshape(B * T, -1)
        h = rmsnorm(x @ W_in.T, in_norm_w)
        logits = h @ Wr.T
        _, idx = jax.lax.top_k(logits + expert_bias, TOP_K)
        sel = jnp.take_along_axis(logits, idx, axis=-1)
        g_topk = jax.nn.softmax(sel, axis=-1)
        N = logits.shape[0]
        gates = jnp.zeros_like(logits).at[jnp.arange(N)[:, None], idx].set(g_topk)
        out = jnp.zeros_like(h)
        for e in range(Wg.shape[0]):
            gate = jax.nn.silu(h @ Wg[e].T)
            up = h @ Wu[e].T
            oe = rmsnorm(gate * up @ Wd[e].T, enorm_w[e])
            out = out + gates[:, e:e + 1] * oe
        s_hat = rmsnorm(out, out_norm_w) @ W_out.T
        return s_hat.reshape(B, T, -1)

    def _L3_attn_ref(x, WQ, WK, WV, WO):
        import jax, jax.numpy as jnp
        import numpy as np
        import math
        D_MODEL = 128
        NUM_HEADS = 16
        D_HEAD = D_MODEL // NUM_HEADS
        BATCH = 4
        SEQ = 256

        def _trunc_normal(key, shape, sd):
            return sd * jax.random.truncated_normal(key, -3.0, 3.0, shape, dtype=jnp.float32)
        Q = jnp.einsum('bsd,hkd->bhsk', x, WQ)
        K = jnp.einsum('bsd,hkd->bhsk', x, WK)
        V = jnp.einsum('bsd,hkd->bhsk', x, WV)
        d_k = Q.shape[-1]
        scores = jnp.einsum('bhqd,bhkd->bhqk', Q, K) / math.sqrt(d_k)
        seq_len = x.shape[-2]
        causal = jnp.tril(jnp.ones((seq_len, seq_len), dtype=bool))
        scores = jnp.where(causal, scores, -jnp.inf)
        probs = jax.nn.softmax(scores, axis=-1)
        attn = jnp.einsum('bhqk,bhkv->bhqv', probs, V)
        return jnp.einsum('bhsv,hdv->bsd', attn, WO)

    def _L3_ffn_ref(hidden_states, gate_w, w_gate_up, w_down, shared_w_gate_up, shared_w_down):
        import jax, jax.numpy as jnp
        import numpy as np
        E = 32
        K = 4
        H = 128
        I = 64
        B, S = (2, 256)
        T = B * S
        C = 128
        ROUTED_SCALE = 1.0

        def _silu_and_mul(gu):
            g, u = jnp.split(gu, 2, axis=-1)
            return jax.nn.silu(g) * u
        b, s, h = hidden_states.shape
        x = hidden_states.reshape(-1, h)
        t = x.shape[0]
        logits = x @ gate_w.T
        probs = jax.nn.softmax(logits, axis=-1)
        topk_w, topk_idx = jax.lax.top_k(probs, K)
        topk_w = topk_w / jnp.sum(topk_w, axis=-1, keepdims=True)
        topk_w = topk_w * ROUTED_SCALE
        e_flat = topk_idx.reshape(-1)
        w_flat = topk_w.reshape(-1)
        t_flat = jnp.repeat(jnp.arange(t), K)
        order = jnp.argsort(e_flat)
        e_s, w_s, t_s = (e_flat[order], w_flat[order], t_flat[order])
        counts = jax.ops.segment_sum(jnp.ones_like(e_s), e_s, num_segments=E)
        starts = jnp.cumsum(counts) - counts
        pos = jnp.arange(t * K) - starts[e_s]
        slot = jnp.minimum(pos, C)
        buf = jnp.zeros((E, C + 1, h), x.dtype).at[e_s, slot].set(x[t_s])
        gu = jnp.einsum('ech,ehi->eci', buf[:, :C], w_gate_up)
        expert_out = jnp.einsum('eci,eih->ech', _silu_and_mul(gu), w_down)
        expert_out = jnp.pad(expert_out, ((0, 0), (0, 1), (0, 0)))
        gate = jnp.where(pos < C, w_s, 0.0)[:, None]
        routed = jnp.zeros_like(x).at[t_s].add(expert_out[e_s, slot] * gate)
        shared = _silu_and_mul(x @ shared_w_gate_up) @ shared_w_down
        return (routed + shared).reshape(b, s, h)
    x = L0_attn_X
    x = x + 0.5 * _L0_ffn_ref(_layernorm(x, axis=-1), L0_ffn_gate_w, L0_ffn_w1, L0_ffn_b1, L0_ffn_w2, L0_ffn_b2)
    x = x + _L0_attn_ref(_layernorm(x, axis=-1), L0_attn_Wq, L0_attn_Wk, L0_attn_Wv, L0_attn_Wpost)
    x = x + 0.5 * _L0_ffn_ref(_layernorm(x, axis=-1), L0_ffn_gate_w, L0_ffn_w1, L0_ffn_b1, L0_ffn_w2, L0_ffn_b2)
    x = x + 0.5 * _L1_ffn_ref(_layernorm(x, axis=-1), L1_ffn_wqkv, L1_ffn_q_scale, L1_ffn_k_scale, L1_ffn_wo, L1_ffn_ln_g, L1_ffn_ln_b, L1_ffn_w1, L1_ffn_b1, L1_ffn_w2, L1_ffn_b2)
    x = x + _L1_attn_ref(_layernorm(x, axis=-1), L1_attn_ln_g, L1_attn_ln_b, L1_attn_w_qkv, L1_attn_b_qkv, L1_attn_w_rel, L1_attn_w_out, L1_attn_b_out)
    x = x + 0.5 * _L1_ffn_ref(_layernorm(x, axis=-1), L1_ffn_wqkv, L1_ffn_q_scale, L1_ffn_k_scale, L1_ffn_wo, L1_ffn_ln_g, L1_ffn_ln_b, L1_ffn_w1, L1_ffn_b1, L1_ffn_w2, L1_ffn_b2)
    x = x + 0.5 * _L2_ffn_ref(_layernorm(x, axis=-1), L2_ffn_W_in, L2_ffn_in_norm_w, L2_ffn_Wr, L2_ffn_expert_bias, L2_ffn_Wg, L2_ffn_Wu, L2_ffn_Wd, L2_ffn_enorm_w, L2_ffn_out_norm_w, L2_ffn_W_out)
    x = x + _L2_attn_ref(_layernorm(x, axis=-1), L2_attn_log_dt, L2_attn_log_A_real, L2_attn_A_imag, L2_attn_C_real, L2_attn_C_imag, L2_attn_W, L2_attn_b)
    x = x + 0.5 * _L2_ffn_ref(_layernorm(x, axis=-1), L2_ffn_W_in, L2_ffn_in_norm_w, L2_ffn_Wr, L2_ffn_expert_bias, L2_ffn_Wg, L2_ffn_Wu, L2_ffn_Wd, L2_ffn_enorm_w, L2_ffn_out_norm_w, L2_ffn_W_out)
    x = x + 0.5 * _L3_ffn_ref(_layernorm(x, axis=-1), L3_ffn_gate_w, L3_ffn_w_gate_up, L3_ffn_w_down, L3_ffn_shared_w_gate_up, L3_ffn_shared_w_down)
    x = x + _L3_attn_ref(_layernorm(x, axis=-1), L3_attn_WQ, L3_attn_WK, L3_attn_WV, L3_attn_WO)
    x = x + 0.5 * _L3_ffn_ref(_layernorm(x, axis=-1), L3_ffn_gate_w, L3_ffn_w_gate_up, L3_ffn_w_down, L3_ffn_shared_w_gate_up, L3_ffn_shared_w_down)
    return x

_drawn_inputs = setup_inputs


def setup_inputs(seed=0):
    import zlib

    import numpy as np

    out = dict(_drawn_inputs(seed))
    spreads = {'L0_ffn_b1': (0.0, 0.8),
     'L0_ffn_b2': (0.0, 0.535),
     'L1_attn_ln_g': (1.0, 0.6),
     'L1_attn_ln_b': (0.0, 0.8),
     'L1_attn_b_qkv': (0.0, 0.589),
     'L1_attn_b_out': (0.0, 0.8),
     'L1_ffn_q_scale': (1.0, 0.6),
     'L1_ffn_k_scale': (1.0, 0.6),
     'L1_ffn_ln_g': (1.0, 0.6),
     'L1_ffn_ln_b': (0.0, 0.8),
     'L1_ffn_b1': (0.0, 0.8),
     'L1_ffn_b2': (0.0, 0.8),
     'L2_attn_log_A_real': (-0.6931471824645996, 0.565),
     'L2_ffn_in_norm_w': (1.0, 0.6),
     'L2_ffn_expert_bias': (0.0, 0.8),
     'L2_ffn_enorm_w': (1.0, 0.6),
     'L2_ffn_out_norm_w': (1.0, 0.6)}
    factors = {'L0_attn_Wq': 8.0,
     'L0_attn_Wk': 8.0,
     'L0_attn_Wv': 8.0,
     'L0_attn_Wpost': 8.0,
     'L0_ffn_gate_w': 3.363,
     'L0_ffn_w1': 6.114,
     'L0_ffn_w2': 4.875,
     'L1_attn_w_qkv': 8.0,
     'L1_attn_w_rel': 64.0,
     'L1_attn_w_out': 4.137,
     'L1_ffn_wqkv': 4.351,
     'L1_ffn_wo': 4.253,
     'L1_ffn_w1': 7.835,
     'L1_ffn_w2': 7.446,
     'L2_attn_b': 64.0,
     'L3_ffn_gate_w': 24.088,
     'L3_ffn_w_gate_up': 24.151,
     'L3_ffn_w_down': 24.413,
     'L3_ffn_shared_w_gate_up': 8.0,
     'L3_ffn_shared_w_down': 8.0,
     'L2_attn_C_imag': 3.691,
     'L2_ffn_W_in': 5.417,
     'L2_ffn_Wr': 8.0,
     'L2_ffn_Wg': 6.101,
     'L2_ffn_Wu': 4.88,
     'L2_ffn_Wd': 5.088,
     'L2_ffn_W_out': 5.21,
     'L3_attn_WQ': 8.0,
     'L3_attn_WK': 8.0}
    for name, (base, spread) in spreads.items():
        noise = np.random.default_rng([zlib.crc32(name.encode()), seed]).standard_normal(out[name].shape)
        drawn = base * np.exp(spread * noise) if base else spread * noise
        out[name] = jnp.asarray(drawn.astype(out[name].dtype))
    for name, factor in factors.items():
        out[name] = (out[name] * factor).astype(out[name].dtype)
    return out
```

```python
import math

import numpy as np
import concourse.bass as bass
from concourse import mybir
from contextlib import ExitStack

F32 = mybir.dt.float32
ALU = mybir.AluOpType
ACT = mybir.ActivationFunctionType
X_AXIS = mybir.AxisListType.X

P = 128
BATCH, SEQ, DIM = 4, 512, 128
TOKENS = BATCH * SEQ
TILES = TOKENS // P
GROUPS = 4
GROUP = TOKENS // GROUPS
TPG = TILES // GROUPS
LN_EPS = 1e-5
F32_EPS = float(np.finfo(np.float32).eps)
NEG = -3.0e38

ONE = 1
FROM_ONE = {
    "tensor": [
        "moe0_down", "values", "gelu_turned", "att_projected", "lf_projected", "lf_values",
        "lf_out_projected", "lf_scores", "lf_down", "lf_turned", "probs_turned"],
    "vector": [
        "moe0_hidden", "heads_done", "lf_rotated", "lf_out", "lf_added", "lf_probs_copied_dve",
        "lf_hidden", "lf_ffn_added", "s4_kernel", "att_added"],
    "scalar": [
        "probs", "lf_squared", "lf_keys", "lf_probs", "lf_probs_copied_act", "lf_out_copied"],
}


class Arena:

    def __init__(self, tensor, floats):
        self.tensor, self.floats, self.at = tensor, floats, 0

    def reset(self, at=0):
        self.at = at

    def take(self, *shape, parts=P):
        n = int(np.prod(shape))
        assert self.at + n <= self.floats, (self.at, n)
        view = self.tensor[0:parts, self.at:self.at + n]
        self.at += n
        if len(shape) == 2:
            view = view.rearrange("p (a b) -> p a b", a=shape[0])
        elif len(shape) == 3:
            view = view.rearrange("p (a b c) -> p a b c", a=shape[0], b=shape[1])
        elif len(shape) == 4:
            view = view.rearrange("p (a b c d) -> p a b c d", a=shape[0], b=shape[1], c=shape[2])
        return view


class Program:

    def __init__(self, nc, ctx, ins, out, scratch):
        self.nc, self.ins, self.out, self.scratch = nc, ins, out, scratch
        self.ctx = ctx
        self.x = ctx.enter_context(nc.sbuf_tensor("x", [P, TILES, DIM], F32))
        self.xn = ctx.enter_context(nc.sbuf_tensor("xn", [P, TILES, DIM], F32))
        self.xT = ctx.enter_context(nc.sbuf_tensor("xT", [P, TOKENS], F32))
        self.ident = ctx.enter_context(nc.sbuf_tensor("ident", [P, P], F32))
        self.ln_a = ctx.enter_context(nc.sbuf_tensor("ln_a", [P, TILES], F32))
        self.ln_b = ctx.enter_context(nc.sbuf_tensor("ln_b", [P, TILES], F32))
        floats = 45600
        self.arena = Arena(ctx.enter_context(nc.sbuf_tensor("arena", [P, floats], F32)), floats)
        self.ps = ctx.enter_context(nc.psum_tensor("ps", [P, 8, 512], F32))
        self.sems, self.blocks = {}, 0

    def sem(self, name):
        if name not in self.sems:
            self.sems[name] = self.ctx.enter_context(self.nc.semaphore(name))
        return self.sems[name]


def bc(ap, n):
    return ap.unsqueeze(2).broadcast_to([ap.shape[0], ap.shape[1], n])


def hold(k, eng, name, value):
    eng.wait_ge(k.sem(name), value)
    eng.sem_inc(k.sem("holds"), 1)



def norm_dve(k, v, n, src, dst, sq, eps=LN_EPS, center=True):
    if center:
        v.drain()
        v.tensor_reduce(k.ln_a[:, :], src, X_AXIS, ALU.add)
        v.drain()
        v.tensor_scalar(k.ln_a[:, :], k.ln_a[:, :], -1.0 / DIM, None, ALU.mult)
        v.drain()
        v.tensor_tensor(dst, src, bc(k.ln_a[:, :], DIM), ALU.add).then_inc(k.sem("ln_centered"), 1)
    else:
        v.drain()
        v.tensor_copy(dst, src).then_inc(k.sem("ln_centered"), 1)
    v.wait_ge(k.sem("ln_squared"), n + 1)
    v.tensor_reduce(k.ln_a[:, :], sq, X_AXIS, ALU.add)
    v.drain()
    v.tensor_scalar(k.ln_a[:, :], k.ln_a[:, :], 1.0 / DIM, eps, ALU.mult, ALU.add).then_inc(k.sem("ln_var"), 1)
    v.wait_ge(k.sem("ln_sd"), n + 1)
    v.reciprocal(k.ln_b[:, :], k.ln_b[:, :])
    v.drain()
    v.tensor_tensor(dst, dst, bc(k.ln_b[:, :], DIM), ALU.mult).then_inc(k.sem("ln_done"), 1)


def norm_act(k, a, n, dst, sq):
    a.wait_ge(k.sem("ln_centered"), n + 1)
    a.activation(sq, dst, ACT.Square).then_inc(k.sem("ln_squared"), 1)
    a.wait_ge(k.sem("ln_var"), n + 1)
    a.activation(k.ln_b[:, :], k.ln_a[:, :], ACT.Sqrt).then_inc(k.sem("ln_sd"), 1)


def transpose_pe(k, pe, n, src):
    for g in range(GROUPS):
        for j in range(TPG):
            t = pe.transpose(k.ps[:, g, j * P:(j + 1) * P], src[:, g * TPG + j, :], k.ident[:, :])
        t.then_inc(k.sem("ln_transposed"), 1)


def transpose_act(k, a, n, dst, gain=None, shift=None):
    for g in range(GROUPS):
        a.wait_ge(k.sem("ln_transposed"), n * GROUPS + g + 1)
        to = dst[:, g * GROUP:(g + 1) * GROUP]
        if gain is None:
            a.activation(to, k.ps[:, g, :], ACT.Copy).then_inc(k.sem("xT_ready"), 1)
        else:
            a.activation(to, k.ps[:, g, :], ACT.Identity, bias=shift, scale=gain).then_inc(k.sem("xT_ready"), 1)



def add_back_act(k, a, n, yT, scale):
    for g in range(GROUPS):
        a.activation(yT[:, g * GROUP:(g + 1) * GROUP], k.ps[:, g, :], ACT.Copy, scale=scale)\
            .then_inc(k.sem("y_evacuated"), 1)


def add_back_pe(k, pe, n, yT):
    for g in range(GROUPS):
        pe.wait_ge(k.sem("y_evacuated"), n * GROUPS + g + 1)
        for j in range(TPG):
            t = pe.transpose(k.ps[:, 4 + g, j * P:(j + 1) * P],
                             yT[:, g * GROUP + j * P:g * GROUP + (j + 1) * P], k.ident[:, :])
        t.then_inc(k.sem("y_back"), 1)


def add_back_dve(k, v, n):
    for g in range(GROUPS):
        v.wait_ge(k.sem("y_back"), n * GROUPS + g + 1)
        xg = k.x[:, g * TPG:(g + 1) * TPG, :]
        done = v.tensor_tensor(xg, k.ps[:, 4 + g, :].rearrange("p (a b) -> p a b", a=TPG), xg, ALU.add)
    done.then_inc(k.sem("x_updated"), 1)



def gate_logits_pe(k, pe, n, gate_w, experts):
    pe.wait_ge(k.sem("xT_ready"), (n + 1) * GROUPS)
    for t in range(TILES):
        m = pe.matmul(k.ps[:, 4, t * experts:(t + 1) * experts], k.xT[:, t * P:(t + 1) * P], gate_w,
                      start=True, stop=True)
    m.then_inc(k.sem("gate_logits"), 1)


def first_of_largest(k, v, cur, best, mask, rank, top):
    experts = cur.shape[2]
    v.drain()
    v.tensor_reduce(best, cur, X_AXIS, ALU.max)
    v.drain()
    v.tensor_tensor(mask, cur, bc(best, experts), ALU.is_ge)
    v.drain()
    v.tensor_tensor(mask, mask, rank[:, 0:experts].unsqueeze(1).broadcast_to([P, TILES, experts]), ALU.mult)
    v.drain()
    v.tensor_reduce(top, mask, X_AXIS, ALU.max)
    v.drain()
    v.tensor_tensor(mask, mask, bc(top, experts), ALU.is_equal)
    v.drain()


def gates_out_pe(k, pe, n, gates, chunks):
    pe.wait_ge(k.sem("gates_ready"), n + 1)
    flat = gates.rearrange("p e t -> p (e t)")
    for c in range(chunks):
        t = pe.transpose(k.ps[:, 5, c * P:(c + 1) * P], flat[:, c * P:(c + 1) * P], k.ident[:, :])
    t.then_inc(k.sem("gates_turned"), 1)


def gates_out_act(k, a, n, rows, chunks, dram_count, pairs_before):
    a.wait_ge(k.sem("gates_turned"), n + 1)
    a.activation(rows, k.ps[:, 5, 0:chunks * P], ACT.Copy).then_inc(k.sem("gate_rows"), 1)
    a.wait_ge(k.sem("gate_rows"), n + 1)
    dst = k.gates_dram[0:chunks * P, :].rearrange("(c q) p -> q c p", c=chunks)
    a.dma_start(dst, rows.rearrange("q (c p) -> q c p", c=chunks)).then_inc(k.sem("gates_stored"), 16)



E0, F0 = 8, 512
C0 = F0 // P
W0_COLS = F0 + F0 + C0


def relu_moe_layout(k):
    a = k.arena
    a.reset()
    b = {}
    b["yT"] = a.take(TOKENS)
    b["sq"] = b["yT"].rearrange("p (a b) -> p a b", a=TILES)
    b["gate_w"] = a.take(E0)
    b["rank"] = a.take(32)
    b["b2"] = a.take(P)[0:E0, :]
    b["gateT"] = a.take(TOKENS)[0:E0, :]
    b["logits"] = a.take(TILES, E0)
    b["mask"] = a.take(TILES, E0)
    b["gates"] = a.take(E0, TILES)
    b["best"], b["top"], b["sum"] = a.take(TILES), a.take(TILES), a.take(TILES)
    b["rows"] = a.take(P)
    b["w"] = a.take(2, W0_COLS)
    b["gb"] = a.take(2, TOKENS)
    b["relu"] = a.take(4, GROUP)
    b["hid"] = a.take(4, GROUP)
    return b


STEPS0 = GROUPS * C0


def relu_moe_sync(k, sp, m, n, ln):
    b = relu_moe_layout(k)
    sp.wait_ge(k.sem("x_updated"), m + 1)
    sp.dma_start(b["gate_w"], k.ins["l0_gate_w"]).then_inc(k.sem("moe0_gate_w"), 16)
    sp.dma_start(b["rank"], k.ins["rank"].partition_broadcast(P)).then_inc(k.sem("moe0_gate_w"), 16)
    sp.dma_start(b["b2"], k.ins["l0_b2"]).then_inc(k.sem("moe0_gate_w"), 16)
    sp.wait_ge(k.sem("gates_stored"), 16 * (k.gate_stores[m] + 1))
    sp.dma_start(b["gateT"], k.gates_dram[0:E0 * TILES, :].rearrange("(e t) p -> e (t p)", e=E0))\
        .then_inc(k.sem("moe0_gateT"), 16)
    base = n * E0 * STEPS0

    def load(s, e):
        sp.dma_start(b["w"][:, s, :], k.ins["l0_w"][bass.ds(e, 1), :, :].rearrange("a p c -> (a p) c"))\
            .then_inc(k.sem(f"moe0_w{s}"), 16)
        sp.dma_start(b["gb"][:, s, :], k.gates_dram[bass.ds(e * TILES, TILES), :]
                     .rearrange("t p -> (t p)").partition_broadcast(P)).then_inc(k.sem(f"moe0_w{s}"), 16)

    load(0, 0)
    load(1, 1)
    with sp.Fori(0, E0 // 2 - 1) as i:
        for s in range(2):
            sp.wait_ge(k.sem("moe0_down"), ONE + base + i * (2 * STEPS0) + (s + 1) * STEPS0)
            load(s, i * 2 + (2 + s))


def relu_moe_pe(k, pe, m, n, ln):
    b = relu_moe_layout(k)
    pe.wait_ge(k.sem("ln_done"), ln + 1)
    transpose_pe(k, pe, ln, k.xn)
    pe.wait_ge(k.sem("moe0_gate_w"), 48 * (n + 1))
    gate_logits_pe(k, pe, k.xt_calls[m], b["gate_w"], E0)
    gates_out_pe(k, pe, k.gate_stores[m], b["gates"], 1)
    pe.wait_ge(k.sem("gate_rows"), k.gate_stores[m] + 1)
    pe.wait_ge(k.sem("moe0_gateT"), 16 * (n + 1))
    for g in range(GROUPS):
        pe.matmul(k.ps[:, g, :], b["b2"], b["gateT"][:, g * GROUP:(g + 1) * GROUP], start=True, stop=True)
    base = n * E0 * STEPS0
    wbase = 16 * E0 * n
    with pe.Fori(0, E0 // 2) as i:
        for s in range(2):
            at = base + i * (2 * STEPS0) + s * STEPS0
            w = b["w"][:, s, :]
            pe.wait_ge(k.sem(f"moe0_w{s}"), wbase + 32 * i + 32)

            def up(step):
                g, c = divmod(step, C0)
                if step >= 4:
                    pe.wait_ge(k.sem("moe0_relu"), at + step - 3)
                pe.matmul(k.ps[:, 4 + step % 4, :], w[:, c * P:(c + 1) * P],
                          k.xT[:, g * GROUP:(g + 1) * GROUP], start=True, stop=True)\
                    .then_inc(k.sem("moe0_up"), 1)

            for step in range(3):
                up(step)
            for step in range(STEPS0):
                if step + 3 < STEPS0:
                    up(step + 3)
                g, c = divmod(step, C0)
                pe.wait_ge(k.sem("moe0_hidden"), ONE + at + step + 1)
                pe.matmul(k.ps[:, g, :], w[:, F0 + c * P:F0 + (c + 1) * P], b["hid"][:, step % 4, :],
                          start=False, stop=True, skip_group_check=True).then_inc(k.sem("moe0_down"), 1)
    add_back_pe(k, pe, k.back_calls[m], b["yT"])


def relu_moe_act(k, a, m, n, ln):
    b = relu_moe_layout(k)
    norm_act(k, a, ln, k.xn[:, :, :], b["sq"])
    transpose_act(k, a, k.xt_calls[m], k.xT)
    a.wait_ge(k.sem("gate_shifted"), n + 1)
    a.activation(b["logits"], b["logits"], ACT.Exp).then_inc(k.sem("gate_exp"), 1)
    gates_out_act(k, a, k.gate_stores[m], b["rows"], 1, None, None)
    base = n * E0 * STEPS0
    with a.Fori(0, E0 // 2) as i:
        for s in range(2):
            at = base + i * (2 * STEPS0) + s * STEPS0
            a.wait_ge(k.sem("moe0_hidden"), ONE + at)
            for step in range(STEPS0):
                c = step % C0
                a.wait_ge(k.sem("moe0_up"), at + step + 1)
                if step >= 4:
                    a.wait_ge(k.sem("moe0_hidden"), ONE + at + step - 3)
                a.activation(b["relu"][:, step % 4, :], k.ps[:, 4 + step % 4, :], ACT.Relu,
                             bias=b["w"][:, s, 2 * F0 + c:2 * F0 + c + 1]).then_inc(k.sem("moe0_relu"), 1)
    a.wait_ge(k.sem("moe0_down"), ONE + base + E0 * STEPS0)
    add_back_act(k, a, k.back_calls[m], b["yT"], 0.5)


def relu_moe_dve(k, v, m, n, ln):
    b = relu_moe_layout(k)
    norm_dve(k, v, ln, k.x[:, :, :], k.xn[:, :, :], b["sq"])
    gc = k.gate_calls[m]
    v.wait_ge(k.sem("gate_logits"), gc + 1)
    v.tensor_copy(b["logits"], k.ps[:, 4, 0:TILES * E0].rearrange("p (t e) -> p t e", t=TILES))
    first_of_largest(k, v, b["logits"], b["best"], b["mask"], b["rank"], b["top"])
    v.tensor_tensor(b["logits"], b["logits"], bc(b["best"], E0), ALU.subtract).then_inc(k.sem("gate_shifted"), 1)
    v.wait_ge(k.sem("gate_exp"), n + 1)
    v.tensor_reduce(b["sum"], b["logits"], X_AXIS, ALU.add)
    v.drain()
    v.reciprocal(b["sum"], b["sum"])
    v.drain()
    v.tensor_tensor(b["gates"].rearrange("p e t -> p t e"), b["mask"], bc(b["sum"], E0), ALU.mult)\
        .then_inc(k.sem("gates_ready"), 1)
    base = n * E0 * STEPS0
    wbase = 16 * E0 * n
    with v.Fori(0, E0 // 2) as i:
        for s in range(2):
            at = base + i * (2 * STEPS0) + s * STEPS0
            v.wait_ge(k.sem(f"moe0_w{s}"), wbase + 32 * i + 32)
            v.wait_ge(k.sem("moe0_down"), ONE + at)
            for step in range(STEPS0):
                g = step // C0
                v.wait_ge(k.sem("moe0_relu"), at + step + 1)
                if step >= 4:
                    v.wait_ge(k.sem("moe0_down"), ONE + at + step - 3)
                v.tensor_tensor(b["hid"][:, step % 4, :], b["relu"][:, step % 4, :],
                                b["gb"][:, s, g * GROUP:(g + 1) * GROUP], ALU.mult)\
                    .then_inc(k.sem("moe0_hidden"), 1)
    add_back_dve(k, v, k.back_calls[m])



HD0, HD1 = 64, 8
HEADS = 16
STEPS = 8
ITS = BATCH * HEADS // 2
KTILES = SEQ // P
SPAN = SEQ + KTILES * P - P


class Attention:
    def __init__(self, name, blocks, width, causal=False, bias=False):
        self.name, self.blocks, self.width, self.causal, self.bias = name, blocks, width, causal, bias
        self.heads = P // width
        self.pairs = self.heads // 2


A0 = Attention("a0", 8, HD0)
A1 = Attention("a1", 1, HD1, bias=True)
A3 = Attention("a3", 1, HD1, causal=True)


def attention_layout(k, c):
    a = k.arena
    a.reset()
    b = {}
    b["w"] = a.take(3 * P)
    b["mask"] = a.take(c.heads)
    b["q"], b["k"] = a.take(TOKENS), a.take(TOKENS)
    b["v"] = a.take(TILES, P)
    b["qm"] = a.take(2, SEQ)
    b["p"] = a.take(2, SEQ)
    b["pT"] = a.take(2, SEQ)
    b["negmax"], b["sum"] = a.take(STEPS), a.take(STEPS)
    b["att"] = a.take(TILES, c.blocks * P)
    b["w_out"] = a.take(c.blocks, P)
    b["tri"] = a.take(P)
    if c.bias:
        b["s"] = a.take(2, SEQ)
        b["toeplitz"] = a.take(2, SPAN)
        b["v_bias"], b["out_bias"] = a.take(P), a.take(P)
        b["vec"] = a.take(4)
        b["w_rel"] = a.take(HEADS)[0:HD1, :]
        b["rel_pe"] = a.take(2 * SEQ)[0:HD1, :]
        b["rel"] = a.take(2 * SEQ)[0:HEADS, :]
    if c.blocks > 1:
        b["gelu"] = a.take(2, c.blocks * P)
        b["gT"] = a.take(2, c.blocks * P)
    else:
        b["attT"] = a.take(TOKENS)
    b["sq"] = b["p"].rearrange("p a b -> p (a b)")
    b["sq"] = b["v"]
    return b


def attention_sync(k, sp, m, n, ln, c):
    b = attention_layout(k, c)
    w = k.ins[c.name + "_w"]
    sp.wait_ge(k.sem("x_updated"), m + 1)
    ready = k.sem(c.name + "_loaded")
    sp.dma_start(b["mask"], k.ins[c.name + "_mask"]).then_inc(ready, 16)
    sp.dma_start(b["w_out"], k.ins[c.name + "_w_out"]).then_inc(ready, 16)
    sp.dma_start(b["tri"], k.ins["tri"]).then_inc(ready, 16)
    weights = k.sem("att_w")
    wb = k.att_blocks[m]

    def load(i):
        sp.dma_start(b["w"], w[bass.ds(i, 1), :, :].rearrange("a p c -> (a p) c")).then_inc(weights, 16)

    load(0)
    if c.blocks > 1:
        with sp.Fori(0, c.blocks - 1) as i:
            sp.wait_ge(k.sem("v_projected"), (wb + 1) * GROUPS + i * GROUPS)
            load(i + 1)
    if c.bias:
        sp.dma_start(b["vec"], k.ins["a1_vec"]).then_inc(ready, 16)
        sp.dma_start(b["v_bias"], k.ins["a1_v_bias"].partition_broadcast(P)).then_inc(ready, 16)
        sp.dma_start(b["out_bias"], k.ins["a1_out_bias"].partition_broadcast(P)).then_inc(ready, 16)
        sp.dma_start(b["w_rel"], k.ins["a1_w_rel"]).then_inc(k.sem("rel_loaded"), 16)
        sp.dma_start(b["rel_pe"], k.ins["rel_pe"]).then_inc(k.sem("rel_loaded"), 16)
        sp.wait_ge(k.sem("rel_ready"), 1)
        sp.dma_start(k.rel_dram, b["rel"]).then_inc(k.sem("rel_stored"), 16)
        sp.wait_ge(k.sem("rel_stored"), 16)
        shifted = bass.AP(tensor=k.rel_dram.tensor, offset=k.rel_dram.offset + P - 1,
                          ap=[[2 * SEQ, HEADS], [-1, P], [1, SPAN]])
        sp.dma_start(k.toeplitz_dram, shifted).then_inc(k.sem("toeplitz_stored"), 16)
        sp.wait_ge(k.sem("toeplitz_stored"), 16)
        at = k.att_calls[m] * ITS
        with sp.Fori(0, BATCH) as bt:
            with sp.Fori(0, c.pairs) as hp:
                for s in range(2):
                    sp.wait_ge(k.sem("toeplitz_used"), (bt * c.pairs + hp) * 2 + (s + 1))
                    src = k.toeplitz_dram[bass.ds(hp * 2 + s, 1), :, :].rearrange("h p m -> (h p) m")
                    sp.dma_start(b["toeplitz"][:, s, :], src).then_inc(k.sem(f"toeplitz{s}"), 16)


def attention_pe(k, pe, m, n, ln, c):
    b = attention_layout(k, c)
    at0, wb = k.att_calls[m] * ITS, k.att_blocks[m]
    pe.wait_ge(k.sem("ln_done"), ln + (2 if c.bias else 1))
    transpose_pe(k, pe, ln, k.xn)
    pe.wait_ge(k.sem("xT_ready"), (k.xt_calls[m] + 1) * GROUPS)
    if c.bias:
        pe.wait_ge(k.sem("rel_loaded"), 32)
        for h in range(2):
            r = pe.matmul(k.ps[0:HEADS, 6 + h, :], b["w_rel"], b["rel_pe"][:, h * SEQ:(h + 1) * SEQ],
                          start=True, stop=True)
        r.then_inc(k.sem("rel_multiplied"), 1)
        pe.wait_ge(k.sem("rel_ready"), 1)
    pe.wait_ge(k.sem(c.name + "_loaded"), 16 * (6 if c.bias else 3))

    def block_of_heads(blk):
        pe.wait_ge(k.sem("att_w"), 16 * (wb + 1) + 16 * blk)
        pe.wait_ge(k.sem("heads_done"), ONE + 2 * at0 + blk * (2 * BATCH * c.pairs))
        for g in range(GROUPS):
            xg = k.xT[:, g * GROUP:(g + 1) * GROUP]
            pe.matmul(k.ps[:, g, :], b["w"][:, 0:P], xg, start=True, stop=True).then_inc(k.sem("qk_projected"), 1)
            pe.matmul(k.ps[:, 4 + g, :], b["w"][:, P:2 * P], xg, start=True, stop=True)\
                .then_inc(k.sem("qk_projected"), 1)
        for g in range(GROUPS):
            pe.wait_ge(k.sem("qk_ready"), 8 * wb + 2 * g + 1 + 8 * blk)
            for j in range(TPG):
                t = g * TPG + j
                o = pe.matmul(k.ps[:, g, j * P:(j + 1) * P], k.xT[:, t * P:(t + 1) * P], b["w"][:, 2 * P:3 * P],
                              start=True, stop=True)
            o.then_inc(k.sem("v_projected"), 1)
        pe.wait_ge(k.sem("qk_ready"), 8 * (wb + 1) + 8 * blk)
        hold(k, pe, "v_ready", GROUPS * (wb + 1) + GROUPS * blk)

    def core(it, bt):
        at = it * STEPS

        def scores(step):
            s, j = divmod(step, KTILES)
            if j == 0:
                pe.wait_ge(k.sem("queries_masked"), it * 2 + (s + 1))
            if step >= 2:
                if c.bias:
                    pe.wait_ge(k.sem("maxima"), at + (step - 1))
                else:
                    pe.wait_ge(k.sem("probs"), ONE + at + (step - 1))

            cols = (j + 1) * P if c.causal else SEQ
            o = pe.matmul(k.ps[:, step % 2, 0:cols], b["qm"][:, s, j * P:(j + 1) * P],
                          b["k"][:, bass.ds(bt * SEQ, cols)], start=True, stop=not c.causal)
            if c.causal:
                o = pe.matmul(k.ps[:, step % 2, j * P:(j + 1) * P], k.ident[:, :], b["tri"],
                              start=False, stop=True)
            o.then_inc(k.sem("scores"), 1)

        def turn(step):
            tiles = step % KTILES + 1 if c.causal else KTILES
            pe.wait_ge(k.sem("probs"), ONE + at + (step + 1))
            if step >= 2:
                pe.wait_ge(k.sem("probs_copied"), at + (step - 1))
            for t in range(tiles):
                o = pe.transpose(k.ps[:, 2 + step % 2, t * P:(t + 1) * P],
                                 b["p"][:, step % 2, t * P:(t + 1) * P], k.ident[:, :])
            o.then_inc(k.sem("probs_turned"), 1)

        def values(step, head):
            s, j = divmod(step, KTILES)
            tiles = j + 1 if c.causal else KTILES
            pe.wait_ge(k.sem("probs_copied"), at + (step + 1))
            for t in range(tiles):
                o = pe.matmul(k.ps[:, 4 + s, j * c.width:(j + 1) * c.width],
                              b["pT"][:, step % 2, t * P:(t + 1) * P],
                              b["v"].rearrange("p t d -> p (t d)")[:, bass.ds(bt * SEQ + t * P + head * c.width, c.width)],
                              start=(t == 0), stop=(t == tiles - 1))
            o.then_inc(k.sem("values"), 1)
        return scores, turn, values

    def iteration(it, bt, pair):
        scores, turn, values = core(it, bt)
        pe.wait_ge(k.sem("heads_done"), ONE + it * 2)
        scores(0)
        scores(1)
        for step in range(STEPS):
            turn(step)
            if step + 2 < STEPS:
                scores(step + 2)
            if step >= 1:
                values(step - 1, pair * 2 + (step - 1) // KTILES)
        values(STEPS - 1, pair * 2 + 1)

    if c.blocks > 1:
        with pe.Fori(0, c.blocks) as blk:
            block_of_heads(blk)
            with pe.Fori(0, BATCH) as bt:
                iteration(at0 + blk * BATCH + bt, bt, 0)
    else:
        block_of_heads(0)
        with pe.Fori(0, BATCH) as bt:
            with pe.Fori(0, c.pairs) as hp:
                iteration(at0 + bt * c.pairs + hp, bt, hp)

    pe.wait_ge(k.sem("heads_done"), ONE + 2 * (at0 + ITS))
    if c.blocks > 1:
        with pe.Fori(0, TILES // 2) as i:
            for s in range(2):
                pe.wait_ge(k.sem("att_gelu"), i * 2 + (s + 1))
                for h in range(2):
                    for j in range(4):
                        cc = 4 * h + j
                        o = pe.transpose(k.ps[:, 2 * s + h, j * P:(j + 1) * P],
                                         b["gelu"][:, s, cc * P:(cc + 1) * P], k.ident[:, :])
                    o.then_inc(k.sem("gelu_turned"), 1)
            for s in range(2):
                pe.wait_ge(k.sem("gelu_copied"), i * 4 + (2 * s + 2))
                pe.wait_ge(k.sem("att_added"), ONE + i * 2)
                for cc in range(c.blocks):
                    o = pe.matmul(k.ps[:, 4 + s, 0:P], b["gT"][:, s, cc * P:(cc + 1) * P], b["w_out"][:, cc, :],
                                  start=(cc == 0), stop=(cc == c.blocks - 1))
                o.then_inc(k.sem("att_projected"), 1)
    else:
        for g in range(GROUPS):
            for j in range(TPG):
                t = g * TPG + j
                o = pe.transpose(k.ps[:, g, j * P:(j + 1) * P], b["att"][:, t, :], k.ident[:, :])
            o.then_inc(k.sem("att_turned"), 1)
        for g in range(GROUPS):
            pe.wait_ge(k.sem("att_copied"), (n + k.flat_calls[m]) * GROUPS + g + 1)
            for j in range(TPG):
                t = g * TPG + j
                o = pe.matmul(k.ps[:, 4 + g, j * P:(j + 1) * P], b["attT"][:, t * P:(t + 1) * P], b["w_out"][:, 0, :],
                              start=True, stop=True)
            o.then_inc(k.sem("flat_projected"), 1)


def attention_act(k, a, m, n, ln, c):
    b = attention_layout(k, c)
    at0, wb = k.att_calls[m] * ITS, k.att_blocks[m]
    norm_act(k, a, ln, k.xn[:, :, :], b["sq"])
    if c.bias:
        norm_act(k, a, ln + 1, k.xn[:, :, :], b["sq"])
        a.wait_ge(k.sem("a1_loaded"), 16 * 6)
        transpose_act(k, a, k.xt_calls[m], k.xT, b["vec"][:, 0:1], b["vec"][:, 1:2])
        a.wait_ge(k.sem("rel_multiplied"), 1)
        a.activation(b["rel"].rearrange("h (a b) -> h a b", a=2), k.ps[0:HEADS, 6:8, :], ACT.Copy)\
            .then_inc(k.sem("rel_ready"), 1)
    else:
        transpose_act(k, a, k.xt_calls[m], k.xT)

    def block_of_heads(blk):
        a.wait_ge(k.sem("heads_done"), ONE + 2 * at0 + blk * (2 * BATCH * c.pairs))
        for g in range(GROUPS):
            for half, dst in enumerate((b["q"], b["k"])):
                a.wait_ge(k.sem("qk_projected"), 8 * wb + 2 * g + half + 1 + 8 * blk)
                to, src = dst[:, g * GROUP:(g + 1) * GROUP], k.ps[:, 4 * half + g, :]
                if c.bias:
                    o = a.activation(to, src, ACT.Identity, bias=b["vec"][:, 2 + half:3 + half])
                else:
                    o = a.activation(to, src, ACT.Copy)
                o.then_inc(k.sem("qk_ready"), 1)

    def iteration(it):
        at = it * STEPS
        a.wait_ge(k.sem("probs_turned"), ONE + at)
        for step in range(STEPS):
            cols = (step % KTILES + 1) * P if c.causal else SEQ
            a.wait_ge(k.sem("maxima"), at + (step + 1))
            if step >= 2:
                a.wait_ge(k.sem("probs_turned"), ONE + at + (step - 1))
            src = b["s"][:, step % 2, :] if c.bias else k.ps[:, step % 2, 0:cols]
            a.activation(b["p"][:, step % 2, 0:cols], src, ACT.Exp, bias=b["negmax"][:, step:step + 1],
                         scale=-1.0 if c.bias else 1.0, accum_out=b["sum"][:, step:step + 1])\
                .then_inc(k.sem("probs"), 1)

    if c.blocks > 1:
        with a.Fori(0, c.blocks) as blk:
            block_of_heads(blk)
            with a.Fori(0, BATCH) as bt:
                iteration(at0 + blk * BATCH + bt)
    else:
        block_of_heads(0)
        with a.Fori(0, ITS) as i:
            iteration(at0 + i)

    a.wait_ge(k.sem("heads_done"), ONE + 2 * (at0 + ITS))
    if c.blocks > 1:
        with a.Fori(0, TILES // 2) as i:
            for s in range(2):
                a.wait_ge(k.sem("gelu_turned"), ONE + i * 4)
                a.activation(b["gelu"][:, s, :], b["att"][:, bass.ds(i * 2 + s, 1), :].rearrange("p a c -> p (a c)"),
                             ACT.Gelu).then_inc(k.sem("att_gelu"), 1)
            for s in range(2):
                for h in range(2):
                    a.wait_ge(k.sem("gelu_turned"), ONE + i * 4 + (2 * s + h + 1))
                    if s == 0 and h == 0:
                        a.wait_ge(k.sem("att_projected"), ONE + i * 2)
                    a.activation(b["gT"][:, s, h * 512:(h + 1) * 512], k.ps[:, 2 * s + h, :], ACT.Copy)\
                        .then_inc(k.sem("gelu_copied"), 1)
    else:
        for g in range(GROUPS):
            a.wait_ge(k.sem("att_turned"), (n + k.flat_calls[m]) * GROUPS + g + 1)
            a.activation(b["attT"][:, g * GROUP:(g + 1) * GROUP], k.ps[:, g, :], ACT.Copy)\
                .then_inc(k.sem("att_copied"), 1)


def attention_dve(k, v, m, n, ln, c):
    b = attention_layout(k, c)
    at0, wb = k.att_calls[m] * ITS, k.att_blocks[m]
    norm_dve(k, v, ln, k.x[:, :, :], k.xn[:, :, :], b["sq"])
    if c.bias:
        norm_dve(k, v, ln + 1, k.xn[:, :, :], k.xn[:, :, :], b["sq"])
    v.wait_ge(k.sem(c.name + "_loaded"), 16 * (6 if c.bias else 3))

    def block_of_heads(blk):
        for g in range(GROUPS):
            v.wait_ge(k.sem("v_projected"), GROUPS * wb + g + 1 + GROUPS * blk)
            to, src = b["v"][:, g * TPG:(g + 1) * TPG, :], k.ps[:, g, :].rearrange("p (a b) -> p a b", a=TPG)
            if c.bias:
                o = v.tensor_tensor(to, src, b["v_bias"].unsqueeze(1).broadcast_to([P, TPG, P]), ALU.add)
            else:
                o = v.tensor_copy(to, src)
            o.then_inc(k.sem("v_ready"), 1)
        hold(k, v, "qk_ready", 8 * (wb + 1) + 8 * blk)

    def iteration(it, blk, bt, pair):
        at = it * STEPS

        def mask(s):
            v.tensor_scalar(b["qm"][:, s, :], b["q"][:, bass.ds(bt * SEQ, SEQ)],
                            b["mask"][:, bass.ds(pair * 2 + s, 1)], None, ALU.mult)\
                .then_inc(k.sem("queries_masked"), 1)

        def maximum(step):
            s, j = divmod(step, KTILES)
            cols = (j + 1) * P if c.causal else SEQ
            if not c.bias:
                v.wait_ge(k.sem("scores"), at + (step + 1))
            if c.bias:
                if j == 0:
                    v.wait_ge(k.sem(f"toeplitz{s}"), 16 + (it - at0) * 16)
                if step >= 2:
                    v.wait_ge(k.sem("probs"), ONE + at + (step - 1))
                hold(k, v, "scores", at + (step + 1))
                v.tensor_tensor_reduce(b["s"][:, step % 2, :], k.ps[:, step % 2, :],
                                       b["toeplitz"][:, s, 384 - j * P:384 - j * P + SEQ], -1.0, 3.0e38,
                                       ALU.add, ALU.min, b["negmax"][:, step:step + 1])\
                    .then_inc(k.sem("maxima"), 1)
                if j == KTILES - 1:
                    v.wait_ge(k.sem("maxima"), at + (step + 1))
                    v.sem_inc(k.sem("toeplitz_used"), 1)
            else:
                v.tensor_reduce(b["negmax"][:, step:step + 1], k.ps[:, step % 2, 0:cols], X_AXIS, ALU.max,
                                negate=True).then_inc(k.sem("maxima"), 1)

        def copy(step):
            cols = (step % KTILES + 1) * P if c.causal else SEQ
            v.wait_ge(k.sem("probs_turned"), ONE + at + (step + 1))
            if step >= 2:
                v.wait_ge(k.sem("values"), ONE + at + (step - 1))
            v.tensor_copy(b["pT"][:, step % 2, 0:cols], k.ps[:, 2 + step % 2, 0:cols])\
                .then_inc(k.sem("probs_copied"), 1)

        def finish(s):
            v.wait_ge(k.sem("values"), ONE + at + (4 * s + 4))
            v.reciprocal(b["sum"][:, 4 * s:4 * s + 4], b["sum"][:, 4 * s:4 * s + 4])
            v.drain()
            out = b["att"][:, bass.ds(bt * KTILES, KTILES), bass.ds(blk * P + (pair * 2 + s) * c.width, c.width)]
            v.tensor_tensor(out, k.ps[:, 4 + s, 0:KTILES * c.width].rearrange("p (a b) -> p a b", a=KTILES),
                            bc(b["sum"][:, 4 * s:4 * s + 4], c.width), ALU.mult).then_inc(k.sem("heads_done"), 1)

        v.wait_ge(k.sem("probs"), ONE + at)
        v.wait_ge(k.sem("values"), ONE + at)
        mask(0)
        mask(1)
        maximum(0)
        maximum(1)
        for step in range(STEPS):
            copy(step)
            if step + 2 < STEPS:
                maximum(step + 2)
            if step == 5:
                finish(0)
        finish(1)

    if c.bias:
        v.sem_inc(k.sem("toeplitz_used"), 2)
    if c.blocks > 1:
        with v.Fori(0, c.blocks) as blk:
            block_of_heads(blk)
            with v.Fori(0, BATCH) as bt:
                iteration(at0 + blk * BATCH + bt, blk, bt, 0)
        v.tensor_tensor(k.x[:, :, :], k.x[:, :, :], k.xn[:, :, :], ALU.add)
        with v.Fori(0, TILES // 2) as i:
            for s in range(2):
                xt = k.x[:, bass.ds(i * 2 + s, 1), :].rearrange("p a d -> p (a d)")
                v.drain()
                v.wait_ge(k.sem("att_projected"), ONE + i * 2 + (s + 1))
                v.tensor_tensor(xt, k.ps[:, 4 + s, 0:P], xt, ALU.add).then_inc(k.sem("att_added"), 1)
        v.drain()
        v.tensor_copy(k.ln_a[:, :], k.x[:, :, 0]).then_inc(k.sem("x_updated"), 1)
    else:
        block_of_heads(0)
        with v.Fori(0, BATCH) as bt:
            with v.Fori(0, c.pairs) as hp:
                iteration(at0 + bt * c.pairs + hp, 0, bt, hp)
        if c.bias:
            v.tensor_tensor(k.x[:, :, :], k.x[:, :, :], b["out_bias"].unsqueeze(1).broadcast_to([P, TILES, P]), ALU.add)
            v.drain()
        for g in range(GROUPS):
            v.wait_ge(k.sem("flat_projected"), (n + k.flat_calls[m]) * GROUPS + g + 1)
            xg = k.x[:, g * TPG:(g + 1) * TPG, :]
            o = v.tensor_tensor(xg, k.ps[:, 4 + g, :].rearrange("p (a b) -> p a b", a=TPG), xg, ALU.add)
        o.then_inc(k.sem("x_updated"), 1)


def lay_out_attention(a, i):
    import numpy as _np

    c, f = _np.ascontiguousarray, _np.float32
    feature = _np.arange(P)
    for at, n in ((A0, "a0"), (A1, "a1"), (A3, "a3")):
        a[n + "_mask"] = c((feature[:, None] // at.width == _np.arange(at.heads)[None, :]).astype(f)
                           * f(1.0 / math.sqrt(at.width)))
    a["tri"] = _np.where(feature[:, None] >= feature[None, :], f(0), f(-1e30)).astype(f)
    a["a0_w"] = c(_np.stack([i["L0_attn_Wq"], i["L0_attn_Wk"], i["L0_attn_Wv"]]).reshape(3, P, 8, P)
                  .transpose(2, 1, 0, 3).reshape(8, P, 3 * P))
    a["a0_w_out"] = c(i["L0_attn_Wpost"].reshape(8, P, P).transpose(1, 0, 2))
    a["a1_w"] = c(i["L1_attn_w_qkv"][None])
    a["a1_w_out"] = c(i["L1_attn_w_out"].reshape(P, 1, P))
    bq = i["L1_attn_b_qkv"].reshape(3, P)
    a["a1_vec"] = c(_np.stack([i["L1_attn_ln_g"], i["L1_attn_ln_b"], bq[0], bq[1]], axis=1))
    a["a1_v_bias"], a["a1_out_bias"], a["a1_w_rel"] = c(bq[2]), i["L1_attn_b_out"], i["L1_attn_w_rel"]
    a["a3_w"] = c(_np.stack([i["L3_attn_WQ"], i["L3_attn_WK"], i["L3_attn_WV"]]).reshape(3, P, P)
                  .transpose(2, 0, 1).reshape(1, P, 3 * P))
    a["a3_w_out"] = c(i["L3_attn_WO"].transpose(0, 2, 1).reshape(P, 1, P))
    pos = _np.arange(-(SEQ - 1), SEQ, dtype=f)[:, None]
    div = _np.exp(_np.arange(0, HD1, 2, dtype=f) * f(-math.log(10000.0) / HD1)).astype(f)
    angle = (pos * div).astype(_np.float64)
    pe = _np.zeros((2 * SEQ, HD1), f)
    pe[:2 * SEQ - 1, 0::2], pe[:2 * SEQ - 1, 1::2] = _np.sin(angle)[::-1], _np.cos(angle)[::-1]
    a["rel_pe"] = c(pe.T)



E2, F2 = 8, 512
C2 = F2 // P
W2_COLS = 3 * F2
STEPS2 = GROUPS * C2


def swiglu_layout(k):
    a = k.arena
    a.reset()
    b = {}
    b["small"] = a.take(2 * P + E2 + 32 + 2)
    b["w_in"], b["w_out"] = b["small"][:, 0:P], b["small"][:, P:2 * P]
    b["router"] = b["small"][:, 2 * P:2 * P + E2]
    b["gains"] = b["small"][:, 2 * P + E2 + 32:]
    b["rank"] = a.take(32)
    b["e_bias"] = a.take(E2)
    b["h"] = a.take(TILES, P)
    b["hT"] = a.take(TOKENS)
    b["sq"] = a.take(TILES, P)
    for name in ("logits", "cur", "mask1", "mask2", "pick"):
        b[name] = a.take(TILES, E2)
    b["best"], b["top"] = a.take(TILES), a.take(TILES)
    b["l"] = a.take(2, TILES)
    b["g"] = a.take(2, TILES)
    b["gates"] = a.take(E2, TILES)
    b["ms"], b["factor"] = a.take(TILES), a.take(TILES)
    b["w"] = a.take(2, W2_COLS)
    b["enorm"] = a.take(2, P)
    b["silu"] = a.take(2, GROUP)
    b["hid"] = a.take(2, C2, GROUP)
    b["scaled"] = a.take(TILES, P)
    b["acc"] = a.take(TILES, P)
    return b


def swiglu_sync(k, sp, m, n, ln):
    b = swiglu_layout(k)
    sp.wait_ge(k.sem("x_updated"), m + 1)
    ready = k.sem("moe2_loaded")
    sp.dma_start(b["small"], k.ins["l2_small"]).then_inc(ready, 16)
    sp.dma_start(b["rank"], k.ins["rank"].partition_broadcast(P)).then_inc(ready, 16)
    sp.dma_start(b["e_bias"], k.ins["l2_e_bias"].partition_broadcast(P)).then_inc(ready, 16)

    def load(s, e):
        sp.dma_start(b["w"][:, s, :], k.ins["l2_w"][bass.ds(e, 1), :, :].rearrange("a p c -> (a p) c"))\
            .then_inc(k.sem(f"moe2_w{s}"), 16)
        sp.dma_start(b["enorm"][:, s, :], k.ins["l2_enorm"][bass.ds(e, 1), :].rearrange("a c -> (a c)")
                     .partition_broadcast(P)).then_inc(k.sem(f"moe2_w{s}"), 16)

    load(0, 0)
    load(1, 1)
    with sp.Fori(0, E2 // 2 - 1) as i:
        for s in range(2):
            sp.wait_ge(k.sem("moe2_summed"), n * E2 + i * 2 + (s + 1))
            load(s, i * 2 + (s + 2))


def swiglu_pairs(eng, body):
    body(0, 0, True)
    body(1, 1, False)
    with eng.Fori(1, E2 // 2) as i:
        for s in range(2):
            body(i * 2 + s, s, False)


def project_back_pe(k, pe, b, n, src, w, signal):
    for g in range(GROUPS):
        for j in range(TPG):
            t = g * TPG + j
            o = pe.matmul(k.ps[:, 4 + g, j * P:(j + 1) * P], src[:, t * P:(t + 1) * P], w, start=True, stop=True)
        o.then_inc(k.sem(signal), 1)


def swiglu_pe(k, pe, m, n, ln):
    b = swiglu_layout(k)
    xt = k.xt_calls[m]
    pe.wait_ge(k.sem("ln_done"), ln + 1)
    transpose_pe(k, pe, xt, k.xn)
    pe.wait_ge(k.sem("moe2_loaded"), 48 * (n + 1))
    pe.wait_ge(k.sem("xT_ready"), (xt + 1) * GROUPS)
    project_back_pe(k, pe, b, n, k.xT, b["w_in"], "h_projected")
    pe.wait_ge(k.sem("ln_done"), ln + 2)
    transpose_pe(k, pe, xt + 1, b["h"])
    pe.wait_ge(k.sem("xT_ready"), (xt + 2) * GROUPS)
    for t in range(TILES):
        o = pe.matmul(k.ps[:, 4, t * E2:(t + 1) * E2], b["hT"][:, t * P:(t + 1) * P], b["router"],
                      start=True, stop=True)
    o.then_inc(k.sem("gate_logits"), 1)
    pe.wait_ge(k.sem("logits_copied"), n + 1)

    def body(e, s, first):
        ee = e + n * E2
        w = b["w"][:, s, :]
        if isinstance(e, int):
            pe.wait_ge(k.sem(f"moe2_w{s}"), 16 * E2 * n + 32)
        else:
            pe.wait_ge(k.sem(f"moe2_w{s}"), 16 * E2 * n + (e - s) * 16 + 32)

        def up(g):
            for c in range(C2):
                step = g * C2 + c
                if step >= 2:
                    pe.wait_ge(k.sem("moe2_hidden"), ee * STEPS2 + (step - 1))
                for half in range(2):
                    o = pe.matmul(k.ps[:, 4 + 2 * (step % 2) + half, :],
                                  w[:, half * F2 + c * P:half * F2 + (c + 1) * P],
                                  b["hT"][:, g * GROUP:(g + 1) * GROUP], start=True, stop=True)
                o.then_inc(k.sem("moe2_up"), 1)

        def down(g):
            pe.wait_ge(k.sem("moe2_hidden"), ee * STEPS2 + C2 * (g + 1))
            for j in range(TPG):
                for c in range(C2):
                    o = pe.matmul(k.ps[:, g, j * P:(j + 1) * P], b["hid"][:, g % 2, c, j * P:(j + 1) * P],
                                  w[:, 2 * F2 + c * P:2 * F2 + (c + 1) * P], start=(c == 0), stop=(c == C2 - 1))
            o.then_inc(k.sem("moe2_down"), 1)

        up(0)
        up(1)
        pe.wait_ge(k.sem("moe2_taken"), ee)
        down(0)
        up(2)
        down(1)
        up(3)
        down(2)
        down(3)

    swiglu_pairs(pe, body)
    pe.wait_ge(k.sem("ln_done"), ln + 3)
    transpose_pe(k, pe, xt + 2, b["acc"])
    pe.wait_ge(k.sem("xT_ready"), (xt + 3) * GROUPS)
    project_back_pe(k, pe, b, n, b["hT"], b["w_out"], "out_projected")


def swiglu_act(k, a, m, n, ln):
    b = swiglu_layout(k)
    xt = k.xt_calls[m]
    norm_act(k, a, ln, k.xn[:, :, :], b["sq"])
    transpose_act(k, a, xt, k.xT)
    norm_act(k, a, ln + 1, b["h"], b["sq"])
    a.wait_ge(k.sem("moe2_loaded"), 48 * (n + 1))
    transpose_act(k, a, xt + 1, b["hT"], b["gains"][:, 0:1], 0.0)
    a.wait_ge(k.sem("pair_shifted"), n + 1)
    a.activation(b["g"], b["l"], ACT.Exp).then_inc(k.sem("pair_exp"), 1)

    def output_norm(ee):
        a.wait_ge(k.sem("moe2_down"), ee * GROUPS)
        a.activation(b["sq"].rearrange("p (g a) b -> p g (a b)", g=GROUPS), k.ps[:, 0:4, :], ACT.Square).then_inc(k.sem("moe2_squared"), 1)
        a.wait_ge(k.sem("moe2_mean"), ee)
        a.activation(b["factor"], b["ms"], ACT.Sqrt).then_inc(k.sem("moe2_root"), 1)

    def body(e, s, first):
        ee = e + n * E2
        for step in range(STEPS2):
            a.wait_ge(k.sem("moe2_up"), ee * STEPS2 + (step + 1))
            if step >= 2:
                a.wait_ge(k.sem("moe2_hidden"), ee * STEPS2 + (step - 1))
            a.activation(b["silu"][:, step % 2, :], k.ps[:, 4 + 2 * (step % 2), :], ACT.Silu)\
                .then_inc(k.sem("moe2_silu"), 1)
            if step == C2 - 1 and not first:
                output_norm(ee)

    swiglu_pairs(a, body)
    output_norm((n + 1) * E2)
    norm_act(k, a, ln + 2, b["acc"], b["sq"])
    transpose_act(k, a, xt + 2, b["hT"], b["gains"][:, 1:2], 0.0)


def swiglu_dve(k, v, m, n, ln):
    b = swiglu_layout(k)
    norm_dve(k, v, ln, k.x[:, :, :], k.xn[:, :, :], b["sq"])
    for g in range(GROUPS):
        v.wait_ge(k.sem("h_projected"), n * GROUPS + g + 1)
        v.tensor_copy(b["h"][:, g * TPG:(g + 1) * TPG, :], k.ps[:, 4 + g, :].rearrange("p (a b) -> p a b", a=TPG))
    norm_dve(k, v, ln + 1, b["h"], b["h"], b["sq"], F32_EPS, center=False)
    v.wait_ge(k.sem("moe2_loaded"), 48 * (n + 1))
    v.wait_ge(k.sem("gate_logits"), k.gate_calls[m] + 1)
    v.tensor_copy(b["logits"], k.ps[:, 4, 0:TILES * E2].rearrange("p (t e) -> p t e", t=TILES))\
        .then_inc(k.sem("logits_copied"), 1)
    v.drain()
    v.tensor_tensor(b["cur"], b["logits"], b["e_bias"].unsqueeze(1).broadcast_to([P, TILES, E2]), ALU.add)
    first_of_largest(k, v, b["cur"], b["best"], b["mask1"], b["rank"], b["top"])
    v.scalar_tensor_tensor(b["cur"], b["mask1"], NEG, b["cur"], ALU.mult, ALU.add)
    first_of_largest(k, v, b["cur"], b["best"], b["mask2"], b["rank"], b["top"])
    for r, mask in enumerate(("mask1", "mask2")):
        v.tensor_tensor(b["pick"], b["logits"], b[mask], ALU.mult)
        v.drain()
        v.tensor_reduce(b["l"][:, r, :], b["pick"], X_AXIS, ALU.add)
        v.drain()
    v.tensor_tensor(b["best"], b["l"][:, 0, :], b["l"][:, 1, :], ALU.max)
    v.drain()
    v.tensor_tensor(b["l"], b["l"], b["best"].unsqueeze(1).broadcast_to([P, 2, TILES]), ALU.subtract)\
        .then_inc(k.sem("pair_shifted"), 1)
    v.wait_ge(k.sem("pair_exp"), n + 1)
    v.tensor_tensor(b["best"], b["g"][:, 0, :], b["g"][:, 1, :], ALU.add)
    v.drain()
    v.reciprocal(b["best"], b["best"])
    v.drain()
    v.tensor_tensor(b["g"], b["g"], b["best"].unsqueeze(1).broadcast_to([P, 2, TILES]), ALU.mult)
    v.drain()
    v.tensor_tensor(b["mask1"], b["mask1"], bc(b["g"][:, 0, :], E2), ALU.mult)
    v.tensor_tensor(b["mask2"], b["mask2"], bc(b["g"][:, 1, :], E2), ALU.mult)
    v.drain()
    v.tensor_tensor(b["gates"].rearrange("p e t -> p t e"), b["mask1"], b["mask2"], ALU.add)
    v.memset(b["acc"], 0.0)
    v.drain()

    def output_norm(ee, e, s):
        v.wait_ge(k.sem("moe2_squared"), ee)
        v.tensor_reduce(b["ms"], b["sq"], X_AXIS, ALU.add)
        v.drain()
        v.tensor_scalar(b["ms"], b["ms"], 1.0 / DIM, F32_EPS, ALU.mult, ALU.add).then_inc(k.sem("moe2_mean"), 1)
        v.wait_ge(k.sem("moe2_root"), ee)
        v.reciprocal(b["factor"], b["factor"])
        v.drain()
        v.tensor_tensor(b["factor"], b["factor"], b["gates"][:, bass.ds(e - 1, 1), :].rearrange("p a t -> p (a t)"),
                        ALU.mult)
        v.drain()
        for g in range(GROUPS):
            o = v.tensor_tensor(b["scaled"][:, g * TPG:(g + 1) * TPG, :],
                                k.ps[:, g, :].rearrange("p (a b) -> p a b", a=TPG),
                                bc(b["factor"][:, g * TPG:(g + 1) * TPG], P), ALU.mult)
        o.then_inc(k.sem("moe2_taken"), 1)
        v.drain()
        v.tensor_tensor(b["scaled"], b["scaled"], b["enorm"][:, 1 - s, :].unsqueeze(1).broadcast_to([P, TILES, P]),
                        ALU.mult)
        v.drain()
        v.tensor_tensor(b["acc"], b["acc"], b["scaled"], ALU.add).then_inc(k.sem("moe2_summed"), 1)
        v.drain()

    def body(e, s, first):
        ee = e + n * E2
        for g in range(GROUPS):
            if g >= 2:
                v.wait_ge(k.sem("moe2_down"), ee * GROUPS + (g - 1))
            elif not first:
                v.wait_ge(k.sem("moe2_down"), ee * GROUPS + g - 1)
            for c in range(C2):
                step = g * C2 + c
                v.wait_ge(k.sem("moe2_silu"), ee * STEPS2 + (step + 1))
                v.tensor_tensor(b["hid"][:, g % 2, c, :], b["silu"][:, step % 2, :], k.ps[:, 5 + 2 * (step % 2), :],
                                ALU.mult).then_inc(k.sem("moe2_hidden"), 1)
            if g == 0 and not first:
                output_norm(ee, e, s)

    swiglu_pairs(v, body)
    output_norm((n + 1) * E2, E2, 0)
    norm_dve(k, v, ln + 2, b["acc"], b["acc"], b["sq"], F32_EPS, center=False)
    for g in range(GROUPS):
        v.wait_ge(k.sem("out_projected"), n * GROUPS + g + 1)
        xg = k.x[:, g * TPG:(g + 1) * TPG, :].rearrange("p a b -> p (a b)")
        o = v.scalar_tensor_tensor(xg, k.ps[:, 4 + g, :], 0.5, xg, ALU.mult, ALU.add)
    o.then_inc(k.sem("x_updated"), 1)


def lay_out_swiglu(a, i):
    import numpy as _np

    c, f = _np.ascontiguousarray, _np.float32
    a["l2_small"] = c(_np.concatenate([
        i["L2_ffn_W_in"].T, i["L2_ffn_W_out"].T, i["L2_ffn_Wr"].T, _np.zeros((P, 32), f),
        i["L2_ffn_in_norm_w"][:, None], i["L2_ffn_out_norm_w"][:, None]], axis=1))
    a["l2_e_bias"], a["l2_enorm"] = i["L2_ffn_expert_bias"], i["L2_ffn_enorm_w"]
    down = i["L2_ffn_Wd"].transpose(0, 2, 1).reshape(E2, C2, P, DIM).transpose(0, 2, 1, 3).reshape(E2, P, C2 * DIM)
    a["l2_w"] = c(_np.concatenate([i["L2_ffn_Wg"].transpose(0, 2, 1), i["L2_ffn_Wu"].transpose(0, 2, 1), down], axis=2))



E3, I3, TOP3, CAPACITY = 32, 64, 4, 128
UNITS = E3 // 2 + 1


def small_layout(k):
    a = k.arena
    a.reset()
    b = {}
    b["yT"] = a.take(TOKENS)
    b["sq"] = b["yT"].rearrange("p (a b) -> p a b", a=TILES)
    b["gate_w"] = a.take(E3)
    b["before"], b["ones"] = a.take(P), a.take(P)
    b["rank"] = a.take(E3)
    for name in ("logits", "cur", "mask", "chosen", "probs"):
        b[name] = a.take(TILES, E3)
    b["gates"] = a.take(E3, TILES)
    b["best"], b["top"], b["sum"] = a.take(TILES), a.take(TILES), a.take(TILES)
    b["rows"] = a.take(4 * P)
    b["shared"] = a.take(3 * P)
    b["w"] = a.take(2, 3 * P)
    b["gb"] = a.take(2, TOKENS)
    b["silu"] = a.take(2, GROUP)
    b["prod"] = a.take(2, GROUP)
    b["hid"] = a.take(2, GROUP)
    return b


def small_sync(k, sp, m, n, ln):
    b = small_layout(k)
    sp.wait_ge(k.sem("x_updated"), m + 1)
    ready = k.sem("moe3_loaded")
    sp.dma_start(b["gate_w"], k.ins["l3_gate_w"]).then_inc(ready, 16)
    sp.dma_start(b["before"], k.ins["before"]).then_inc(ready, 16)
    sp.dma_start(b["rank"], k.ins["rank"].partition_broadcast(P)).then_inc(ready, 16)
    sp.dma_start(b["shared"], k.ins["l3_w"][0, :, :]).then_inc(ready, 16)
    sp.wait_ge(k.sem("gates_stored"), 16 * (k.gate_stores[m] + 1))

    def load(s, pair):
        got = k.sem(f"moe3_w{s}")
        sp.dma_start(b["w"][:, s, :], k.ins["l3_w"][bass.ds(pair + 1, 1), :, :].rearrange("a p c -> (a p) c"))\
            .then_inc(got, 16)
        for h in range(2):
            row = k.gates_dram[bass.ds(pair * (2 * TILES) + h * TILES, TILES), :].rearrange("t p -> (t p)")
            sp.dma_start(b["gb"][h * I3:(h + 1) * I3, s, :], row.partition_broadcast(I3)).then_inc(got, 16)

    load(0, 0)
    load(1, 1)
    with sp.Fori(0, E3 // 4 - 1) as i:
        for s in range(2):
            sp.wait_ge(k.sem("moe3_down"), (n * UNITS + 1) * GROUPS + i * (2 * GROUPS) + (s + 1) * GROUPS)
            load(s, i * 2 + (s + 2))


def small_units(eng, body):
    body(0, 1)
    with eng.Fori(0, E3 // 4) as i:
        body(i * 2 + 1, 2, i)


def small_pe(k, pe, m, n, ln):
    b = small_layout(k)
    xt = k.xt_calls[m]
    pe.wait_ge(k.sem("ln_done"), ln + 1)
    transpose_pe(k, pe, xt, k.xn)
    pe.wait_ge(k.sem("moe3_loaded"), 64 * (n + 1))
    gate_logits_pe(k, pe, xt, b["gate_w"], E3)
    pe.wait_ge(k.sem("chosen_ready"), n + 1)
    pe.matmul(k.ps[:, 5, :], b["before"], b["chosen"].rearrange("p t e -> p (t e)"), start=True, stop=False)
    for t in range(TILES - 1):
        rest = TILES - 1 - t
        o = pe.matmul(k.ps[:, 5, (t + 1) * E3:], b["ones"],
                      b["chosen"][:, t, :].unsqueeze(1).broadcast_to([P, rest, E3]),
                      start=False, stop=(rest == 1))
    o.then_inc(k.sem("places_ready"), 1)
    gates_out_pe(k, pe, k.gate_stores[m], b["gates"], 4)

    def body(unit, units, i=None):
        at = (n * UNITS + unit) * GROUPS

        def weights(step):
            return b["shared"] if units == 1 else b["w"][:, step // GROUPS, :]

        def up(step):
            if units == 2 and step % GROUPS == 0:
                pe.wait_ge(k.sem(f"moe3_w{step // GROUPS}"), 48 * (E3 // 4) * n + 48 * i + 48)
            if step >= 2:
                pe.wait_ge(k.sem("moe3_multiplied"), at + (step - 1))
            g = step % GROUPS
            for half in range(2):
                o = pe.matmul(k.ps[:, 4 + 2 * (step % 2) + half, :], weights(step)[:, half * P:(half + 1) * P],
                              k.xT[:, g * GROUP:(g + 1) * GROUP], start=True, stop=True)
            o.then_inc(k.sem("moe3_up"), 1)

        up(0)
        up(1)
        for step in range(units * GROUPS):
            if step + 2 < units * GROUPS:
                up(step + 2)
            pe.wait_ge(k.sem("moe3_hidden"), at + (step + 1))
            pe.matmul(k.ps[:, step % GROUPS, :], weights(step)[:, 2 * P:3 * P], b["hid"][:, step % 2, :],
                      start=(units == 1), stop=True, skip_group_check=(units == 2)).then_inc(k.sem("moe3_down"), 1)

    pe.wait_ge(k.sem("gate_rows"), k.gate_stores[m] + 1)
    small_units(pe, body)
    add_back_pe(k, pe, k.back_calls[m], b["yT"])


def small_act(k, a, m, n, ln):
    b = small_layout(k)
    norm_act(k, a, ln, k.xn[:, :, :], b["sq"])
    transpose_act(k, a, k.xt_calls[m], k.xT)
    a.wait_ge(k.sem("moe3_shifted"), n + 1)
    a.activation(b["probs"], b["probs"], ACT.Exp).then_inc(k.sem("moe3_exp"), 1)
    gates_out_act(k, a, k.gate_stores[m], b["rows"], 4, None, None)

    def body(unit, units, i=None):
        at = (n * UNITS + unit) * GROUPS
        a.wait_ge(k.sem("moe3_multiplied"), at)
        for step in range(units * GROUPS):
            a.wait_ge(k.sem("moe3_up"), at + (step + 1))
            if step >= 2:
                a.wait_ge(k.sem("moe3_multiplied"), at + (step - 1))
            a.activation(b["silu"][:, step % 2, :], k.ps[:, 4 + 2 * (step % 2), :], ACT.Silu)\
                .then_inc(k.sem("moe3_silu"), 1)

    small_units(a, body)
    a.wait_ge(k.sem("moe3_down"), (n + 1) * UNITS * GROUPS)
    add_back_act(k, a, k.back_calls[m], b["yT"], 0.5)


def small_dve(k, v, m, n, ln):
    b = small_layout(k)
    norm_dve(k, v, ln, k.x[:, :, :], k.xn[:, :, :], b["sq"])
    v.memset(b["ones"], 1.0)
    v.memset(b["chosen"], 0.0)
    v.wait_ge(k.sem("gate_logits"), k.gate_calls[m] + 1)
    v.wait_ge(k.sem("moe3_loaded"), 64 * (n + 1))
    v.tensor_copy(b["logits"], k.ps[:, 4, :].rearrange("p (t e) -> p t e", t=TILES))
    v.drain()
    v.tensor_copy(b["cur"], b["logits"])
    for r in range(TOP3):
        first_of_largest(k, v, b["cur"], b["best"], b["mask"], b["rank"], b["top"])
        if r == 0:
            v.tensor_tensor(b["probs"], b["logits"], bc(b["best"], E3), ALU.subtract)\
                .then_inc(k.sem("moe3_shifted"), 1)
        v.tensor_tensor(b["chosen"], b["chosen"], b["mask"], ALU.add)
        if r < TOP3 - 1:
            v.scalar_tensor_tensor(b["cur"], b["mask"], NEG, b["cur"], ALU.mult, ALU.add)
    v.drain()
    v.tensor_copy(b["top"], b["best"]).then_inc(k.sem("chosen_ready"), 1)
    v.wait_ge(k.sem("moe3_exp"), n + 1)
    v.tensor_reduce(b["sum"], b["probs"], X_AXIS, ALU.add)
    v.drain()
    v.reciprocal(b["sum"], b["sum"])
    v.drain()
    v.tensor_tensor(b["probs"], b["probs"], bc(b["sum"], E3), ALU.mult)
    v.drain()
    v.tensor_tensor(b["probs"], b["probs"], b["chosen"], ALU.mult)
    v.drain()
    v.tensor_reduce(b["sum"], b["probs"], X_AXIS, ALU.add)
    v.drain()
    v.reciprocal(b["sum"], b["sum"])
    v.drain()
    v.tensor_tensor(b["probs"], b["probs"], bc(b["sum"], E3), ALU.mult)
    v.wait_ge(k.sem("places_ready"), n + 1)
    v.tensor_scalar(b["mask"], k.ps[:, 5, :].rearrange("p (t e) -> p t e", t=TILES), float(CAPACITY), None, ALU.is_lt)
    v.drain()
    v.tensor_tensor(b["gates"].rearrange("p e t -> p t e"), b["probs"], b["mask"], ALU.mult)\
        .then_inc(k.sem("gates_ready"), 1)

    def body(unit, units, i=None):
        at = (n * UNITS + unit) * GROUPS
        v.wait_ge(k.sem("moe3_down"), at)
        for step in range(units * GROUPS):
            s, g = divmod(step, GROUPS)
            if units == 2 and g == 0:
                v.wait_ge(k.sem(f"moe3_w{s}"), 48 * (E3 // 4) * n + 48 * i + 48)
            if step >= 2:
                v.wait_ge(k.sem("moe3_down"), at + (step - 1))
            v.wait_ge(k.sem("moe3_silu"), at + (step + 1))
            to = b["hid"] if units == 1 else b["prod"]
            o = v.tensor_tensor(to[:, step % 2, :], b["silu"][:, step % 2, :], k.ps[:, 5 + 2 * (step % 2), :], ALU.mult)
            o.then_inc(k.sem("moe3_multiplied"), 1)
            v.drain()
            if units == 1:
                v.sem_inc(k.sem("moe3_hidden"), 1)
            else:
                v.tensor_tensor(b["hid"][:, step % 2, :], b["prod"][:, step % 2, :],
                                b["gb"][:, s, g * GROUP:(g + 1) * GROUP], ALU.mult).then_inc(k.sem("moe3_hidden"), 1)

    small_units(v, body)
    add_back_dve(k, v, k.back_calls[m])


def lay_out_small(a, i):
    import numpy as _np

    c, f = _np.ascontiguousarray, _np.float32
    feature = _np.arange(P)
    a["before"] = (feature[:, None] < feature[None, :]).astype(f)
    a["l3_gate_w"] = c(i["L3_ffn_gate_w"].T)
    none = _np.zeros((P, I3), f)
    up = i["L3_ffn_w_gate_up"].reshape(E3 // 2, 2, DIM, 2, I3).transpose(0, 2, 3, 1, 4).reshape(E3 // 2, DIM, 4 * I3)
    down = i["L3_ffn_w_down"].reshape(E3 // 2, 2 * I3, DIM)
    gu = i["L3_ffn_shared_w_gate_up"]
    shared_up = _np.concatenate([gu[:, :I3], none, gu[:, I3:], none], axis=1)
    shared_down = _np.concatenate([i["L3_ffn_shared_w_down"], none.T], axis=0)
    a["l3_w"] = c(_np.concatenate([_np.concatenate([shared_up, shared_down], axis=1)[None],
                                   _np.concatenate([up, down], axis=2)], axis=0))



N2, RSTEP, QSTEPS = 32, 32, SEQ // 32
H4 = 2 * N2
CHUNK4 = 16
TWO_PI = 2.0 * math.pi
PI1 = 6.28125
PI2 = float(np.float32(np.round((TWO_PI - PI1) * 2 ** 20) / 2 ** 20))
PI3 = TWO_PI - PI1 - PI2
LN2_1 = 0.693359375
LN2_2 = math.log(2.0) - LN2_1
ROUNDER = 12582912.0
EXP_TERMS = 8


def s4d_layout(k):
    a = k.arena
    a.reset()
    b = {}

    def half(*shape):
        return a.take(*shape)[0:H4]
    b["par"] = half(5, P)
    b["steps"] = half(RSTEP + QSTEPS)
    b["turns"] = half(3)
    b["rads"] = half(3)
    b["ex"], b["ek"], b["er"] = half(2, P), half(2, P), half(2, P)
    for name in ("zr", "zi", "ar", "den", "nr", "ni", "cr", "ci", "t1", "t2", "mag1"):
        b[name] = half(P)
    b["unit"] = half(2, P)
    b["ph"] = half(P, RSTEP)
    b["turn"] = half(P, RSTEP)
    b["magr"] = half(P, RSTEP)
    b["tr"] = half(P, RSTEP)
    b["phq"] = half(P, QSTEPS)
    b["magq"] = half(P, QSTEPS)
    b["q1"], b["q2"] = half(P, QSTEPS), half(P, QSTEPS)
    b["sr"], b["sq_"] = half(2, CHUNK4 * RSTEP), half(2, CHUNK4 * QSTEPS)
    b["k32"] = a.take(QSTEPS, P)[0:RSTEP]
    tables = a.at
    b["fwd"] = a.take(4, 2 * SEQ)
    b["kt"] = a.take(4, P)
    b["kf"] = a.take(8, P)
    b["w"] = a.take(P)
    b["bias"] = a.take(P)
    b["p1"], b["p2"] = a.take(SEQ), a.take(SEQ)
    a.reset(P * 5 + 600)
    b["y"] = a.take(8, SEQ)
    b["back"] = a.take(8, SEQ)
    b["yg"] = a.take(TILES, P)
    b["yT"] = a.take(TOKENS)
    b["sq"] = b["yg"]
    assert a.at <= tables, (a.at, tables)
    return b


def s4d_sync(k, sp, m, n, ln):
    b = s4d_layout(k)
    sp.wait_ge(k.sem("x_updated"), m + 1)
    par = k.sem("s4_parameters")
    sp.dma_start(b["par"][:, 0, :], k.ins["s4_log_dt"].partition_broadcast(H4)).then_inc(par, 16)
    sp.dma_start(b["par"][:, 1:5, :], k.ins["s4_par"]).then_inc(par, 16)
    sp.dma_start(b["steps"], k.ins["s4_steps"].partition_broadcast(H4)).then_inc(par, 16)
    sp.dma_start(b["turns"], k.ins["s4_shifts"][:, 0:3]).then_inc(par, 16)
    sp.dma_start(b["rads"], k.ins["s4_shifts"][:, 3:6]).then_inc(par, 16)
    sp.dma_start(b["fwd"], k.ins["dft_forward"]).then_inc(k.sem("s4_forward"), 16)
    sp.dma_start(b["w"], k.ins["s4_w"]).then_inc(k.sem("s4_weights"), 16)
    sp.dma_start(b["bias"], k.ins["s4_bias"].partition_broadcast(P)).then_inc(k.sem("s4_weights"), 16)
    sp.wait_ge(k.sem("s4_kernel"), ONE + P // CHUNK4)
    src = b["k32"].rearrange("r (q a) d -> r q a d", a=4)
    for a_ in range(4):
        sp.dma_start(b["kt"][32 * a_:32 * a_ + 32, :, :], src[:, :, a_, :]).then_inc(k.sem("s4_kernel_moved"), 16)
    sp.wait_ge(k.sem("s4_kernel_moved"), 64)
    sp.dma_start(b["back"], k.ins["dft_back"]).then_inc(k.sem("s4_back"), 16)


def s4d_pe(k, pe, m, n, ln):
    b = s4d_layout(k)
    iters = P // CHUNK4
    with pe.Fori(0, iters) as i:
        pe.wait_ge(k.sem("s4_staged"), i + 1)
        hold(k, pe, "s4_kernel", ONE + i)
        for d in range(CHUNK4):
            o = pe.matmul(k.ps[0:RSTEP, 7, d * QSTEPS:(d + 1) * QSTEPS], b["sr"][:, 0, d * RSTEP:(d + 1) * RSTEP],
                          b["sq_"][:, 0, d * QSTEPS:(d + 1) * QSTEPS], start=True, stop=True)
        o.then_inc(k.sem("s4_products"), 1)
    pe.wait_ge(k.sem("s4_forward"), 16)
    pe.wait_ge(k.sem("s4_kernel_moved"), 64)
    for half in range(2):
        for f in range(4):
            for t in range(4):
                o = pe.matmul(k.ps[:, 4 + half, f * P:(f + 1) * P],
                              b["fwd"][:, t, half * SEQ + f * P:half * SEQ + (f + 1) * P], b["kt"][:, t, :],
                              start=(t == 0), stop=(t == 3))
    o.then_inc(k.sem("s4_kernel_spectrum"), 1)
    pe.wait_ge(k.sem("ln_done"), ln + 1)
    xv = k.xn[:, :, :].rearrange("p (b t) d -> p b t d", t=4)
    for f in range(4):
        if f >= 2:
            pe.wait_ge(k.sem("s4_multiplied"), f - 1)
        for half in range(2):
            for t in range(4):
                o = pe.matmul(k.ps[:, 2 * (f % 2) + half, :],
                              b["fwd"][:, t, half * SEQ + f * P:half * SEQ + (f + 1) * P], xv[:, :, t, :],
                              start=(t == 0), stop=(t == 3))
        o.then_inc(k.sem("s4_spectrum"), 1)
    pe.wait_ge(k.sem("s4_multiplied"), 4)
    pe.wait_ge(k.sem("s4_back"), 16)
    for t in range(4):
        for f in range(8):
            o = pe.matmul(k.ps[:, 4 + t, :], b["back"][:, f, t * P:(t + 1) * P], b["y"][:, f, :],
                          start=(f == 0), stop=(f == 7))
        o.then_inc(k.sem("s4_convolved"), 1)
    pe.wait_ge(k.sem("s4_gelu"), 4)
    transpose_pe(k, pe, ln, b["yg"])
    pe.wait_ge(k.sem("xT_ready"), (k.xt_calls[m] + 1) * GROUPS)
    pe.wait_ge(k.sem("s4_weights"), 32)
    project_back_pe(k, pe, b, n, b["yT"], b["w"], "s4_projected")


def s4d_act(k, a, m, n, ln):
    b = s4d_layout(k)
    a.wait_ge(k.sem("s4_exponents"), 1)
    a.activation(b["mag1"], b["zr"], ACT.Exp).then_inc(k.sem("s4_magnitudes"), 1)
    a.activation(b["magr"], b["magr"], ACT.Exp).then_inc(k.sem("s4_magnitudes"), 1)
    a.activation(b["magq"], b["magq"], ACT.Exp).then_inc(k.sem("s4_magnitudes"), 1)
    for j, what in enumerate((b["unit"], b["q1"], b["q2"], b["tr"])):
        a.wait_ge(k.sem("s4_angles"), j + 1)
        a.activation(what, what, ACT.Sin).then_inc(k.sem("s4_sines"), 1)
    norm_act(k, a, ln, k.xn[:, :, :], b["sq"])
    a.wait_ge(k.sem("s4_kernel_spectrum"), 1)
    a.activation(b["kf"].rearrange("p (h f) d -> p h (f d)", h=2), k.ps[:, 4:6, :], ACT.Copy)\
        .then_inc(k.sem("s4_kernel_copied"), 1)
    yg = b["yg"].rearrange("p (b t) d -> p b t d", t=4)
    for t in range(4):
        a.wait_ge(k.sem("s4_convolved"), t + 1)
        a.activation(yg[:, :, t, :], k.ps[:, 4 + t, :].rearrange("p (b d) -> p b d", b=BATCH), ACT.Gelu)\
            .then_inc(k.sem("s4_gelu"), 1)
    transpose_act(k, a, k.xt_calls[m], b["yT"])


def s4d_dve(k, v, m, n, ln):
    b = s4d_layout(k)
    v.wait_ge(k.sem("s4_parameters"), 80)
    T = ALU

    def tt(out, x, y, op):
        v.drain()
        return v.tensor_tensor(out, x, y, op)

    def ts(out, x, s1, s2, op0, op1):
        v.drain()
        return v.tensor_scalar(out, x, s1, s2, op0, op1)

    y, j, r = b["par"][:, 0:2, :], b["ek"], b["er"]
    ts(j, y, 1.0 / math.log(2.0), ROUNDER, T.mult, T.add)
    ts(j, j, ROUNDER, None, T.subtract, ALU.bypass)
    v.drain()
    v.scalar_tensor_tensor(r, j, -LN2_1, y, T.mult, T.add)
    v.drain()
    v.scalar_tensor_tensor(r, j, -LN2_2, r, T.mult, T.add)
    ts(b["ex"], r, 1.0 / math.factorial(EXP_TERMS), 1.0 / math.factorial(EXP_TERMS - 1), T.mult, T.add)
    for term in range(EXP_TERMS - 2, -1, -1):
        tt(b["ex"], b["ex"], r, T.mult)
        ts(b["ex"], b["ex"], 1.0 / math.factorial(term), None, T.add, ALU.bypass)
    ts(r.bitcast(mybir.dt.int32), j, 127.0, float(2 ** 23), T.add, T.mult)
    tt(b["ex"], b["ex"], r, T.mult)
    dt, mre = b["ex"][:, 0, :], b["ex"][:, 1, :]
    ai, c_re, c_im = b["par"][:, 2, :], b["par"][:, 3, :], b["par"][:, 4, :]
    ts(b["ar"], mre, -1.0, None, T.mult, ALU.bypass)
    tt(b["zr"], b["ar"], dt, T.mult)
    tt(b["zi"], ai, dt, T.mult)
    fine = b["steps"][:, 0:RSTEP].unsqueeze(1).broadcast_to([H4, P, RSTEP])
    coarse = b["steps"][:, RSTEP:].unsqueeze(1).broadcast_to([H4, P, QSTEPS])
    tt(b["magr"], bc(b["zr"], RSTEP), fine, T.mult)
    tt(b["magq"], bc(b["zr"], QSTEPS), coarse, T.mult).then_inc(k.sem("s4_exponents"), 1)
    tt(b["ph"], bc(b["zi"], RSTEP), fine, T.mult)
    tt(b["phq"], bc(b["zi"], QSTEPS), coarse, T.mult)

    def angle(out, phase, turns, turn, rad):
        ts(turns, phase, 1.0 / TWO_PI, turn, T.mult, T.add)
        ts(turns, turns, ROUNDER, ROUNDER, T.add, T.subtract)
        v.drain()
        v.scalar_tensor_tensor(out, turns, -PI1, phase, T.mult, T.add)
        v.drain()
        v.scalar_tensor_tensor(out, turns, -PI2, out, T.mult, T.add)
        v.drain()
        v.scalar_tensor_tensor(out, turns, -PI3, out, T.mult, T.add)
        ts(out, out, rad, None, T.add, ALU.bypass)
        return ts(out, out, 3.1415925, -3.1415925, T.min, T.max)

    scratch = b["turn"].rearrange("p a b -> p (a b)")
    angle(b["unit"][:, 0, :], b["zi"], scratch[:, 0:P], 0.25, math.pi / 2)
    angle(b["unit"][:, 1, :], b["zi"], scratch[:, 0:P], 0.0, 0.0).then_inc(k.sem("s4_angles"), 1)
    sq = scratch[:, 0:P * QSTEPS].rearrange("p (a b) -> p a b", a=P)
    angle(b["q1"], b["phq"], sq, b["turns"][:, 1:2], b["rads"][:, 1:2]).then_inc(k.sem("s4_angles"), 1)
    angle(b["q2"], b["phq"], sq, b["turns"][:, 2:3], b["rads"][:, 2:3]).then_inc(k.sem("s4_angles"), 1)
    angle(b["tr"], b["ph"], b["turn"], b["turns"][:, 0:1], b["rads"][:, 0:1]).then_inc(k.sem("s4_angles"), 1)
    v.wait_ge(k.sem("s4_magnitudes"), 3)
    v.wait_ge(k.sem("s4_sines"), 1)
    tt(b["nr"], b["mag1"], b["unit"][:, 0, :], T.mult)
    ts(b["nr"], b["nr"], -1.0, None, T.add, ALU.bypass)
    tt(b["ni"], b["mag1"], b["unit"][:, 1, :], T.mult)

    def product(out, x1, y1, x2, y2, op):
        tt(b["t1"], x1, y1, T.mult)
        tt(b["t2"], x2, y2, T.mult)
        tt(out, b["t1"], b["t2"], op)

    product(b["cr"], c_re, b["nr"], c_im, b["ni"], T.subtract)
    product(b["ci"], c_re, b["ni"], c_im, b["nr"], T.add)
    product(b["den"], b["ar"], b["ar"], ai, ai, T.add)
    v.drain()
    v.reciprocal(b["den"], b["den"])
    ts(b["den"], b["den"], 2.0, None, T.mult, ALU.bypass)
    product(b["nr"], b["cr"], b["ar"], b["ci"], ai, T.add)
    product(b["ni"], b["ci"], b["ar"], b["cr"], ai, T.subtract)
    tt(b["cr"], b["nr"], b["den"], T.mult)
    tt(b["ci"], b["ni"], b["den"], T.mult)
    v.wait_ge(k.sem("s4_sines"), 3)
    tt(b["q1"], b["q1"], bc(b["cr"], QSTEPS), T.mult)
    tt(b["q2"], b["q2"], bc(b["ci"], QSTEPS), T.mult)
    tt(b["q1"], b["q1"], b["q2"], T.add)
    tt(b["q1"], b["q1"], b["magq"], T.mult)
    v.wait_ge(k.sem("s4_sines"), 4)
    tt(b["tr"], b["tr"], b["magr"], T.mult)
    v.drain()
    fr, fq = b["tr"].rearrange("p a b -> p (a b)"), b["q1"].rearrange("p a b -> p (a b)")
    with v.Fori(0, P // CHUNK4) as i:
        v.tensor_copy(b["sr"][:, 0, :], fr[:, bass.ts(i, CHUNK4 * RSTEP)])
        v.tensor_copy(b["sq_"][:, 0, :], fq[:, bass.ts(i, CHUNK4 * QSTEPS)])
        v.drain()
        v.sem_inc(k.sem("s4_staged"), 1)
        v.wait_ge(k.sem("s4_products"), i + 1)
        v.tensor_copy(b["k32"][:, :, bass.ts(i, CHUNK4)].rearrange("r q d -> r d q"),
                      k.ps[0:RSTEP, 7, 0:CHUNK4 * QSTEPS].rearrange("r (d q) -> r d q", d=CHUNK4))\
            .then_inc(k.sem("s4_kernel"), 1)
    norm_dve(k, v, ln, k.x[:, :, :], k.xn[:, :, :], b["sq"])
    v.wait_ge(k.sem("s4_kernel_copied"), 1)
    kf = b["kf"]
    p1, p2 = (b[p].rearrange("p (b d) -> p b d", b=BATCH) for p in ("p1", "p2"))
    for f in range(4):
        v.wait_ge(k.sem("s4_spectrum"), f + 1)
        xr, xi = (k.ps[:, 2 * (f % 2) + h, :].rearrange("p (b d) -> p b d", b=BATCH) for h in range(2))
        kr, ki = (kf[:, 4 * h + f, :].unsqueeze(1).broadcast_to([P, BATCH, P]) for h in range(2))
        yr, yi = (b["y"][:, 4 * h + f, :].rearrange("p (b d) -> p b d", b=BATCH) for h in range(2))
        v.drain()
        v.tensor_tensor(p1, xr, kr, T.mult)
        v.tensor_tensor(p2, xi, ki, T.mult)
        v.drain()
        v.tensor_tensor(yr, p1, p2, T.subtract)
        v.drain()
        v.tensor_tensor(p1, xr, ki, T.mult)
        v.tensor_tensor(p2, xi, kr, T.mult)
        v.drain()
        v.tensor_tensor(yi, p1, p2, T.add).then_inc(k.sem("s4_multiplied"), 1)
    v.wait_ge(k.sem("s4_weights"), 32)
    v.tensor_tensor(k.x[:, :, :], k.x[:, :, :], b["bias"].unsqueeze(1).broadcast_to([P, TILES, P]), T.add)
    v.drain()
    for g in range(GROUPS):
        v.wait_ge(k.sem("s4_projected"), g + 1)
        xg = k.x[:, g * TPG:(g + 1) * TPG, :]
        o = v.tensor_tensor(xg, k.ps[:, 4 + g, :].rearrange("p (a b) -> p a b", a=TPG), xg, T.add)
    o.then_inc(k.sem("x_updated"), 1)


def lay_out_s4d(a, i):
    import numpy as _np

    c, f = _np.ascontiguousarray, _np.float32
    a["s4_log_dt"] = i["L2_attn_log_dt"]
    par = _np.stack([i["L2_attn_" + name].T for name in ("log_A_real", "A_imag", "C_real", "C_imag")], axis=1)
    a["s4_par"] = c(_np.concatenate([par, par], axis=0))
    a["s4_steps"] = _np.concatenate([_np.arange(RSTEP), RSTEP * _np.arange(QSTEPS)]).astype(f)
    turns = _np.repeat(_np.array([[0.25, 0.25, 0.5], [0.0, 0.5, 0.75]]), N2, axis=0)
    a["s4_shifts"] = c(_np.concatenate([turns, turns * TWO_PI], axis=1).astype(f))
    steps, freq = _np.arange(SEQ), _np.arange(SEQ)
    angle = ((2 * freq[None, :] + 1) * steps[:, None] % (4 * SEQ)) * (TWO_PI / (4 * SEQ))
    both = _np.concatenate([_np.cos(angle), -_np.sin(angle)], axis=1)
    a["dft_forward"] = c(both.reshape(4, P, 2 * SEQ).transpose(1, 0, 2).astype(f))
    a["dft_back"] = c((both.T / SEQ).reshape(8, P, SEQ).transpose(1, 0, 2).astype(f))
    a["s4_w"], a["s4_bias"] = c(i["L2_attn_W"].T), i["L2_attn_b"]



HEADSL, HDL, WINDOW = 8, 64, 64
INNER = HEADSL * HDL
PAIRS = HEADSL // 2
LAYERS = 2
QK_SCALE = 8.0
HID = int(DIM * 4 * 2 / 3)
CH = -(-HID // P)
KEYS = 2 * P
HALVES = 2 * TPG


def local_layout(k):
    a = k.arena
    a.reset()
    b = {}
    b["y"] = a.take(TILES, P)
    b["wqkv"] = a.take(3, INNER)
    b["wo"] = a.take(PAIRS, P)
    b["w1"] = a.take(2, CH, P)
    b["w2"] = a.take(CH, P)
    b["vec"] = a.take(2 + 2 * CH)
    b["scales"] = a.take(2, HDL)
    b["b2"] = a.take(P)
    b["mask"] = a.take(2, KEYS)
    b["half"] = a.take(2)
    b["cos"], b["sin"] = a.take(TPG, 2, HDL), a.take(TPG, 2, HDL)
    b["tc"], b["ts"] = a.take(TPG, 2, HDL), a.take(TPG, 2, HDL)
    b["qT"] = a.take(PAIRS, TOKENS)
    b["kT"] = a.take(PAIRS, P + TOKENS)
    b["v"] = a.take(1 + TILES, INNER)
    temp = a.at
    b["hs"] = a.take(2, P)
    b["qk"] = a.take(2, 2 * INNER)
    b["qsq"] = a.take(2, 2 * INNER)
    b["norms"] = a.take(2, 2 * HEADSL)
    b["rot"] = a.take(2 * INNER)
    b["swp"] = a.take(2 * INNER)
    b["qr"] = a.take(2, 2 * INNER)
    a.reset(temp)
    b["qm"] = a.take(2, HEADSL, P)
    b["s"] = a.take(2, 4, KEYS)
    b["p"] = a.take(2, 4, KEYS)
    b["pT"] = a.take(2, 4, KEYS)
    b["negmax"] = a.take(2, 4)
    b["sum"] = a.take(2, HEADSL)
    b["o"] = a.take(2, INNER)
    b["oT"] = a.take(2, INNER)
    a.reset(temp)
    b["sq"] = a.take(TILES, P)
    b["ge"] = a.take(2, GROUP)
    b["hid"] = a.take(2, CH, GROUP)
    return b


def local_sync(k, sp, m, n, ln):
    b = local_layout(k)
    sp.wait_ge(k.sem("x_updated"), m + 1)
    once = k.sem("lf_tables")
    sp.dma_start(b["mask"], k.ins["lf_mask"]).then_inc(once, 16)
    sp.dma_start(b["half"], k.ins["a0_mask"]).then_inc(once, 16)
    sp.dma_start(b["cos"], k.ins["lf_cos"]).then_inc(once, 16)
    sp.dma_start(b["sin"], k.ins["lf_sin"]).then_inc(once, 16)
    low, high = slice(0, DIM // 2), slice(DIM // 2, DIM)
    for layer in range(LAYERS):
        ll = n * LAYERS + layer
        w, w_ffn = k.sem("lf_weights"), k.sem("lf_ffn_weights")
        if layer:
            sp.wait_ge(k.sem("lf_layer_done"), ll)
        sp.dma_start(b["wqkv"], k.ins["lf_wqkv"][layer, :, :]).then_inc(w, 16)
        sp.dma_start(b["scales"], k.ins["lf_scales"][layer, :].partition_broadcast(P)).then_inc(w, 16)
        sp.dma_start(b["wo"], k.ins["lf_wo"][layer, :, :]).then_inc(w_ffn, 16)
        sp.dma_start(b["w1"], k.ins["lf_w1"][layer, :, :]).then_inc(w_ffn, 16)
        sp.dma_start(b["w2"], k.ins["lf_w2"][layer, :, :]).then_inc(w_ffn, 16)
        sp.dma_start(b["vec"], k.ins["lf_vec"][layer, :, :]).then_inc(w_ffn, 16)
        sp.dma_start(b["b2"], k.ins["lf_b2"][layer, :].partition_broadcast(P)).then_inc(w_ffn, 16)
        for part in range(2):
            sp.wait_ge(k.sem("lf_y_ready"), 2 * ll + part + 1)
            moved = k.sem("lf_shifted")
            sp.dma_start(k.xn[1:P, :, high], b["y"][0:P - 1, :, high]).then_inc(moved, 16)
            for bt in range(BATCH):
                t = bt * TPG
                sp.dma_start(k.xn[0:1, t + 1:t + TPG, high], b["y"][P - 1:P, t:t + TPG - 1, high]).then_inc(moved, 16)


SHIFTS = 16 * (1 + BATCH)


def local_pe(k, pe, m, n, ln):
    b = local_layout(k)
    for layer in range(LAYERS):
        ll = n * LAYERS + layer
        pe.wait_ge(k.sem("lf_halves_joined"), 2 * ll + 1)
        pe.wait_ge(k.sem("lf_shifted"), SHIFTS * (2 * ll + 1))
        transpose_pe(k, pe, 0, k.xn)
        pe.wait_ge(k.sem("xT_ready"), (k.xt_calls[m] + 2 * layer + 1) * GROUPS)
        pe.wait_ge(k.sem("lf_weights"), 32 * (ll + 1))

        with pe.Fori(0, TILES // 2) as i:
            tile = ll * TILES + i * 2
            for s in range(2):
                pe.wait_ge(k.sem("lf_staged"), tile + (s + 1))
                pe.wait_ge(k.sem("lf_squared"), ONE + tile)
                for part in range(3):
                    o = pe.matmul(k.ps[:, 3 * s + part, :], b["hs"][:, s, :], b["wqkv"][:, part, :],
                                  start=True, stop=True)
                o.then_inc(k.sem("lf_projected"), 1)
            for s in range(2):
                pe.wait_ge(k.sem("lf_rotated"), ONE + tile + (s + 1))
                pe.wait_ge(k.sem("lf_keys"), ONE + tile + s)
                for c in range(2 * PAIRS):
                    o = pe.transpose(k.ps[:, 6 + c // PAIRS, c % PAIRS * P:(c % PAIRS + 1) * P],
                                     b["qr"][:, s, c * P:(c + 1) * P], k.ident[:, :])
                o.then_inc(k.sem("lf_turned"), 1)

        pe.wait_ge(k.sem("lf_keys"), ONE + (ll + 1) * TILES)
        pe.wait_ge(k.sem("lf_ffn_weights"), 80 * (ll + 1))
        with pe.Fori(0, BATCH) as bt:
            at = ll * BATCH * HALVES + bt * HALVES
            tile = ll * TILES + bt * TPG

            def scores(u):
                t = u // 2
                if u % 2 == 0:
                    pe.wait_ge(k.sem("lf_queries_masked"), tile + (t + 1))
                if u >= 2:
                    pe.wait_ge(k.sem("lf_maxima"), at + (u - 1))
                for h in range(4):
                    head = 4 * (u % 2) + h
                    o = pe.matmul(k.ps[:, 2 * (u % 2) + h // 2, h % 2 * KEYS:(h % 2 + 1) * KEYS],
                                  b["qm"][:, t % 2, head, :],
                                  b["kT"].rearrange("p a c -> p (a c)")
                                  [:, bass.ds(bt * SEQ + head // 2 * (P + TOKENS) + t * P, KEYS)],
                                  start=True, stop=True)
                o.then_inc(k.sem("lf_scores"), 1)

            def turn(u):
                pe.wait_ge(k.sem("lf_probs"), ONE + at + (u + 1))
                pe.wait_ge(k.sem("lf_probs_copied_act"), ONE + at + u)
                pe.wait_ge(k.sem("lf_probs_copied_dve"), ONE + at + u)
                for c in range(8):
                    o = pe.transpose(k.ps[:, 4 + c // 4, c % 4 * P:(c % 4 + 1) * P],
                                     b["p"][:, u % 2, c // 2, c % 2 * P:(c % 2 + 1) * P], k.ident[:, :])
                o.then_inc(k.sem("lf_probs_turned"), 1)

            def values(u):
                t = u // 2
                pe.wait_ge(k.sem("lf_probs_copied_act"), ONE + at + (u + 1))
                pe.wait_ge(k.sem("lf_probs_copied_dve"), ONE + at + (u + 1))
                if u % 2 == 0:
                    pe.wait_ge(k.sem("lf_added"), ONE + tile + t)
                for h in range(4):
                    head = 4 * (u % 2) + h
                    for c in range(2):
                        o = pe.matmul(k.ps[:, 6, head * HDL:(head + 1) * HDL],
                                      b["pT"][:, u % 2, h, c * P:(c + 1) * P],
                                      b["v"].rearrange("p t d -> p (t d)")
                                      [:, bass.ds(bt * (TPG * INNER) + (t + c) * INNER + head * HDL, HDL)],
                                      start=(c == 0), stop=(c == 1))
                o.then_inc(k.sem("lf_values"), 1)

            def turn_out(t):
                pe.wait_ge(k.sem("lf_out"), ONE + tile + (t + 1))
                pe.wait_ge(k.sem("lf_out_copied"), ONE + tile + t)
                for c in range(PAIRS):
                    o = pe.transpose(k.ps[:, 7, c * P:(c + 1) * P], b["o"][:, t % 2, c * P:(c + 1) * P], k.ident[:, :])
                o.then_inc(k.sem("lf_out_turned"), 1)

            def project_out(t):
                pe.wait_ge(k.sem("lf_out_copied"), ONE + tile + (t + 1))
                for c in range(PAIRS):
                    o = pe.matmul(k.ps[:, 6, 0:P], b["oT"][:, t % 2, c * P:(c + 1) * P], b["wo"][:, c, :],
                                  start=(c == 0), stop=(c == PAIRS - 1))
                o.then_inc(k.sem("lf_out_projected"), 1)

            scores(0)
            scores(1)
            for u in range(HALVES):
                turn(u)
                if u + 2 < HALVES:
                    scores(u + 2)
                if u % 2 == 0 and u:
                    project_out(u // 2 - 1)
                values(u)
                if u % 2:
                    turn_out(u // 2)
            project_out(TPG - 1)

        pe.wait_ge(k.sem("ln_done"), ln + 2 + layer)
        transpose_pe(k, pe, 0, k.xn)
        pe.wait_ge(k.sem("xT_ready"), (k.xt_calls[m] + 2 * layer + 2) * GROUPS)
        with pe.Fori(0, GROUPS // 2) as i:
            at = ll * GROUPS * CH + i * (2 * CH)
            group = ll * GROUPS + i * 2

            def up(step):
                g, c = divmod(step, CH)
                if step >= 2:
                    pe.wait_ge(k.sem("lf_hidden"), ONE + at + (step - 1))
                for half in range(2):
                    o = pe.matmul(k.ps[:, 2 * (step % 2) + half, :], b["w1"][:, half, c, :],
                                  k.xT[:, bass.ds(i * (2 * GROUP) + g * GROUP, GROUP)], start=True, stop=True)
                o.then_inc(k.sem("lf_up"), 1)

            def down(g):
                pe.wait_ge(k.sem("lf_hidden"), ONE + at + CH * (g + 1))
                pe.wait_ge(k.sem("lf_ffn_added"), ONE + group)
                for j in range(TPG):
                    for c in range(CH):
                        o = pe.matmul(k.ps[:, 4 + g, j * P:(j + 1) * P], b["hid"][:, g, c, j * P:(j + 1) * P],
                                      b["w2"][:, c, :], start=(c == 0), stop=(c == CH - 1))
                o.then_inc(k.sem("lf_down"), 1)

            for step in range(CH + 2):
                up(step)
            down(0)
            up(2 * CH - 1)
            down(1)


def local_act(k, a, m, n, ln):
    b = local_layout(k)
    norm_act(k, a, ln, k.xn[:, :, :], b["sq"])
    for layer in range(LAYERS):
        ll = n * LAYERS + layer
        transpose_act(k, a, k.xt_calls[m] + 2 * layer, k.xT)
        if layer == 0:
            a.wait_ge(k.sem("lf_cleared"), n + 1)
        with a.Fori(0, TILES // 2) as i:
            tile = ll * TILES + i * 2
            for s in range(2):
                a.wait_ge(k.sem("lf_projected"), ONE + tile + (s + 1))
                a.wait_ge(k.sem("lf_rotated"), ONE + tile)
                a.activation(b["qk"][:, s, :].rearrange("p (a b) -> p a b", a=2), k.ps[:, 3 * s:3 * s + 2, :], ACT.Copy)
                a.activation(b["v"].rearrange("p t d -> p (t d)")[:, bass.ds(i * (2 * INNER) + (s + 1) * INNER, INNER)],
                             k.ps[:, 3 * s + 2, :], ACT.Copy)
                a.activation(b["qsq"][:, s, :].rearrange("p (a b) -> p a b", a=2), k.ps[:, 3 * s:3 * s + 2, :], ACT.Square)\
                    .then_inc(k.sem("lf_squared"), 1)
            for s in range(2):
                a.wait_ge(k.sem("lf_summed"), tile + (s + 1))
                a.activation(b["norms"][:, s, :], b["norms"][:, s, :], ACT.Sqrt).then_inc(k.sem("lf_lengths"), 1)
            for s in range(2):
                a.wait_ge(k.sem("lf_turned"), ONE + tile + (s + 1))
                for half, (dst, first, width) in enumerate((("qT", 0, TOKENS), ("kT", P, P + TOKENS))):
                    o = a.activation(b[dst][:, :, bass.ds(i * (2 * P) + (s * P + first), P)],
                                     k.ps[:, 6 + half, :].rearrange("p (a b) -> p a b", a=PAIRS), ACT.Copy)
                o.then_inc(k.sem("lf_keys"), 1)
        a.wait_ge(k.sem("lf_rotated"), ONE + (ll + 1) * TILES)

        with a.Fori(0, BATCH) as bt:
            at = ll * BATCH * HALVES + bt * HALVES
            tile = ll * TILES + bt * TPG

            def out_copy(t):
                a.wait_ge(k.sem("lf_out_turned"), tile + (t + 1))
                if t >= 2:
                    a.wait_ge(k.sem("lf_out_projected"), ONE + tile + (t - 1))
                a.activation(b["oT"][:, t % 2, :], k.ps[:, 7, :], ACT.Copy).then_inc(k.sem("lf_out_copied"), 1)

            a.wait_ge(k.sem("lf_values"), ONE + at)
            a.wait_ge(k.sem("lf_out_projected"), ONE + tile)
            a.wait_ge(k.sem("lf_out"), ONE + tile)
            for u in range(HALVES):
                a.wait_ge(k.sem("lf_maxima"), at + (u + 1))
                if u >= 4 and u % 2 == 0:
                    a.wait_ge(k.sem("lf_out"), ONE + tile + (u // 2 - 1))
                for h in range(4):
                    o = a.activation(b["p"][:, u % 2, h, :], b["s"][:, u % 2, h, :], ACT.Exp, scale=-1.0,
                                     bias=b["negmax"][:, u % 2, h:h + 1],
                                     accum_out=b["sum"][:, u // 2 % 2, 4 * (u % 2) + h:4 * (u % 2) + h + 1])
                o.then_inc(k.sem("lf_probs"), 1)
                if u % 2 == 0 and u:
                    out_copy(u // 2 - 1)
                a.wait_ge(k.sem("lf_probs_turned"), at + (u + 1))
                if u >= 2:
                    a.wait_ge(k.sem("lf_values"), ONE + at + (u - 1))
                a.activation(b["pT"][:, u % 2, 0:2, :], k.ps[:, 4, :].rearrange("p (a b) -> p a b", a=2), ACT.Copy)\
                    .then_inc(k.sem("lf_probs_copied_act"), 1)
            out_copy(TPG - 1)

        a.wait_ge(k.sem("lf_added"), ONE + (ll + 1) * TILES)
        norm_act(k, a, ln + 1 + layer, k.xn[:, :, :], b["sq"])
        transpose_act(k, a, k.xt_calls[m] + 2 * layer + 1, k.xT, b["vec"][:, 0:1], b["vec"][:, 1:2])
        with a.Fori(0, GROUPS // 2) as i:
            at = ll * GROUPS * CH + i * (2 * CH)
            a.wait_ge(k.sem("lf_hidden"), ONE + at)
            for step in range(2 * CH):
                c = step % CH
                a.wait_ge(k.sem("lf_up"), at + (step + 1))
                if step >= 2:
                    a.wait_ge(k.sem("lf_hidden"), ONE + at + (step - 1))
                a.activation(b["ge"][:, step % 2, :], k.ps[:, 2 * (step % 2) + 1, :], ACT.Gelu,
                             bias=b["vec"][:, 2 + CH + c:3 + CH + c]).then_inc(k.sem("lf_gelu"), 1)


def local_dve(k, v, m, n, ln):
    b = local_layout(k)
    low = slice(0, DIM // 2)
    norm_dve(k, v, ln, k.x[:, :, :], k.xn[:, :, :], b["sq"])
    v.drain()
    v.tensor_copy(b["y"], k.xn[:, :, :])
    v.drain()
    v.memset(k.xn[:, :, :], 0.0)
    v.memset(b["kT"][:, :, 0:P], 0.0)
    v.memset(b["v"][:, 0, :], 0.0).then_inc(k.sem("lf_cleared"), 1)
    v.drain()
    v.sem_inc(k.sem("lf_y_ready"), 1)
    v.wait_ge(k.sem("lf_tables"), 64 * (n + 1))
    for layer in range(LAYERS):
        ll = n * LAYERS + layer
        v.tensor_copy(k.xn[:, :, low], b["y"][:, :, low]).then_inc(k.sem("lf_halves_joined"), 1)
        v.wait_ge(k.sem("lf_weights"), 32 * (ll + 1))
        sc = b["scales"].unsqueeze(1)
        v.tensor_tensor(b["tc"], b["cos"], sc.broadcast_to([P, TPG, 2, HDL]), ALU.mult)
        for half in range(2):
            own, other = (slice(half * 32, half * 32 + 32), slice((1 - half) * 32, (1 - half) * 32 + 32))
            v.tensor_tensor(b["ts"][:, :, :, own], b["sin"][:, :, :, own],
                            b["scales"][:, :, other].unsqueeze(1).broadcast_to([P, TPG, 2, 32]), ALU.mult)
        v.wait_ge(k.sem("xT_ready"), (k.xt_calls[m] + 2 * layer + 1) * GROUPS)
        v.drain()

        def pair(bt, j):
            i = bt * 2 + j
            tile = ll * TILES + i * 2
            v.wait_ge(k.sem("lf_projected"), ONE + tile)
            for s in range(2):
                v.tensor_copy(b["hs"][:, s, :], k.xT[:, bass.ds(i * (2 * P) + s * P, P)]).then_inc(k.sem("lf_staged"), 1)
            for s in range(2):
                v.wait_ge(k.sem("lf_squared"), ONE + tile + (s + 1))
                v.tensor_reduce(b["norms"][:, s, :], b["qsq"][:, s, :].rearrange("p (h d) -> p h d", d=HDL), X_AXIS,
                                ALU.add).then_inc(k.sem("lf_summed"), 1)
            for s in range(2):
                v.wait_ge(k.sem("lf_lengths"), tile + (s + 1))
                norms = b["norms"][:, s, :]
                v.tensor_scalar(norms, norms, 1e-12, None, ALU.max)
                v.drain()
                v.reciprocal(norms, norms)
                v.drain()
                qk = b["qk"][:, s, :].rearrange("p (h d) -> p h d", d=HDL)
                v.tensor_tensor(qk, qk, bc(norms, HDL), ALU.mult)
                v.drain()
                for part in range(2):
                    heads = slice(part * HEADSL, (part + 1) * HEADSL)
                    sp_ = slice(part * INNER, (part + 1) * INNER)
                    q3 = b["qk"][:, s, sp_].rearrange("p (h d) -> p h d", d=HDL)
                    tcs = b["tc"][:, bass.ds(j * 2 + s, 1), part, :].rearrange("p a d -> p (a d)")
                    r3 = b["rot"][:, sp_].rearrange("p (h d) -> p h d", d=HDL)
                    w3 = b["swp"][:, sp_].rearrange("p (h d) -> p h d", d=HDL)
                    v.tensor_tensor(r3, q3, tcs[:, 0:HDL].unsqueeze(1).broadcast_to([P, HEADSL, HDL]), ALU.mult)
                    tss = b["ts"][:, bass.ds(j * 2 + s, 1), part, :].rearrange("p a d -> p (a d)")
                    for half in range(2):
                        own, other = (slice(half * 32, half * 32 + 32), slice((1 - half) * 32, (1 - half) * 32 + 32))
                        v.tensor_tensor(w3[:, :, own], q3[:, :, other],
                                        tss[:, own].unsqueeze(1).broadcast_to([P, HEADSL, 32]), ALU.mult)
                v.drain()
                v.wait_ge(k.sem("lf_turned"), ONE + tile + s)
                v.tensor_tensor(b["qr"][:, s, :], b["rot"], b["swp"], ALU.add).then_inc(k.sem("lf_rotated"), 1)
                v.drain()

        with v.Fori(0, BATCH) as bt:
            with v.Fori(0, 2) as j:
                pair(bt, j)
        v.wait_ge(k.sem("lf_keys"), ONE + (ll + 1) * TILES)

        with v.Fori(0, BATCH) as bt:
            at = ll * BATCH * HALVES + bt * HALVES
            tile = ll * TILES + bt * TPG

            def queries(t):
                for half in range(2):
                    o = v.tensor_scalar(b["qm"][:, t % 2, :, :].rearrange("p (a h) c -> p a h c", h=2)[:, :, half, :],
                                        b["qT"][:, :, bass.ds(bt * SEQ + t * P, P)], b["half"][:, half:half + 1], QK_SCALE * math.sqrt(HDL),
                                        ALU.mult, ALU.mult)
                o.then_inc(k.sem("lf_queries_masked"), 1)

            def maxima(u):
                if u >= 2:
                    v.wait_ge(k.sem("lf_probs"), ONE + at + (u - 1))
                hold(k, v, "lf_scores", ONE + at + (u + 1))
                for h in range(4):
                    o = v.tensor_tensor_reduce(b["s"][:, u % 2, h, :],
                                               k.ps[:, 2 * (u % 2) + h // 2, h % 2 * KEYS:(h % 2 + 1) * KEYS],
                                               b["mask"][:, min(u // 2, 1), :], -1.0, 3.0e38, ALU.add, ALU.min,
                                               b["negmax"][:, u % 2, h:h + 1])
                o.then_inc(k.sem("lf_maxima"), 1)

            def copy(u):
                v.wait_ge(k.sem("lf_probs_turned"), at + (u + 1))
                if u >= 2:
                    v.wait_ge(k.sem("lf_values"), ONE + at + (u - 1))
                v.tensor_copy(b["pT"][:, u % 2, 2:4, :], k.ps[:, 5, :].rearrange("p (a b) -> p a b", a=2))\
                    .then_inc(k.sem("lf_probs_copied_dve"), 1)

            def out(t):
                v.wait_ge(k.sem("lf_values"), ONE + at + (2 * t + 2))
                total = b["sum"][:, t % 2, :]
                v.reciprocal(total, total)
                v.drain()
                v.tensor_tensor(b["o"][:, t % 2, :].rearrange("p (h d) -> p h d", d=HDL),
                                k.ps[:, 6, :].rearrange("p (h d) -> p h d", d=HDL), bc(total, HDL), ALU.mult)\
                    .then_inc(k.sem("lf_out"), 1)

            def add(t):
                v.wait_ge(k.sem("lf_out_projected"), ONE + tile + (t + 1))
                yt = b["y"][:, bass.ds(bt * TPG + t, 1), :].rearrange("p a d -> p (a d)")
                v.tensor_tensor(yt, k.ps[:, 6, 0:P], yt, ALU.add).then_inc(k.sem("lf_added"), 1)

            v.wait_ge(k.sem("lf_scores"), ONE + at)
            v.wait_ge(k.sem("lf_probs"), ONE + at)
            queries(0)
            queries(1)
            maxima(0)
            maxima(1)
            for u in range(HALVES):
                copy(u)
                if u + 2 < HALVES:
                    maxima(u + 2)
                if u % 2 == 0 and u:
                    add(u // 2 - 1)
                if u % 2:
                    out(u // 2)
                    if u // 2 + 2 < TPG:
                        queries(u // 2 + 2)
            add(TPG - 1)

        v.wait_ge(k.sem("lf_added"), ONE + (ll + 1) * TILES)
        v.sem_inc(k.sem("lf_y_ready"), 1)
        v.tensor_copy(k.xn[:, :, low], b["y"][:, :, low]).then_inc(k.sem("lf_halves_joined"), 1)
        v.wait_ge(k.sem("lf_ffn_weights"), 80 * (ll + 1))
        v.wait_ge(k.sem("lf_shifted"), SHIFTS * (2 * ll + 2))
        norm_dve(k, v, ln + 1 + layer, k.xn[:, :, :], k.xn[:, :, :], b["sq"])
        v.tensor_tensor(b["y"], b["y"], b["b2"].unsqueeze(1).broadcast_to([P, TILES, P]), ALU.add)
        v.drain()
        with v.Fori(0, GROUPS // 2) as i:
            at = ll * GROUPS * CH + i * (2 * CH)
            group = ll * GROUPS + i * 2
            v.wait_ge(k.sem("lf_down"), ONE + group)

            def add(g):
                v.wait_ge(k.sem("lf_down"), ONE + group + (g + 1))
                yg = b["y"][:, bass.ds(i * (2 * TPG) + g * TPG, TPG), :]
                v.tensor_tensor(yg, k.ps[:, 4 + g, :].rearrange("p (a b) -> p a b", a=TPG), yg, ALU.add)\
                    .then_inc(k.sem("lf_ffn_added"), 1)

            for step in range(2 * CH):
                g, c = divmod(step, CH)
                v.wait_ge(k.sem("lf_gelu"), at + (step + 1))
                v.scalar_tensor_tensor(b["hid"][:, g, c, :], k.ps[:, 2 * (step % 2), :], b["vec"][:, 2 + c:3 + c],
                                       b["ge"][:, step % 2, :], ALU.add, ALU.mult).then_inc(k.sem("lf_hidden"), 1)
            add(0)
            add(1)
        v.drain()
        if layer + 1 < LAYERS:
            v.memset(k.xn[0:1, 0:TILES:TPG, DIM // 2:DIM], 0.0)
            v.drain()
            v.sem_inc(k.sem("lf_y_ready"), 1)
            v.sem_inc(k.sem("lf_layer_done"), 1)
        else:
            v.scalar_tensor_tensor(k.x[:, :, :].rearrange("p t d -> p (t d)"), b["y"].rearrange("p t d -> p (t d)"), 0.5,
                                   k.x[:, :, :].rearrange("p t d -> p (t d)"), ALU.mult, ALU.add)
            v.drain()
            v.sem_inc(k.sem("lf_layer_done"), 1)
            v.sem_inc(k.sem("x_updated"), 1)


def lay_out_local(a, i):
    import numpy as _np

    c, f = _np.ascontiguousarray, _np.float32
    a["lf_wqkv"] = i["L1_ffn_wqkv"]
    a["lf_scales"] = c(_np.concatenate([i["L1_ffn_q_scale"], i["L1_ffn_k_scale"]], axis=1))
    a["lf_wo"] = c(i["L1_ffn_wo"].reshape(LAYERS, PAIRS, P, DIM).transpose(0, 2, 1, 3).reshape(LAYERS, P, PAIRS * DIM))
    w1 = _np.zeros((LAYERS, DIM, 2, CH * P), f)
    w1[:, :, :, :HID] = i["L1_ffn_w1"].reshape(LAYERS, DIM, 2, HID)
    a["lf_w1"] = w1.reshape(LAYERS, DIM, 2 * CH * P)
    w2 = _np.zeros((LAYERS, CH * P, DIM), f)
    w2[:, :HID] = i["L1_ffn_w2"]
    a["lf_w2"] = c(w2.reshape(LAYERS, CH, P, DIM).transpose(0, 2, 1, 3).reshape(LAYERS, P, CH * DIM))
    b1 = _np.zeros((LAYERS, 2, CH * P), f)
    b1[:, :, :HID] = i["L1_ffn_b1"].reshape(LAYERS, 2, HID)
    a["lf_vec"] = c(_np.concatenate([i["L1_ffn_ln_g"][:, :, None], i["L1_ffn_ln_b"][:, :, None],
                                     b1.reshape(LAYERS, 2 * CH, P).transpose(0, 2, 1)], axis=2))
    a["lf_b2"] = i["L1_ffn_b2"]
    q, key = _np.arange(P)[:, None], _np.arange(KEYS)[None, :] - P
    seen = (key <= q) & (key >= q - WINDOW)
    a["lf_mask"] = c(_np.stack([_np.where(seen & (key >= 0), 0, -1e30), _np.where(seen, 0, -1e30)], axis=1).astype(f))
    half = _np.arange(0, HDL, 2, dtype=f)
    inv = (f(1.0) / f(10000.0) ** (half / f(HDL))).astype(f)
    t = _np.arange(SEQ, dtype=f)
    freqs = (t[:, None] * inv[None, :]).astype(_np.float64)
    base = ((half + 0.4 * HDL) / (1.4 * HDL)).astype(_np.float64)
    scale = base[None, :] ** ((t - SEQ // 2) / float(WINDOW // 2))[:, None]
    cos, sin = _np.cos(freqs), _np.sin(freqs)

    def table(x, lower):
        both = _np.stack([_np.concatenate([lower * x * z, x * z], axis=1) for z in (scale, 1.0 / scale)], axis=1)
        return c(both.reshape(TPG, P, 2, HDL).transpose(1, 0, 2, 3).astype(f))

    a["lf_cos"], a["lf_sin"] = table(cos, 1.0), table(sin, -1.0)

relu_moe = {"norms": 1, "transposes": 1, "gates": 1, "stores": 1, "backs": 1, "sync": relu_moe_sync, "tensor": relu_moe_pe,
            "scalar": relu_moe_act, "vector": relu_moe_dve}

swiglu_moe = {"norms": 3, "transposes": 3, "gates": 1, "stores": 0, "backs": 0, "sync": swiglu_sync,
              "tensor": swiglu_pe, "scalar": swiglu_act, "vector": swiglu_dve}
small_moe = {"norms": 1, "transposes": 1, "gates": 1, "stores": 1, "backs": 1, "sync": small_sync,
             "tensor": small_pe, "scalar": small_act, "vector": small_dve}


def attention_kind(c, norms):
    def bind(f):
        return lambda k, eng, m, n, ln: f(k, eng, m, n, ln, c)
    return {"norms": norms, "transposes": 1, "gates": 0, "backs": 0, "att_blocks": c.blocks, "flat": c.blocks == 1,
            "sync": bind(attention_sync), "tensor": bind(attention_pe), "scalar": bind(attention_act),
            "vector": bind(attention_dve)}


attn0, attn1, attn3 = attention_kind(A0, 1), attention_kind(A1, 2), attention_kind(A3, 1)
s4d = {"norms": 1, "transposes": 1, "gates": 0, "backs": 0, "sync": s4d_sync, "tensor": s4d_pe, "scalar": s4d_act,
       "vector": s4d_dve}
local_ffn = {"norms": 3, "transposes": 4, "gates": 0, "backs": 0, "sync": local_sync, "tensor": local_pe,
             "scalar": local_act, "vector": local_dve}



KINDS = {"ffn0": relu_moe, "attn0": attn0, "ffn1": local_ffn, "attn1": attn1, "ffn2": swiglu_moe, "attn2": s4d,
         "ffn3": small_moe, "attn3": attn3}
STAGES = ["ffn0", "attn0", "ffn0", "ffn1", "attn1", "ffn1", "ffn2", "attn2", "ffn2", "ffn3", "attn3", "ffn3"]


def build(nc, ins, out, stages=STAGES):
    scratch = nc.dram_tensor("gates_dram", (32 * TILES, P), F32, kind="Internal").ap()
    with ExitStack() as ctx:
        k = Program(nc, ctx, ins, out, scratch)
        k.gates_dram = scratch
        k.toeplitz_dram = nc.dram_tensor("toeplitz_dram", (HEADS, P, SPAN), F32, kind="Internal").ap()
        k.rel_dram = nc.dram_tensor("rel_dram", (HEADS, 2 * SEQ), F32, kind="Internal").ap()
        k.ln_calls, k.xt_calls, k.gate_calls, k.back_calls, k.kind_calls = [], [], [], [], []
        k.att_calls, k.att_blocks, k.flat_calls, k.gate_stores = [], [], [], []
        lns = xts = gates = backs = atts = blocks = flats = stores = 0
        seen = {}
        for s in stages:
            kind = KINDS[s]
            k.ln_calls.append(lns), k.xt_calls.append(xts), k.gate_calls.append(gates), k.back_calls.append(backs)
            k.kind_calls.append(seen.get(s, 0))
            seen[s] = seen.get(s, 0) + 1
            lns += kind["norms"]
            xts += kind["transposes"]
            gates += kind["gates"]
            backs += kind["backs"]
            k.att_calls.append(atts), k.att_blocks.append(blocks), k.flat_calls.append(flats - seen[s] + 1)
            k.gate_stores.append(stores)
            stores += kind.get("stores", 0)
            atts += "att_blocks" in kind
            blocks += kind.get("att_blocks", 0)
            flats += bool(kind.get("flat"))
        x_in = ins["x"].rearrange("b (t p) d -> p (b t) d", p=P)
        x_out = out.rearrange("b (t p) d -> p (b t) d", p=P)
        block = ctx.enter_context(nc.Block())

        def run(which, eng):
            for name in FROM_ONE.get(which, []):
                eng.sem_inc(k.sem(name), ONE)
            for m, s in enumerate(stages):
                KINDS[s][which](k, eng, m, k.kind_calls[m], k.ln_calls[m])

        @block.sync
        def _(sp):
            sp.dma_start(k.x[:, :, :], x_in).then_inc(k.sem("x_loaded"), 16)
            sp.dma_start(k.ident[:, :], ins["ident"]).then_inc(k.sem("x_loaded"), 16)
            run("sync", sp)
            sp.wait_ge(k.sem("x_updated"), len(stages) + 1)
            sp.dma_start(x_out, k.x[:, :, :]).then_inc(k.sem("x_stored"), 16)
            sp.wait_ge(k.sem("x_stored"), 16)

        @block.vector
        def _(v):
            v.wait_ge(k.sem("x_loaded"), 32)
            v.tensor_copy(k.ln_a[:, :], k.x[:, :, 0]).then_inc(k.sem("x_updated"), 1)
            run("vector", v)

        @block.tensor
        def _(pe):
            pe.wait_ge(k.sem("x_updated"), 1)
            run("tensor", pe)

        @block.scalar
        def _(a):
            run("scalar", a)


def lay_out(i):
    import numpy as _np

    c = _np.ascontiguousarray
    f = _np.float32
    a = {"x": i["L0_attn_X"], "ident": _np.eye(P, dtype=f), "rank": _np.arange(32, 0, -1).astype(f)}
    a["l0_gate_w"] = c(i["L0_ffn_gate_w"].T)
    a["l0_b2"] = i["L0_ffn_b2"]
    a["l0_w"] = c(_np.concatenate([
        i["L0_ffn_w1"],
        i["L0_ffn_w2"].reshape(E0, C0, P, DIM).transpose(0, 2, 1, 3).reshape(E0, P, C0 * DIM),
        i["L0_ffn_b1"].reshape(E0, C0, P).transpose(0, 2, 1)], axis=2))
    for more in (lay_out_attention, lay_out_swiglu, lay_out_small, lay_out_local, lay_out_s4d):
        more(a, i)
    return a


def kernel(**inputs):
    import numpy as _np
    import concourse.bacc as _bacc
    from concourse import mybir as _mybir
    from concourse.bass_utils import run_bass_kernel_spmd as _run

    nc = _bacc.Bacc("TRN2", target_bir_lowering=False, num_devices=1)
    arrays, ins = {}, {}
    for name, a in lay_out({n: _np.asarray(v) for n, v in inputs.items()}).items():
        arrays[f"in_{name}"] = a
        ins[name] = nc.dram_tensor(f"in_{name}", a.shape, _mybir.dt.from_np(a.dtype), kind="ExternalInput").ap()
    out = nc.dram_tensor("out_x", (BATCH, SEQ, DIM), _mybir.dt.float32, kind="ExternalOutput").ap()
    build(nc, ins, out)
    return _run(nc, [arrays], core_ids=[0]).results[0]["out_x"]
```

```python
import math

import numpy as np
import concourse.bass as bass
from concourse import mybir
from contextlib import ExitStack

F32 = mybir.dt.float32
ALU = mybir.AluOpType
ACT = mybir.ActivationFunctionType
X_AXIS = mybir.AxisListType.X

P = 128
BATCH, SEQ, DIM = 4, 512, 128
TOKENS = BATCH * SEQ
TILES = TOKENS // P
GROUPS = 4
GROUP = TOKENS // GROUPS
TPG = TILES // GROUPS
LN_EPS = 1e-5
F32_EPS = float(np.finfo(np.float32).eps)
NEG = -3.0e38

LEAD = 2
LED = {
    "tensor": [
        "moe0_down", "values", "gelu_turned", "att_projected", "lf_projected", "lf_values",
        "lf_out_projected", "lf_scores", "lf_down", "lf_turned", "probs_turned", "scores"],
    "vector": [
        "moe0_hidden", "heads_done", "lf_rotated", "lf_out", "lf_added", "lf_probs_copied_dve",
        "lf_hidden", "lf_ffn_added", "s4_kernel", "att_added", "maxima", "probs_copied"],
    "scalar": [
        "probs", "lf_squared", "lf_keys", "lf_probs", "lf_probs_copied_act", "lf_out_copied"],
}


class Arena:

    def __init__(self, tensor, floats):
        self.tensor, self.floats, self.at = tensor, floats, 0

    def reset(self, at=0):
        self.at = at

    def take(self, *shape, parts=P):
        n = int(np.prod(shape))
        assert self.at + n <= self.floats, (self.at, n)
        view = self.tensor[0:parts, self.at:self.at + n]
        self.at += n
        if len(shape) == 2:
            view = view.rearrange("p (a b) -> p a b", a=shape[0])
        elif len(shape) == 3:
            view = view.rearrange("p (a b c) -> p a b c", a=shape[0], b=shape[1])
        elif len(shape) == 4:
            view = view.rearrange("p (a b c d) -> p a b c d", a=shape[0], b=shape[1], c=shape[2])
        return view


class Program:

    def __init__(self, nc, ctx, ins, out, scratch):
        self.nc, self.ins, self.out, self.scratch = nc, ins, out, scratch
        self.ctx = ctx
        self.x = ctx.enter_context(nc.sbuf_tensor("x", [P, TILES, DIM], F32))
        self.xn = ctx.enter_context(nc.sbuf_tensor("xn", [P, TILES, DIM], F32))
        self.xT = ctx.enter_context(nc.sbuf_tensor("xT", [P, TOKENS], F32))
        self.ident = ctx.enter_context(nc.sbuf_tensor("ident", [P, P], F32))
        self.stats = ctx.enter_context(nc.sbuf_tensor("stats", [P, TILES, 6], F32))
        self.moments = ctx.enter_context(nc.sbuf_tensor("moments", [P, TILES, 2], F32))
        self.ln_a = ctx.enter_context(nc.sbuf_tensor("ln_a", [P, TILES], F32))
        self.spare = ctx.enter_context(nc.sbuf_tensor("spare", [P, 1], F32))
        self.ln_b = ctx.enter_context(nc.sbuf_tensor("ln_b", [P, TILES], F32))
        floats = 45600
        self.arena = Arena(ctx.enter_context(nc.sbuf_tensor("arena", [P, floats], F32)), floats)
        self.ps = ctx.enter_context(nc.psum_tensor("ps", [P, 8, 512], F32))
        self.sems, self.blocks = {}, 0

    def sem(self, name):
        if name not in self.sems:
            self.sems[name] = self.ctx.enter_context(self.nc.semaphore(name))
        return self.sems[name]


def bc(ap, n):
    return ap.unsqueeze(2).broadcast_to([ap.shape[0], ap.shape[1], n])


def hold(k, eng, name, value):
    eng.wait_ge(k.sem(name), value)
    eng.sem_inc(k.sem("holds"), 1)


def use_table(k, a, function):
    a.activation(k.spare[:, :], k.ident[:, 0:1], function)



def norm_dve(k, v, n, src, dst, eps=LN_EPS, center=True):
    v.drain()
    for t in range(TILES):
        v.bn_stats(k.stats[:, t, :], src[:, t, :])
    v.drain()
    for t in range(TILES):
        v.bn_aggr(k.moments[:, t, :], k.stats[:, t, :])
    v.drain()
    mean, var = k.moments[:, :, 0], k.moments[:, :, 1]
    if not center:
        v.tensor_tensor(k.ln_a[:, :], mean, mean, ALU.mult)
        v.drain()
        v.tensor_tensor(k.moments[:, :, 1], k.ln_a[:, :], var, ALU.add)
        v.drain()
    v.tensor_scalar(k.ln_a[:, :], var, eps, None, ALU.add).then_inc(k.sem("ln_var"), 1)
    v.wait_ge(k.sem("ln_sd"), n + 1)
    v.reciprocal(k.ln_b[:, :], k.ln_b[:, :])
    v.drain()
    for t in range(TILES):
        if center:
            o = v.tensor_scalar(dst[:, t, :], src[:, t, :], k.moments[:, t, 0:1], k.ln_b[:, t:t + 1],
                                ALU.subtract, ALU.mult)
        else:
            o = v.tensor_scalar(dst[:, t, :], src[:, t, :], k.ln_b[:, t:t + 1], None, ALU.mult)
        if t % TPG == TPG - 1:
            o.then_inc(k.sem("ln_done"), 1)


def norm_act(k, a, n):
    a.wait_ge(k.sem("ln_var"), n + 1)
    a.activation(k.ln_b[:, :], k.ln_a[:, :], ACT.Sqrt).then_inc(k.sem("ln_sd"), 1)


def transpose_pe(k, pe, src, ln=None):
    for g in range(GROUPS):
        if ln is not None:
            pe.wait_ge(k.sem("ln_done"), ln * GROUPS + g + 1)
        for j in range(TPG):
            t = pe.transpose(k.ps[:, g, j * P:(j + 1) * P], src[:, g * TPG + j, :], k.ident[:, :])
        t.then_inc(k.sem("ln_transposed"), 1)


def transpose_act(k, a, n, dst, gain=None, shift=None):
    for g in range(GROUPS):
        a.wait_ge(k.sem("ln_transposed"), n * GROUPS + g + 1)
        to = dst[:, g * GROUP:(g + 1) * GROUP]
        if gain is None:
            a.activation(to, k.ps[:, g, :], ACT.Copy).then_inc(k.sem("xT_ready"), 1)
        else:
            a.activation(to, k.ps[:, g, :], ACT.Identity, bias=shift, scale=gain).then_inc(k.sem("xT_ready"), 1)



def add_back_act(k, a, n, yT, scale):
    for g in range(GROUPS):
        a.activation(yT[:, g * GROUP:(g + 1) * GROUP], k.ps[:, g, :], ACT.Copy, scale=scale)\
            .then_inc(k.sem("y_evacuated"), 1)


def add_back_pe(k, pe, n, yT):
    for g in range(GROUPS):
        pe.wait_ge(k.sem("y_evacuated"), n * GROUPS + g + 1)
        for j in range(TPG):
            t = pe.transpose(k.ps[:, 4 + g, j * P:(j + 1) * P],
                             yT[:, g * GROUP + j * P:g * GROUP + (j + 1) * P], k.ident[:, :])
        t.then_inc(k.sem("y_back"), 1)


def add_back_dve(k, v, n):
    for g in range(GROUPS):
        v.wait_ge(k.sem("y_back"), n * GROUPS + g + 1)
        xg = k.x[:, g * TPG:(g + 1) * TPG, :]
        done = v.tensor_tensor(xg, k.ps[:, 4 + g, :].rearrange("p (a b) -> p a b", a=TPG), xg, ALU.add)
    done.then_inc(k.sem("x_updated"), 1)



def gate_logits_pe(k, pe, n, gate_w, experts):
    pe.wait_ge(k.sem("xT_ready"), (n + 1) * GROUPS)
    for t in range(TILES):
        m = pe.matmul(k.ps[:, 4, t * experts:(t + 1) * experts], k.xT[:, t * P:(t + 1) * P], gate_w,
                      start=True, stop=True)
    m.then_inc(k.sem("gate_logits"), 1)


def first_of_largest(k, v, cur, best, mask, rank, top):
    experts = cur.shape[2]
    v.drain()
    v.tensor_reduce(best, cur, X_AXIS, ALU.max)
    v.drain()
    v.tensor_tensor(mask, cur, bc(best, experts), ALU.is_ge)
    v.drain()
    v.tensor_tensor(mask, mask, rank[:, 0:experts].unsqueeze(1).broadcast_to([P, TILES, experts]), ALU.mult)
    v.drain()
    v.tensor_reduce(top, mask, X_AXIS, ALU.max)
    v.drain()
    v.tensor_tensor(mask, mask, bc(top, experts), ALU.is_equal)
    v.drain()


def gates_out_pe(k, pe, n, gates, chunks):
    pe.wait_ge(k.sem("gates_ready"), n + 1)
    flat = gates.rearrange("p e t -> p (e t)")
    for c in range(chunks):
        t = pe.transpose(k.ps[:, 5, c * P:(c + 1) * P], flat[:, c * P:(c + 1) * P], k.ident[:, :])
    t.then_inc(k.sem("gates_turned"), 1)


def gates_out_act(k, a, n, rows, chunks, dram_count, pairs_before):
    a.wait_ge(k.sem("gates_turned"), n + 1)
    a.activation(rows, k.ps[:, 5, 0:chunks * P], ACT.Copy).then_inc(k.sem("gate_rows"), 1)
    a.wait_ge(k.sem("gate_rows"), n + 1)
    dst = k.gates_dram[0:chunks * P, :].rearrange("(c q) p -> q c p", c=chunks)
    a.dma_start(dst, rows.rearrange("q (c p) -> q c p", c=chunks)).then_inc(k.sem("gates_stored"), 16)



E0, F0 = 8, 512
C0 = F0 // P
W0_COLS = F0 + F0 + C0


def relu_moe_layout(k):
    a = k.arena
    a.reset()
    b = {}
    b["yT"] = a.take(TOKENS)
    b["gate_w"] = a.take(E0)
    b["rank"] = a.take(32)
    b["b2"] = a.take(P)[0:E0, :]
    b["gateT"] = a.take(TOKENS)[0:E0, :]
    b["logits"] = a.take(TILES, E0)
    b["mask"] = a.take(TILES, E0)
    b["gates"] = a.take(E0, TILES)
    b["best"], b["top"], b["sum"] = a.take(TILES), a.take(TILES), a.take(TILES)
    b["rows"] = a.take(P)
    b["w"] = a.take(2, W0_COLS)
    b["gb"] = a.take(2, TOKENS)
    b["relu"] = a.take(4, GROUP)
    b["hid"] = a.take(4, GROUP)
    return b


STEPS0 = GROUPS * C0


def relu_moe_sync(k, sp, m, n, ln):
    b = relu_moe_layout(k)
    sp.wait_ge(k.sem("x_updated"), m + 1)
    sp.dma_start(b["gate_w"], k.ins["l0_gate_w"]).then_inc(k.sem("moe0_gate_w"), 16)
    sp.dma_start(b["rank"], k.ins["rank"].partition_broadcast(P)).then_inc(k.sem("moe0_gate_w"), 16)
    sp.dma_start(b["b2"], k.ins["l0_b2"]).then_inc(k.sem("moe0_gate_w"), 16)
    sp.wait_ge(k.sem("gates_stored"), 16 * (k.gate_stores[m] + 1))
    sp.dma_start(b["gateT"], k.gates_dram[0:E0 * TILES, :].rearrange("(e t) p -> e (t p)", e=E0))\
        .then_inc(k.sem("moe0_gateT"), 16)
    base = n * E0 * STEPS0

    def load(s, e):
        sp.dma_start(b["w"][:, s, :], k.ins["l0_w"][bass.ds(e, 1), :, :].rearrange("a p c -> (a p) c"))\
            .then_inc(k.sem(f"moe0_w{s}"), 16)
        sp.dma_start(b["gb"][:, s, :], k.gates_dram[bass.ds(e * TILES, TILES), :]
                     .rearrange("t p -> (t p)").partition_broadcast(P)).then_inc(k.sem(f"moe0_w{s}"), 16)

    load(0, 0)
    load(1, 1)
    with sp.Fori(0, E0 // 2 - 1) as i:
        for s in range(2):
            sp.wait_ge(k.sem("moe0_down"), LEAD + base + i * (2 * STEPS0) + (s + 1) * STEPS0)
            load(s, i * 2 + (2 + s))


def relu_moe_pe(k, pe, m, n, ln):
    b = relu_moe_layout(k)
    transpose_pe(k, pe, k.xn, ln)
    pe.wait_ge(k.sem("moe0_gate_w"), 48 * (n + 1))
    gate_logits_pe(k, pe, k.xt_calls[m], b["gate_w"], E0)
    gates_out_pe(k, pe, k.gate_stores[m], b["gates"], 1)
    pe.wait_ge(k.sem("gate_rows"), k.gate_stores[m] + 1)
    pe.wait_ge(k.sem("moe0_gateT"), 16 * (n + 1))
    for g in range(GROUPS):
        pe.matmul(k.ps[:, g, :], b["b2"], b["gateT"][:, g * GROUP:(g + 1) * GROUP], start=True, stop=True)
    base = n * E0 * STEPS0
    wbase = 16 * E0 * n
    with pe.Fori(0, E0 // 2) as i:
        for s in range(2):
            at = base + i * (2 * STEPS0) + s * STEPS0
            w = b["w"][:, s, :]
            pe.wait_ge(k.sem(f"moe0_w{s}"), wbase + 32 * i + 32)

            def up(step):
                g, c = divmod(step, C0)
                if step >= 4:
                    pe.wait_ge(k.sem("moe0_relu"), at + step - 3)
                pe.matmul(k.ps[:, 4 + step % 4, :], w[:, c * P:(c + 1) * P],
                          k.xT[:, g * GROUP:(g + 1) * GROUP], start=True, stop=True)\
                    .then_inc(k.sem("moe0_up"), 1)

            for step in range(3):
                up(step)
            for step in range(STEPS0):
                if step + 3 < STEPS0:
                    up(step + 3)
                g, c = divmod(step, C0)
                pe.wait_ge(k.sem("moe0_hidden"), at + (step + 1 + LEAD))
                pe.matmul(k.ps[:, g, :], w[:, F0 + c * P:F0 + (c + 1) * P], b["hid"][:, step % 4, :],
                          start=False, stop=True, skip_group_check=True).then_inc(k.sem("moe0_down"), 1)
    add_back_pe(k, pe, k.back_calls[m], b["yT"])


def relu_moe_act(k, a, m, n, ln):
    b = relu_moe_layout(k)
    norm_act(k, a, ln)
    transpose_act(k, a, k.xt_calls[m], k.xT)
    a.wait_ge(k.sem("gate_shifted"), n + 1)
    a.activation(b["logits"], b["logits"], ACT.Exp).then_inc(k.sem("gate_exp"), 1)
    gates_out_act(k, a, k.gate_stores[m], b["rows"], 1, None, None)
    base = n * E0 * STEPS0
    with a.Fori(0, E0 // 2) as i:
        for s in range(2):
            at = base + i * (2 * STEPS0) + s * STEPS0
            a.wait_ge(k.sem("moe0_hidden"), at + LEAD)
            for step in range(STEPS0):
                c = step % C0
                a.wait_ge(k.sem("moe0_up"), at + step + 1)
                if step >= 4:
                    a.wait_ge(k.sem("moe0_hidden"), at + (step - 3 + LEAD))
                a.activation(b["relu"][:, step % 4, :], k.ps[:, 4 + step % 4, :], ACT.Relu,
                             bias=b["w"][:, s, 2 * F0 + c:2 * F0 + c + 1]).then_inc(k.sem("moe0_relu"), 1)
    a.wait_ge(k.sem("moe0_down"), LEAD + base + E0 * STEPS0)
    add_back_act(k, a, k.back_calls[m], b["yT"], 0.5)


def relu_moe_dve(k, v, m, n, ln):
    b = relu_moe_layout(k)
    norm_dve(k, v, ln, k.x[:, :, :], k.xn[:, :, :])
    gc = k.gate_calls[m]
    v.wait_ge(k.sem("gate_logits"), gc + 1)
    v.tensor_copy(b["logits"], k.ps[:, 4, 0:TILES * E0].rearrange("p (t e) -> p t e", t=TILES))
    first_of_largest(k, v, b["logits"], b["best"], b["mask"], b["rank"], b["top"])
    v.tensor_tensor(b["logits"], b["logits"], bc(b["best"], E0), ALU.subtract).then_inc(k.sem("gate_shifted"), 1)
    v.wait_ge(k.sem("gate_exp"), n + 1)
    v.tensor_reduce(b["sum"], b["logits"], X_AXIS, ALU.add)
    v.drain()
    v.reciprocal(b["sum"], b["sum"])
    v.drain()
    v.tensor_tensor(b["gates"].rearrange("p e t -> p t e"), b["mask"], bc(b["sum"], E0), ALU.mult)\
        .then_inc(k.sem("gates_ready"), 1)
    base = n * E0 * STEPS0
    wbase = 16 * E0 * n
    with v.Fori(0, E0 // 2) as i:
        for s in range(2):
            at = base + i * (2 * STEPS0) + s * STEPS0
            v.wait_ge(k.sem(f"moe0_w{s}"), wbase + 32 * i + 32)
            v.wait_ge(k.sem("moe0_down"), at + LEAD)
            for step in range(STEPS0):
                g = step // C0
                v.wait_ge(k.sem("moe0_relu"), at + step + 1)
                if step >= 4:
                    v.wait_ge(k.sem("moe0_down"), at + (step - 3 + LEAD))
                v.tensor_tensor(b["hid"][:, step % 4, :], b["relu"][:, step % 4, :],
                                b["gb"][:, s, g * GROUP:(g + 1) * GROUP], ALU.mult)\
                    .then_inc(k.sem("moe0_hidden"), 1)
    add_back_dve(k, v, k.back_calls[m])



HD0, HD1 = 64, 8
HEADS = 16
HEAD_RUNS = BATCH * HEADS
KTILES = SEQ // P
SPAN = SEQ + KTILES * P - P


class Attention:
    def __init__(self, name, blocks, width, causal=False, bias=False):
        self.name, self.blocks, self.width, self.causal, self.bias = name, blocks, width, causal, bias
        self.heads = P // width
        self.hold = min(self.heads, 4)
        self.steps = self.hold * KTILES
        self.rounds = self.heads // self.hold


A0 = Attention("a0", 8, HD0)
A1 = Attention("a1", 1, HD1, bias=True)
A3 = Attention("a3", 1, HD1, causal=True)


def attention_layout(k, c):
    a = k.arena
    a.reset()
    b = {}
    b["w"] = a.take(3 * P)
    b["mask"] = a.take(c.heads)
    b["q"], b["k"] = a.take(TOKENS), a.take(TOKENS)
    b["v"] = a.take(TILES, P)
    b["qm"] = a.take(c.hold, SEQ)
    b["p"] = a.take(2, SEQ)
    b["pT"] = a.take(2, SEQ)
    b["negmax"], b["sum"] = a.take(c.steps), a.take(c.steps)
    b["att"] = a.take(TILES, c.blocks * P)
    b["w_out"] = a.take(c.blocks, P)
    b["tri"] = a.take(P)
    if c.bias:
        b["s"] = a.take(2, SEQ)
        b["toeplitz"] = a.take(c.hold, SPAN)
        b["v_bias"], b["out_bias"] = a.take(P), a.take(P)
        b["vec"] = a.take(4)
        b["w_rel"] = a.take(HEADS)[0:HD1, :]
        b["rel_pe"] = a.take(2 * SEQ)[0:HD1, :]
        b["rel"] = a.take(2 * SEQ)[0:HEADS, :]
    if c.blocks > 1:
        b["gelu"] = a.take(2, c.blocks * P)
        b["gT"] = a.take(2, c.blocks * P)
    else:
        b["attT"] = a.take(TOKENS)
    return b


def attention_sync(k, sp, m, n, ln, c):
    b = attention_layout(k, c)
    w = k.ins[c.name + "_w"]
    sp.wait_ge(k.sem("x_updated"), m + 1)
    ready = k.sem(c.name + "_loaded")
    sp.dma_start(b["mask"], k.ins[c.name + "_mask"]).then_inc(ready, 16)
    sp.dma_start(b["w_out"], k.ins[c.name + "_w_out"]).then_inc(ready, 16)
    sp.dma_start(b["tri"], k.ins["tri"]).then_inc(ready, 16)
    weights = k.sem("att_w")
    wb = k.att_blocks[m]

    def load(i):
        sp.dma_start(b["w"], w[bass.ds(i, 1), :, :].rearrange("a p c -> (a p) c")).then_inc(weights, 16)

    load(0)
    if c.blocks > 1:
        with sp.Fori(0, c.blocks - 1) as i:
            sp.wait_ge(k.sem("v_projected"), (wb + 1) * GROUPS + i * GROUPS)
            load(i + 1)
    if c.bias:
        sp.dma_start(b["vec"], k.ins["a1_vec"]).then_inc(ready, 16)
        sp.dma_start(b["v_bias"], k.ins["a1_v_bias"].partition_broadcast(P)).then_inc(ready, 16)
        sp.dma_start(b["out_bias"], k.ins["a1_out_bias"].partition_broadcast(P)).then_inc(ready, 16)
        sp.dma_start(b["w_rel"], k.ins["a1_w_rel"]).then_inc(k.sem("rel_loaded"), 16)
        sp.dma_start(b["rel_pe"], k.ins["rel_pe"]).then_inc(k.sem("rel_loaded"), 16)
        sp.wait_ge(k.sem("rel_ready"), 1)
        sp.dma_start(k.rel_dram, b["rel"]).then_inc(k.sem("rel_stored"), 16)
        sp.wait_ge(k.sem("rel_stored"), 16)
        shifted = bass.AP(tensor=k.rel_dram.tensor, offset=k.rel_dram.offset + P - 1,
                          ap=[[2 * SEQ, HEADS], [-1, P], [1, SPAN]])
        sp.dma_start(k.toeplitz_dram, shifted).then_inc(k.sem("toeplitz_stored"), 16)
        sp.wait_ge(k.sem("toeplitz_stored"), 16)
        with sp.Fori(0, BATCH) as bt:
            with sp.Fori(0, c.rounds) as r:
                for s in range(c.hold):
                    sp.wait_ge(k.sem("toeplitz_used"), bt * c.heads + r * c.hold + (s + 1))
                    src = k.toeplitz_dram[bass.ds(r * c.hold + s, 1), :, :].rearrange("h p m -> (h p) m")
                    sp.dma_start(b["toeplitz"][:, s, :], src).then_inc(k.sem(f"toeplitz{s}"), 16)


def attention_loops(eng, c, head0, block_of_heads, begin, iteration):
    if c.blocks > 1:
        with eng.Fori(0, c.blocks) as blk:
            head = head0 + blk * (BATCH * c.heads)
            block_of_heads(blk)
            begin(head, 0)
            with eng.Fori(0, BATCH - 1) as bt:
                iteration(head0 + blk * (BATCH * c.heads) + bt * c.heads, bt, 0, False)
            iteration(head + (BATCH - 1) * c.heads, BATCH - 1, 0, True)
    else:
        block_of_heads(0)
        with eng.Fori(0, BATCH) as bt:
            head = head0 + bt * c.heads
            begin(head, bt)
            with eng.Fori(0, c.rounds - 1) as r:
                iteration(head0 + bt * c.heads + r * c.hold, bt, r, False)
            iteration(head + (c.rounds - 1) * c.hold, bt, c.rounds - 1, True)


def attention_pe(k, pe, m, n, ln, c):
    b = attention_layout(k, c)
    head0, wb = k.att_calls[m] * HEAD_RUNS, k.att_blocks[m]
    transpose_pe(k, pe, k.xn, ln + (1 if c.bias else 0))
    pe.wait_ge(k.sem("xT_ready"), (k.xt_calls[m] + 1) * GROUPS)
    if c.bias:
        pe.wait_ge(k.sem("rel_loaded"), 32)
        for h in range(2):
            r = pe.matmul(k.ps[0:HEADS, 6 + h, :], b["w_rel"], b["rel_pe"][:, h * SEQ:(h + 1) * SEQ],
                          start=True, stop=True)
        r.then_inc(k.sem("rel_multiplied"), 1)
        pe.wait_ge(k.sem("rel_ready"), 1)
    pe.wait_ge(k.sem(c.name + "_loaded"), 16 * (6 if c.bias else 3))

    def block_of_heads(blk):
        pe.wait_ge(k.sem("att_w"), 16 * (wb + 1) + 16 * blk)
        pe.wait_ge(k.sem("heads_done"), LEAD + head0 + blk * (BATCH * c.heads))
        for g in range(GROUPS):
            xg = k.xT[:, g * GROUP:(g + 1) * GROUP]
            pe.matmul(k.ps[:, g, :], b["w"][:, 0:P], xg, start=True, stop=True).then_inc(k.sem("qk_projected"), 1)
            pe.matmul(k.ps[:, 4 + g, :], b["w"][:, P:2 * P], xg, start=True, stop=True)\
                .then_inc(k.sem("qk_projected"), 1)
        for g in range(GROUPS):
            pe.wait_ge(k.sem("qk_ready"), 8 * wb + 2 * g + 1 + 8 * blk)
            for j in range(TPG):
                t = g * TPG + j
                o = pe.matmul(k.ps[:, g, j * P:(j + 1) * P], k.xT[:, t * P:(t + 1) * P], b["w"][:, 2 * P:3 * P],
                              start=True, stop=True)
            o.then_inc(k.sem("v_projected"), 1)
        pe.wait_ge(k.sem("qk_ready"), 8 * (wb + 1) + 8 * blk)
        hold(k, pe, "v_ready", GROUPS * (wb + 1) + GROUPS * blk)

    def scores(head, bt, step):
        s, j = divmod(step % c.steps, KTILES)
        at = head * KTILES
        if j == 0:
            pe.wait_ge(k.sem("queries_masked"), head + (step // KTILES + 1))
        if c.bias:
            pe.wait_ge(k.sem("maxima"), at + (step - 1 + LEAD))
        else:
            pe.wait_ge(k.sem("probs"), at + (step - 1 + LEAD))
        cols = (j + 1) * P if c.causal else SEQ
        o = pe.matmul(k.ps[:, step % 2, 0:cols], b["qm"][:, s, j * P:(j + 1) * P],
                      b["k"][:, bass.ds(bt * SEQ, cols)], start=True, stop=not c.causal)
        if c.causal:
            o = pe.matmul(k.ps[:, step % 2, j * P:(j + 1) * P], k.ident[:, :], b["tri"],
                          start=False, stop=True)
        o.then_inc(k.sem("scores"), 1)

    def iteration(head, bt, r, last):
        at = head * KTILES

        def turn(step):
            tiles = step % KTILES + 1 if c.causal else KTILES
            pe.wait_ge(k.sem("probs"), at + (step + 1 + LEAD))
            pe.wait_ge(k.sem("probs_copied"), at + (step - 1 + LEAD))
            for t in range(tiles):
                o = pe.transpose(k.ps[:, 2 + step % 2, t * P:(t + 1) * P],
                                 b["p"][:, step % 2, t * P:(t + 1) * P], k.ident[:, :])
            o.then_inc(k.sem("probs_turned"), 1)

        def values(step):
            s, j = divmod(step, KTILES)
            tiles = j + 1 if c.causal else KTILES
            pe.wait_ge(k.sem("probs_copied"), at + (step + 1 + LEAD))
            if j == 0:
                pe.wait_ge(k.sem("heads_done"), head + (s - 1 + LEAD))
            for t in range(tiles):
                o = pe.matmul(k.ps[:, 4 + s % 2, j * c.width:(j + 1) * c.width],
                              b["pT"][:, step % 2, t * P:(t + 1) * P],
                              b["v"].rearrange("p t d -> p (t d)")
                              [:, bass.ds(bt * SEQ + r * (c.hold * c.width) + (t * P + s * c.width), c.width)],
                              start=(t == 0), stop=(t == tiles - 1))
            o.then_inc(k.sem("values"), 1)

        for step in range(c.steps):
            turn(step)
            if step + 2 < c.steps:
                scores(head, bt, step + 2)
            elif not last:
                scores(head, bt + (1 if c.rounds == 1 else 0), step + 2)
            if step >= 1:
                values(step - 1)
        values(c.steps - 1)

    def begin(head, bt):
        scores(head, bt, 0)
        scores(head, bt, 1)

    attention_loops(pe, c, head0, block_of_heads, begin, iteration)

    pe.wait_ge(k.sem("heads_done"), LEAD + head0 + HEAD_RUNS)
    if c.blocks > 1:
        with pe.Fori(0, TILES // 2) as i:
            for s in range(2):
                pe.wait_ge(k.sem("att_gelu"), i * 2 + (s + 1))
                for h in range(2):
                    for j in range(4):
                        cc = 4 * h + j
                        o = pe.transpose(k.ps[:, 2 * s + h, j * P:(j + 1) * P],
                                         b["gelu"][:, s, cc * P:(cc + 1) * P], k.ident[:, :])
                    o.then_inc(k.sem("gelu_turned"), 1)
            for s in range(2):
                pe.wait_ge(k.sem("gelu_copied"), i * 4 + (2 * s + 2))
                pe.wait_ge(k.sem("att_added"), LEAD + i * 2)
                for cc in range(c.blocks):
                    o = pe.matmul(k.ps[:, 4 + s, 0:P], b["gT"][:, s, cc * P:(cc + 1) * P], b["w_out"][:, cc, :],
                                  start=(cc == 0), stop=(cc == c.blocks - 1))
                o.then_inc(k.sem("att_projected"), 1)
    else:
        for g in range(GROUPS):
            for j in range(TPG):
                t = g * TPG + j
                o = pe.transpose(k.ps[:, g, j * P:(j + 1) * P], b["att"][:, t, :], k.ident[:, :])
            o.then_inc(k.sem("att_turned"), 1)
        for g in range(GROUPS):
            pe.wait_ge(k.sem("att_copied"), (n + k.flat_calls[m]) * GROUPS + g + 1)
            for j in range(TPG):
                t = g * TPG + j
                o = pe.matmul(k.ps[:, 4 + g, j * P:(j + 1) * P], b["attT"][:, t * P:(t + 1) * P], b["w_out"][:, 0, :],
                              start=True, stop=True)
            o.then_inc(k.sem("flat_projected"), 1)


def attention_act(k, a, m, n, ln, c):
    b = attention_layout(k, c)
    head0, wb = k.att_calls[m] * HEAD_RUNS, k.att_blocks[m]
    norm_act(k, a, ln)
    if c.bias:
        norm_act(k, a, ln + 1)
        a.wait_ge(k.sem("a1_loaded"), 16 * 6)
        transpose_act(k, a, k.xt_calls[m], k.xT, b["vec"][:, 0:1], b["vec"][:, 1:2])
        a.wait_ge(k.sem("rel_multiplied"), 1)
        a.activation(b["rel"].rearrange("h (a b) -> h a b", a=2), k.ps[0:HEADS, 6:8, :], ACT.Copy)\
            .then_inc(k.sem("rel_ready"), 1)
    else:
        transpose_act(k, a, k.xt_calls[m], k.xT)

    def block_of_heads(blk):
        a.wait_ge(k.sem("heads_done"), LEAD + head0 + blk * (BATCH * c.heads))
        for g in range(GROUPS):
            for half, dst in enumerate((b["q"], b["k"])):
                a.wait_ge(k.sem("qk_projected"), 8 * wb + 2 * g + half + 1 + 8 * blk)
                to, src = dst[:, g * GROUP:(g + 1) * GROUP], k.ps[:, 4 * half + g, :]
                if c.bias:
                    o = a.activation(to, src, ACT.Identity, bias=b["vec"][:, 2 + half:3 + half])
                else:
                    o = a.activation(to, src, ACT.Copy)
                o.then_inc(k.sem("qk_ready"), 1)

    def iteration(head, bt, r, last):
        at = head * KTILES
        for step in range(c.steps):
            cols = (step % KTILES + 1) * P if c.causal else SEQ
            a.wait_ge(k.sem("maxima"), at + (step + 1 + LEAD))
            a.wait_ge(k.sem("probs_turned"), at + (step - 1 + LEAD))
            src = b["s"][:, step % 2, :] if c.bias else k.ps[:, step % 2, 0:cols]
            a.activation(b["p"][:, step % 2, 0:cols], src, ACT.Exp, bias=b["negmax"][:, step:step + 1],
                         scale=-1.0 if c.bias else 1.0, accum_out=b["sum"][:, step:step + 1])\
                .then_inc(k.sem("probs"), 1)

    use_table(k, a, ACT.Exp)
    attention_loops(a, c, head0, block_of_heads, lambda head, bt: None, iteration)

    a.wait_ge(k.sem("heads_done"), LEAD + head0 + HEAD_RUNS)
    if c.blocks > 1:
        use_table(k, a, ACT.Gelu)
        with a.Fori(0, TILES // 2) as i:
            for s in range(2):
                a.wait_ge(k.sem("gelu_turned"), LEAD + i * 4)
                a.activation(b["gelu"][:, s, :], b["att"][:, bass.ds(i * 2 + s, 1), :].rearrange("p a c -> p (a c)"),
                             ACT.Gelu).then_inc(k.sem("att_gelu"), 1)
            for s in range(2):
                for h in range(2):
                    a.wait_ge(k.sem("gelu_turned"), i * 4 + (2 * s + h + 1 + LEAD))
                    if s == 0 and h == 0:
                        a.wait_ge(k.sem("att_projected"), LEAD + i * 2)
                    a.activation(b["gT"][:, s, h * 512:(h + 1) * 512], k.ps[:, 2 * s + h, :], ACT.Copy)\
                        .then_inc(k.sem("gelu_copied"), 1)
    else:
        for g in range(GROUPS):
            a.wait_ge(k.sem("att_turned"), (n + k.flat_calls[m]) * GROUPS + g + 1)
            a.activation(b["attT"][:, g * GROUP:(g + 1) * GROUP], k.ps[:, g, :], ACT.Copy)\
                .then_inc(k.sem("att_copied"), 1)


def attention_dve(k, v, m, n, ln, c):
    b = attention_layout(k, c)
    head0, wb = k.att_calls[m] * HEAD_RUNS, k.att_blocks[m]
    norm_dve(k, v, ln, k.x[:, :, :], k.xn[:, :, :])
    if c.bias:
        norm_dve(k, v, ln + 1, k.xn[:, :, :], k.xn[:, :, :])
    v.wait_ge(k.sem(c.name + "_loaded"), 16 * (6 if c.bias else 3))

    def block_of_heads(blk):
        for g in range(GROUPS):
            v.wait_ge(k.sem("v_projected"), GROUPS * wb + g + 1 + GROUPS * blk)
            to, src = b["v"][:, g * TPG:(g + 1) * TPG, :], k.ps[:, g, :].rearrange("p (a b) -> p a b", a=TPG)
            if c.bias:
                o = v.tensor_tensor(to, src, b["v_bias"].unsqueeze(1).broadcast_to([P, TPG, P]), ALU.add)
            else:
                o = v.tensor_copy(to, src)
            o.then_inc(k.sem("v_ready"), 1)
        hold(k, v, "qk_ready", 8 * (wb + 1) + 8 * blk)

    def mask(head, bt, r, s):
        if s >= c.hold:
            v.wait_ge(k.sem("scores"), head * KTILES + ((s - c.hold + 1) * KTILES + LEAD))
        v.tensor_scalar(b["qm"][:, s % c.hold, :], b["q"][:, bass.ds(bt * SEQ, SEQ)],
                        b["mask"][:, bass.ds(r * c.hold + s % c.hold, 1)], None, ALU.mult)\
            .then_inc(k.sem("queries_masked"), 1)

    def maximum(head, step):
        at = head * KTILES
        s, j = divmod(step % c.steps, KTILES)
        cols = (j + 1) * P if c.causal else SEQ
        negmax = b["negmax"][:, step % c.steps:step % c.steps + 1]
        if c.bias:
            if j == 0:
                v.wait_ge(k.sem(f"toeplitz{s}"), head * (16 // c.hold) + (16 - head0 * (16 // c.hold)
                                                                     + (16 if step >= c.steps else 0)))
            v.wait_ge(k.sem("probs"), at + (step - 1 + LEAD))
            hold(k, v, "scores", at + (step + 1 + LEAD))
            v.tensor_tensor_reduce(b["s"][:, step % 2, :], k.ps[:, step % 2, :],
                                   b["toeplitz"][:, s, 384 - j * P:384 - j * P + SEQ], -1.0, 3.0e38,
                                   ALU.add, ALU.min, negmax).then_inc(k.sem("maxima"), 1)
            if j == KTILES - 1:
                v.drain()
                v.sem_inc(k.sem("toeplitz_used"), 1)
        else:
            v.wait_ge(k.sem("scores"), at + (step + 1 + LEAD))
            v.tensor_reduce(negmax, k.ps[:, step % 2, 0:cols], X_AXIS, ALU.max, negate=True)\
                .then_inc(k.sem("maxima"), 1)

    blocks_loop = {}

    def iteration(head, bt, r, last):
        at = head * KTILES

        def copy(step):
            cols = (step % KTILES + 1) * P if c.causal else SEQ
            v.wait_ge(k.sem("values"), at + (step - 1 + LEAD))
            v.wait_ge(k.sem("probs_turned"), at + (step + 1 + LEAD))
            v.tensor_copy(b["pT"][:, step % 2, 0:cols], k.ps[:, 2 + step % 2, 0:cols])\
                .then_inc(k.sem("probs_copied"), 1)

        def finish(s):
            total = b["sum"][:, KTILES * s:KTILES * s + KTILES]
            v.wait_ge(k.sem("values"), at + (KTILES * (s + 1) + LEAD))
            v.reciprocal(total, total)
            v.drain()
            col = r * (c.hold * c.width) + s * c.width
            if c.blocks > 1:
                col = blocks_loop["blk"] * P + col
            out = b["att"][:, bass.ds(bt * KTILES, KTILES), bass.ds(col, c.width)]
            v.tensor_tensor(out, k.ps[:, 4 + s % 2, 0:KTILES * c.width].rearrange("p (a b) -> p a b", a=KTILES),
                            bc(total, c.width), ALU.mult).then_inc(k.sem("heads_done"), 1)

        for step in range(c.steps):
            copy(step)
            s, j = divmod(step, KTILES)
            if not last and j == KTILES - 3 and s:
                mask(head, bt + 1 if c.rounds == 1 else bt, r if c.rounds == 1 else r + 1, c.hold + s - 1)
            if step + 2 < c.steps or not last:
                maximum(head, step + 2)
            if j == 1 and s:
                finish(s - 1)
        if not last:
            mask(head, bt + 1 if c.rounds == 1 else bt, r if c.rounds == 1 else r + 1, 2 * c.hold - 1)
        finish(c.hold - 1)

    def begin(head, bt):
        for s in range(c.hold):
            mask(head, bt, 0, s)
        maximum(head, 0)
        maximum(head, 1)

    def first_block(blk):
        blocks_loop["blk"] = blk
        block_of_heads(blk)

    if c.bias:
        v.sem_inc(k.sem("toeplitz_used"), c.hold)
    attention_loops(v, c, head0, first_block, begin, iteration)
    if c.blocks > 1:
        v.tensor_tensor(k.x[:, :, :], k.x[:, :, :], k.xn[:, :, :], ALU.add)
        with v.Fori(0, TILES // 2) as i:
            for s in range(2):
                xt = k.x[:, bass.ds(i * 2 + s, 1), :].rearrange("p a d -> p (a d)")
                v.drain()
                v.wait_ge(k.sem("att_projected"), i * 2 + (s + 1 + LEAD))
                v.tensor_tensor(xt, k.ps[:, 4 + s, 0:P], xt, ALU.add).then_inc(k.sem("att_added"), 1)
        v.drain()
        v.tensor_copy(k.ln_a[:, :], k.x[:, :, 0]).then_inc(k.sem("x_updated"), 1)
    else:
        if c.bias:
            v.tensor_tensor(k.x[:, :, :], k.x[:, :, :], b["out_bias"].unsqueeze(1).broadcast_to([P, TILES, P]), ALU.add)
            v.drain()
        for g in range(GROUPS):
            v.wait_ge(k.sem("flat_projected"), (n + k.flat_calls[m]) * GROUPS + g + 1)
            xg = k.x[:, g * TPG:(g + 1) * TPG, :]
            o = v.tensor_tensor(xg, k.ps[:, 4 + g, :].rearrange("p (a b) -> p a b", a=TPG), xg, ALU.add)
        o.then_inc(k.sem("x_updated"), 1)


def lay_out_attention(a, i):
    import numpy as _np

    c, f = _np.ascontiguousarray, _np.float32
    feature = _np.arange(P)
    for at, n in ((A0, "a0"), (A1, "a1"), (A3, "a3")):
        a[n + "_mask"] = c((feature[:, None] // at.width == _np.arange(at.heads)[None, :]).astype(f)
                           * f(1.0 / math.sqrt(at.width)))
    a["tri"] = _np.where(feature[:, None] >= feature[None, :], f(0), f(-1e30)).astype(f)
    a["a0_w"] = c(_np.stack([i["L0_attn_Wq"], i["L0_attn_Wk"], i["L0_attn_Wv"]]).reshape(3, P, 8, P)
                  .transpose(2, 1, 0, 3).reshape(8, P, 3 * P))
    a["a0_w_out"] = c(i["L0_attn_Wpost"].reshape(8, P, P).transpose(1, 0, 2))
    a["a1_w"] = c(i["L1_attn_w_qkv"][None])
    a["a1_w_out"] = c(i["L1_attn_w_out"].reshape(P, 1, P))
    bq = i["L1_attn_b_qkv"].reshape(3, P)
    a["a1_vec"] = c(_np.stack([i["L1_attn_ln_g"], i["L1_attn_ln_b"], bq[0], bq[1]], axis=1))
    a["a1_v_bias"], a["a1_out_bias"], a["a1_w_rel"] = c(bq[2]), i["L1_attn_b_out"], i["L1_attn_w_rel"]
    a["a3_w"] = c(_np.stack([i["L3_attn_WQ"], i["L3_attn_WK"], i["L3_attn_WV"]]).reshape(3, P, P)
                  .transpose(2, 0, 1).reshape(1, P, 3 * P))
    a["a3_w_out"] = c(i["L3_attn_WO"].transpose(0, 2, 1).reshape(P, 1, P))
    pos = _np.arange(-(SEQ - 1), SEQ, dtype=f)[:, None]
    div = _np.exp(_np.arange(0, HD1, 2, dtype=f) * f(-math.log(10000.0) / HD1)).astype(f)
    angle = (pos * div).astype(_np.float64)
    pe = _np.zeros((2 * SEQ, HD1), f)
    pe[:2 * SEQ - 1, 0::2], pe[:2 * SEQ - 1, 1::2] = _np.sin(angle)[::-1], _np.cos(angle)[::-1]
    a["rel_pe"] = c(pe.T)



E2, F2 = 8, 512
C2 = F2 // P
W2_COLS = 3 * F2
STEPS2 = GROUPS * C2


def swiglu_layout(k):
    a = k.arena
    a.reset()
    b = {}
    b["small"] = a.take(2 * P + E2 + 32 + 2)
    b["w_in"], b["w_out"] = b["small"][:, 0:P], b["small"][:, P:2 * P]
    b["router"] = b["small"][:, 2 * P:2 * P + E2]
    b["gains"] = b["small"][:, 2 * P + E2 + 32:]
    b["rank"] = a.take(32)
    b["e_bias"] = a.take(E2)
    b["h"] = a.take(TILES, P)
    b["hT"] = a.take(TOKENS)
    b["sq"] = a.take(TILES, P)
    for name in ("logits", "cur", "mask1", "mask2", "pick"):
        b[name] = a.take(TILES, E2)
    b["best"], b["top"] = a.take(TILES), a.take(TILES)
    b["l"] = a.take(2, TILES)
    b["g"] = a.take(2, TILES)
    b["gates"] = a.take(E2, TILES)
    b["ms"], b["factor"] = a.take(TILES), a.take(TILES)
    b["w"] = a.take(2, W2_COLS)
    b["enorm"] = a.take(2, P)
    b["silu"] = a.take(2, GROUP)
    b["hid"] = a.take(2, C2, GROUP)
    b["scaled"] = a.take(TILES, P)
    b["acc"] = a.take(TILES, P)
    return b


def swiglu_sync(k, sp, m, n, ln):
    b = swiglu_layout(k)
    sp.wait_ge(k.sem("x_updated"), m + 1)
    ready = k.sem("moe2_loaded")
    sp.dma_start(b["small"], k.ins["l2_small"]).then_inc(ready, 16)
    sp.dma_start(b["rank"], k.ins["rank"].partition_broadcast(P)).then_inc(ready, 16)
    sp.dma_start(b["e_bias"], k.ins["l2_e_bias"].partition_broadcast(P)).then_inc(ready, 16)

    def load(s, e):
        sp.dma_start(b["w"][:, s, :], k.ins["l2_w"][bass.ds(e, 1), :, :].rearrange("a p c -> (a p) c"))\
            .then_inc(k.sem(f"moe2_w{s}"), 16)
        sp.dma_start(b["enorm"][:, s, :], k.ins["l2_enorm"][bass.ds(e, 1), :].rearrange("a c -> (a c)")
                     .partition_broadcast(P)).then_inc(k.sem(f"moe2_w{s}"), 16)

    load(0, 0)
    load(1, 1)
    with sp.Fori(0, E2 // 2 - 1) as i:
        for s in range(2):
            sp.wait_ge(k.sem("moe2_summed"), n * E2 + i * 2 + (s + 1))
            load(s, i * 2 + (s + 2))


def swiglu_pairs(eng, body):
    body(0, 0, True)
    body(1, 1, False)
    with eng.Fori(1, E2 // 2) as i:
        for s in range(2):
            body(i * 2 + s, s, False)


def project_back_pe(k, pe, b, n, src, w, signal):
    for g in range(GROUPS):
        for j in range(TPG):
            t = g * TPG + j
            o = pe.matmul(k.ps[:, 4 + g, j * P:(j + 1) * P], src[:, t * P:(t + 1) * P], w, start=True, stop=True)
        o.then_inc(k.sem(signal), 1)


def swiglu_pe(k, pe, m, n, ln):
    b = swiglu_layout(k)
    xt = k.xt_calls[m]
    transpose_pe(k, pe, k.xn, ln)
    pe.wait_ge(k.sem("moe2_loaded"), 48 * (n + 1))
    pe.wait_ge(k.sem("xT_ready"), (xt + 1) * GROUPS)
    project_back_pe(k, pe, b, n, k.xT, b["w_in"], "h_projected")
    transpose_pe(k, pe, b["h"], ln + 1)
    pe.wait_ge(k.sem("xT_ready"), (xt + 2) * GROUPS)
    for t in range(TILES):
        o = pe.matmul(k.ps[:, 4, t * E2:(t + 1) * E2], b["hT"][:, t * P:(t + 1) * P], b["router"],
                      start=True, stop=True)
    o.then_inc(k.sem("gate_logits"), 1)
    pe.wait_ge(k.sem("logits_copied"), n + 1)

    def body(e, s, first):
        ee = e + n * E2
        w = b["w"][:, s, :]
        if isinstance(e, int):
            pe.wait_ge(k.sem(f"moe2_w{s}"), 16 * E2 * n + 32)
        else:
            pe.wait_ge(k.sem(f"moe2_w{s}"), 16 * E2 * n + (e - s) * 16 + 32)

        def up(g):
            for c in range(C2):
                step = g * C2 + c
                if step >= 2:
                    pe.wait_ge(k.sem("moe2_hidden"), ee * STEPS2 + (step - 1))
                for half in range(2):
                    o = pe.matmul(k.ps[:, 4 + 2 * (step % 2) + half, :],
                                  w[:, half * F2 + c * P:half * F2 + (c + 1) * P],
                                  b["hT"][:, g * GROUP:(g + 1) * GROUP], start=True, stop=True)
                o.then_inc(k.sem("moe2_up"), 1)

        def down(g):
            pe.wait_ge(k.sem("moe2_hidden"), ee * STEPS2 + C2 * (g + 1))
            for j in range(TPG):
                for c in range(C2):
                    o = pe.matmul(k.ps[:, g, j * P:(j + 1) * P], b["hid"][:, g % 2, c, j * P:(j + 1) * P],
                                  w[:, 2 * F2 + c * P:2 * F2 + (c + 1) * P], start=(c == 0), stop=(c == C2 - 1))
            o.then_inc(k.sem("moe2_down"), 1)

        up(0)
        up(1)
        pe.wait_ge(k.sem("moe2_taken"), ee)
        down(0)
        up(2)
        down(1)
        up(3)
        down(2)
        down(3)

    swiglu_pairs(pe, body)
    transpose_pe(k, pe, b["acc"], ln + 2)
    pe.wait_ge(k.sem("xT_ready"), (xt + 3) * GROUPS)
    project_back_pe(k, pe, b, n, b["hT"], b["w_out"], "out_projected")


def swiglu_act(k, a, m, n, ln):
    b = swiglu_layout(k)
    xt = k.xt_calls[m]
    norm_act(k, a, ln)
    transpose_act(k, a, xt, k.xT)
    norm_act(k, a, ln + 1)
    a.wait_ge(k.sem("moe2_loaded"), 48 * (n + 1))
    transpose_act(k, a, xt + 1, b["hT"], b["gains"][:, 0:1], 0.0)
    a.wait_ge(k.sem("pair_shifted"), n + 1)
    a.activation(b["g"], b["l"], ACT.Exp).then_inc(k.sem("pair_exp"), 1)

    def output_norm(ee):
        a.wait_ge(k.sem("moe2_down"), ee * GROUPS)
        a.activation(b["sq"].rearrange("p (g a) b -> p g (a b)", g=GROUPS), k.ps[:, 0:4, :], ACT.Square).then_inc(k.sem("moe2_squared"), 1)
        a.wait_ge(k.sem("moe2_mean"), ee)
        a.activation(b["factor"], b["ms"], ACT.Sqrt).then_inc(k.sem("moe2_root"), 1)

    def body(e, s, first):
        ee = e + n * E2
        for step in range(STEPS2):
            a.wait_ge(k.sem("moe2_up"), ee * STEPS2 + (step + 1))
            if step >= 2:
                a.wait_ge(k.sem("moe2_hidden"), ee * STEPS2 + (step - 1))
            a.activation(b["silu"][:, step % 2, :], k.ps[:, 4 + 2 * (step % 2), :], ACT.Silu)\
                .then_inc(k.sem("moe2_silu"), 1)
            if step == C2 - 1 and not first:
                output_norm(ee)

    swiglu_pairs(a, body)
    output_norm((n + 1) * E2)
    norm_act(k, a, ln + 2)
    transpose_act(k, a, xt + 2, b["hT"], b["gains"][:, 1:2], 0.0)


def swiglu_dve(k, v, m, n, ln):
    b = swiglu_layout(k)
    norm_dve(k, v, ln, k.x[:, :, :], k.xn[:, :, :])
    for g in range(GROUPS):
        v.wait_ge(k.sem("h_projected"), n * GROUPS + g + 1)
        v.tensor_copy(b["h"][:, g * TPG:(g + 1) * TPG, :], k.ps[:, 4 + g, :].rearrange("p (a b) -> p a b", a=TPG))
    norm_dve(k, v, ln + 1, b["h"], b["h"], F32_EPS, center=False)
    v.wait_ge(k.sem("moe2_loaded"), 48 * (n + 1))
    v.wait_ge(k.sem("gate_logits"), k.gate_calls[m] + 1)
    v.tensor_copy(b["logits"], k.ps[:, 4, 0:TILES * E2].rearrange("p (t e) -> p t e", t=TILES))\
        .then_inc(k.sem("logits_copied"), 1)
    v.drain()
    v.tensor_tensor(b["cur"], b["logits"], b["e_bias"].unsqueeze(1).broadcast_to([P, TILES, E2]), ALU.add)
    first_of_largest(k, v, b["cur"], b["best"], b["mask1"], b["rank"], b["top"])
    v.scalar_tensor_tensor(b["cur"], b["mask1"], NEG, b["cur"], ALU.mult, ALU.add)
    first_of_largest(k, v, b["cur"], b["best"], b["mask2"], b["rank"], b["top"])
    for r, mask in enumerate(("mask1", "mask2")):
        v.tensor_tensor(b["pick"], b["logits"], b[mask], ALU.mult)
        v.drain()
        v.tensor_reduce(b["l"][:, r, :], b["pick"], X_AXIS, ALU.add)
        v.drain()
    v.tensor_tensor(b["best"], b["l"][:, 0, :], b["l"][:, 1, :], ALU.max)
    v.drain()
    v.tensor_tensor(b["l"], b["l"], b["best"].unsqueeze(1).broadcast_to([P, 2, TILES]), ALU.subtract)\
        .then_inc(k.sem("pair_shifted"), 1)
    v.wait_ge(k.sem("pair_exp"), n + 1)
    v.tensor_tensor(b["best"], b["g"][:, 0, :], b["g"][:, 1, :], ALU.add)
    v.drain()
    v.reciprocal(b["best"], b["best"])
    v.drain()
    v.tensor_tensor(b["g"], b["g"], b["best"].unsqueeze(1).broadcast_to([P, 2, TILES]), ALU.mult)
    v.drain()
    v.tensor_tensor(b["mask1"], b["mask1"], bc(b["g"][:, 0, :], E2), ALU.mult)
    v.tensor_tensor(b["mask2"], b["mask2"], bc(b["g"][:, 1, :], E2), ALU.mult)
    v.drain()
    v.tensor_tensor(b["gates"].rearrange("p e t -> p t e"), b["mask1"], b["mask2"], ALU.add)
    v.memset(b["acc"], 0.0)
    v.drain()

    def output_norm(ee, e, s):
        v.wait_ge(k.sem("moe2_squared"), ee)
        v.tensor_reduce(b["ms"], b["sq"], X_AXIS, ALU.add)
        v.drain()
        v.tensor_scalar(b["ms"], b["ms"], 1.0 / DIM, F32_EPS, ALU.mult, ALU.add).then_inc(k.sem("moe2_mean"), 1)
        v.wait_ge(k.sem("moe2_root"), ee)
        v.reciprocal(b["factor"], b["factor"])
        v.drain()
        v.tensor_tensor(b["factor"], b["factor"], b["gates"][:, bass.ds(e - 1, 1), :].rearrange("p a t -> p (a t)"),
                        ALU.mult)
        v.drain()
        for g in range(GROUPS):
            o = v.tensor_tensor(b["scaled"][:, g * TPG:(g + 1) * TPG, :],
                                k.ps[:, g, :].rearrange("p (a b) -> p a b", a=TPG),
                                bc(b["factor"][:, g * TPG:(g + 1) * TPG], P), ALU.mult)
        o.then_inc(k.sem("moe2_taken"), 1)
        v.drain()
        v.tensor_tensor(b["scaled"], b["scaled"], b["enorm"][:, 1 - s, :].unsqueeze(1).broadcast_to([P, TILES, P]),
                        ALU.mult)
        v.drain()
        v.tensor_tensor(b["acc"], b["acc"], b["scaled"], ALU.add).then_inc(k.sem("moe2_summed"), 1)
        v.drain()

    def body(e, s, first):
        ee = e + n * E2
        for g in range(GROUPS):
            if g >= 2:
                v.wait_ge(k.sem("moe2_down"), ee * GROUPS + (g - 1))
            elif not first:
                v.wait_ge(k.sem("moe2_down"), ee * GROUPS + g - 1)
            for c in range(C2):
                step = g * C2 + c
                v.wait_ge(k.sem("moe2_silu"), ee * STEPS2 + (step + 1))
                v.tensor_tensor(b["hid"][:, g % 2, c, :], b["silu"][:, step % 2, :], k.ps[:, 5 + 2 * (step % 2), :],
                                ALU.mult).then_inc(k.sem("moe2_hidden"), 1)
            if g == 0 and not first:
                output_norm(ee, e, s)

    swiglu_pairs(v, body)
    output_norm((n + 1) * E2, E2, 0)
    norm_dve(k, v, ln + 2, b["acc"], b["acc"], F32_EPS, center=False)
    for g in range(GROUPS):
        v.wait_ge(k.sem("out_projected"), n * GROUPS + g + 1)
        xg = k.x[:, g * TPG:(g + 1) * TPG, :].rearrange("p a b -> p (a b)")
        o = v.scalar_tensor_tensor(xg, k.ps[:, 4 + g, :], 0.5, xg, ALU.mult, ALU.add)
    o.then_inc(k.sem("x_updated"), 1)


def lay_out_swiglu(a, i):
    import numpy as _np

    c, f = _np.ascontiguousarray, _np.float32
    a["l2_small"] = c(_np.concatenate([
        i["L2_ffn_W_in"].T, i["L2_ffn_W_out"].T, i["L2_ffn_Wr"].T, _np.zeros((P, 32), f),
        i["L2_ffn_in_norm_w"][:, None], i["L2_ffn_out_norm_w"][:, None]], axis=1))
    a["l2_e_bias"], a["l2_enorm"] = i["L2_ffn_expert_bias"], i["L2_ffn_enorm_w"]
    down = i["L2_ffn_Wd"].transpose(0, 2, 1).reshape(E2, C2, P, DIM).transpose(0, 2, 1, 3).reshape(E2, P, C2 * DIM)
    a["l2_w"] = c(_np.concatenate([i["L2_ffn_Wg"].transpose(0, 2, 1), i["L2_ffn_Wu"].transpose(0, 2, 1), down], axis=2))



E3, I3, TOP3, CAPACITY = 32, 64, 4, 128
UNITS = E3 // 2 + 1


def small_layout(k):
    a = k.arena
    a.reset()
    b = {}
    b["yT"] = a.take(TOKENS)
    b["gate_w"] = a.take(E3)
    b["before"], b["ones"] = a.take(P), a.take(P)
    b["rank"] = a.take(E3)
    for name in ("logits", "cur", "mask", "chosen", "probs"):
        b[name] = a.take(TILES, E3)
    b["gates"] = a.take(E3, TILES)
    b["best"], b["top"], b["sum"] = a.take(TILES), a.take(TILES), a.take(TILES)
    b["rows"] = a.take(4 * P)
    b["shared"] = a.take(3 * P)
    b["w"] = a.take(2, 3 * P)
    b["gb"] = a.take(2, TOKENS)
    b["silu"] = a.take(2, GROUP)
    b["prod"] = a.take(2, GROUP)
    b["hid"] = a.take(2, GROUP)
    return b


def small_sync(k, sp, m, n, ln):
    b = small_layout(k)
    sp.wait_ge(k.sem("x_updated"), m + 1)
    ready = k.sem("moe3_loaded")
    sp.dma_start(b["gate_w"], k.ins["l3_gate_w"]).then_inc(ready, 16)
    sp.dma_start(b["before"], k.ins["before"]).then_inc(ready, 16)
    sp.dma_start(b["rank"], k.ins["rank"].partition_broadcast(P)).then_inc(ready, 16)
    sp.dma_start(b["shared"], k.ins["l3_w"][0, :, :]).then_inc(ready, 16)
    sp.wait_ge(k.sem("gates_stored"), 16 * (k.gate_stores[m] + 1))

    def load(s, pair):
        got = k.sem(f"moe3_w{s}")
        sp.dma_start(b["w"][:, s, :], k.ins["l3_w"][bass.ds(pair + 1, 1), :, :].rearrange("a p c -> (a p) c"))\
            .then_inc(got, 16)
        for h in range(2):
            row = k.gates_dram[bass.ds(pair * (2 * TILES) + h * TILES, TILES), :].rearrange("t p -> (t p)")
            sp.dma_start(b["gb"][h * I3:(h + 1) * I3, s, :], row.partition_broadcast(I3)).then_inc(got, 16)

    load(0, 0)
    load(1, 1)
    with sp.Fori(0, E3 // 4 - 1) as i:
        for s in range(2):
            sp.wait_ge(k.sem("moe3_down"), (n * UNITS + 1) * GROUPS + i * (2 * GROUPS) + (s + 1) * GROUPS)
            load(s, i * 2 + (s + 2))


def small_units(eng, body):
    body(0, 1)
    with eng.Fori(0, E3 // 4) as i:
        body(i * 2 + 1, 2, i)


def small_pe(k, pe, m, n, ln):
    b = small_layout(k)
    xt = k.xt_calls[m]
    transpose_pe(k, pe, k.xn, ln)
    pe.wait_ge(k.sem("moe3_loaded"), 64 * (n + 1))
    gate_logits_pe(k, pe, xt, b["gate_w"], E3)
    pe.wait_ge(k.sem("chosen_ready"), n + 1)
    pe.matmul(k.ps[:, 5, :], b["before"], b["chosen"].rearrange("p t e -> p (t e)"), start=True, stop=False)
    for t in range(TILES - 1):
        rest = TILES - 1 - t
        o = pe.matmul(k.ps[:, 5, (t + 1) * E3:], b["ones"],
                      b["chosen"][:, t, :].unsqueeze(1).broadcast_to([P, rest, E3]),
                      start=False, stop=(rest == 1))
    o.then_inc(k.sem("places_ready"), 1)
    gates_out_pe(k, pe, k.gate_stores[m], b["gates"], 4)

    def body(unit, units, i=None):
        at = (n * UNITS + unit) * GROUPS

        def weights(step):
            return b["shared"] if units == 1 else b["w"][:, step // GROUPS, :]

        def up(step):
            if units == 2 and step % GROUPS == 0:
                pe.wait_ge(k.sem(f"moe3_w{step // GROUPS}"), 48 * (E3 // 4) * n + 48 * i + 48)
            if step >= 2:
                pe.wait_ge(k.sem("moe3_multiplied"), at + (step - 1))
            g = step % GROUPS
            for half in range(2):
                o = pe.matmul(k.ps[:, 4 + 2 * (step % 2) + half, :], weights(step)[:, half * P:(half + 1) * P],
                              k.xT[:, g * GROUP:(g + 1) * GROUP], start=True, stop=True)
            o.then_inc(k.sem("moe3_up"), 1)

        up(0)
        up(1)
        for step in range(units * GROUPS):
            if step + 2 < units * GROUPS:
                up(step + 2)
            pe.wait_ge(k.sem("moe3_hidden"), at + (step + 1))
            pe.matmul(k.ps[:, step % GROUPS, :], weights(step)[:, 2 * P:3 * P], b["hid"][:, step % 2, :],
                      start=(units == 1), stop=True, skip_group_check=(units == 2)).then_inc(k.sem("moe3_down"), 1)

    pe.wait_ge(k.sem("gate_rows"), k.gate_stores[m] + 1)
    small_units(pe, body)
    add_back_pe(k, pe, k.back_calls[m], b["yT"])


def small_act(k, a, m, n, ln):
    b = small_layout(k)
    norm_act(k, a, ln)
    transpose_act(k, a, k.xt_calls[m], k.xT)
    a.wait_ge(k.sem("moe3_shifted"), n + 1)
    a.activation(b["probs"], b["probs"], ACT.Exp).then_inc(k.sem("moe3_exp"), 1)
    gates_out_act(k, a, k.gate_stores[m], b["rows"], 4, None, None)

    def body(unit, units, i=None):
        at = (n * UNITS + unit) * GROUPS
        a.wait_ge(k.sem("moe3_multiplied"), at)
        for step in range(units * GROUPS):
            a.wait_ge(k.sem("moe3_up"), at + (step + 1))
            if step >= 2:
                a.wait_ge(k.sem("moe3_multiplied"), at + (step - 1))
            a.activation(b["silu"][:, step % 2, :], k.ps[:, 4 + 2 * (step % 2), :], ACT.Silu)\
                .then_inc(k.sem("moe3_silu"), 1)

    use_table(k, a, ACT.Silu)
    small_units(a, body)
    a.wait_ge(k.sem("moe3_down"), (n + 1) * UNITS * GROUPS)
    add_back_act(k, a, k.back_calls[m], b["yT"], 0.5)


def small_dve(k, v, m, n, ln):
    b = small_layout(k)
    norm_dve(k, v, ln, k.x[:, :, :], k.xn[:, :, :])
    v.memset(b["ones"], 1.0)
    v.memset(b["chosen"], 0.0)
    v.wait_ge(k.sem("gate_logits"), k.gate_calls[m] + 1)
    v.wait_ge(k.sem("moe3_loaded"), 64 * (n + 1))
    v.tensor_copy(b["logits"], k.ps[:, 4, :].rearrange("p (t e) -> p t e", t=TILES))
    v.drain()
    v.tensor_copy(b["cur"], b["logits"])
    for r in range(TOP3):
        first_of_largest(k, v, b["cur"], b["best"], b["mask"], b["rank"], b["top"])
        if r == 0:
            v.tensor_tensor(b["probs"], b["logits"], bc(b["best"], E3), ALU.subtract)\
                .then_inc(k.sem("moe3_shifted"), 1)
        v.tensor_tensor(b["chosen"], b["chosen"], b["mask"], ALU.add)
        if r < TOP3 - 1:
            v.scalar_tensor_tensor(b["cur"], b["mask"], NEG, b["cur"], ALU.mult, ALU.add)
    v.drain()
    v.tensor_copy(b["top"], b["best"]).then_inc(k.sem("chosen_ready"), 1)
    v.wait_ge(k.sem("moe3_exp"), n + 1)
    v.tensor_reduce(b["sum"], b["probs"], X_AXIS, ALU.add)
    v.drain()
    v.reciprocal(b["sum"], b["sum"])
    v.drain()
    v.tensor_tensor(b["probs"], b["probs"], bc(b["sum"], E3), ALU.mult)
    v.drain()
    v.tensor_tensor(b["probs"], b["probs"], b["chosen"], ALU.mult)
    v.drain()
    v.tensor_reduce(b["sum"], b["probs"], X_AXIS, ALU.add)
    v.drain()
    v.reciprocal(b["sum"], b["sum"])
    v.drain()
    v.tensor_tensor(b["probs"], b["probs"], bc(b["sum"], E3), ALU.mult)
    v.wait_ge(k.sem("places_ready"), n + 1)
    v.tensor_scalar(b["mask"], k.ps[:, 5, :].rearrange("p (t e) -> p t e", t=TILES), float(CAPACITY), None, ALU.is_lt)
    v.drain()
    v.tensor_tensor(b["gates"].rearrange("p e t -> p t e"), b["probs"], b["mask"], ALU.mult)\
        .then_inc(k.sem("gates_ready"), 1)

    def body(unit, units, i=None):
        at = (n * UNITS + unit) * GROUPS
        v.wait_ge(k.sem("moe3_down"), at)
        for step in range(units * GROUPS):
            s, g = divmod(step, GROUPS)
            if units == 2 and g == 0:
                v.wait_ge(k.sem(f"moe3_w{s}"), 48 * (E3 // 4) * n + 48 * i + 48)
            if step >= 2:
                v.wait_ge(k.sem("moe3_down"), at + (step - 1))
            v.wait_ge(k.sem("moe3_silu"), at + (step + 1))
            to = b["hid"] if units == 1 else b["prod"]
            o = v.tensor_tensor(to[:, step % 2, :], b["silu"][:, step % 2, :], k.ps[:, 5 + 2 * (step % 2), :], ALU.mult)
            o.then_inc(k.sem("moe3_multiplied"), 1)
            v.drain()
            if units == 1:
                v.sem_inc(k.sem("moe3_hidden"), 1)
            else:
                v.tensor_tensor(b["hid"][:, step % 2, :], b["prod"][:, step % 2, :],
                                b["gb"][:, s, g * GROUP:(g + 1) * GROUP], ALU.mult).then_inc(k.sem("moe3_hidden"), 1)

    small_units(v, body)
    add_back_dve(k, v, k.back_calls[m])


def lay_out_small(a, i):
    import numpy as _np

    c, f = _np.ascontiguousarray, _np.float32
    feature = _np.arange(P)
    a["before"] = (feature[:, None] < feature[None, :]).astype(f)
    a["l3_gate_w"] = c(i["L3_ffn_gate_w"].T)
    none = _np.zeros((P, I3), f)
    up = i["L3_ffn_w_gate_up"].reshape(E3 // 2, 2, DIM, 2, I3).transpose(0, 2, 3, 1, 4).reshape(E3 // 2, DIM, 4 * I3)
    down = i["L3_ffn_w_down"].reshape(E3 // 2, 2 * I3, DIM)
    gu = i["L3_ffn_shared_w_gate_up"]
    shared_up = _np.concatenate([gu[:, :I3], none, gu[:, I3:], none], axis=1)
    shared_down = _np.concatenate([i["L3_ffn_shared_w_down"], none.T], axis=0)
    a["l3_w"] = c(_np.concatenate([_np.concatenate([shared_up, shared_down], axis=1)[None],
                                   _np.concatenate([up, down], axis=2)], axis=0))



N2, RSTEP, QSTEPS = 32, 32, SEQ // 32
H4 = 2 * N2
CHUNK4 = 16
TWO_PI = 2.0 * math.pi
PI1 = 6.28125
PI2 = float(np.float32(np.round((TWO_PI - PI1) * 2 ** 20) / 2 ** 20))
PI3 = TWO_PI - PI1 - PI2
LN2_1 = 0.693359375
LN2_2 = math.log(2.0) - LN2_1
ROUNDER = 12582912.0
EXP_TERMS = 8


def s4d_layout(k):
    a = k.arena
    a.reset()
    b = {}

    def half(*shape):
        return a.take(*shape)[0:H4]
    b["par"] = half(5, P)
    b["steps"] = half(RSTEP + QSTEPS)
    b["turns"] = half(3)
    b["rads"] = half(3)
    b["ex"], b["ek"], b["er"] = half(2, P), half(2, P), half(2, P)
    for name in ("zr", "zi", "ar", "den", "nr", "ni", "cr", "ci", "t1", "t2", "mag1"):
        b[name] = half(P)
    b["unit"] = half(2, P)
    b["ph"] = half(P, RSTEP)
    b["turn"] = half(P, RSTEP)
    b["magr"] = half(P, RSTEP)
    b["tr"] = half(P, RSTEP)
    b["phq"] = half(P, QSTEPS)
    b["magq"] = half(P, QSTEPS)
    b["q1"], b["q2"] = half(P, QSTEPS), half(P, QSTEPS)
    b["sr"], b["sq_"] = half(2, CHUNK4 * RSTEP), half(2, CHUNK4 * QSTEPS)
    b["k32"] = a.take(QSTEPS, P)[0:RSTEP]
    tables = a.at
    b["fwd"] = a.take(4, 2 * SEQ)
    b["kt"] = a.take(4, P)
    b["kf"] = a.take(8, P)
    b["w"] = a.take(P)
    b["bias"] = a.take(P)
    b["p1"], b["p2"] = a.take(SEQ), a.take(SEQ)
    a.reset(P * 5 + 600)
    b["y"] = a.take(8, SEQ)
    b["back"] = a.take(8, SEQ)
    b["yg"] = a.take(TILES, P)
    b["yT"] = a.take(TOKENS)
    assert a.at <= tables, (a.at, tables)
    return b


def s4d_sync(k, sp, m, n, ln):
    b = s4d_layout(k)
    sp.wait_ge(k.sem("x_updated"), m + 1)
    par = k.sem("s4_parameters")
    sp.dma_start(b["par"][:, 0, :], k.ins["s4_log_dt"].partition_broadcast(H4)).then_inc(par, 16)
    sp.dma_start(b["par"][:, 1:5, :], k.ins["s4_par"]).then_inc(par, 16)
    sp.dma_start(b["steps"], k.ins["s4_steps"].partition_broadcast(H4)).then_inc(par, 16)
    sp.dma_start(b["turns"], k.ins["s4_shifts"][:, 0:3]).then_inc(par, 16)
    sp.dma_start(b["rads"], k.ins["s4_shifts"][:, 3:6]).then_inc(par, 16)
    sp.dma_start(b["fwd"], k.ins["dft_forward"]).then_inc(k.sem("s4_forward"), 16)
    sp.dma_start(b["w"], k.ins["s4_w"]).then_inc(k.sem("s4_weights"), 16)
    sp.dma_start(b["bias"], k.ins["s4_bias"].partition_broadcast(P)).then_inc(k.sem("s4_weights"), 16)
    sp.wait_ge(k.sem("s4_kernel"), LEAD + P // CHUNK4)
    src = b["k32"].rearrange("r (q a) d -> r q a d", a=4)
    for a_ in range(4):
        sp.dma_start(b["kt"][32 * a_:32 * a_ + 32, :, :], src[:, :, a_, :]).then_inc(k.sem("s4_kernel_moved"), 16)
    sp.wait_ge(k.sem("s4_kernel_moved"), 64)
    sp.dma_start(b["back"], k.ins["dft_back"]).then_inc(k.sem("s4_back"), 16)


def s4d_pe(k, pe, m, n, ln):
    b = s4d_layout(k)
    iters = P // CHUNK4
    with pe.Fori(0, iters) as i:
        pe.wait_ge(k.sem("s4_staged"), i + 1)
        hold(k, pe, "s4_kernel", LEAD + i)
        for d in range(CHUNK4):
            o = pe.matmul(k.ps[0:RSTEP, 7, d * QSTEPS:(d + 1) * QSTEPS], b["sr"][:, 0, d * RSTEP:(d + 1) * RSTEP],
                          b["sq_"][:, 0, d * QSTEPS:(d + 1) * QSTEPS], start=True, stop=True)
        o.then_inc(k.sem("s4_products"), 1)
    pe.wait_ge(k.sem("s4_forward"), 16)
    pe.wait_ge(k.sem("s4_kernel_moved"), 64)
    for half in range(2):
        for f in range(4):
            for t in range(4):
                o = pe.matmul(k.ps[:, 4 + half, f * P:(f + 1) * P],
                              b["fwd"][:, t, half * SEQ + f * P:half * SEQ + (f + 1) * P], b["kt"][:, t, :],
                              start=(t == 0), stop=(t == 3))
    o.then_inc(k.sem("s4_kernel_spectrum"), 1)
    pe.wait_ge(k.sem("ln_done"), (ln + 1) * GROUPS)
    xv = k.xn[:, :, :].rearrange("p (b t) d -> p b t d", t=4)
    for f in range(4):
        if f >= 2:
            pe.wait_ge(k.sem("s4_multiplied"), f - 1)
        for half in range(2):
            for t in range(4):
                o = pe.matmul(k.ps[:, 2 * (f % 2) + half, :],
                              b["fwd"][:, t, half * SEQ + f * P:half * SEQ + (f + 1) * P], xv[:, :, t, :],
                              start=(t == 0), stop=(t == 3))
        o.then_inc(k.sem("s4_spectrum"), 1)
    pe.wait_ge(k.sem("s4_multiplied"), 4)
    pe.wait_ge(k.sem("s4_back"), 16)
    for t in range(4):
        for f in range(8):
            o = pe.matmul(k.ps[:, 4 + t, :], b["back"][:, f, t * P:(t + 1) * P], b["y"][:, f, :],
                          start=(f == 0), stop=(f == 7))
        o.then_inc(k.sem("s4_convolved"), 1)
    pe.wait_ge(k.sem("s4_gelu"), 4)
    transpose_pe(k, pe, b["yg"])
    pe.wait_ge(k.sem("xT_ready"), (k.xt_calls[m] + 1) * GROUPS)
    pe.wait_ge(k.sem("s4_weights"), 32)
    project_back_pe(k, pe, b, n, b["yT"], b["w"], "s4_projected")


def s4d_act(k, a, m, n, ln):
    b = s4d_layout(k)
    a.wait_ge(k.sem("s4_exponents"), 1)
    a.activation(b["mag1"], b["zr"], ACT.Exp).then_inc(k.sem("s4_magnitudes"), 1)
    a.activation(b["magr"], b["magr"], ACT.Exp).then_inc(k.sem("s4_magnitudes"), 1)
    a.activation(b["magq"], b["magq"], ACT.Exp).then_inc(k.sem("s4_magnitudes"), 1)
    for j, what in enumerate((b["unit"], b["q1"], b["q2"], b["tr"])):
        a.wait_ge(k.sem("s4_angles"), j + 1)
        a.activation(what, what, ACT.Sin).then_inc(k.sem("s4_sines"), 1)
    norm_act(k, a, ln)
    a.wait_ge(k.sem("s4_kernel_spectrum"), 1)
    a.activation(b["kf"].rearrange("p (h f) d -> p h (f d)", h=2), k.ps[:, 4:6, :], ACT.Copy)\
        .then_inc(k.sem("s4_kernel_copied"), 1)
    yg = b["yg"].rearrange("p (b t) d -> p b t d", t=4)
    for t in range(4):
        a.wait_ge(k.sem("s4_convolved"), t + 1)
        a.activation(yg[:, :, t, :], k.ps[:, 4 + t, :].rearrange("p (b d) -> p b d", b=BATCH), ACT.Gelu)\
            .then_inc(k.sem("s4_gelu"), 1)
    transpose_act(k, a, k.xt_calls[m], b["yT"])


def s4d_dve(k, v, m, n, ln):
    b = s4d_layout(k)
    v.wait_ge(k.sem("s4_parameters"), 80)
    T = ALU

    def tt(out, x, y, op):
        v.drain()
        return v.tensor_tensor(out, x, y, op)

    def ts(out, x, s1, s2, op0, op1):
        v.drain()
        return v.tensor_scalar(out, x, s1, s2, op0, op1)

    y, j, r = b["par"][:, 0:2, :], b["ek"], b["er"]
    ts(j, y, 1.0 / math.log(2.0), ROUNDER, T.mult, T.add)
    ts(j, j, ROUNDER, None, T.subtract, ALU.bypass)
    v.drain()
    v.scalar_tensor_tensor(r, j, -LN2_1, y, T.mult, T.add)
    v.drain()
    v.scalar_tensor_tensor(r, j, -LN2_2, r, T.mult, T.add)
    ts(b["ex"], r, 1.0 / math.factorial(EXP_TERMS), 1.0 / math.factorial(EXP_TERMS - 1), T.mult, T.add)
    for term in range(EXP_TERMS - 2, -1, -1):
        tt(b["ex"], b["ex"], r, T.mult)
        ts(b["ex"], b["ex"], 1.0 / math.factorial(term), None, T.add, ALU.bypass)
    ts(r.bitcast(mybir.dt.int32), j, 127.0, float(2 ** 23), T.add, T.mult)
    tt(b["ex"], b["ex"], r, T.mult)
    dt, mre = b["ex"][:, 0, :], b["ex"][:, 1, :]
    ai, c_re, c_im = b["par"][:, 2, :], b["par"][:, 3, :], b["par"][:, 4, :]
    ts(b["ar"], mre, -1.0, None, T.mult, ALU.bypass)
    tt(b["zr"], b["ar"], dt, T.mult)
    tt(b["zi"], ai, dt, T.mult)
    fine = b["steps"][:, 0:RSTEP].unsqueeze(1).broadcast_to([H4, P, RSTEP])
    coarse = b["steps"][:, RSTEP:].unsqueeze(1).broadcast_to([H4, P, QSTEPS])
    tt(b["magr"], bc(b["zr"], RSTEP), fine, T.mult)
    tt(b["magq"], bc(b["zr"], QSTEPS), coarse, T.mult).then_inc(k.sem("s4_exponents"), 1)
    tt(b["ph"], bc(b["zi"], RSTEP), fine, T.mult)
    tt(b["phq"], bc(b["zi"], QSTEPS), coarse, T.mult)

    def angle(out, phase, turns, turn, rad):
        ts(turns, phase, 1.0 / TWO_PI, turn, T.mult, T.add)
        ts(turns, turns, ROUNDER, ROUNDER, T.add, T.subtract)
        v.drain()
        v.scalar_tensor_tensor(out, turns, -PI1, phase, T.mult, T.add)
        v.drain()
        v.scalar_tensor_tensor(out, turns, -PI2, out, T.mult, T.add)
        v.drain()
        v.scalar_tensor_tensor(out, turns, -PI3, out, T.mult, T.add)
        ts(out, out, rad, None, T.add, ALU.bypass)
        return ts(out, out, 3.1415925, -3.1415925, T.min, T.max)

    scratch = b["turn"].rearrange("p a b -> p (a b)")
    angle(b["unit"][:, 0, :], b["zi"], scratch[:, 0:P], 0.25, math.pi / 2)
    angle(b["unit"][:, 1, :], b["zi"], scratch[:, 0:P], 0.0, 0.0).then_inc(k.sem("s4_angles"), 1)
    sq = scratch[:, 0:P * QSTEPS].rearrange("p (a b) -> p a b", a=P)
    angle(b["q1"], b["phq"], sq, b["turns"][:, 1:2], b["rads"][:, 1:2]).then_inc(k.sem("s4_angles"), 1)
    angle(b["q2"], b["phq"], sq, b["turns"][:, 2:3], b["rads"][:, 2:3]).then_inc(k.sem("s4_angles"), 1)
    angle(b["tr"], b["ph"], b["turn"], b["turns"][:, 0:1], b["rads"][:, 0:1]).then_inc(k.sem("s4_angles"), 1)
    v.wait_ge(k.sem("s4_magnitudes"), 3)
    v.wait_ge(k.sem("s4_sines"), 1)
    tt(b["nr"], b["mag1"], b["unit"][:, 0, :], T.mult)
    ts(b["nr"], b["nr"], -1.0, None, T.add, ALU.bypass)
    tt(b["ni"], b["mag1"], b["unit"][:, 1, :], T.mult)

    def product(out, x1, y1, x2, y2, op):
        tt(b["t1"], x1, y1, T.mult)
        tt(b["t2"], x2, y2, T.mult)
        tt(out, b["t1"], b["t2"], op)

    product(b["cr"], c_re, b["nr"], c_im, b["ni"], T.subtract)
    product(b["ci"], c_re, b["ni"], c_im, b["nr"], T.add)
    product(b["den"], b["ar"], b["ar"], ai, ai, T.add)
    v.drain()
    v.reciprocal(b["den"], b["den"])
    ts(b["den"], b["den"], 2.0, None, T.mult, ALU.bypass)
    product(b["nr"], b["cr"], b["ar"], b["ci"], ai, T.add)
    product(b["ni"], b["ci"], b["ar"], b["cr"], ai, T.subtract)
    tt(b["cr"], b["nr"], b["den"], T.mult)
    tt(b["ci"], b["ni"], b["den"], T.mult)
    v.wait_ge(k.sem("s4_sines"), 3)
    tt(b["q1"], b["q1"], bc(b["cr"], QSTEPS), T.mult)
    tt(b["q2"], b["q2"], bc(b["ci"], QSTEPS), T.mult)
    tt(b["q1"], b["q1"], b["q2"], T.add)
    tt(b["q1"], b["q1"], b["magq"], T.mult)
    v.wait_ge(k.sem("s4_sines"), 4)
    tt(b["tr"], b["tr"], b["magr"], T.mult)
    v.drain()
    fr, fq = b["tr"].rearrange("p a b -> p (a b)"), b["q1"].rearrange("p a b -> p (a b)")
    with v.Fori(0, P // CHUNK4) as i:
        v.tensor_copy(b["sr"][:, 0, :], fr[:, bass.ts(i, CHUNK4 * RSTEP)])
        v.tensor_copy(b["sq_"][:, 0, :], fq[:, bass.ts(i, CHUNK4 * QSTEPS)])
        v.drain()
        v.sem_inc(k.sem("s4_staged"), 1)
        v.wait_ge(k.sem("s4_products"), i + 1)
        v.tensor_copy(b["k32"][:, :, bass.ts(i, CHUNK4)].rearrange("r q d -> r d q"),
                      k.ps[0:RSTEP, 7, 0:CHUNK4 * QSTEPS].rearrange("r (d q) -> r d q", d=CHUNK4))\
            .then_inc(k.sem("s4_kernel"), 1)
    norm_dve(k, v, ln, k.x[:, :, :], k.xn[:, :, :])
    v.wait_ge(k.sem("s4_kernel_copied"), 1)
    kf = b["kf"]
    p1, p2 = (b[p].rearrange("p (b d) -> p b d", b=BATCH) for p in ("p1", "p2"))
    for f in range(4):
        v.wait_ge(k.sem("s4_spectrum"), f + 1)
        xr, xi = (k.ps[:, 2 * (f % 2) + h, :].rearrange("p (b d) -> p b d", b=BATCH) for h in range(2))
        kr, ki = (kf[:, 4 * h + f, :].unsqueeze(1).broadcast_to([P, BATCH, P]) for h in range(2))
        yr, yi = (b["y"][:, 4 * h + f, :].rearrange("p (b d) -> p b d", b=BATCH) for h in range(2))
        v.drain()
        v.tensor_tensor(p1, xr, kr, T.mult)
        v.tensor_tensor(p2, xi, ki, T.mult)
        v.drain()
        v.tensor_tensor(yr, p1, p2, T.subtract)
        v.drain()
        v.tensor_tensor(p1, xr, ki, T.mult)
        v.tensor_tensor(p2, xi, kr, T.mult)
        v.drain()
        v.tensor_tensor(yi, p1, p2, T.add).then_inc(k.sem("s4_multiplied"), 1)
    v.wait_ge(k.sem("s4_weights"), 32)
    v.tensor_tensor(k.x[:, :, :], k.x[:, :, :], b["bias"].unsqueeze(1).broadcast_to([P, TILES, P]), T.add)
    v.drain()
    for g in range(GROUPS):
        v.wait_ge(k.sem("s4_projected"), g + 1)
        xg = k.x[:, g * TPG:(g + 1) * TPG, :]
        o = v.tensor_tensor(xg, k.ps[:, 4 + g, :].rearrange("p (a b) -> p a b", a=TPG), xg, T.add)
    o.then_inc(k.sem("x_updated"), 1)


def lay_out_s4d(a, i):
    import numpy as _np

    c, f = _np.ascontiguousarray, _np.float32
    a["s4_log_dt"] = i["L2_attn_log_dt"]
    par = _np.stack([i["L2_attn_" + name].T for name in ("log_A_real", "A_imag", "C_real", "C_imag")], axis=1)
    a["s4_par"] = c(_np.concatenate([par, par], axis=0))
    a["s4_steps"] = _np.concatenate([_np.arange(RSTEP), RSTEP * _np.arange(QSTEPS)]).astype(f)
    turns = _np.repeat(_np.array([[0.25, 0.25, 0.5], [0.0, 0.5, 0.75]]), N2, axis=0)
    a["s4_shifts"] = c(_np.concatenate([turns, turns * TWO_PI], axis=1).astype(f))
    steps, freq = _np.arange(SEQ), _np.arange(SEQ)
    angle = ((2 * freq[None, :] + 1) * steps[:, None] % (4 * SEQ)) * (TWO_PI / (4 * SEQ))
    both = _np.concatenate([_np.cos(angle), -_np.sin(angle)], axis=1)
    a["dft_forward"] = c(both.reshape(4, P, 2 * SEQ).transpose(1, 0, 2).astype(f))
    a["dft_back"] = c((both.T / SEQ).reshape(8, P, SEQ).transpose(1, 0, 2).astype(f))
    a["s4_w"], a["s4_bias"] = c(i["L2_attn_W"].T), i["L2_attn_b"]



HEADSL, HDL, WINDOW = 8, 64, 64
INNER = HEADSL * HDL
PAIRS = HEADSL // 2
LAYERS = 2
QK_SCALE = 8.0
HID = int(DIM * 4 * 2 / 3)
CH = -(-HID // P)
KEYS, SEEN = 2 * P, WINDOW + P
HALVES = 2 * TPG


def local_layout(k):
    a = k.arena
    a.reset()
    b = {}
    b["y"] = a.take(TILES, P)
    b["wqkv"] = a.take(3, INNER)
    b["wo"] = a.take(PAIRS, P)
    b["w1"] = a.take(2, CH, P)
    b["w2"] = a.take(CH, P)
    b["vec"] = a.take(2 + 2 * CH)
    b["scales"] = a.take(2, HDL)
    b["b2"] = a.take(P)
    b["mask"] = a.take(2, SEEN)
    b["half"] = a.take(2)
    b["cos"], b["sin"] = a.take(TPG, 2, HDL), a.take(TPG, 2, HDL)
    b["tc"], b["ts"] = a.take(TPG, 2, HDL), a.take(TPG, 2, HDL)
    b["qT"] = a.take(PAIRS, TOKENS)
    b["kT"] = a.take(PAIRS, P + TOKENS)
    b["v"] = a.take(1 + TILES, INNER)
    temp = a.at
    b["hs"] = a.take(TPG, P)
    b["qk"] = a.take(TPG, 2 * INNER)
    b["qsq"] = a.take(2, 2 * INNER)
    b["norms"] = a.take(2, 2 * HEADSL)
    b["swp"] = a.take(2 * INNER)
    b["qr"] = a.take(2, 2 * INNER)
    a.reset(temp)
    b["qm"] = a.take(2, HEADSL, P)
    b["s"] = a.take(2, 4, SEEN)
    b["p"] = a.take(2, 4, KEYS)
    b["pT"] = a.take(2, 4, KEYS)
    b["negmax"] = a.take(2, 4)
    b["sum"] = a.take(2, HEADSL)
    b["o"] = a.take(2, INNER)
    b["oT"] = a.take(2, INNER)
    a.reset(temp)
    b["ge"] = a.take(2, GROUP)
    b["hid"] = a.take(2, CH, GROUP)
    return b


def local_sync(k, sp, m, n, ln):
    b = local_layout(k)
    sp.wait_ge(k.sem("x_updated"), m + 1)
    once = k.sem("lf_tables")
    sp.dma_start(b["mask"], k.ins["lf_mask"]).then_inc(once, 16)
    sp.dma_start(b["half"], k.ins["a0_mask"]).then_inc(once, 16)
    sp.dma_start(b["cos"], k.ins["lf_cos"]).then_inc(once, 16)
    sp.dma_start(b["sin"], k.ins["lf_sin"]).then_inc(once, 16)
    low, high = slice(0, DIM // 2), slice(DIM // 2, DIM)
    for layer in range(LAYERS):
        ll = n * LAYERS + layer
        w, w_ffn = k.sem("lf_weights"), k.sem("lf_ffn_weights")
        if layer:
            sp.wait_ge(k.sem("lf_layer_done"), ll)
        sp.dma_start(b["wqkv"], k.ins["lf_wqkv"][layer, :, :]).then_inc(w, 16)
        sp.dma_start(b["scales"], k.ins["lf_scales"][layer, :].partition_broadcast(P)).then_inc(w, 16)
        sp.dma_start(b["wo"], k.ins["lf_wo"][layer, :, :]).then_inc(w_ffn, 16)
        sp.dma_start(b["w1"], k.ins["lf_w1"][layer, :, :]).then_inc(w_ffn, 16)
        sp.dma_start(b["w2"], k.ins["lf_w2"][layer, :, :]).then_inc(w_ffn, 16)
        sp.dma_start(b["vec"], k.ins["lf_vec"][layer, :, :]).then_inc(w_ffn, 16)
        sp.dma_start(b["b2"], k.ins["lf_b2"][layer, :].partition_broadcast(P)).then_inc(w_ffn, 16)
        for part in range(2):
            sp.wait_ge(k.sem("lf_y_ready"), 2 * ll + part + 1)
            moved = k.sem("lf_shifted")
            sp.dma_start(k.xn[1:P, :, high], b["y"][0:P - 1, :, high]).then_inc(moved, 16)
            for bt in range(BATCH):
                t = bt * TPG
                sp.dma_start(k.xn[0:1, t + 1:t + TPG, high], b["y"][P - 1:P, t:t + TPG - 1, high]).then_inc(moved, 16)


def sequences(eng, sequence):
    with eng.Fori(0, BATCH - 1) as bt:
        sequence(bt, False)
    sequence(BATCH - 1, True)


SHIFTS = 16 * (1 + BATCH)


def local_pe(k, pe, m, n, ln):
    b = local_layout(k)
    for layer in range(LAYERS):
        ll = n * LAYERS + layer
        pe.wait_ge(k.sem("lf_halves_joined"), 2 * ll + 1)
        pe.wait_ge(k.sem("lf_shifted"), SHIFTS * (2 * ll + 1))
        transpose_pe(k, pe, k.xn)
        pe.wait_ge(k.sem("xT_ready"), (k.xt_calls[m] + 2 * layer + 1) * GROUPS)
        pe.wait_ge(k.sem("lf_weights"), 32 * (ll + 1))

        def project(tile, t):
            pe.wait_ge(k.sem("lf_staged"), tile + (t + 1))
            pe.wait_ge(k.sem("lf_squared"), tile + (t - 1 + LEAD))
            for part in range(3):
                o = pe.matmul(k.ps[:, 3 * (t % 2) + part, :], b["hs"][:, t % TPG, :], b["wqkv"][:, part, :],
                              start=True, stop=True)
            o.then_inc(k.sem("lf_projected"), 1)

        def sequence(bt, last):
            tile = ll * TILES + bt * TPG
            for t in range(TPG):
                if t + 3 < TPG or not last:
                    project(tile, t + 3)
                pe.wait_ge(k.sem("lf_rotated"), tile + (t + 1 + LEAD))
                pe.wait_ge(k.sem("lf_keys"), tile + (t + LEAD))
                for c in range(2 * PAIRS):
                    o = pe.transpose(k.ps[:, 6 + c // PAIRS, c % PAIRS * P:(c % PAIRS + 1) * P],
                                     b["qr"][:, t % 2, c * P:(c + 1) * P], k.ident[:, :])
                o.then_inc(k.sem("lf_turned"), 1)

        for t in range(3):
            project(ll * TILES, t)
        sequences(pe, sequence)

        pe.wait_ge(k.sem("lf_keys"), LEAD + (ll + 1) * TILES)
        pe.wait_ge(k.sem("lf_ffn_weights"), 80 * (ll + 1))

        def scores(bt, u):
            at, tile, t = ll * BATCH * HALVES + bt * HALVES, ll * TILES + bt * TPG, u // 2
            if u % 2 == 0:
                pe.wait_ge(k.sem("lf_queries_masked"), tile + (t + 1))
            if u >= 2:
                pe.wait_ge(k.sem("lf_maxima"), at + (u - 1))
            for h in range(4):
                head = 4 * (u % 2) + h
                o = pe.matmul(k.ps[:, 2 * (u % 2) + h // 2, h % 2 * SEEN:(h % 2 + 1) * SEEN],
                              b["qm"][:, t % 2, head, :],
                              b["kT"].rearrange("p a c -> p (a c)")
                              [:, bass.ds(bt * SEQ + (head // 2 * (P + TOKENS) + t * P + KEYS - SEEN), SEEN)],
                              start=True, stop=True)
            o.then_inc(k.sem("lf_scores"), 1)

        def sequence(bt, last):
            at, tile = ll * BATCH * HALVES + bt * HALVES, ll * TILES + bt * TPG

            def turn(u):
                pe.wait_ge(k.sem("lf_probs"), at + (u + 1 + LEAD))
                pe.wait_ge(k.sem("lf_probs_copied_act"), at + (u + LEAD))
                pe.wait_ge(k.sem("lf_probs_copied_dve"), at + (u + LEAD))
                for c in range(8):
                    o = pe.transpose(k.ps[:, 4 + c // 4, c % 4 * P:(c % 4 + 1) * P],
                                     b["p"][:, u % 2, c // 2, c % 2 * P:(c % 2 + 1) * P], k.ident[:, :])
                o.then_inc(k.sem("lf_probs_turned"), 1)

            def values(u):
                t = u // 2
                pe.wait_ge(k.sem("lf_probs_copied_act"), at + (u + 1 + LEAD))
                pe.wait_ge(k.sem("lf_probs_copied_dve"), at + (u + 1 + LEAD))
                if u % 2 == 0:
                    pe.wait_ge(k.sem("lf_out"), tile + (t + LEAD))
                for h in range(4):
                    head = 4 * (u % 2) + h
                    for c in range(2):
                        o = pe.matmul(k.ps[:, 6, head * HDL:(head + 1) * HDL],
                                      b["pT"][:, u % 2, h, c * P:(c + 1) * P],
                                      b["v"].rearrange("p t d -> p (t d)")
                                      [:, bass.ds(bt * (TPG * INNER) + ((t + c) * INNER + head * HDL), HDL)],
                                      start=(c == 0), stop=(c == 1))
                o.then_inc(k.sem("lf_values"), 1)

            def turn_out(t):
                pe.wait_ge(k.sem("lf_out"), tile + (t + 1 + LEAD))
                pe.wait_ge(k.sem("lf_added"), tile + (t + LEAD))
                for c in range(PAIRS):
                    o = pe.transpose(k.ps[:, 7, c * P:(c + 1) * P], b["o"][:, t % 2, c * P:(c + 1) * P], k.ident[:, :])
                o.then_inc(k.sem("lf_out_turned"), 1)

            def project_out(t):
                pe.wait_ge(k.sem("lf_out_copied"), tile + (t + 1 + LEAD))
                for c in range(PAIRS):
                    o = pe.matmul(k.ps[:, 7, 0:P], b["oT"][:, t % 2, c * P:(c + 1) * P],
                                  b["wo"][:, c, :], start=(c == 0), stop=(c == PAIRS - 1))
                o.then_inc(k.sem("lf_out_projected"), 1)

            for u in range(HALVES):
                turn(u)
                if u + 2 < HALVES or not last:
                    scores(bt, u + 2)
                if u % 2 == 0 and u:
                    turn_out(u // 2 - 1)
                values(u)
                if u % 2 == 0 and u:
                    project_out(u // 2 - 1)
            turn_out(TPG - 1)
            project_out(TPG - 1)

        scores(0, 0)
        scores(0, 1)
        sequences(pe, sequence)

        transpose_pe(k, pe, k.xn, ln + 1 + layer)
        pe.wait_ge(k.sem("xT_ready"), (k.xt_calls[m] + 2 * layer + 2) * GROUPS)
        with pe.Fori(0, GROUPS // 2) as i:
            at = ll * GROUPS * CH + i * (2 * CH)
            group = ll * GROUPS + i * 2

            def up(step):
                g, c = divmod(step, CH)
                if step >= 2:
                    pe.wait_ge(k.sem("lf_hidden"), at + (step - 1 + LEAD))
                for half in range(2):
                    o = pe.matmul(k.ps[:, 2 * (step % 2) + half, :], b["w1"][:, half, c, :],
                                  k.xT[:, bass.ds(i * (2 * GROUP) + g * GROUP, GROUP)], start=True, stop=True)
                o.then_inc(k.sem("lf_up"), 1)

            def down(g):
                pe.wait_ge(k.sem("lf_hidden"), LEAD + at + CH * (g + 1))
                pe.wait_ge(k.sem("lf_ffn_added"), group + LEAD)
                for j in range(TPG):
                    for c in range(CH):
                        o = pe.matmul(k.ps[:, 4 + g, j * P:(j + 1) * P], b["hid"][:, g, c, j * P:(j + 1) * P],
                                      b["w2"][:, c, :], start=(c == 0), stop=(c == CH - 1))
                o.then_inc(k.sem("lf_down"), 1)

            for step in range(CH + 2):
                up(step)
            down(0)
            up(2 * CH - 1)
            down(1)


def local_act(k, a, m, n, ln):
    b = local_layout(k)
    norm_act(k, a, ln)
    for layer in range(LAYERS):
        ll = n * LAYERS + layer
        transpose_act(k, a, k.xt_calls[m] + 2 * layer, k.xT)
        if layer == 0:
            a.wait_ge(k.sem("lf_cleared"), n + 1)
        use_table(k, a, ACT.Sqrt)

        def keep(bt, tile, t):
            a.wait_ge(k.sem("lf_projected"), tile + (t + 1 + LEAD))
            a.wait_ge(k.sem("lf_rotated"), tile + (t - 3 + LEAD if t > 1 else LEAD))
            qk = k.ps[:, 3 * (t % 2):3 * (t % 2) + 2, :]
            if t > 1:
                a.wait_ge(k.sem("lf_summed"), tile + (t - 1))
            a.activation(b["qsq"][:, t % 2, :].rearrange("p (a b) -> p a b", a=2), qk, ACT.Square)
            a.activation(b["qk"][:, t % TPG, :].rearrange("p (a b) -> p a b", a=2), qk, ACT.Copy)
            a.activation(b["v"].rearrange("p t d -> p (t d)")[:, bass.ds(bt * (TPG * INNER) + (t + 1) * INNER, INNER)],
                         k.ps[:, 3 * (t % 2) + 2, :], ACT.Copy).then_inc(k.sem("lf_squared"), 1)

        def lengths(tile, t):
            a.wait_ge(k.sem("lf_summed"), tile + (t + 1))
            a.activation(b["norms"][:, t % 2, :], b["norms"][:, t % 2, :], ACT.Sqrt).then_inc(k.sem("lf_lengths"), 1)

        def sequence(bt, last):
            tile = ll * TILES + bt * TPG
            for t in range(TPG):
                if t + 2 < TPG or not last:
                    keep(bt, tile, t + 2)
                if t + 1 < TPG or not last:
                    lengths(tile, t + 1)
                a.wait_ge(k.sem("lf_turned"), tile + (t + 1 + LEAD))
                for half, (dst, first) in enumerate((("qT", 0), ("kT", P))):
                    o = a.activation(b[dst][:, :, bass.ds(bt * SEQ + (t * P + first), P)],
                                     k.ps[:, 6 + half, :].rearrange("p (a b) -> p a b", a=PAIRS), ACT.Copy)
                o.then_inc(k.sem("lf_keys"), 1)

        keep(0, ll * TILES, 0)
        keep(0, ll * TILES, 1)
        lengths(ll * TILES, 0)
        sequences(a, sequence)
        a.wait_ge(k.sem("lf_rotated"), LEAD + (ll + 1) * TILES)

        use_table(k, a, ACT.Exp)

        def exps(bt, u):
            at, tile, t = ll * BATCH * HALVES + bt * HALVES, ll * TILES + bt * TPG, u // 2
            a.wait_ge(k.sem("lf_maxima"), at + (u + 1))
            if u % 2 == 0:
                a.wait_ge(k.sem("lf_out"), tile + (t - 1 + LEAD))
            if u > 1:
                a.wait_ge(k.sem("lf_probs_turned"), at + (u - 1))
            for h in range(4):
                o = a.activation(b["p"][:, u % 2, h, KEYS - SEEN:], b["s"][:, u % 2, h, :], ACT.Exp, scale=-1.0,
                                 bias=b["negmax"][:, u % 2, h:h + 1],
                                 accum_out=b["sum"][:, t % 2, 4 * (u % 2) + h:4 * (u % 2) + h + 1])
            o.then_inc(k.sem("lf_probs"), 1)

        def sequence(bt, last):
            at, tile = ll * BATCH * HALVES + bt * HALVES, ll * TILES + bt * TPG

            def out_copy(t):
                a.wait_ge(k.sem("lf_out_turned"), tile + (t + 1))
                a.wait_ge(k.sem("lf_out_projected"), tile + (t - 1 + LEAD))
                a.activation(b["oT"][:, t % 2, :], k.ps[:, 7, :], ACT.Copy).then_inc(k.sem("lf_out_copied"), 1)

            for u in range(HALVES):
                if u + 1 < HALVES or not last:
                    exps(bt, u + 1)
                a.wait_ge(k.sem("lf_probs_turned"), at + (u + 1))
                a.wait_ge(k.sem("lf_values"), at + (u - 1 + LEAD))
                a.activation(b["pT"][:, u % 2, 0:2, :], k.ps[:, 4, :].rearrange("p (a b) -> p a b", a=2), ACT.Copy)\
                    .then_inc(k.sem("lf_probs_copied_act"), 1)
                if u % 2 == 0 and u:
                    out_copy(u // 2 - 1)
            out_copy(TPG - 1)

        exps(0, 0)
        sequences(a, sequence)

        a.wait_ge(k.sem("lf_added"), LEAD + (ll + 1) * TILES)
        norm_act(k, a, ln + 1 + layer)
        transpose_act(k, a, k.xt_calls[m] + 2 * layer + 1, k.xT, b["vec"][:, 0:1], b["vec"][:, 1:2])
        use_table(k, a, ACT.Gelu)
        with a.Fori(0, GROUPS // 2) as i:
            at = ll * GROUPS * CH + i * (2 * CH)
            a.wait_ge(k.sem("lf_hidden"), at + LEAD)
            for step in range(2 * CH):
                c = step % CH
                a.wait_ge(k.sem("lf_up"), at + (step + 1))
                if step >= 2:
                    a.wait_ge(k.sem("lf_hidden"), at + (step - 1 + LEAD))
                a.activation(b["ge"][:, step % 2, :], k.ps[:, 2 * (step % 2) + 1, :], ACT.Gelu,
                             bias=b["vec"][:, 2 + CH + c:3 + CH + c]).then_inc(k.sem("lf_gelu"), 1)


def local_dve(k, v, m, n, ln):
    b = local_layout(k)
    low = slice(0, DIM // 2)
    norm_dve(k, v, ln, k.x[:, :, :], k.xn[:, :, :])
    v.drain()
    v.tensor_copy(b["y"], k.xn[:, :, :])
    v.drain()
    v.memset(k.xn[:, :, :], 0.0)
    v.memset(b["kT"][:, :, 0:P], 0.0)
    v.memset(b["v"][:, 0, :], 0.0).then_inc(k.sem("lf_cleared"), 1)
    v.drain()
    v.sem_inc(k.sem("lf_y_ready"), 1)
    v.wait_ge(k.sem("lf_tables"), 64 * (n + 1))
    for layer in range(LAYERS):
        ll = n * LAYERS + layer
        v.tensor_copy(k.xn[:, :, low], b["y"][:, :, low]).then_inc(k.sem("lf_halves_joined"), 1)
        v.wait_ge(k.sem("lf_weights"), 32 * (ll + 1))
        sc = b["scales"].unsqueeze(1)
        v.tensor_tensor(b["tc"], b["cos"], sc.broadcast_to([P, TPG, 2, HDL]), ALU.mult)
        for half in range(2):
            own, other = (slice(half * 32, half * 32 + 32), slice((1 - half) * 32, (1 - half) * 32 + 32))
            v.tensor_tensor(b["ts"][:, :, :, own], b["sin"][:, :, :, own],
                            b["scales"][:, :, other].unsqueeze(1).broadcast_to([P, TPG, 2, 32]), ALU.mult)
        v.wait_ge(k.sem("xT_ready"), (k.xt_calls[m] + 2 * layer + 1) * GROUPS)
        v.drain()

        def stage(bt, tile, t):
            v.wait_ge(k.sem("lf_projected"), tile + (t - 3 + LEAD if t > 1 else LEAD))
            v.tensor_copy(b["hs"][:, t % TPG, :], k.xT[:, bass.ds(bt * SEQ + t * P, P)]).then_inc(k.sem("lf_staged"), 1)

        def add_squares(tile, t):
            v.wait_ge(k.sem("lf_squared"), tile + (t + 1 + LEAD))
            v.tensor_reduce(b["norms"][:, t % 2, :], b["qsq"][:, t % 2, :].rearrange("p (h d) -> p h d", d=HDL), X_AXIS,
                            ALU.add).then_inc(k.sem("lf_summed"), 1)

        def rotate(tile, t):
            norms = b["norms"][:, t % 2, :]
            v.wait_ge(k.sem("lf_lengths"), tile + (t + 1))
            v.tensor_scalar(norms, norms, 1e-12, None, ALU.max)
            v.drain()
            v.reciprocal(norms, norms)
            v.drain()
            qk = b["qk"][:, t, :].rearrange("p (h d) -> p h d", d=HDL)
            v.tensor_tensor(qk, qk, bc(norms, HDL), ALU.mult)
            v.drain()
            qk, turned, swapped = (x.rearrange("p (a h d) -> p a h d", a=2, d=HDL)
                                   for x in (b["qk"][:, t, :], b["qr"][:, t % 2, :], b["swp"]))
            for half in range(2):
                own, other = (slice(half * 32, half * 32 + 32), slice((1 - half) * 32, (1 - half) * 32 + 32))
                v.tensor_tensor(swapped[:, :, :, own], qk[:, :, :, other],
                                b["ts"][:, t, :, own].unsqueeze(2).broadcast_to([P, 2, HEADSL, 32]), ALU.mult)
            v.wait_ge(k.sem("lf_turned"), tile + (t - 1 + LEAD))
            v.tensor_tensor(turned, qk, b["tc"][:, t, :, :].unsqueeze(2).broadcast_to([P, 2, HEADSL, HDL]), ALU.mult)
            v.drain()
            v.tensor_tensor(b["qr"][:, t % 2, :], b["qr"][:, t % 2, :], b["swp"], ALU.add).then_inc(k.sem("lf_rotated"), 1)
            v.drain()

        def sequence(bt, last):
            tile = ll * TILES + bt * TPG
            for t in range(TPG):
                if t + 1 < TPG or not last:
                    add_squares(tile, t + 1)
                if not last:
                    stage(bt, tile, t + TPG)
                rotate(tile, t)

        for t in range(TPG):
            stage(0, ll * TILES, t)
        add_squares(ll * TILES, 0)
        sequences(v, sequence)
        v.wait_ge(k.sem("lf_keys"), LEAD + (ll + 1) * TILES)

        v.memset(b["p"][:, :, :, 0:KEYS - SEEN], 0.0)

        def queries(bt, t):
            for half in range(2):
                o = v.tensor_scalar(b["qm"][:, t % 2, :, :].rearrange("p (a h) c -> p a h c", h=2)[:, :, half, :],
                                    b["qT"][:, :, bass.ds(bt * SEQ + t * P, P)], b["half"][:, half:half + 1],
                                    QK_SCALE * math.sqrt(HDL), ALU.mult, ALU.mult)
            o.then_inc(k.sem("lf_queries_masked"), 1)

        def maxima(bt, u):
            at = ll * BATCH * HALVES + bt * HALVES
            v.wait_ge(k.sem("lf_probs"), at + (u - 1 + LEAD))
            hold(k, v, "lf_scores", at + (u + 1 + LEAD))
            for h in range(4):
                o = v.tensor_tensor_reduce(b["s"][:, u % 2, h, :],
                                           k.ps[:, 2 * (u % 2) + h // 2, h % 2 * SEEN:(h % 2 + 1) * SEEN],
                                           b["mask"][:, min(u % HALVES // 2, 1), :], -1.0, 3.0e38, ALU.add, ALU.min,
                                           b["negmax"][:, u % 2, h:h + 1])
            o.then_inc(k.sem("lf_maxima"), 1)

        def sequence(bt, last):
            at, tile = ll * BATCH * HALVES + bt * HALVES, ll * TILES + bt * TPG

            def copy(u):
                v.wait_ge(k.sem("lf_values"), at + (u - 1 + LEAD))
                v.wait_ge(k.sem("lf_probs_turned"), at + (u + 1))
                v.tensor_copy(b["pT"][:, u % 2, 2:4, :], k.ps[:, 5, :].rearrange("p (a b) -> p a b", a=2))\
                    .then_inc(k.sem("lf_probs_copied_dve"), 1)

            def out(t):
                v.wait_ge(k.sem("lf_values"), at + (2 * t + 2 + LEAD))
                total = b["sum"][:, t % 2, :]
                v.reciprocal(total, total)
                v.drain()
                v.tensor_tensor(b["o"][:, t % 2, :].rearrange("p (h d) -> p h d", d=HDL),
                                k.ps[:, 6, :].rearrange("p (h d) -> p h d", d=HDL), bc(total, HDL), ALU.mult)\
                    .then_inc(k.sem("lf_out"), 1)

            def add(t):
                v.wait_ge(k.sem("lf_out_projected"), tile + (t + 1 + LEAD))
                yt = b["y"][:, bass.ds(bt * TPG + t, 1), :].rearrange("p a d -> p (a d)")
                v.tensor_tensor(yt, k.ps[:, 7, 0:P], yt, ALU.add)\
                    .then_inc(k.sem("lf_added"), 1)

            for u in range(HALVES):
                t = u // 2
                copy(u)
                if u + 2 < HALVES or not last:
                    maxima(bt, u + 2)
                if u % 2:
                    if t:
                        add(t - 1)
                    out(t)
                    if t + 2 < TPG or not last:
                        queries(bt, t + 2)
            add(TPG - 1)

        queries(0, 0)
        queries(0, 1)
        maxima(0, 0)
        maxima(0, 1)
        sequences(v, sequence)

        v.wait_ge(k.sem("lf_added"), LEAD + (ll + 1) * TILES)
        v.sem_inc(k.sem("lf_y_ready"), 1)
        v.tensor_copy(k.xn[:, :, low], b["y"][:, :, low]).then_inc(k.sem("lf_halves_joined"), 1)
        v.wait_ge(k.sem("lf_ffn_weights"), 80 * (ll + 1))
        v.wait_ge(k.sem("lf_shifted"), SHIFTS * (2 * ll + 2))
        norm_dve(k, v, ln + 1 + layer, k.xn[:, :, :], k.xn[:, :, :])
        v.tensor_tensor(b["y"], b["y"], b["b2"].unsqueeze(1).broadcast_to([P, TILES, P]), ALU.add)
        v.drain()
        with v.Fori(0, GROUPS // 2) as i:
            at = ll * GROUPS * CH + i * (2 * CH)
            group = ll * GROUPS + i * 2
            v.wait_ge(k.sem("lf_down"), group + LEAD)

            def add(g):
                v.wait_ge(k.sem("lf_down"), group + (g + 1 + LEAD))
                yg = b["y"][:, bass.ds(i * (2 * TPG) + g * TPG, TPG), :]
                v.tensor_tensor(yg, k.ps[:, 4 + g, :].rearrange("p (a b) -> p a b", a=TPG), yg, ALU.add)\
                    .then_inc(k.sem("lf_ffn_added"), 1)

            for step in range(2 * CH):
                g, c = divmod(step, CH)
                v.wait_ge(k.sem("lf_gelu"), at + (step + 1))
                v.scalar_tensor_tensor(b["hid"][:, g, c, :], k.ps[:, 2 * (step % 2), :], b["vec"][:, 2 + c:3 + c],
                                       b["ge"][:, step % 2, :], ALU.add, ALU.mult).then_inc(k.sem("lf_hidden"), 1)
            add(0)
            add(1)
        v.drain()
        if layer + 1 < LAYERS:
            v.memset(k.xn[0:1, 0:TILES:TPG, DIM // 2:DIM], 0.0)
            v.drain()
            v.sem_inc(k.sem("lf_y_ready"), 1)
            v.sem_inc(k.sem("lf_layer_done"), 1)
        else:
            v.scalar_tensor_tensor(k.x[:, :, :].rearrange("p t d -> p (t d)"), b["y"].rearrange("p t d -> p (t d)"), 0.5,
                                   k.x[:, :, :].rearrange("p t d -> p (t d)"), ALU.mult, ALU.add)
            v.drain()
            v.sem_inc(k.sem("lf_layer_done"), 1)
            v.sem_inc(k.sem("x_updated"), 1)


def lay_out_local(a, i):
    import numpy as _np

    c, f = _np.ascontiguousarray, _np.float32
    a["lf_wqkv"] = i["L1_ffn_wqkv"]
    a["lf_scales"] = c(_np.concatenate([i["L1_ffn_q_scale"], i["L1_ffn_k_scale"]], axis=1))
    a["lf_wo"] = c(i["L1_ffn_wo"].reshape(LAYERS, PAIRS, P, DIM).transpose(0, 2, 1, 3).reshape(LAYERS, P, PAIRS * DIM))
    w1 = _np.zeros((LAYERS, DIM, 2, CH * P), f)
    w1[:, :, :, :HID] = i["L1_ffn_w1"].reshape(LAYERS, DIM, 2, HID)
    a["lf_w1"] = w1.reshape(LAYERS, DIM, 2 * CH * P)
    w2 = _np.zeros((LAYERS, CH * P, DIM), f)
    w2[:, :HID] = i["L1_ffn_w2"]
    a["lf_w2"] = c(w2.reshape(LAYERS, CH, P, DIM).transpose(0, 2, 1, 3).reshape(LAYERS, P, CH * DIM))
    b1 = _np.zeros((LAYERS, 2, CH * P), f)
    b1[:, :, :HID] = i["L1_ffn_b1"].reshape(LAYERS, 2, HID)
    a["lf_vec"] = c(_np.concatenate([i["L1_ffn_ln_g"][:, :, None], i["L1_ffn_ln_b"][:, :, None],
                                     b1.reshape(LAYERS, 2 * CH, P).transpose(0, 2, 1)], axis=2))
    a["lf_b2"] = i["L1_ffn_b2"]
    q, key = _np.arange(P)[:, None], _np.arange(SEEN)[None, :] - WINDOW
    seen = (key <= q) & (key >= q - WINDOW)
    a["lf_mask"] = c(_np.stack([_np.where(seen & (key >= 0), 0, -1e30), _np.where(seen, 0, -1e30)], axis=1).astype(f))
    half = _np.arange(0, HDL, 2, dtype=f)
    inv = (f(1.0) / f(10000.0) ** (half / f(HDL))).astype(f)
    t = _np.arange(SEQ, dtype=f)
    freqs = (t[:, None] * inv[None, :]).astype(_np.float64)
    base = ((half + 0.4 * HDL) / (1.4 * HDL)).astype(_np.float64)
    scale = base[None, :] ** ((t - SEQ // 2) / float(WINDOW // 2))[:, None]
    cos, sin = _np.cos(freqs), _np.sin(freqs)

    def table(x, lower):
        both = _np.stack([_np.concatenate([lower * x * z, x * z], axis=1) for z in (scale, 1.0 / scale)], axis=1)
        return c(both.reshape(TPG, P, 2, HDL).transpose(1, 0, 2, 3).astype(f))

    a["lf_cos"], a["lf_sin"] = table(cos, 1.0), table(sin, -1.0)

relu_moe = {"norms": 1, "transposes": 1, "gates": 1, "stores": 1, "backs": 1, "sync": relu_moe_sync, "tensor": relu_moe_pe,
            "scalar": relu_moe_act, "vector": relu_moe_dve}

swiglu_moe = {"norms": 3, "transposes": 3, "gates": 1, "stores": 0, "backs": 0, "sync": swiglu_sync,
              "tensor": swiglu_pe, "scalar": swiglu_act, "vector": swiglu_dve}
small_moe = {"norms": 1, "transposes": 1, "gates": 1, "stores": 1, "backs": 1, "sync": small_sync,
             "tensor": small_pe, "scalar": small_act, "vector": small_dve}


def attention_kind(c, norms):
    def bind(f):
        return lambda k, eng, m, n, ln: f(k, eng, m, n, ln, c)
    return {"norms": norms, "transposes": 1, "gates": 0, "backs": 0, "att_blocks": c.blocks, "flat": c.blocks == 1,
            "sync": bind(attention_sync), "tensor": bind(attention_pe), "scalar": bind(attention_act),
            "vector": bind(attention_dve)}


attn0, attn1, attn3 = attention_kind(A0, 1), attention_kind(A1, 2), attention_kind(A3, 1)
s4d = {"norms": 1, "transposes": 1, "gates": 0, "backs": 0, "sync": s4d_sync, "tensor": s4d_pe, "scalar": s4d_act,
       "vector": s4d_dve}
local_ffn = {"norms": 3, "transposes": 4, "gates": 0, "backs": 0, "sync": local_sync, "tensor": local_pe,
             "scalar": local_act, "vector": local_dve}



KINDS = {"ffn0": relu_moe, "attn0": attn0, "ffn1": local_ffn, "attn1": attn1, "ffn2": swiglu_moe, "attn2": s4d,
         "ffn3": small_moe, "attn3": attn3}
STAGES = ["ffn0", "attn0", "ffn0", "ffn1", "attn1", "ffn1", "ffn2", "attn2", "ffn2", "ffn3", "attn3", "ffn3"]


def build(nc, ins, out, stages=STAGES):
    scratch = nc.dram_tensor("gates_dram", (32 * TILES, P), F32, kind="Internal").ap()
    with ExitStack() as ctx:
        k = Program(nc, ctx, ins, out, scratch)
        k.gates_dram = scratch
        k.toeplitz_dram = nc.dram_tensor("toeplitz_dram", (HEADS, P, SPAN), F32, kind="Internal").ap()
        k.rel_dram = nc.dram_tensor("rel_dram", (HEADS, 2 * SEQ), F32, kind="Internal").ap()
        k.ln_calls, k.xt_calls, k.gate_calls, k.back_calls, k.kind_calls = [], [], [], [], []
        k.att_calls, k.att_blocks, k.flat_calls, k.gate_stores = [], [], [], []
        lns = xts = gates = backs = atts = blocks = flats = stores = 0
        seen = {}
        for s in stages:
            kind = KINDS[s]
            k.ln_calls.append(lns), k.xt_calls.append(xts), k.gate_calls.append(gates), k.back_calls.append(backs)
            k.kind_calls.append(seen.get(s, 0))
            seen[s] = seen.get(s, 0) + 1
            lns += kind["norms"]
            xts += kind["transposes"]
            gates += kind["gates"]
            backs += kind["backs"]
            k.att_calls.append(atts), k.att_blocks.append(blocks), k.flat_calls.append(flats - seen[s] + 1)
            k.gate_stores.append(stores)
            stores += kind.get("stores", 0)
            atts += "att_blocks" in kind
            blocks += kind.get("att_blocks", 0)
            flats += bool(kind.get("flat"))
        x_in = ins["x"].rearrange("b (t p) d -> p (b t) d", p=P)
        x_out = out.rearrange("b (t p) d -> p (b t) d", p=P)
        block = ctx.enter_context(nc.Block())

        def run(which, eng):
            for name in LED.get(which, []):
                eng.sem_inc(k.sem(name), LEAD)
            for m, s in enumerate(stages):
                KINDS[s][which](k, eng, m, k.kind_calls[m], k.ln_calls[m])

        @block.sync
        def _(sp):
            sp.dma_start(k.x[:, :, :], x_in).then_inc(k.sem("x_loaded"), 16)
            sp.dma_start(k.ident[:, :], ins["ident"]).then_inc(k.sem("x_loaded"), 16)
            run("sync", sp)
            sp.wait_ge(k.sem("x_updated"), len(stages) + 1)
            sp.dma_start(x_out, k.x[:, :, :]).then_inc(k.sem("x_stored"), 16)
            sp.wait_ge(k.sem("x_stored"), 16)

        @block.vector
        def _(v):
            v.wait_ge(k.sem("x_loaded"), 32)
            v.tensor_copy(k.ln_a[:, :], k.x[:, :, 0]).then_inc(k.sem("x_updated"), 1)
            run("vector", v)

        @block.tensor
        def _(pe):
            pe.wait_ge(k.sem("x_updated"), 1)
            run("tensor", pe)

        @block.scalar
        def _(a):
            run("scalar", a)


def lay_out(i):
    import numpy as _np

    c = _np.ascontiguousarray
    f = _np.float32
    a = {"x": i["L0_attn_X"], "ident": _np.eye(P, dtype=f), "rank": _np.arange(32, 0, -1).astype(f)}
    a["l0_gate_w"] = c(i["L0_ffn_gate_w"].T)
    a["l0_b2"] = i["L0_ffn_b2"]
    a["l0_w"] = c(_np.concatenate([
        i["L0_ffn_w1"],
        i["L0_ffn_w2"].reshape(E0, C0, P, DIM).transpose(0, 2, 1, 3).reshape(E0, P, C0 * DIM),
        i["L0_ffn_b1"].reshape(E0, C0, P).transpose(0, 2, 1)], axis=2))
    for more in (lay_out_attention, lay_out_swiglu, lay_out_small, lay_out_local, lay_out_s4d):
        more(a, i)
    return a


def kernel(**inputs):
    import numpy as _np
    import concourse.bacc as _bacc
    from concourse import mybir as _mybir
    from concourse.bass_utils import run_bass_kernel_spmd as _run

    nc = _bacc.Bacc("TRN2", target_bir_lowering=False, num_devices=1)
    arrays, ins = {}, {}
    for name, a in lay_out({n: _np.asarray(v) for n, v in inputs.items()}).items():
        arrays[f"in_{name}"] = a
        ins[name] = nc.dram_tensor(f"in_{name}", a.shape, _mybir.dt.from_np(a.dtype), kind="ExternalInput").ap()
    out = nc.dram_tensor("out_x", (BATCH, SEQ, DIM), _mybir.dt.float32, kind="ExternalOutput").ap()
    build(nc, ins, out)
    return _run(nc, [arrays], core_ids=[0]).results[0]["out_x"]
```

```python
import math

import numpy as np
import concourse.bass as bass
from concourse import mybir
from contextlib import ExitStack

F32 = mybir.dt.float32
ALU = mybir.AluOpType
ACT = mybir.ActivationFunctionType
X_AXIS = mybir.AxisListType.X

P = 128
BATCH, SEQ, DIM = 4, 512, 128
TOKENS = BATCH * SEQ
TILES = TOKENS // P
GROUPS = 4
GROUP = TOKENS // GROUPS
TPG = TILES // GROUPS
LN_EPS = 1e-5
F32_EPS = float(np.finfo(np.float32).eps)
NEG = -3.0e38

LEAD = 4
LED = {
    "tensor": [
        "moe0_down", "values", "gelu_turned", "att_projected", "lf_projected", "lf_values",
        "lf_out_projected", "lf_scores", "lf_down", "lf_turned", "probs_turned", "scores"],
    "vector": [
        "moe0_hidden", "heads_done", "lf_rotated", "lf_out", "lf_added", "lf_probs_copied_dve",
        "lf_hidden", "lf_ffn_added", "s4_kernel", "att_added", "maxima", "probs_copied"],
    "scalar": [
        "probs", "lf_kept", "lf_keys", "lf_probs", "lf_probs_copied_act", "lf_out_copied"],
}


class Arena:

    def __init__(self, tensor, floats):
        self.tensor, self.floats, self.at = tensor, floats, 0

    def reset(self, at=0):
        self.at = at

    def take(self, *shape, parts=P):
        n = int(np.prod(shape))
        assert self.at + n <= self.floats, (self.at, n)
        view = self.tensor[0:parts, self.at:self.at + n]
        self.at += n
        if len(shape) == 2:
            view = view.rearrange("p (a b) -> p a b", a=shape[0])
        elif len(shape) == 3:
            view = view.rearrange("p (a b c) -> p a b c", a=shape[0], b=shape[1])
        elif len(shape) == 4:
            view = view.rearrange("p (a b c d) -> p a b c d", a=shape[0], b=shape[1], c=shape[2])
        return view


class Program:

    def __init__(self, nc, ctx, ins):
        self.nc, self.ins = nc, ins
        self.ctx = ctx
        self.x = ctx.enter_context(nc.sbuf_tensor("x", [P, TILES, DIM], F32))
        self.xn = ctx.enter_context(nc.sbuf_tensor("xn", [P, TILES, DIM], F32))
        self.xT = ctx.enter_context(nc.sbuf_tensor("xT", [P, TOKENS], F32))
        self.ident = ctx.enter_context(nc.sbuf_tensor("ident", [P, P], F32))
        self.stats = ctx.enter_context(nc.sbuf_tensor("stats", [P, TILES, 6], F32))
        self.moments = ctx.enter_context(nc.sbuf_tensor("moments", [P, TILES, 2], F32))
        self.ln_a = ctx.enter_context(nc.sbuf_tensor("ln_a", [P, TILES], F32))
        self.spare = ctx.enter_context(nc.sbuf_tensor("spare", [P, 1], F32))
        self.ln_b = ctx.enter_context(nc.sbuf_tensor("ln_b", [P, TILES], F32))
        floats = 45760
        self.arena = Arena(ctx.enter_context(nc.sbuf_tensor("arena", [P, floats], F32)), floats)
        self.ps = ctx.enter_context(nc.psum_tensor("ps", [P, 8, 512], F32))
        self.sems = {}

    def sem(self, name):
        if name not in self.sems:
            self.sems[name] = self.ctx.enter_context(self.nc.semaphore(name))
        return self.sems[name]


def bc(ap, n):
    return ap.unsqueeze(2).broadcast_to([ap.shape[0], ap.shape[1], n])


def hold(k, eng, name, value):
    eng.wait_ge(k.sem(name), value)
    eng.sem_inc(k.sem("holds"), 1)


def use_table(k, a, function):
    a.activation(k.spare[:, :], k.ident[:, 0:1], function)



def mean_square(k, v):
    mean, var = k.moments[:, :, 0], k.moments[:, :, 1]
    v.drain()
    v.tensor_tensor(k.ln_a[:, :], mean, mean, ALU.mult)
    v.drain()
    v.tensor_tensor(var, k.ln_a[:, :], var, ALU.add)
    v.drain()


def norm_dve(k, v, n, src, dst, eps=LN_EPS, center=True):
    v.drain()
    for t in range(TILES):
        v.bn_stats(k.stats[:, t, :], src[:, t, :])
    v.drain()
    for t in range(TILES):
        v.bn_aggr(k.moments[:, t, :], k.stats[:, t, :])
    v.drain()
    if not center:
        mean_square(k, v)
    v.tensor_scalar(k.ln_a[:, :], k.moments[:, :, 1], eps, None, ALU.add).then_inc(k.sem("ln_var"), 1)
    v.wait_ge(k.sem("ln_sd"), n + 1)
    v.reciprocal(k.ln_b[:, :], k.ln_b[:, :])
    v.drain()
    for t in range(TILES):
        if center:
            o = v.tensor_scalar(dst[:, t, :], src[:, t, :], k.moments[:, t, 0:1], k.ln_b[:, t:t + 1],
                                ALU.subtract, ALU.mult)
        else:
            o = v.tensor_scalar(dst[:, t, :], src[:, t, :], k.ln_b[:, t:t + 1], None, ALU.mult)
        if t % TPG == TPG - 1:
            o.then_inc(k.sem("ln_done"), 1)


def norm_act(k, a, n):
    a.wait_ge(k.sem("ln_var"), n + 1)
    a.activation(k.ln_b[:, :], k.ln_a[:, :], ACT.Sqrt).then_inc(k.sem("ln_sd"), 1)


def transpose_pe(k, pe, src, ln=None):
    for g in range(GROUPS):
        if ln is not None:
            pe.wait_ge(k.sem("ln_done"), ln * GROUPS + g + 1)
        for j in range(TPG):
            t = pe.transpose(k.ps[:, g, j * P:(j + 1) * P], src[:, g * TPG + j, :], k.ident[:, :])
        t.then_inc(k.sem("ln_transposed"), 1)


def transpose_act(k, a, n, dst, gain=None, shift=None):
    for g in range(GROUPS):
        a.wait_ge(k.sem("ln_transposed"), n * GROUPS + g + 1)
        to = dst[:, g * GROUP:(g + 1) * GROUP]
        if gain is None:
            a.activation(to, k.ps[:, g, :], ACT.Copy).then_inc(k.sem("xT_ready"), 1)
        else:
            a.activation(to, k.ps[:, g, :], ACT.Identity, bias=shift, scale=gain).then_inc(k.sem("xT_ready"), 1)



def add_back_act(k, a, n, yT, scale):
    for g in range(GROUPS):
        a.activation(yT[:, g * GROUP:(g + 1) * GROUP], k.ps[:, g, :], ACT.Copy, scale=scale)\
            .then_inc(k.sem("y_evacuated"), 1)


def add_back_pe(k, pe, n, yT):
    for g in range(GROUPS):
        pe.wait_ge(k.sem("y_evacuated"), n * GROUPS + g + 1)
        for j in range(TPG):
            t = pe.transpose(k.ps[:, 4 + g, j * P:(j + 1) * P],
                             yT[:, g * GROUP + j * P:g * GROUP + (j + 1) * P], k.ident[:, :])
        t.then_inc(k.sem("y_back"), 1)


def add_back_dve(k, v, n):
    for g in range(GROUPS):
        v.wait_ge(k.sem("y_back"), n * GROUPS + g + 1)
        xg = k.x[:, g * TPG:(g + 1) * TPG, :]
        done = v.tensor_tensor(xg, k.ps[:, 4 + g, :].rearrange("p (a b) -> p a b", a=TPG), xg, ALU.add)
    done.then_inc(k.sem("x_updated"), 1)



def gate_logits_pe(k, pe, n, gate_w, experts):
    pe.wait_ge(k.sem("xT_ready"), (n + 1) * GROUPS)
    for t in range(TILES):
        m = pe.matmul(k.ps[:, 4, t * experts:(t + 1) * experts], k.xT[:, t * P:(t + 1) * P], gate_w,
                      start=True, stop=True)
    m.then_inc(k.sem("gate_logits"), 1)


def first_of_largest(k, v, cur, best, mask, rank, top):
    experts = cur.shape[2]
    v.drain()
    v.tensor_reduce(best, cur, X_AXIS, ALU.max)
    v.drain()
    v.tensor_tensor(mask, cur, bc(best, experts), ALU.is_ge)
    v.drain()
    v.tensor_tensor(mask, mask, rank[:, 0:experts].unsqueeze(1).broadcast_to([P, TILES, experts]), ALU.mult)
    v.drain()
    v.tensor_reduce(top, mask, X_AXIS, ALU.max)
    v.drain()
    v.tensor_tensor(mask, mask, bc(top, experts), ALU.is_equal)
    v.drain()


def gates_out_pe(k, pe, n, gates, chunks):
    pe.wait_ge(k.sem("gates_ready"), n + 1)
    flat = gates.rearrange("p e t -> p (e t)")
    for c in range(chunks):
        t = pe.transpose(k.ps[:, 5, c * P:(c + 1) * P], flat[:, c * P:(c + 1) * P], k.ident[:, :])
    t.then_inc(k.sem("gates_turned"), 1)


def gates_out_act(k, a, n, rows, chunks):
    a.wait_ge(k.sem("gates_turned"), n + 1)
    a.activation(rows, k.ps[:, 5, 0:chunks * P], ACT.Copy).then_inc(k.sem("gate_rows"), 1)
    a.wait_ge(k.sem("gate_rows"), n + 1)
    dst = k.gates_dram[0:chunks * P, :].rearrange("(c q) p -> q c p", c=chunks)
    a.dma_start(dst, rows.rearrange("q (c p) -> q c p", c=chunks)).then_inc(k.sem("gates_stored"), 16)



E0, F0 = 8, 512
C0 = F0 // P
W0_COLS = F0 + F0 + C0


def relu_moe_layout(k):
    a = k.arena
    a.reset()
    b = {}
    b["yT"] = a.take(TOKENS)
    b["gate_w"] = a.take(E0)
    b["rank"] = a.take(32)
    b["b2"] = a.take(P)[0:E0, :]
    b["gateT"] = a.take(TOKENS)[0:E0, :]
    b["logits"] = a.take(TILES, E0)
    b["mask"] = a.take(TILES, E0)
    b["gates"] = a.take(E0, TILES)
    b["best"], b["top"], b["sum"] = a.take(TILES), a.take(TILES), a.take(TILES)
    b["rows"] = a.take(P)
    b["w"] = a.take(2, W0_COLS)
    b["gb"] = a.take(2, TOKENS)
    b["relu"] = a.take(4, GROUP)
    b["hid"] = a.take(4, GROUP)
    return b


STEPS0 = GROUPS * C0


def relu_moe_sync(k, sp, m, n, ln):
    b = relu_moe_layout(k)
    sp.wait_ge(k.sem("x_updated"), m + 1)
    sp.dma_start(b["gate_w"], k.ins["l0_gate_w"]).then_inc(k.sem("moe0_gate_w"), 16)
    sp.dma_start(b["rank"], k.ins["rank"].partition_broadcast(P)).then_inc(k.sem("moe0_gate_w"), 16)
    sp.dma_start(b["b2"], k.ins["l0_b2"]).then_inc(k.sem("moe0_gate_w"), 16)
    sp.wait_ge(k.sem("gates_stored"), 16 * (k.gate_stores[m] + 1))
    sp.dma_start(b["gateT"], k.gates_dram[0:E0 * TILES, :].rearrange("(e t) p -> e (t p)", e=E0))\
        .then_inc(k.sem("moe0_gateT"), 16)
    base = n * E0 * STEPS0

    def load(s, e):
        sp.dma_start(b["w"][:, s, :], k.ins["l0_w"][bass.ds(e, 1), :, :].rearrange("a p c -> (a p) c"))\
            .then_inc(k.sem(f"moe0_w{s}"), 16)
        sp.dma_start(b["gb"][:, s, :], k.gates_dram[bass.ds(e * TILES, TILES), :]
                     .rearrange("t p -> (t p)").partition_broadcast(P)).then_inc(k.sem(f"moe0_w{s}"), 16)

    load(0, 0)
    load(1, 1)
    with sp.Fori(0, E0 // 2 - 1) as i:
        for s in range(2):
            sp.wait_ge(k.sem("moe0_down"), LEAD + base + i * (2 * STEPS0) + (s + 1) * STEPS0)
            load(s, i * 2 + (2 + s))


def expert_pairs(eng, body):
    with eng.Fori(0, E0 // 2 - 1) as i:
        for s in range(2):
            body(i, s, False)
    for s in range(2):
        body(E0 // 2 - 1, s, s == 1)


def relu_moe_pe(k, pe, m, n, ln):
    b = relu_moe_layout(k)
    transpose_pe(k, pe, k.xn, ln)
    pe.wait_ge(k.sem("moe0_gate_w"), 48 * (n + 1))
    gate_logits_pe(k, pe, k.xt_calls[m], b["gate_w"], E0)
    gates_out_pe(k, pe, k.gate_stores[m], b["gates"], 1)
    pe.wait_ge(k.sem("gate_rows"), k.gate_stores[m] + 1)
    pe.wait_ge(k.sem("moe0_gateT"), 16 * (n + 1))
    for g in range(GROUPS):
        pe.matmul(k.ps[:, g, :], b["b2"], b["gateT"][:, g * GROUP:(g + 1) * GROUP], start=True, stop=True)
    base = n * E0 * STEPS0
    wbase = 16 * E0 * n

    def up(i, s, step):
        over, own = divmod(step, STEPS0)
        g, c = divmod(own, C0)
        slot = (s + over) % 2
        if own == 0:
            pe.wait_ge(k.sem(f"moe0_w{slot}"), wbase + 32 * i + (64 if s + over == 2 else 32))
        if step >= 4:
            pe.wait_ge(k.sem("moe0_relu"), base + i * (2 * STEPS0) + (s * STEPS0 + step - 3))
        pe.matmul(k.ps[:, 4 + step % 4, :], b["w"][:, slot, c * P:(c + 1) * P], k.xT[:, g * GROUP:(g + 1) * GROUP],
                  start=True, stop=True).then_inc(k.sem("moe0_up"), 1)

    def body(i, s, last):
        for step in range(STEPS0):
            if step + 3 < STEPS0 or not last:
                up(i, s, step + 3)
            g, c = divmod(step, C0)
            pe.wait_ge(k.sem("moe0_hidden"), base + i * (2 * STEPS0) + (s * STEPS0 + step + 1 + LEAD))
            pe.matmul(k.ps[:, g, :], b["w"][:, s, F0 + c * P:F0 + (c + 1) * P], b["hid"][:, step % 4, :],
                      start=False, stop=True, skip_group_check=True).then_inc(k.sem("moe0_down"), 1)

    for step in range(3):
        up(0, 0, step)
    expert_pairs(pe, body)
    add_back_pe(k, pe, k.back_calls[m], b["yT"])


def relu_moe_act(k, a, m, n, ln):
    b = relu_moe_layout(k)
    norm_act(k, a, ln)
    transpose_act(k, a, k.xt_calls[m], k.xT)
    a.wait_ge(k.sem("gate_shifted"), n + 1)
    a.activation(b["logits"], b["logits"], ACT.Exp).then_inc(k.sem("gate_exp"), 1)
    gates_out_act(k, a, k.gate_stores[m], b["rows"], 1)
    base = n * E0 * STEPS0

    def body(i, s, last):
        for step in range(STEPS0):
            at, c = base + i * (2 * STEPS0), step % C0
            a.wait_ge(k.sem("moe0_up"), at + (s * STEPS0 + step + 1))
            a.wait_ge(k.sem("moe0_hidden"), at + (s * STEPS0 + step - 3 + LEAD))
            a.activation(b["relu"][:, step % 4, :], k.ps[:, 4 + step % 4, :], ACT.Relu,
                         bias=b["w"][:, s, 2 * F0 + c:2 * F0 + c + 1]).then_inc(k.sem("moe0_relu"), 1)

    expert_pairs(a, body)
    a.wait_ge(k.sem("moe0_down"), LEAD + base + E0 * STEPS0)
    add_back_act(k, a, k.back_calls[m], b["yT"], 0.5)


def relu_moe_dve(k, v, m, n, ln):
    b = relu_moe_layout(k)
    norm_dve(k, v, ln, k.x[:, :, :], k.xn[:, :, :])
    gc = k.gate_calls[m]
    v.wait_ge(k.sem("gate_logits"), gc + 1)
    v.tensor_copy(b["logits"], k.ps[:, 4, 0:TILES * E0].rearrange("p (t e) -> p t e", t=TILES))
    first_of_largest(k, v, b["logits"], b["best"], b["mask"], b["rank"], b["top"])
    v.tensor_tensor(b["logits"], b["logits"], bc(b["best"], E0), ALU.subtract).then_inc(k.sem("gate_shifted"), 1)
    v.wait_ge(k.sem("gate_exp"), n + 1)
    v.tensor_reduce(b["sum"], b["logits"], X_AXIS, ALU.add)
    v.drain()
    v.reciprocal(b["sum"], b["sum"])
    v.drain()
    v.tensor_tensor(b["gates"].rearrange("p e t -> p t e"), b["mask"], bc(b["sum"], E0), ALU.mult)\
        .then_inc(k.sem("gates_ready"), 1)
    base = n * E0 * STEPS0
    wbase = 16 * E0 * n

    def body(i, s, last):
        for step in range(STEPS0):
            at, g = base + i * (2 * STEPS0), step // C0
            if step == 0:
                v.wait_ge(k.sem(f"moe0_w{s}"), wbase + 32 * i + 32)
            v.wait_ge(k.sem("moe0_relu"), at + (s * STEPS0 + step + 1))
            v.wait_ge(k.sem("moe0_down"), at + (s * STEPS0 + step - 3 + LEAD))
            v.tensor_tensor(b["hid"][:, step % 4, :], b["relu"][:, step % 4, :],
                            b["gb"][:, s, g * GROUP:(g + 1) * GROUP], ALU.mult).then_inc(k.sem("moe0_hidden"), 1)

    expert_pairs(v, body)
    add_back_dve(k, v, k.back_calls[m])



HD0, HD1 = 64, 8
HEADS = 16
HEAD_RUNS = BATCH * HEADS
KTILES = SEQ // P
SLOTS = 4
AHEAD = SLOTS - 1
SCORE_BANKS = (0, 1, 6, 7)
V_BANKS, Q_BANKS, K_BANKS = (6, 7, 2, 3), (0, 1, 6, 7), (2, 3, 4, 5)
SPAN = SEQ + KTILES * P - P


class Attention:
    def __init__(self, name, blocks, width, causal=False, bias=False):
        self.name, self.blocks, self.width, self.causal, self.bias = name, blocks, width, causal, bias
        self.heads = P // width
        self.hold = min(self.heads, 4)
        self.steps = self.hold * KTILES
        self.rounds = self.heads // self.hold


A0 = Attention("a0", 8, HD0)
A1 = Attention("a1", 1, HD1, bias=True)
A3 = Attention("a3", 1, HD1, causal=True)


def attention_layout(k, c):
    a = k.arena
    a.reset()
    b = {}
    b["w"] = a.take(3 * P)
    b["mask"] = a.take(c.heads)
    b["q"], b["k"] = a.take(TOKENS), a.take(TOKENS)
    b["v"] = a.take(TILES, P)
    b["qm"] = a.take(c.hold, SEQ)
    b["p"] = a.take(SLOTS, SEQ)
    b["pT"] = a.take(2, SEQ)
    b["negmax"], b["sum"] = a.take(c.steps), a.take(c.steps)
    b["att"] = a.take(TILES, c.blocks * P)
    b["w_out"] = a.take(c.blocks, P)
    b["tri"] = a.take(P)
    if c.bias:
        b["s"] = a.take(SLOTS, SEQ)
        b["toeplitz"] = a.take(c.hold, SPAN)
        b["v_bias"], b["out_bias"] = a.take(P), a.take(P)
        b["vec"] = a.take(4)
        b["w_rel"] = a.take(HEADS)[0:HD1, :]
        b["rel_pe"] = a.take(2 * SEQ)[0:HD1, :]
        b["rel"] = a.take(2 * SEQ)[0:HEADS, :]
    if c.blocks > 1:
        b["gelu"] = a.take(2, c.blocks * P)
        b["gT"] = a.take(2, c.blocks * P)
    else:
        b["attT"] = a.take(TOKENS)
    return b


def attention_sync(k, sp, m, n, ln, c):
    b = attention_layout(k, c)
    w = k.ins[c.name + "_w"]
    sp.wait_ge(k.sem("x_updated"), m + 1)
    if c.bias:
        sp.dma_start(b["w_rel"], k.ins["a1_w_rel"]).then_inc(k.sem("rel_loaded"), 16)
        sp.dma_start(b["rel_pe"], k.ins["rel_pe"]).then_inc(k.sem("rel_loaded"), 16)
    ready = k.sem(c.name + "_loaded")
    sp.dma_start(b["mask"], k.ins[c.name + "_mask"]).then_inc(ready, 16)
    sp.dma_start(b["w_out"], k.ins[c.name + "_w_out"]).then_inc(ready, 16)
    sp.dma_start(b["tri"], k.ins["tri"]).then_inc(ready, 16)
    weights = k.sem("att_w")
    wb = k.att_blocks[m]

    def load(i):
        sp.dma_start(b["w"], w[bass.ds(i, 1), :, :].rearrange("a p c -> (a p) c")).then_inc(weights, 16)

    load(0)
    if c.blocks > 1:
        with sp.Fori(0, c.blocks - 1) as i:
            sp.wait_ge(k.sem("qk_projected"), (wb + 1) * 2 * GROUPS + i * (2 * GROUPS))
            load(i + 1)
    if c.bias:
        sp.dma_start(b["vec"], k.ins["a1_vec"]).then_inc(ready, 16)
        sp.dma_start(b["v_bias"], k.ins["a1_v_bias"].partition_broadcast(P)).then_inc(ready, 16)
        sp.dma_start(b["out_bias"], k.ins["a1_out_bias"].partition_broadcast(P)).then_inc(ready, 16)
        sp.wait_ge(k.sem("rel_ready"), 1)
        sp.dma_start(k.rel_dram, b["rel"]).then_inc(k.sem("rel_stored"), 16)
        sp.wait_ge(k.sem("rel_stored"), 16)
        shifted = bass.AP(tensor=k.rel_dram.tensor, offset=k.rel_dram.offset + P - 1,
                          ap=[[2 * SEQ, HEADS], [-1, P], [1, SPAN]])
        sp.dma_start(k.toeplitz_dram, shifted).then_inc(k.sem("toeplitz_stored"), 16)
        sp.wait_ge(k.sem("toeplitz_stored"), 16)
        with sp.Fori(0, BATCH) as bt:
            with sp.Fori(0, c.rounds) as r:
                for s in range(c.hold):
                    sp.wait_ge(k.sem("toeplitz_used"), bt * c.heads + r * c.hold + (s + 1))
                    src = k.toeplitz_dram[bass.ds(r * c.hold + s, 1), :, :].rearrange("h p m -> (h p) m")
                    sp.dma_start(b["toeplitz"][:, s, :], src).then_inc(k.sem(f"toeplitz{s}"), 16)


def attention_loops(eng, c, head0, block_of_heads, begin, iteration):
    if c.blocks > 1:
        with eng.Fori(0, c.blocks) as blk:
            head = head0 + blk * (BATCH * c.heads)
            block_of_heads(blk)
            begin(head, 0)
            with eng.Fori(0, BATCH - 1) as bt:
                iteration(head0 + blk * (BATCH * c.heads) + bt * c.heads, bt, 0, False)
            iteration(head + (BATCH - 1) * c.heads, BATCH - 1, 0, True)
    else:
        block_of_heads(0)
        with eng.Fori(0, BATCH) as bt:
            head = head0 + bt * c.heads
            begin(head, bt)
            with eng.Fori(0, c.rounds - 1) as r:
                iteration(head0 + bt * c.heads + r * c.hold, bt, r, False)
            iteration(head + (c.rounds - 1) * c.hold, bt, c.rounds - 1, True)


def attention_pe(k, pe, m, n, ln, c):
    b = attention_layout(k, c)
    head0, wb = k.att_calls[m] * HEAD_RUNS, k.att_blocks[m]
    if c.bias:
        pe.wait_ge(k.sem("rel_loaded"), 32)
        for h in range(2):
            r = pe.matmul(k.ps[0:HEADS, 6 + h, :], b["w_rel"], b["rel_pe"][:, h * SEQ:(h + 1) * SEQ],
                          start=True, stop=True)
        r.then_inc(k.sem("rel_multiplied"), 1)
    transpose_pe(k, pe, k.xn, ln + (1 if c.bias else 0))
    pe.wait_ge(k.sem("xT_ready"), (k.xt_calls[m] + 1) * GROUPS)
    if c.bias:
        pe.wait_ge(k.sem("rel_ready"), 1)
    pe.wait_ge(k.sem(c.name + "_loaded"), 16 * (6 if c.bias else 3))

    block_now = []

    def block_of_heads(blk):
        block_now[:] = [blk]
        pe.wait_ge(k.sem("att_w"), 16 * (wb + 1) + 16 * blk)
        for g in range(GROUPS):
            for j in range(TPG):
                t = g * TPG + j
                o = pe.matmul(k.ps[:, V_BANKS[g], j * P:(j + 1) * P], k.xT[:, t * P:(t + 1) * P], b["w"][:, 2 * P:3 * P],
                              start=True, stop=True)
            o.then_inc(k.sem("v_projected"), 1)
        for half, banks in enumerate((Q_BANKS, K_BANKS)):
            for g in range(GROUPS):
                if banks[g] in V_BANKS:
                    pe.wait_ge(k.sem("v_ready"), GROUPS * wb + V_BANKS.index(banks[g]) + 1 + GROUPS * blk)
                if banks[g] == 4:
                    pe.wait_ge(k.sem("heads_done"), LEAD + head0 + blk * (BATCH * c.heads))
                pe.matmul(k.ps[:, banks[g], :], b["w"][:, half * P:(half + 1) * P], k.xT[:, g * GROUP:(g + 1) * GROUP],
                          start=True, stop=True).then_inc(k.sem("qk_projected"), 1)
        hold(k, pe, "qk_ready", 8 * wb + (GROUPS + 1) + 8 * blk)

    def scores(head, bt, step):
        s, j = divmod(step % c.steps, KTILES)
        at = head * KTILES
        if j == 0:
            pe.wait_ge(k.sem("queries_masked"), head + (step // KTILES + 1))
        if c.bias:
            pe.wait_ge(k.sem("maxima"), at + (step - AHEAD + LEAD))
        else:
            pe.wait_ge(k.sem("probs"), at + (step - AHEAD + LEAD))
        cols = (j + 1) * P if c.causal else SEQ
        o = pe.matmul(k.ps[:, SCORE_BANKS[step % SLOTS], 0:cols], b["qm"][:, s, j * P:(j + 1) * P],
                      b["k"][:, bass.ds(bt * SEQ, cols)], start=True, stop=not c.causal)
        if c.causal:
            o = pe.matmul(k.ps[:, SCORE_BANKS[step % SLOTS], j * P:(j + 1) * P], k.ident[:, :], b["tri"],
                          start=False, stop=True)
        o.then_inc(k.sem("scores"), 1)

    def iteration(head, bt, r, last):
        at = head * KTILES

        def turn(step):
            tiles = step % KTILES + 1 if c.causal else KTILES
            pe.wait_ge(k.sem("probs"), at + (step + 1 + LEAD))
            pe.wait_ge(k.sem("probs_copied"), at + (step - 1 + LEAD))
            for t in range(tiles):
                o = pe.transpose(k.ps[:, 2 + step % 2, t * P:(t + 1) * P],
                                 b["p"][:, step % SLOTS, t * P:(t + 1) * P], k.ident[:, :])
            o.then_inc(k.sem("probs_turned"), 1)

        def values(step):
            s, j = divmod(step, KTILES)
            tiles = j + 1 if c.causal else KTILES
            pe.wait_ge(k.sem("probs_copied"), at + (step + 1 + LEAD))
            if j == 0:
                pe.wait_ge(k.sem("heads_done"), head + (s - 1 + LEAD))
            for t in range(tiles):
                o = pe.matmul(k.ps[:, 4 + s % 2, j * c.width:(j + 1) * c.width],
                              b["pT"][:, step % 2, t * P:(t + 1) * P],
                              b["v"].rearrange("p t d -> p (t d)")
                              [:, bass.ds(bt * SEQ + r * (c.hold * c.width) + (t * P + s * c.width), c.width)],
                              start=(t == 0), stop=(t == tiles - 1))
            o.then_inc(k.sem("values"), 1)

        for step in range(c.steps):
            turn(step)
            if step + AHEAD < c.steps:
                scores(head, bt, step + AHEAD)
            elif not last:
                scores(head, bt + (1 if c.rounds == 1 else 0), step + AHEAD)
            if step >= 1:
                values(step - 1)
        values(c.steps - 1)

    def begin(head, bt):
        scores(head, bt, 0)
        scores(head, bt, 1)
        pe.wait_ge(k.sem("qk_ready"), 8 * (wb + 1) + 8 * block_now[0])
        scores(head, bt, 2)

    attention_loops(pe, c, head0, block_of_heads, begin, iteration)

    pe.wait_ge(k.sem("heads_done"), LEAD + head0 + HEAD_RUNS)
    if c.blocks > 1:
        with pe.Fori(0, TILES // 2) as i:
            for s in range(2):
                pe.wait_ge(k.sem("att_gelu"), i * 2 + (s + 1))
                for h in range(2):
                    for j in range(4):
                        cc = 4 * h + j
                        o = pe.transpose(k.ps[:, 2 * s + h, j * P:(j + 1) * P],
                                         b["gelu"][:, s, cc * P:(cc + 1) * P], k.ident[:, :])
                    o.then_inc(k.sem("gelu_turned"), 1)
            for s in range(2):
                pe.wait_ge(k.sem("gelu_copied"), i * 4 + (2 * s + 2))
                pe.wait_ge(k.sem("att_added"), LEAD + i * 2)
                for cc in range(c.blocks):
                    o = pe.matmul(k.ps[:, 4 + s, 0:P], b["gT"][:, s, cc * P:(cc + 1) * P], b["w_out"][:, cc, :],
                                  start=(cc == 0), stop=(cc == c.blocks - 1))
                o.then_inc(k.sem("att_projected"), 1)
    else:
        for g in range(GROUPS):
            for j in range(TPG):
                t = g * TPG + j
                o = pe.transpose(k.ps[:, g, j * P:(j + 1) * P], b["att"][:, t, :], k.ident[:, :])
            o.then_inc(k.sem("att_turned"), 1)
        for g in range(GROUPS):
            pe.wait_ge(k.sem("att_copied"), (n + k.flat_calls[m]) * GROUPS + g + 1)
            for j in range(TPG):
                t = g * TPG + j
                o = pe.matmul(k.ps[:, 4 + g, j * P:(j + 1) * P], b["attT"][:, t * P:(t + 1) * P], b["w_out"][:, 0, :],
                              start=True, stop=True)
            o.then_inc(k.sem("flat_projected"), 1)


def attention_act(k, a, m, n, ln, c):
    b = attention_layout(k, c)
    head0, wb = k.att_calls[m] * HEAD_RUNS, k.att_blocks[m]
    if c.bias:
        a.wait_ge(k.sem("rel_multiplied"), 1)
        a.activation(b["rel"].rearrange("h (a b) -> h a b", a=2), k.ps[0:HEADS, 6:8, :], ACT.Copy)\
            .then_inc(k.sem("rel_ready"), 1)
    norm_act(k, a, ln)
    if c.bias:
        norm_act(k, a, ln + 1)
        a.wait_ge(k.sem("a1_loaded"), 16 * 6)
        transpose_act(k, a, k.xt_calls[m], k.xT, b["vec"][:, 0:1], b["vec"][:, 1:2])
    else:
        transpose_act(k, a, k.xt_calls[m], k.xT)

    def block_of_heads(blk):
        a.wait_ge(k.sem("heads_done"), LEAD + head0 + blk * (BATCH * c.heads))
        for half, (dst, banks) in enumerate(((b["q"], Q_BANKS), (b["k"], K_BANKS))):
            for g in range(GROUPS):
                a.wait_ge(k.sem("qk_projected"), 8 * wb + GROUPS * half + g + 1 + 8 * blk)
                to, src = dst[:, g * GROUP:(g + 1) * GROUP], k.ps[:, banks[g], :]
                if c.bias:
                    o = a.activation(to, src, ACT.Identity, bias=b["vec"][:, 2 + half:3 + half])
                else:
                    o = a.activation(to, src, ACT.Copy)
                o.then_inc(k.sem("qk_ready"), 1)

    def iteration(head, bt, r, last):
        at = head * KTILES
        for step in range(c.steps):
            cols = (step % KTILES + 1) * P if c.causal else SEQ
            a.wait_ge(k.sem("maxima"), at + (step + 1 + LEAD))
            a.wait_ge(k.sem("probs_turned"), at + (step - AHEAD + LEAD))
            src = b["s"][:, step % SLOTS, :] if c.bias else k.ps[:, SCORE_BANKS[step % SLOTS], 0:cols]
            a.activation(b["p"][:, step % SLOTS, 0:cols], src, ACT.Exp, bias=b["negmax"][:, step:step + 1],
                         scale=-1.0 if c.bias else 1.0, accum_out=b["sum"][:, step:step + 1])\
                .then_inc(k.sem("probs"), 1)

    use_table(k, a, ACT.Exp)
    attention_loops(a, c, head0, block_of_heads, lambda head, bt: None, iteration)

    a.wait_ge(k.sem("heads_done"), LEAD + head0 + HEAD_RUNS)
    if c.blocks > 1:
        use_table(k, a, ACT.Gelu)
        with a.Fori(0, TILES // 2) as i:
            for s in range(2):
                a.wait_ge(k.sem("gelu_turned"), LEAD + i * 4)
                a.activation(b["gelu"][:, s, :], b["att"][:, bass.ds(i * 2 + s, 1), :].rearrange("p a c -> p (a c)"),
                             ACT.Gelu).then_inc(k.sem("att_gelu"), 1)
            for s in range(2):
                for h in range(2):
                    a.wait_ge(k.sem("gelu_turned"), i * 4 + (2 * s + h + 1 + LEAD))
                    if s == 0 and h == 0:
                        a.wait_ge(k.sem("att_projected"), LEAD + i * 2)
                    a.activation(b["gT"][:, s, h * 512:(h + 1) * 512], k.ps[:, 2 * s + h, :], ACT.Copy)\
                        .then_inc(k.sem("gelu_copied"), 1)
    else:
        for g in range(GROUPS):
            a.wait_ge(k.sem("att_turned"), (n + k.flat_calls[m]) * GROUPS + g + 1)
            a.activation(b["attT"][:, g * GROUP:(g + 1) * GROUP], k.ps[:, g, :], ACT.Copy)\
                .then_inc(k.sem("att_copied"), 1)


def attention_dve(k, v, m, n, ln, c):
    b = attention_layout(k, c)
    head0, wb = k.att_calls[m] * HEAD_RUNS, k.att_blocks[m]
    norm_dve(k, v, ln, k.x[:, :, :], k.xn[:, :, :])
    if c.bias:
        norm_dve(k, v, ln + 1, k.xn[:, :, :], k.xn[:, :, :])
    v.wait_ge(k.sem(c.name + "_loaded"), 16 * (6 if c.bias else 3))

    def block_of_heads(blk):
        for g in range(GROUPS):
            v.wait_ge(k.sem("v_projected"), GROUPS * wb + g + 1 + GROUPS * blk)
            to, src = b["v"][:, g * TPG:(g + 1) * TPG, :], k.ps[:, V_BANKS[g], :].rearrange("p (a b) -> p a b", a=TPG)
            if c.bias:
                o = v.tensor_tensor(to, src, b["v_bias"].unsqueeze(1).broadcast_to([P, TPG, P]), ALU.add)
            else:
                o = v.tensor_copy(to, src)
            o.then_inc(k.sem("v_ready"), 1)
        hold(k, v, "qk_ready", 8 * wb + GROUPS + 8 * blk)

    def mask(head, bt, r, s):
        if s >= c.hold:
            v.wait_ge(k.sem("scores"), head * KTILES + ((s - c.hold + 1) * KTILES + LEAD))
        v.tensor_scalar(b["qm"][:, s % c.hold, :], b["q"][:, bass.ds(bt * SEQ, SEQ)],
                        b["mask"][:, bass.ds(r * c.hold + s % c.hold, 1)], None, ALU.mult)\
            .then_inc(k.sem("queries_masked"), 1)

    def maximum(head, step):
        at = head * KTILES
        s, j = divmod(step % c.steps, KTILES)
        cols = (j + 1) * P if c.causal else SEQ
        negmax = b["negmax"][:, step % c.steps:step % c.steps + 1]
        if c.bias:
            if j == 0:
                v.wait_ge(k.sem(f"toeplitz{s}"), head * (16 // c.hold) + (16 - head0 * (16 // c.hold)
                                                                     + (16 if step >= c.steps else 0)))
            v.wait_ge(k.sem("probs"), at + (step - AHEAD + LEAD))
            hold(k, v, "scores", at + (step + 1 + LEAD))
            v.tensor_tensor_reduce(b["s"][:, step % SLOTS, :], k.ps[:, SCORE_BANKS[step % SLOTS], :],
                                   b["toeplitz"][:, s, 384 - j * P:384 - j * P + SEQ], -1.0, 3.0e38,
                                   ALU.add, ALU.min, negmax).then_inc(k.sem("maxima"), 1)
            if j == KTILES - 1:
                v.drain()
                v.sem_inc(k.sem("toeplitz_used"), 1)
        else:
            v.wait_ge(k.sem("scores"), at + (step + 1 + LEAD))
            v.tensor_reduce(negmax, k.ps[:, SCORE_BANKS[step % SLOTS], 0:cols], X_AXIS, ALU.max, negate=True)\
                .then_inc(k.sem("maxima"), 1)

    block_now = []

    def iteration(head, bt, r, last):
        at = head * KTILES

        def copy(step):
            cols = (step % KTILES + 1) * P if c.causal else SEQ
            v.wait_ge(k.sem("values"), at + (step - 1 + LEAD))
            v.wait_ge(k.sem("probs_turned"), at + (step + 1 + LEAD))
            v.tensor_copy(b["pT"][:, step % 2, 0:cols], k.ps[:, 2 + step % 2, 0:cols])\
                .then_inc(k.sem("probs_copied"), 1)

        def finish(s):
            total = b["sum"][:, KTILES * s:KTILES * s + KTILES]
            v.wait_ge(k.sem("values"), at + (KTILES * (s + 1) + LEAD))
            v.reciprocal(total, total)
            v.drain()
            col = r * (c.hold * c.width) + s * c.width
            if c.blocks > 1:
                col = block_now[0] * P + col
            out = b["att"][:, bass.ds(bt * KTILES, KTILES), bass.ds(col, c.width)]
            v.tensor_tensor(out, k.ps[:, 4 + s % 2, 0:KTILES * c.width].rearrange("p (a b) -> p a b", a=KTILES),
                            bc(total, c.width), ALU.mult).then_inc(k.sem("heads_done"), 1)

        for step in range(c.steps):
            copy(step)
            s, j = divmod(step, KTILES)
            if not last and j == 2:
                mask(head, bt + 1 if c.rounds == 1 else bt, r if c.rounds == 1 else r + 1, c.hold + s)
            if j == 1 and s:
                finish(s - 1)
            if step + AHEAD < c.steps or not last:
                maximum(head, step + AHEAD)
        finish(c.hold - 1)

    def begin(head, bt):
        for s in range(c.hold):
            mask(head, bt, 0, s)
        for step in range(AHEAD):
            maximum(head, step)

    def first_block(blk):
        block_now[:] = [blk]
        block_of_heads(blk)

    if c.bias:
        v.sem_inc(k.sem("toeplitz_used"), c.hold)
    attention_loops(v, c, head0, first_block, begin, iteration)
    if c.blocks > 1:
        v.tensor_tensor(k.x[:, :, :], k.x[:, :, :], k.xn[:, :, :], ALU.add)
        with v.Fori(0, TILES // 2) as i:
            for s in range(2):
                xt = k.x[:, bass.ds(i * 2 + s, 1), :].rearrange("p a d -> p (a d)")
                v.drain()
                v.wait_ge(k.sem("att_projected"), i * 2 + (s + 1 + LEAD))
                v.tensor_tensor(xt, k.ps[:, 4 + s, 0:P], xt, ALU.add).then_inc(k.sem("att_added"), 1)
        v.drain()
        v.tensor_copy(k.ln_a[:, :], k.x[:, :, 0]).then_inc(k.sem("x_updated"), 1)
    else:
        if c.bias:
            v.tensor_tensor(k.x[:, :, :], k.x[:, :, :], b["out_bias"].unsqueeze(1).broadcast_to([P, TILES, P]), ALU.add)
            v.drain()
        for g in range(GROUPS):
            v.wait_ge(k.sem("flat_projected"), (n + k.flat_calls[m]) * GROUPS + g + 1)
            xg = k.x[:, g * TPG:(g + 1) * TPG, :]
            o = v.tensor_tensor(xg, k.ps[:, 4 + g, :].rearrange("p (a b) -> p a b", a=TPG), xg, ALU.add)
        o.then_inc(k.sem("x_updated"), 1)


def lay_out_attention(a, i):
    import numpy as _np

    c, f = _np.ascontiguousarray, _np.float32
    feature = _np.arange(P)
    for at, n in ((A0, "a0"), (A1, "a1"), (A3, "a3")):
        a[n + "_mask"] = c((feature[:, None] // at.width == _np.arange(at.heads)[None, :]).astype(f)
                           * f(1.0 / math.sqrt(at.width)))
    a["tri"] = _np.where(feature[:, None] >= feature[None, :], f(0), f(-1e30)).astype(f)
    a["a0_w"] = c(_np.stack([i["L0_attn_Wq"], i["L0_attn_Wk"], i["L0_attn_Wv"]]).reshape(3, P, 8, P)
                  .transpose(2, 1, 0, 3).reshape(8, P, 3 * P))
    a["a0_w_out"] = c(i["L0_attn_Wpost"].reshape(8, P, P).transpose(1, 0, 2))
    a["a1_w"] = c(i["L1_attn_w_qkv"][None])
    a["a1_w_out"] = c(i["L1_attn_w_out"].reshape(P, 1, P))
    bq = i["L1_attn_b_qkv"].reshape(3, P)
    a["a1_vec"] = c(_np.stack([i["L1_attn_ln_g"], i["L1_attn_ln_b"], bq[0], bq[1]], axis=1))
    a["a1_v_bias"], a["a1_out_bias"], a["a1_w_rel"] = c(bq[2]), i["L1_attn_b_out"], i["L1_attn_w_rel"]
    a["a3_w"] = c(_np.stack([i["L3_attn_WQ"], i["L3_attn_WK"], i["L3_attn_WV"]]).reshape(3, P, P)
                  .transpose(2, 0, 1).reshape(1, P, 3 * P))
    a["a3_w_out"] = c(i["L3_attn_WO"].transpose(0, 2, 1).reshape(P, 1, P))
    pos = _np.arange(-(SEQ - 1), SEQ, dtype=f)[:, None]
    div = _np.exp(_np.arange(0, HD1, 2, dtype=f) * f(-math.log(10000.0) / HD1)).astype(f)
    angle = (pos * div).astype(_np.float64)
    pe = _np.zeros((2 * SEQ, HD1), f)
    pe[:2 * SEQ - 1, 0::2], pe[:2 * SEQ - 1, 1::2] = _np.sin(angle)[::-1], _np.cos(angle)[::-1]
    a["rel_pe"] = c(pe.T)



E2, F2 = 8, 512
C2 = F2 // P
W2_COLS = 3 * F2
STEPS2 = GROUPS * C2
NORM_ROOT = 7


def swiglu_layout(k):
    a = k.arena
    a.reset()
    b = {}
    b["small"] = a.take(2 * P + E2 + 32 + 2)
    b["w_in"], b["w_out"] = b["small"][:, 0:P], b["small"][:, P:2 * P]
    b["router"] = b["small"][:, 2 * P:2 * P + E2]
    b["gains"] = b["small"][:, 2 * P + E2 + 32:]
    b["rank"] = a.take(32)
    b["e_bias"] = a.take(E2)
    b["h"] = a.take(TILES, P)
    b["hT"] = a.take(TOKENS)
    for name in ("logits", "cur", "mask1", "mask2", "pick"):
        b[name] = a.take(TILES, E2)
    b["best"], b["top"] = a.take(TILES), a.take(TILES)
    b["l"] = a.take(2, TILES)
    b["g"] = a.take(2, TILES)
    b["gates"] = a.take(E2, TILES)
    b["factor"] = a.take(TILES)
    b["w"] = a.take(2, W2_COLS)
    b["enorm"] = a.take(E2, P)
    b["out"] = a.take(2, TILES, P)
    b["silu"] = a.take(2, GROUP)
    b["hid"] = a.take(2, C2, GROUP)
    b["scaled"] = a.take(TILES, P)
    b["acc"] = a.take(TILES, P)
    return b


def swiglu_sync(k, sp, m, n, ln):
    b = swiglu_layout(k)
    sp.wait_ge(k.sem("x_updated"), m + 1)
    ready = k.sem("moe2_loaded")
    sp.dma_start(b["small"], k.ins["l2_small"]).then_inc(ready, 16)
    sp.dma_start(b["rank"], k.ins["rank"].partition_broadcast(P)).then_inc(ready, 16)
    sp.dma_start(b["e_bias"], k.ins["l2_e_bias"].partition_broadcast(P)).then_inc(ready, 16)

    sp.dma_start(b["enorm"], k.ins["l2_enorm"].rearrange("e c -> (e c)").partition_broadcast(P)).then_inc(ready, 16)

    def load(s, e):
        sp.dma_start(b["w"][:, s, :], k.ins["l2_w"][bass.ds(e, 1), :, :].rearrange("a p c -> (a p) c"))\
            .then_inc(k.sem(f"moe2_w{s}"), 16)

    load(0, 0)
    load(1, 1)
    with sp.Fori(0, E2 // 2 - 1) as i:
        for s in range(2):
            sp.wait_ge(k.sem("moe2_down"), n * E2 * GROUPS + i * (2 * GROUPS) + (s + 1) * GROUPS)
            load(s, i * 2 + (s + 2))


def swiglu_pairs(eng, body):
    body(0, 0, True)
    body(1, 1, False)
    with eng.Fori(1, E2 // 2) as i:
        for s in range(2):
            body(i * 2 + s, s, False)


def project_back_pe(k, pe, src, w, signal):
    for g in range(GROUPS):
        for j in range(TPG):
            t = g * TPG + j
            o = pe.matmul(k.ps[:, 4 + g, j * P:(j + 1) * P], src[:, t * P:(t + 1) * P], w, start=True, stop=True)
        o.then_inc(k.sem(signal), 1)


def swiglu_pe(k, pe, m, n, ln):
    b = swiglu_layout(k)
    xt = k.xt_calls[m]
    transpose_pe(k, pe, k.xn, ln)
    pe.wait_ge(k.sem("moe2_loaded"), 64 * (n + 1))
    pe.wait_ge(k.sem("xT_ready"), (xt + 1) * GROUPS)
    project_back_pe(k, pe, k.xT, b["w_in"], "h_projected")
    transpose_pe(k, pe, b["h"], ln + 1)
    pe.wait_ge(k.sem("xT_ready"), (xt + 2) * GROUPS)
    for t in range(TILES):
        o = pe.matmul(k.ps[:, 4, t * E2:(t + 1) * E2], b["hT"][:, t * P:(t + 1) * P], b["router"],
                      start=True, stop=True)
    o.then_inc(k.sem("gate_logits"), 1)
    pe.wait_ge(k.sem("logits_copied"), n + 1)

    def body(e, s, first):
        ee = e + n * E2
        w = b["w"][:, s, :]
        if isinstance(e, int):
            pe.wait_ge(k.sem(f"moe2_w{s}"), 8 * E2 * n + 16)
        else:
            pe.wait_ge(k.sem(f"moe2_w{s}"), (e - s) * 8 + (8 * E2 * n + 16))

        def up(g):
            for c in range(C2):
                step = g * C2 + c
                if step >= 2:
                    pe.wait_ge(k.sem("moe2_hidden"), ee * STEPS2 + (step - 1))
                for half in range(2):
                    o = pe.matmul(k.ps[:, 4 + 2 * (step % 2) + half, :],
                                  w[:, half * F2 + c * P:half * F2 + (c + 1) * P],
                                  b["hT"][:, g * GROUP:(g + 1) * GROUP], start=True, stop=True)
                o.then_inc(k.sem("moe2_up"), 1)

        def down(g):
            pe.wait_ge(k.sem("moe2_hidden"), ee * STEPS2 + C2 * (g + 1))
            if not first:
                pe.wait_ge(k.sem("moe2_out"), ee * GROUPS + (g + 1 - GROUPS))
            for j in range(TPG):
                for c in range(C2):
                    o = pe.matmul(k.ps[:, g, j * P:(j + 1) * P], b["hid"][:, g % 2, c, j * P:(j + 1) * P],
                                  w[:, 2 * F2 + c * P:2 * F2 + (c + 1) * P], start=(c == 0), stop=(c == C2 - 1))
            o.then_inc(k.sem("moe2_down"), 1)

        up(0)
        up(1)
        down(0)
        up(2)
        down(1)
        up(3)
        down(2)
        down(3)

    swiglu_pairs(pe, body)
    transpose_pe(k, pe, b["acc"], ln + 2)
    pe.wait_ge(k.sem("xT_ready"), (xt + 3) * GROUPS)
    project_back_pe(k, pe, b["hT"], b["w_out"], "out_projected")


def swiglu_act(k, a, m, n, ln):
    b = swiglu_layout(k)
    xt = k.xt_calls[m]
    norm_act(k, a, ln)
    transpose_act(k, a, xt, k.xT)
    norm_act(k, a, ln + 1)
    a.wait_ge(k.sem("moe2_loaded"), 64 * (n + 1))
    transpose_act(k, a, xt + 1, b["hT"], b["gains"][:, 0:1], 0.0)
    a.wait_ge(k.sem("pair_shifted"), n + 1)
    a.activation(b["g"], b["l"], ACT.Exp).then_inc(k.sem("pair_exp"), 1)

    def root(ee):
        a.wait_ge(k.sem("moe2_mean"), ee)
        a.activation(b["factor"], k.ln_a[:, :], ACT.Sqrt).then_inc(k.sem("moe2_root"), 1)

    def body(e, s, first):
        ee = e + n * E2

        def keep(g):
            a.wait_ge(k.sem("moe2_down"), ee * GROUPS + (g + 1))
            a.activation(b["out"][:, s, g * TPG:(g + 1) * TPG, :], k.ps[:, g, :].rearrange("p (a b) -> p a b", a=TPG),
                         ACT.Copy).then_inc(k.sem("moe2_out"), 1)

        for step in range(STEPS2):
            if step in (2 * C2, 3 * C2):
                keep(step // C2 - 2)
            if step == NORM_ROOT and not first:
                root(ee)
            a.wait_ge(k.sem("moe2_up"), ee * STEPS2 + (step + 1))
            if step >= 2:
                a.wait_ge(k.sem("moe2_hidden"), ee * STEPS2 + (step - 1))
            a.activation(b["silu"][:, step % 2, :], k.ps[:, 4 + 2 * (step % 2), :], ACT.Silu)\
                .then_inc(k.sem("moe2_silu"), 1)
        keep(2)
        keep(3)

    swiglu_pairs(a, body)
    root((n + 1) * E2)
    norm_act(k, a, ln + 2)
    transpose_act(k, a, xt + 2, b["hT"], b["gains"][:, 1:2], 0.0)


def swiglu_dve(k, v, m, n, ln):
    b = swiglu_layout(k)
    norm_dve(k, v, ln, k.x[:, :, :], k.xn[:, :, :])
    for g in range(GROUPS):
        v.wait_ge(k.sem("h_projected"), n * GROUPS + g + 1)
        v.tensor_copy(b["h"][:, g * TPG:(g + 1) * TPG, :], k.ps[:, 4 + g, :].rearrange("p (a b) -> p a b", a=TPG))
    norm_dve(k, v, ln + 1, b["h"], b["h"], F32_EPS, center=False)
    v.memset(b["acc"], 0.0)
    v.wait_ge(k.sem("moe2_loaded"), 64 * (n + 1))
    v.wait_ge(k.sem("gate_logits"), k.gate_calls[m] + 1)
    v.tensor_copy(b["logits"], k.ps[:, 4, 0:TILES * E2].rearrange("p (t e) -> p t e", t=TILES))\
        .then_inc(k.sem("logits_copied"), 1)
    v.drain()
    v.tensor_tensor(b["cur"], b["logits"], b["e_bias"].unsqueeze(1).broadcast_to([P, TILES, E2]), ALU.add)
    first_of_largest(k, v, b["cur"], b["best"], b["mask1"], b["rank"], b["top"])
    v.scalar_tensor_tensor(b["cur"], b["mask1"], NEG, b["cur"], ALU.mult, ALU.add)
    first_of_largest(k, v, b["cur"], b["best"], b["mask2"], b["rank"], b["top"])
    for r, mask in enumerate(("mask1", "mask2")):
        v.tensor_tensor(b["pick"], b["logits"], b[mask], ALU.mult)
        v.drain()
        v.tensor_reduce(b["l"][:, r, :], b["pick"], X_AXIS, ALU.add)
        v.drain()
    v.tensor_tensor(b["best"], b["l"][:, 0, :], b["l"][:, 1, :], ALU.max)
    v.drain()
    v.tensor_tensor(b["l"], b["l"], b["best"].unsqueeze(1).broadcast_to([P, 2, TILES]), ALU.subtract)\
        .then_inc(k.sem("pair_shifted"), 1)
    v.wait_ge(k.sem("pair_exp"), n + 1)
    v.tensor_tensor(b["best"], b["g"][:, 0, :], b["g"][:, 1, :], ALU.add)
    v.drain()
    v.reciprocal(b["best"], b["best"])
    v.drain()
    v.tensor_tensor(b["g"], b["g"], b["best"].unsqueeze(1).broadcast_to([P, 2, TILES]), ALU.mult)
    v.drain()
    v.tensor_tensor(b["mask1"], b["mask1"], bc(b["g"][:, 0, :], E2), ALU.mult)
    v.tensor_tensor(b["mask2"], b["mask2"], bc(b["g"][:, 1, :], E2), ALU.mult)
    v.drain()
    v.tensor_tensor(b["gates"].rearrange("p e t -> p t e"), b["mask1"], b["mask2"], ALU.add)
    v.drain()

    def output_norm(step, ee, e, s):
        out = b["out"][:, 1 - s, :, :]
        if step < GROUPS:
            v.wait_ge(k.sem("moe2_out"), ee * GROUPS + (step + 1 - GROUPS))
            for t in range(step * TPG, (step + 1) * TPG):
                v.bn_stats(k.stats[:, t, :], out[:, t, :])
        elif step == GROUPS:
            v.drain()
            for t in range(TILES):
                v.bn_aggr(k.moments[:, t, :], k.stats[:, t, :])
        elif step == GROUPS + 1:
            mean_square(k, v)
            v.tensor_scalar(k.ln_a[:, :], k.moments[:, :, 1], F32_EPS, None, ALU.add).then_inc(k.sem("moe2_mean"), 1)
        elif step == NORM_ROOT + 1:
            v.wait_ge(k.sem("moe2_root"), ee)
            v.reciprocal(b["factor"], b["factor"])
            v.drain()
            v.tensor_tensor(b["factor"], b["factor"], b["gates"][:, bass.ds(e - 1, 1), :].rearrange("p a t -> p (a t)"),
                            ALU.mult)
        elif step > NORM_ROOT + 1:
            piece = step - NORM_ROOT - 2
            v.drain()
            if piece < GROUPS:
                group = slice(piece * TPG, (piece + 1) * TPG)
                v.tensor_tensor(b["scaled"][:, group, :], out[:, group, :], bc(b["factor"][:, group], P), ALU.mult)
            if piece % 2 and piece < 5:
                half = slice((piece - 1) * TPG, (piece + 1) * TPG)
                v.drain()
                v.tensor_tensor(b["scaled"][:, half, :], b["scaled"][:, half, :],
                                b["enorm"][:, bass.ds(e - 1, 1), :].broadcast_to([P, 2 * TPG, P]), ALU.mult)
            if piece in (4, 5):
                half = slice((piece - 4) * 2 * TPG, (piece - 3) * 2 * TPG)
                v.tensor_tensor(b["acc"][:, half, :], b["acc"][:, half, :], b["scaled"][:, half, :], ALU.add)

    def body(e, s, first):
        ee = e + n * E2
        for g in range(GROUPS):
            if g >= 2:
                v.wait_ge(k.sem("moe2_down"), ee * GROUPS + (g - 1))
            elif not first:
                v.wait_ge(k.sem("moe2_down"), ee * GROUPS + g - 1)
            for c in range(C2):
                step = g * C2 + c
                v.wait_ge(k.sem("moe2_silu"), ee * STEPS2 + (step + 1))
                v.tensor_tensor(b["hid"][:, g % 2, c, :], b["silu"][:, step % 2, :], k.ps[:, 5 + 2 * (step % 2), :],
                                ALU.mult).then_inc(k.sem("moe2_hidden"), 1)
                if not first:
                    output_norm(step, ee, e, s)

    swiglu_pairs(v, body)
    for step in range(STEPS2):
        output_norm(step, (n + 1) * E2, E2, 0)
    norm_dve(k, v, ln + 2, b["acc"], b["acc"], F32_EPS, center=False)
    for g in range(GROUPS):
        v.wait_ge(k.sem("out_projected"), n * GROUPS + g + 1)
        xg = k.x[:, g * TPG:(g + 1) * TPG, :].rearrange("p a b -> p (a b)")
        o = v.scalar_tensor_tensor(xg, k.ps[:, 4 + g, :], 0.5, xg, ALU.mult, ALU.add)
    o.then_inc(k.sem("x_updated"), 1)


def lay_out_swiglu(a, i):
    import numpy as _np

    c, f = _np.ascontiguousarray, _np.float32
    a["l2_small"] = c(_np.concatenate([
        i["L2_ffn_W_in"].T, i["L2_ffn_W_out"].T, i["L2_ffn_Wr"].T, _np.zeros((P, 32), f),
        i["L2_ffn_in_norm_w"][:, None], i["L2_ffn_out_norm_w"][:, None]], axis=1))
    a["l2_e_bias"], a["l2_enorm"] = i["L2_ffn_expert_bias"], i["L2_ffn_enorm_w"]
    down = i["L2_ffn_Wd"].transpose(0, 2, 1).reshape(E2, C2, P, DIM).transpose(0, 2, 1, 3).reshape(E2, P, C2 * DIM)
    a["l2_w"] = c(_np.concatenate([i["L2_ffn_Wg"].transpose(0, 2, 1), i["L2_ffn_Wu"].transpose(0, 2, 1), down], axis=2))



E3, I3, TOP3, CAPACITY = 32, 64, 4, 128
UNITS = E3 // 2 + 1


def small_layout(k):
    a = k.arena
    a.reset()
    b = {}
    b["yT"] = a.take(TOKENS)
    b["gate_w"] = a.take(E3)
    b["before"], b["ones"] = a.take(P), a.take(P)
    b["rank"] = a.take(E3)
    for name in ("logits", "cur", "mask", "chosen", "probs"):
        b[name] = a.take(TILES, E3)
    b["gates"] = a.take(E3, TILES)
    b["best"], b["top"], b["sum"] = a.take(TILES), a.take(TILES), a.take(TILES)
    b["rows"] = a.take(4 * P)
    b["shared"] = a.take(3 * P)
    b["w"] = a.take(2, 3 * P)
    b["gb"] = a.take(2, TOKENS)
    b["silu"] = a.take(2, GROUP)
    b["prod"] = a.take(2, GROUP)
    b["hid"] = a.take(2, GROUP)
    return b


def small_sync(k, sp, m, n, ln):
    b = small_layout(k)
    sp.wait_ge(k.sem("x_updated"), m + 1)
    ready = k.sem("moe3_loaded")
    sp.dma_start(b["gate_w"], k.ins["l3_gate_w"]).then_inc(ready, 16)
    sp.dma_start(b["before"], k.ins["before"]).then_inc(ready, 16)
    sp.dma_start(b["rank"], k.ins["rank"].partition_broadcast(P)).then_inc(ready, 16)
    sp.dma_start(b["shared"], k.ins["l3_w"][0, :, :]).then_inc(ready, 16)
    sp.wait_ge(k.sem("gates_stored"), 16 * (k.gate_stores[m] + 1))

    def load(s, pair):
        sp.dma_start(b["w"][:, s, :], k.ins["l3_w"][bass.ds(pair + 1, 1), :, :].rearrange("a p c -> (a p) c"))\
            .then_inc(k.sem(f"moe3_w{s}"), 16)
        for h in range(2):
            row = k.gates_dram[bass.ds(pair * (2 * TILES) + h * TILES, TILES), :].rearrange("t p -> (t p)")
            sp.dma_start(b["gb"][h * I3:(h + 1) * I3, s, :], row.partition_broadcast(I3))\
                .then_inc(k.sem(f"moe3_gates{s}"), 16)

    load(0, 0)
    load(1, 1)
    with sp.Fori(0, E3 // 4 - 1) as i:
        for s in range(2):
            sp.wait_ge(k.sem("moe3_down"), (n * UNITS + 1) * GROUPS + i * (2 * GROUPS) + (s + 1) * GROUPS)
            load(s, i * 2 + (s + 2))


def small_units(eng, body):
    body(0, 1, -1, False)
    with eng.Fori(0, E3 // 4 - 1) as i:
        body(i * 2 + 1, 2, i, False)
    body(E3 // 2 - 1, 2, E3 // 4 - 1, True)


def small_pe(k, pe, m, n, ln):
    b = small_layout(k)
    xt = k.xt_calls[m]
    transpose_pe(k, pe, k.xn, ln)
    pe.wait_ge(k.sem("moe3_loaded"), 64 * (n + 1))
    gate_logits_pe(k, pe, xt, b["gate_w"], E3)
    pe.wait_ge(k.sem("chosen_ready"), n + 1)
    pe.matmul(k.ps[:, 5, :], b["before"], b["chosen"].rearrange("p t e -> p (t e)"), start=True, stop=False)
    for t in range(TILES - 1):
        rest = TILES - 1 - t
        o = pe.matmul(k.ps[:, 5, (t + 1) * E3:], b["ones"],
                      b["chosen"][:, t, :].unsqueeze(1).broadcast_to([P, rest, E3]),
                      start=False, stop=(rest == 1))
    o.then_inc(k.sem("places_ready"), 1)
    gates_out_pe(k, pe, k.gate_stores[m], b["gates"], 4)

    def body(unit, units, i, last):
        at = (n * UNITS + unit) * GROUPS

        def weights(step):
            if units == 1:
                return b["shared"] if step < GROUPS else b["w"][:, 0, :]
            return b["w"][:, step // GROUPS % 2, :]

        def up(step):
            over, own = divmod(step, units * GROUPS)
            if (units == 2 or over) and own % GROUPS == 0:
                pe.wait_ge(k.sem(f"moe3_w{own // GROUPS}"), 16 * (E3 // 4) * n + (16 * (i + over) + 16))
            if step >= 2:
                pe.wait_ge(k.sem("moe3_multiplied"), at + (step - 1))
            g = step % GROUPS
            for half in range(2):
                o = pe.matmul(k.ps[:, 4 + 2 * (step % 2) + half, :], weights(step)[:, half * P:(half + 1) * P],
                              k.xT[:, g * GROUP:(g + 1) * GROUP], start=True, stop=True)
            o.then_inc(k.sem("moe3_up"), 1)

        if units == 1:
            up(0)
            up(1)
        for step in range(units * GROUPS):
            if step + 2 < units * GROUPS or not last:
                up(step + 2)
            pe.wait_ge(k.sem("moe3_hidden"), at + (step + 1))
            pe.matmul(k.ps[:, step % GROUPS, :], weights(step)[:, 2 * P:3 * P], b["hid"][:, step % 2, :],
                      start=(units == 1), stop=True, skip_group_check=(units == 2)).then_inc(k.sem("moe3_down"), 1)

    pe.wait_ge(k.sem("gate_rows"), k.gate_stores[m] + 1)
    small_units(pe, body)
    add_back_pe(k, pe, k.back_calls[m], b["yT"])


def small_act(k, a, m, n, ln):
    b = small_layout(k)
    norm_act(k, a, ln)
    transpose_act(k, a, k.xt_calls[m], k.xT)
    a.wait_ge(k.sem("moe3_shifted"), n + 1)
    a.activation(b["probs"], b["probs"], ACT.Exp).then_inc(k.sem("moe3_exp"), 1)
    gates_out_act(k, a, k.gate_stores[m], b["rows"], 4)

    def body(unit, units, i, last):
        at = (n * UNITS + unit) * GROUPS
        for step in range(units * GROUPS):
            a.wait_ge(k.sem("moe3_up"), at + (step + 1))
            if step >= 2 or units == 2:
                a.wait_ge(k.sem("moe3_multiplied"), at + (step - 1))
            a.activation(b["silu"][:, step % 2, :], k.ps[:, 4 + 2 * (step % 2), :], ACT.Silu)\
                .then_inc(k.sem("moe3_silu"), 1)

    use_table(k, a, ACT.Silu)
    small_units(a, body)
    a.wait_ge(k.sem("moe3_down"), (n + 1) * UNITS * GROUPS)
    add_back_act(k, a, k.back_calls[m], b["yT"], 0.5)


def small_dve(k, v, m, n, ln):
    b = small_layout(k)
    norm_dve(k, v, ln, k.x[:, :, :], k.xn[:, :, :])
    v.memset(b["ones"], 1.0)
    v.memset(b["chosen"], 0.0)
    v.wait_ge(k.sem("gate_logits"), k.gate_calls[m] + 1)
    v.wait_ge(k.sem("moe3_loaded"), 64 * (n + 1))
    v.tensor_copy(b["logits"], k.ps[:, 4, :].rearrange("p (t e) -> p t e", t=TILES))
    v.drain()
    v.tensor_copy(b["cur"], b["logits"])
    for r in range(TOP3):
        first_of_largest(k, v, b["cur"], b["best"], b["mask"], b["rank"], b["top"])
        if r == 0:
            v.tensor_tensor(b["probs"], b["logits"], bc(b["best"], E3), ALU.subtract)\
                .then_inc(k.sem("moe3_shifted"), 1)
        v.tensor_tensor(b["chosen"], b["chosen"], b["mask"], ALU.add)
        if r < TOP3 - 1:
            v.scalar_tensor_tensor(b["cur"], b["mask"], NEG, b["cur"], ALU.mult, ALU.add)
    v.drain()
    v.tensor_copy(b["top"], b["best"]).then_inc(k.sem("chosen_ready"), 1)
    v.wait_ge(k.sem("moe3_exp"), n + 1)
    v.tensor_reduce(b["sum"], b["probs"], X_AXIS, ALU.add)
    v.drain()
    v.reciprocal(b["sum"], b["sum"])
    v.drain()
    v.tensor_tensor(b["probs"], b["probs"], bc(b["sum"], E3), ALU.mult)
    v.drain()
    v.tensor_tensor(b["probs"], b["probs"], b["chosen"], ALU.mult)
    v.drain()
    v.tensor_reduce(b["sum"], b["probs"], X_AXIS, ALU.add)
    v.drain()
    v.reciprocal(b["sum"], b["sum"])
    v.drain()
    v.tensor_tensor(b["probs"], b["probs"], bc(b["sum"], E3), ALU.mult)
    v.wait_ge(k.sem("places_ready"), n + 1)
    v.tensor_scalar(b["mask"], k.ps[:, 5, :].rearrange("p (t e) -> p t e", t=TILES), float(CAPACITY), None, ALU.is_lt)
    v.drain()
    v.tensor_tensor(b["gates"].rearrange("p e t -> p t e"), b["probs"], b["mask"], ALU.mult)\
        .then_inc(k.sem("gates_ready"), 1)

    def body(unit, units, i, last):
        at = (n * UNITS + unit) * GROUPS
        for step in range(units * GROUPS):
            s, g = divmod(step, GROUPS)
            if units == 2 and g == 0:
                v.wait_ge(k.sem(f"moe3_gates{s}"), 32 * (E3 // 4) * n + 32 * i + 32)
            if step >= 2 or units == 2:
                v.wait_ge(k.sem("moe3_down"), at + (step - 1))
            v.wait_ge(k.sem("moe3_silu"), at + (step + 1))
            to = b["hid"] if units == 1 else b["prod"]
            o = v.tensor_tensor(to[:, step % 2, :], b["silu"][:, step % 2, :], k.ps[:, 5 + 2 * (step % 2), :], ALU.mult)
            o.then_inc(k.sem("moe3_multiplied"), 1)
            v.drain()
            if units == 1:
                v.sem_inc(k.sem("moe3_hidden"), 1)
            else:
                v.tensor_tensor(b["hid"][:, step % 2, :], b["prod"][:, step % 2, :],
                                b["gb"][:, s, g * GROUP:(g + 1) * GROUP], ALU.mult).then_inc(k.sem("moe3_hidden"), 1)

    small_units(v, body)
    add_back_dve(k, v, k.back_calls[m])


def lay_out_small(a, i):
    import numpy as _np

    c, f = _np.ascontiguousarray, _np.float32
    feature = _np.arange(P)
    a["before"] = (feature[:, None] < feature[None, :]).astype(f)
    a["l3_gate_w"] = c(i["L3_ffn_gate_w"].T)
    none = _np.zeros((P, I3), f)
    up = i["L3_ffn_w_gate_up"].reshape(E3 // 2, 2, DIM, 2, I3).transpose(0, 2, 3, 1, 4).reshape(E3 // 2, DIM, 4 * I3)
    down = i["L3_ffn_w_down"].reshape(E3 // 2, 2 * I3, DIM)
    gu = i["L3_ffn_shared_w_gate_up"]
    shared_up = _np.concatenate([gu[:, :I3], none, gu[:, I3:], none], axis=1)
    shared_down = _np.concatenate([i["L3_ffn_shared_w_down"], none.T], axis=0)
    a["l3_w"] = c(_np.concatenate([_np.concatenate([shared_up, shared_down], axis=1)[None],
                                   _np.concatenate([up, down], axis=2)], axis=0))



N2, RSTEP, QSTEPS = 32, 32, SEQ // 32
H4 = 2 * N2
CH4 = P // 2
CHUNK4 = 16
TWO_PI = 2.0 * math.pi
PI1 = 6.28125
PI2 = float(np.float32(np.round((TWO_PI - PI1) * 2 ** 20) / 2 ** 20))
PI3 = TWO_PI - PI1 - PI2
LN2_1 = 0.693359375
LN2_2 = math.log(2.0) - LN2_1
ROUNDER = 12582912.0
EXP_TERMS = 8


def s4d_layout(k):
    a = k.arena
    a.reset()
    b = {}
    b["par"] = a.take(5, CH4)
    b["steps"] = a.take(RSTEP + QSTEPS)
    b["turns"], b["rads"] = a.take(3), a.take(3)
    b["ex"], b["ek"], b["er"] = a.take(2, CH4), a.take(2, CH4), a.take(2, CH4)
    for name in ("zr", "zi", "ar", "den", "nr", "ni", "cr", "ci", "t1", "t2", "mag1"):
        b[name] = a.take(CH4)
    b["unit"] = a.take(2, CH4)
    for name in ("ph", "turn", "magr", "tr"):
        b[name] = a.take(CH4, RSTEP)
    for name in ("phq", "magq", "q1", "q2"):
        b[name] = a.take(CH4, QSTEPS)
    b["sr"], b["sq"] = a.take(CHUNK4 * RSTEP), a.take(CHUNK4 * QSTEPS)
    b["k32"] = a.take(QSTEPS, P)[0:RSTEP]
    b["fwd"] = a.take(4, 2 * SEQ)
    b["kt"] = a.take(4, P)
    b["kf"] = a.take(8, P)
    b["w"] = a.take(P)
    b["bias"] = a.take(P)
    b["p1"], b["p2"] = a.take(SEQ), a.take(SEQ)
    b["xf"] = a.take(4, 2, SEQ)
    b["y"] = a.take(8, SEQ)
    b["back"] = a.take(8, SEQ)
    b["yg"] = a.take(TILES, P)
    b["yT"] = a.take(TOKENS)
    return b


def s4d_sync(k, sp, m, n, ln):
    b = s4d_layout(k)
    sp.wait_ge(k.sem("x_updated"), m + 1)
    par = k.sem("s4_parameters")
    for half in range(2):
        sp.dma_start(b["par"][half * H4:(half + 1) * H4, 0, :],
                     k.ins["s4_log_dt"][half * CH4:(half + 1) * CH4].partition_broadcast(H4)).then_inc(par, 16)
    sp.dma_start(b["par"][:, 1:5, :], k.ins["s4_par"]).then_inc(par, 16)
    sp.dma_start(b["steps"], k.ins["s4_steps"].partition_broadcast(P)).then_inc(par, 16)
    sp.dma_start(b["turns"], k.ins["s4_shifts"][:, 0:3]).then_inc(par, 16)
    sp.dma_start(b["rads"], k.ins["s4_shifts"][:, 3:6]).then_inc(par, 16)
    sp.dma_start(b["fwd"], k.ins["dft_forward"]).then_inc(k.sem("s4_forward"), 16)
    sp.dma_start(b["w"], k.ins["s4_w"]).then_inc(k.sem("s4_weights"), 16)
    sp.dma_start(b["bias"], k.ins["s4_bias"].partition_broadcast(P)).then_inc(k.sem("s4_weights"), 16)
    sp.dma_start(b["back"], k.ins["dft_back"]).then_inc(k.sem("s4_back"), 16)
    sp.wait_ge(k.sem("s4_kernel"), LEAD + CH4 // CHUNK4)
    src = b["k32"].rearrange("r (q a) d -> r q a d", a=4)
    for a_ in range(4):
        sp.dma_start(b["kt"][32 * a_:32 * a_ + 32, :, :], src[:, :, a_, :]).then_inc(k.sem("s4_kernel_moved"), 16)


def s4d_pe(k, pe, m, n, ln):
    b = s4d_layout(k)
    pe.wait_ge(k.sem("s4_forward"), 16)
    pe.wait_ge(k.sem("ln_done"), (ln + 1) * GROUPS)
    xv = k.xn[:, :, :].rearrange("p (b t) d -> p b t d", t=4)
    for f in range(4):
        if f >= 2:
            pe.wait_ge(k.sem("s4_spectrum_kept"), f - 1)
        for half in range(2):
            for t in range(4):
                o = pe.matmul(k.ps[:, 2 * (f % 2) + half, :],
                              b["fwd"][:, t, half * SEQ + f * P:half * SEQ + (f + 1) * P], xv[:, :, t, :],
                              start=(t == 0), stop=(t == 3))
        o.then_inc(k.sem("s4_spectrum"), 1)
    with pe.Fori(0, CH4 // CHUNK4) as i:
        pe.wait_ge(k.sem("s4_staged"), i + 1)
        hold(k, pe, "s4_kernel", LEAD + i)
        for half in range(2):
            rows = slice(half * H4, (half + 1) * H4)
            for d in range(CHUNK4):
                o = pe.matmul(k.ps[0:RSTEP, 6 + half, d * QSTEPS:(d + 1) * QSTEPS],
                              b["sr"][rows, d * RSTEP:(d + 1) * RSTEP], b["sq"][rows, d * QSTEPS:(d + 1) * QSTEPS],
                              start=True, stop=True)
        o.then_inc(k.sem("s4_products"), 1)
    pe.wait_ge(k.sem("s4_kernel_moved"), 64)
    for half in range(2):
        for f in range(4):
            for t in range(4):
                o = pe.matmul(k.ps[:, 4 + half, f * P:(f + 1) * P],
                              b["fwd"][:, t, half * SEQ + f * P:half * SEQ + (f + 1) * P], b["kt"][:, t, :],
                              start=(t == 0), stop=(t == 3))
    o.then_inc(k.sem("s4_kernel_spectrum"), 1)
    pe.wait_ge(k.sem("s4_back"), 16)
    for f in range(4):
        pe.wait_ge(k.sem("s4_multiplied"), f + 1)
        for half in range(2):
            for t in range(4):
                o = pe.matmul(k.ps[:, 4 + t, :], b["back"][:, 4 * half + f, t * P:(t + 1) * P],
                              b["y"][:, 4 * half + f, :], start=(f + half == 0), stop=(f + half == 4))
                if f + half == 4:
                    o.then_inc(k.sem("s4_convolved"), 1)
    pe.wait_ge(k.sem("s4_gelu"), 4)
    transpose_pe(k, pe, b["yg"])
    pe.wait_ge(k.sem("xT_ready"), (k.xt_calls[m] + 1) * GROUPS)
    pe.wait_ge(k.sem("s4_weights"), 32)
    project_back_pe(k, pe, b["yT"], b["w"], "s4_projected")


def s4d_act(k, a, m, n, ln):
    b = s4d_layout(k)
    norm_act(k, a, ln)
    for f in range(4):
        a.wait_ge(k.sem("s4_spectrum"), f + 1)
        a.activation(b["xf"][:, f, :, :], k.ps[:, 2 * (f % 2):2 * (f % 2) + 2, :], ACT.Copy)\
            .then_inc(k.sem("s4_spectrum_kept"), 1)
    a.wait_ge(k.sem("s4_exponents"), 1)
    a.activation(b["mag1"], b["zr"], ACT.Exp).then_inc(k.sem("s4_magnitudes"), 1)
    a.activation(b["magr"], b["magr"], ACT.Exp).then_inc(k.sem("s4_magnitudes"), 1)
    a.activation(b["magq"], b["magq"], ACT.Exp).then_inc(k.sem("s4_magnitudes"), 1)
    for j, what in enumerate((b["unit"], b["q1"], b["q2"], b["tr"])):
        a.wait_ge(k.sem("s4_angles"), j + 1)
        a.activation(what, what, ACT.Sin).then_inc(k.sem("s4_sines"), 1)
    a.wait_ge(k.sem("s4_kernel_spectrum"), 1)
    a.activation(b["kf"].rearrange("p (h f) d -> p h (f d)", h=2), k.ps[:, 4:6, :], ACT.Copy)\
        .then_inc(k.sem("s4_kernel_copied"), 1)
    yg = b["yg"].rearrange("p (b t) d -> p b t d", t=4)
    for t in range(4):
        a.wait_ge(k.sem("s4_convolved"), t + 1)
        a.activation(yg[:, :, t, :], k.ps[:, 4 + t, :].rearrange("p (b d) -> p b d", b=BATCH), ACT.Gelu)\
            .then_inc(k.sem("s4_gelu"), 1)
    transpose_act(k, a, k.xt_calls[m], b["yT"])


def s4d_dve(k, v, m, n, ln):
    b = s4d_layout(k)
    norm_dve(k, v, ln, k.x[:, :, :], k.xn[:, :, :])
    v.wait_ge(k.sem("s4_parameters"), 96)
    T = ALU

    def tt(out, x, y, op):
        v.drain()
        return v.tensor_tensor(out, x, y, op)

    def ts(out, x, s1, s2, op0, op1):
        v.drain()
        return v.tensor_scalar(out, x, s1, s2, op0, op1)

    y, j, r = b["par"][:, 0:2, :], b["ek"], b["er"]
    ts(j, y, 1.0 / math.log(2.0), ROUNDER, T.mult, T.add)
    ts(j, j, ROUNDER, None, T.subtract, ALU.bypass)
    v.drain()
    v.scalar_tensor_tensor(r, j, -LN2_1, y, T.mult, T.add)
    v.drain()
    v.scalar_tensor_tensor(r, j, -LN2_2, r, T.mult, T.add)
    ts(b["ex"], r, 1.0 / math.factorial(EXP_TERMS), 1.0 / math.factorial(EXP_TERMS - 1), T.mult, T.add)
    for term in range(EXP_TERMS - 2, -1, -1):
        tt(b["ex"], b["ex"], r, T.mult)
        ts(b["ex"], b["ex"], 1.0 / math.factorial(term), None, T.add, ALU.bypass)
    ts(r.bitcast(mybir.dt.int32), j, 127.0, float(2 ** 23), T.add, T.mult)
    tt(b["ex"], b["ex"], r, T.mult)
    dt, mre = b["ex"][:, 0, :], b["ex"][:, 1, :]
    ai, c_re, c_im = b["par"][:, 2, :], b["par"][:, 3, :], b["par"][:, 4, :]
    ts(b["ar"], mre, -1.0, None, T.mult, ALU.bypass)
    tt(b["zr"], b["ar"], dt, T.mult)
    tt(b["zi"], ai, dt, T.mult)
    fine = b["steps"][:, 0:RSTEP].unsqueeze(1).broadcast_to([P, CH4, RSTEP])
    coarse = b["steps"][:, RSTEP:].unsqueeze(1).broadcast_to([P, CH4, QSTEPS])
    tt(b["magr"], bc(b["zr"], RSTEP), fine, T.mult)
    tt(b["magq"], bc(b["zr"], QSTEPS), coarse, T.mult).then_inc(k.sem("s4_exponents"), 1)
    tt(b["ph"], bc(b["zi"], RSTEP), fine, T.mult)
    tt(b["phq"], bc(b["zi"], QSTEPS), coarse, T.mult)

    def angle(out, phase, turns, turn, rad):
        ts(turns, phase, 1.0 / TWO_PI, turn, T.mult, T.add)
        ts(turns, turns, ROUNDER, ROUNDER, T.add, T.subtract)
        v.drain()
        v.scalar_tensor_tensor(out, turns, -PI1, phase, T.mult, T.add)
        v.drain()
        v.scalar_tensor_tensor(out, turns, -PI2, out, T.mult, T.add)
        v.drain()
        v.scalar_tensor_tensor(out, turns, -PI3, out, T.mult, T.add)
        ts(out, out, rad, None, T.add, ALU.bypass)
        return ts(out, out, 3.1415925, -3.1415925, T.min, T.max)

    scratch = b["turn"].rearrange("p a b -> p (a b)")
    angle(b["unit"][:, 0, :], b["zi"], scratch[:, 0:CH4], 0.25, math.pi / 2)
    angle(b["unit"][:, 1, :], b["zi"], scratch[:, 0:CH4], 0.0, 0.0).then_inc(k.sem("s4_angles"), 1)
    sq = scratch[:, 0:CH4 * QSTEPS].rearrange("p (a b) -> p a b", a=CH4)
    angle(b["q1"], b["phq"], sq, b["turns"][:, 1:2], b["rads"][:, 1:2]).then_inc(k.sem("s4_angles"), 1)
    angle(b["q2"], b["phq"], sq, b["turns"][:, 2:3], b["rads"][:, 2:3]).then_inc(k.sem("s4_angles"), 1)
    angle(b["tr"], b["ph"], b["turn"], b["turns"][:, 0:1], b["rads"][:, 0:1]).then_inc(k.sem("s4_angles"), 1)
    v.wait_ge(k.sem("s4_magnitudes"), 3)
    v.wait_ge(k.sem("s4_sines"), 1)
    tt(b["nr"], b["mag1"], b["unit"][:, 0, :], T.mult)
    ts(b["nr"], b["nr"], -1.0, None, T.add, ALU.bypass)
    tt(b["ni"], b["mag1"], b["unit"][:, 1, :], T.mult)

    def product(out, x1, y1, x2, y2, op):
        tt(b["t1"], x1, y1, T.mult)
        tt(b["t2"], x2, y2, T.mult)
        tt(out, b["t1"], b["t2"], op)

    product(b["cr"], c_re, b["nr"], c_im, b["ni"], T.subtract)
    product(b["ci"], c_re, b["ni"], c_im, b["nr"], T.add)
    product(b["den"], b["ar"], b["ar"], ai, ai, T.add)
    v.drain()
    v.reciprocal(b["den"], b["den"])
    ts(b["den"], b["den"], 2.0, None, T.mult, ALU.bypass)
    product(b["nr"], b["cr"], b["ar"], b["ci"], ai, T.add)
    product(b["ni"], b["ci"], b["ar"], b["cr"], ai, T.subtract)
    tt(b["cr"], b["nr"], b["den"], T.mult)
    tt(b["ci"], b["ni"], b["den"], T.mult)
    v.wait_ge(k.sem("s4_sines"), 3)
    tt(b["q1"], b["q1"], bc(b["cr"], QSTEPS), T.mult)
    tt(b["q2"], b["q2"], bc(b["ci"], QSTEPS), T.mult)
    tt(b["q1"], b["q1"], b["q2"], T.add)
    tt(b["q1"], b["q1"], b["magq"], T.mult)
    v.wait_ge(k.sem("s4_sines"), 4)
    tt(b["tr"], b["tr"], b["magr"], T.mult)
    v.drain()
    fr, fq = b["tr"].rearrange("p a b -> p (a b)"), b["q1"].rearrange("p a b -> p (a b)")
    with v.Fori(0, CH4 // CHUNK4) as i:
        v.tensor_copy(b["sr"], fr[:, bass.ts(i, CHUNK4 * RSTEP)])
        v.tensor_copy(b["sq"], fq[:, bass.ts(i, CHUNK4 * QSTEPS)])
        v.drain()
        v.sem_inc(k.sem("s4_staged"), 1)
        v.wait_ge(k.sem("s4_products"), i + 1)
        for half in range(2):
            o = v.tensor_copy(b["k32"][:, :, bass.ds(i * CHUNK4 + half * CH4, CHUNK4)].rearrange("r q d -> r d q"),
                              k.ps[0:RSTEP, 6 + half, 0:CHUNK4 * QSTEPS].rearrange("r (d q) -> r d q", d=CHUNK4))
        o.then_inc(k.sem("s4_kernel"), 1)
    v.wait_ge(k.sem("s4_spectrum_kept"), 4)
    v.wait_ge(k.sem("s4_kernel_copied"), 1)
    kf = b["kf"]
    p1, p2 = (b[p].rearrange("p (b d) -> p b d", b=BATCH) for p in ("p1", "p2"))
    for f in range(4):
        xr, xi = (b["xf"][:, f, h, :].rearrange("p (b d) -> p b d", b=BATCH) for h in range(2))
        kr, ki = (kf[:, 4 * h + f, :].unsqueeze(1).broadcast_to([P, BATCH, P]) for h in range(2))
        yr, yi = (b["y"][:, 4 * h + f, :].rearrange("p (b d) -> p b d", b=BATCH) for h in range(2))
        v.drain()
        v.tensor_tensor(p1, xr, kr, T.mult)
        v.tensor_tensor(p2, xi, ki, T.mult)
        v.drain()
        v.tensor_tensor(yr, p1, p2, T.subtract)
        v.drain()
        v.tensor_tensor(p1, xr, ki, T.mult)
        v.tensor_tensor(p2, xi, kr, T.mult)
        v.drain()
        v.tensor_tensor(yi, p1, p2, T.add).then_inc(k.sem("s4_multiplied"), 1)
    v.wait_ge(k.sem("s4_weights"), 32)
    v.tensor_tensor(k.x[:, :, :], k.x[:, :, :], b["bias"].unsqueeze(1).broadcast_to([P, TILES, P]), T.add)
    v.drain()
    for g in range(GROUPS):
        v.wait_ge(k.sem("s4_projected"), g + 1)
        xg = k.x[:, g * TPG:(g + 1) * TPG, :]
        o = v.tensor_tensor(xg, k.ps[:, 4 + g, :].rearrange("p (a b) -> p a b", a=TPG), xg, T.add)
    o.then_inc(k.sem("x_updated"), 1)


def lay_out_s4d(a, i):
    import numpy as _np

    c, f = _np.ascontiguousarray, _np.float32
    a["s4_log_dt"] = i["L2_attn_log_dt"]
    par = _np.stack([i["L2_attn_" + name].T for name in ("log_A_real", "A_imag", "C_real", "C_imag")], axis=1)
    halves = [par[:, :, :CH4], par[:, :, CH4:]]
    a["s4_par"] = c(_np.concatenate([halves[0], halves[0], halves[1], halves[1]], axis=0))
    a["s4_steps"] = _np.concatenate([_np.arange(RSTEP), RSTEP * _np.arange(QSTEPS)]).astype(f)
    turns = _np.repeat(_np.array([[0.25, 0.25, 0.5], [0.0, 0.5, 0.75]]), N2, axis=0)
    a["s4_shifts"] = c(_np.tile(_np.concatenate([turns, turns * TWO_PI], axis=1), (2, 1)).astype(f))
    steps, freq = _np.arange(SEQ), _np.arange(SEQ)
    angle = ((2 * freq[None, :] + 1) * steps[:, None] % (4 * SEQ)) * (TWO_PI / (4 * SEQ))
    both = _np.concatenate([_np.cos(angle), -_np.sin(angle)], axis=1)
    a["dft_forward"] = c(both.reshape(4, P, 2 * SEQ).transpose(1, 0, 2).astype(f))
    a["dft_back"] = c((both.T / SEQ).reshape(8, P, SEQ).transpose(1, 0, 2).astype(f))
    a["s4_w"], a["s4_bias"] = c(i["L2_attn_W"].T), i["L2_attn_b"]



HEADSL, HDL, WINDOW = 8, 64, 64
INNER = HEADSL * HDL
PAIRS = HEADSL // 2
LAYERS = 2
QK_SCALE = 8.0
HID = int(DIM * 4 * 2 / 3)
CH = -(-HID // P)
SEEN = WINDOW + P
HALVES = 2 * TPG


def local_layout(k):
    a = k.arena
    a.reset()
    b = {}
    b["y"] = a.take(TILES, P)
    b["wqkv"] = a.take(3, INNER)
    b["wo"] = a.take(PAIRS, P)
    b["w1"] = a.take(2, CH, P)
    b["w2"] = a.take(CH, P)
    b["vec"] = a.take(2 + 2 * CH)
    b["scales"] = a.take(2, HDL)
    b["b2"] = a.take(P)
    b["mask"] = a.take(2, 2, SEEN)
    b["half"] = a.take(2)
    b["cos"], b["sin"] = a.take(TPG, 2, HDL), a.take(TPG, 2, HDL)
    b["tc"], b["ts"] = a.take(TPG, 2, HDL), a.take(TPG, 2, HDL)
    b["qT"] = a.take(PAIRS, TOKENS)
    b["kT"] = a.take(PAIRS, P + TOKENS)
    b["v"] = a.take(1 + TILES, INNER)
    b["early"] = a.take(2, PAIRS, P)
    temp = a.at
    b["hs"] = a.take(TPG, P)
    b["qk"] = a.take(TPG, 2 * INNER)
    b["qsq"] = a.take(2, 2 * INNER)
    b["norms"] = a.take(2, 2 * HEADSL)
    b["swp"] = a.take(2, 2 * INNER)
    b["qr"] = a.take(2, 2 * INNER)
    a.reset(temp)
    b["qm"] = a.take(2, HEADSL, P)
    b["s"] = a.take(2, 4, SEEN)
    b["p"] = a.take(2, 4, SEEN)
    b["pT"] = a.take(2, 6, P)
    b["negmax"] = a.take(2, 4)
    b["sum"] = a.take(2, HEADSL)
    b["o"] = a.take(2, INNER)
    b["oT"] = a.take(2, INNER)
    a.reset(temp)
    b["ge"] = a.take(2, GROUP)
    b["hid"] = a.take(2, CH, GROUP)
    return b


def local_sync(k, sp, m, n, ln):
    b = local_layout(k)
    sp.wait_ge(k.sem("x_updated"), m + 1)
    once = k.sem("lf_tables")
    sp.dma_start(b["mask"], k.ins["lf_mask"]).then_inc(once, 16)
    sp.dma_start(b["half"], k.ins["a0_mask"]).then_inc(once, 16)
    sp.dma_start(b["cos"], k.ins["lf_cos"]).then_inc(once, 16)
    sp.dma_start(b["sin"], k.ins["lf_sin"]).then_inc(once, 16)
    low, high = slice(0, DIM // 2), slice(DIM // 2, DIM)
    for layer in range(LAYERS):
        ll = n * LAYERS + layer
        w, w_ffn = k.sem("lf_weights"), k.sem("lf_ffn_weights")
        if layer:
            sp.wait_ge(k.sem("lf_layer_done"), ll)
        sp.dma_start(b["wqkv"], k.ins["lf_wqkv"][layer, :, :]).then_inc(w, 16)
        sp.dma_start(b["scales"], k.ins["lf_scales"][layer, :].partition_broadcast(P)).then_inc(w, 16)
        sp.dma_start(b["wo"], k.ins["lf_wo"][layer, :, :]).then_inc(w_ffn, 16)
        sp.dma_start(b["w1"], k.ins["lf_w1"][layer, :, :]).then_inc(w_ffn, 16)
        sp.dma_start(b["w2"], k.ins["lf_w2"][layer, :, :]).then_inc(w_ffn, 16)
        sp.dma_start(b["vec"], k.ins["lf_vec"][layer, :, :]).then_inc(w_ffn, 16)
        sp.dma_start(b["b2"], k.ins["lf_b2"][layer, :].partition_broadcast(P)).then_inc(w_ffn, 16)
        for part in range(2):
            if part:
                sp.wait_ge(k.sem("lf_cleared"), n + 1)
                with sp.Fori(0, TILES // 2) as i:
                    for s in range(2):
                        hold(k, sp, "lf_kept", ll * TILES + i * 2 + (s + LEAD))
                        hold(k, sp, "lf_values", 2 * ll * TILES + i * 4 + (2 * s - 2 + LEAD))
                        src = b["v"].rearrange("p t d -> p (t d)")[WINDOW:P, bass.ds(i * (2 * INNER) + s * INNER, INNER)]
                        sp.dma_start(b["early"][0:WINDOW, s, :, 0:HDL],
                                     src.rearrange("p (a h d) -> p a h d", h=2, d=HDL)[:, :, 0, :])\
                            .then_inc(k.sem(f"lf_early{s}"), 16)
            sp.wait_ge(k.sem("lf_y_ready"), 2 * ll + part + 1)
            moved = k.sem("lf_shifted")
            sp.dma_start(k.xn[1:P, :, high], b["y"][0:P - 1, :, high]).then_inc(moved, 16)
            for bt in range(BATCH):
                t = bt * TPG
                sp.dma_start(k.xn[0:1, t + 1:t + TPG, high], b["y"][P - 1:P, t:t + TPG - 1, high]).then_inc(moved, 16)


def sequences(eng, sequence):
    with eng.Fori(0, BATCH - 1) as bt:
        sequence(bt, False)
    sequence(BATCH - 1, True)


SHIFTS = 16 * (1 + BATCH)


def local_pe(k, pe, m, n, ln):
    b = local_layout(k)
    for layer in range(LAYERS):
        ll = n * LAYERS + layer
        pe.wait_ge(k.sem("lf_halves_joined"), 2 * ll + 1)
        pe.wait_ge(k.sem("lf_shifted"), SHIFTS * (2 * ll + 1))
        transpose_pe(k, pe, k.xn)
        pe.wait_ge(k.sem("xT_ready"), (k.xt_calls[m] + 2 * layer + 1) * GROUPS)
        pe.wait_ge(k.sem("lf_weights"), 32 * (ll + 1))

        def project(tile, t):
            pe.wait_ge(k.sem("lf_staged"), tile + (t + 1))
            pe.wait_ge(k.sem("lf_kept"), tile + (t - 1 + LEAD))
            for part in range(3):
                o = pe.matmul(k.ps[:, 3 * (t % 2) + part, :], b["hs"][:, t % TPG, :], b["wqkv"][:, part, :],
                              start=True, stop=True)
            o.then_inc(k.sem("lf_projected"), 1)

        def sequence(bt, last):
            tile = ll * TILES + bt * TPG
            for t in range(TPG):
                if t + 3 < TPG or not last:
                    project(tile, t + 3)
                pe.wait_ge(k.sem("lf_rotated"), tile + (t + 1 + LEAD))
                pe.wait_ge(k.sem("lf_keys"), tile + (t + LEAD))
                for c in range(2 * PAIRS):
                    for part in ("qr", "swp"):
                        o = pe.matmul(k.ps[:, 6 + c // PAIRS, c % PAIRS * P:(c % PAIRS + 1) * P],
                                      b[part][:, t % 2, c * P:(c + 1) * P], k.ident[:, :],
                                      start=(part == "qr"), stop=(part == "swp"))
                o.then_inc(k.sem("lf_turned"), 1)

        for t in range(3):
            project(ll * TILES, t)
        sequences(pe, sequence)

        pe.wait_ge(k.sem("lf_keys"), LEAD + (ll + 1) * TILES)
        pe.wait_ge(k.sem("lf_ffn_weights"), 80 * (ll + 1))

        def scores(bt, u):
            at, tile, t = ll * BATCH * HALVES + bt * HALVES, ll * TILES + bt * TPG, u // 2
            if u % 2 == 0:
                pe.wait_ge(k.sem("lf_queries_masked"), tile + (t + 1))
            if u >= 2:
                pe.wait_ge(k.sem("lf_maxima"), at + (u - 1))
            for h in range(4):
                head = 4 * (u % 2) + h
                for to, key, keys in (((0, P, P), (P, P - WINDOW, WINDOW)) if h % 2 == 0 else ((SEEN, P - WINDOW, SEEN),)):
                    o = pe.matmul(k.ps[:, 2 * (u % 2) + h // 2, to:to + keys], b["qm"][:, t % 2, head, :],
                                  b["kT"].rearrange("p a c -> p (a c)")
                                  [:, bass.ds(bt * SEQ + (head // 2 * (P + TOKENS) + t * P + key), keys)],
                                  start=True, stop=True)
            o.then_inc(k.sem("lf_scores"), 1)

        def sequence(bt, last):
            at, tile = ll * BATCH * HALVES + bt * HALVES, ll * TILES + bt * TPG

            def turn(u):
                pe.wait_ge(k.sem("lf_probs"), at + (u + 1 + LEAD))
                pe.wait_ge(k.sem("lf_probs_copied_act"), at + (u + LEAD))
                pe.wait_ge(k.sem("lf_probs_copied_dve"), at + (u + LEAD))
                for pair in range(2):
                    heads = b["p"][:, u % 2, 2 * pair:2 * pair + 2, :].rearrange("p h c -> p (h c)")
                    for c, first in enumerate((P, 0, 2 * SEEN - P)):
                        o = pe.transpose(k.ps[:, 4 + pair, c * P:(c + 1) * P], heads[:, first:first + P], k.ident[:, :])
                o.then_inc(k.sem("lf_probs_turned"), 1)

            def values(u):
                t = u // 2
                pe.wait_ge(k.sem("lf_probs_copied_act"), at + (u + 1 + LEAD))
                pe.wait_ge(k.sem("lf_probs_copied_dve"), at + (u + 1 + LEAD))
                if u % 2 == 0:
                    pe.wait_ge(k.sem("lf_out"), tile + (t + LEAD))
                    pe.wait_ge(k.sem("lf_early"), tile + (t + 1))
                    pe.wait_ge(k.sem(f"lf_early{t % 2}"), 8 * ll * TILES + 16 * (TPG // 2) * bt + 16 * (t // 2 + 1))
                for pair in range(2):
                    both = 2 * (u % 2) + pair
                    pe.matmul(k.ps[:, 6, both * P:(both + 1) * P], b["pT"][:, u % 2, 3 * pair, :],
                              b["early"][:, t % 2, both, :], start=True, stop=True)
                    for h in range(2):
                        head = 2 * both + h
                        o = pe.matmul(k.ps[:, 6, head * HDL:(head + 1) * HDL], b["pT"][:, u % 2, 3 * pair + 1 + h, :],
                                      b["v"].rearrange("p t d -> p (t d)")
                                      [:, bass.ds(bt * (TPG * INNER) + ((t + 1) * INNER + head * HDL), HDL)],
                                      start=False, stop=True, skip_group_check=True)
                o.then_inc(k.sem("lf_values"), 1)

            def turn_out(t):
                pe.wait_ge(k.sem("lf_out"), tile + (t + 1 + LEAD))
                pe.wait_ge(k.sem("lf_added"), tile + (t + LEAD))
                for c in range(PAIRS):
                    o = pe.transpose(k.ps[:, 7, c * P:(c + 1) * P], b["o"][:, t % 2, c * P:(c + 1) * P], k.ident[:, :])
                o.then_inc(k.sem("lf_out_turned"), 1)

            def project_out(t):
                pe.wait_ge(k.sem("lf_out_copied"), tile + (t + 1 + LEAD))
                for c in range(PAIRS):
                    o = pe.matmul(k.ps[:, 7, 0:P], b["oT"][:, t % 2, c * P:(c + 1) * P],
                                  b["wo"][:, c, :], start=(c == 0), stop=(c == PAIRS - 1))
                o.then_inc(k.sem("lf_out_projected"), 1)

            for u in range(HALVES):
                turn(u)
                if u + 2 < HALVES or not last:
                    scores(bt, u + 2)
                if u % 2 == 0 and u:
                    turn_out(u // 2 - 1)
                values(u)
                if u % 2 == 0 and u:
                    project_out(u // 2 - 1)
            turn_out(TPG - 1)
            project_out(TPG - 1)

        scores(0, 0)
        scores(0, 1)
        sequences(pe, sequence)

        transpose_pe(k, pe, k.xn, ln + 1 + layer)
        pe.wait_ge(k.sem("xT_ready"), (k.xt_calls[m] + 2 * layer + 2) * GROUPS)
        with pe.Fori(0, GROUPS // 2) as i:
            at = ll * GROUPS * CH + i * (2 * CH)
            group = ll * GROUPS + i * 2

            def up(step):
                g, c = divmod(step, CH)
                if step >= 2:
                    pe.wait_ge(k.sem("lf_hidden"), at + (step - 1 + LEAD))
                for half in range(2):
                    o = pe.matmul(k.ps[:, 2 * (step % 2) + half, :], b["w1"][:, half, c, :],
                                  k.xT[:, bass.ds(i * (2 * GROUP) + g * GROUP, GROUP)], start=True, stop=True)
                o.then_inc(k.sem("lf_up"), 1)

            def down(g):
                pe.wait_ge(k.sem("lf_hidden"), LEAD + at + CH * (g + 1))
                pe.wait_ge(k.sem("lf_ffn_added"), group + LEAD)
                for j in range(TPG):
                    for c in range(CH):
                        o = pe.matmul(k.ps[:, 4 + g, j * P:(j + 1) * P], b["hid"][:, g, c, j * P:(j + 1) * P],
                                      b["w2"][:, c, :], start=(c == 0), stop=(c == CH - 1))
                o.then_inc(k.sem("lf_down"), 1)

            for step in range(CH + 2):
                up(step)
            down(0)
            up(2 * CH - 1)
            down(1)


def local_act(k, a, m, n, ln):
    b = local_layout(k)
    norm_act(k, a, ln)
    for layer in range(LAYERS):
        ll = n * LAYERS + layer
        transpose_act(k, a, k.xt_calls[m] + 2 * layer, k.xT)
        if layer == 0:
            a.wait_ge(k.sem("lf_cleared"), n + 1)
        use_table(k, a, ACT.Sqrt)

        def keep(bt, tile, t):
            a.wait_ge(k.sem("lf_projected"), tile + (t + 1 + LEAD))
            a.wait_ge(k.sem("lf_rotated"), tile + (t - 3 + LEAD if t > 1 else LEAD))
            qk = k.ps[:, 3 * (t % 2):3 * (t % 2) + 2, :]
            if t > 1:
                a.wait_ge(k.sem("lf_summed"), tile + (t - 1))
            a.activation(b["qsq"][:, t % 2, :].rearrange("p (a b) -> p a b", a=2), qk, ACT.Square)\
                .then_inc(k.sem("lf_squares"), 1)
            a.activation(b["qk"][:, t % TPG, :].rearrange("p (a b) -> p a b", a=2), qk, ACT.Copy)
            a.activation(b["v"].rearrange("p t d -> p (t d)")[:, bass.ds(bt * (TPG * INNER) + (t + 1) * INNER, INNER)],
                         k.ps[:, 3 * (t % 2) + 2, :], ACT.Copy).then_inc(k.sem("lf_kept"), 1)

        def lengths(tile, t):
            a.wait_ge(k.sem("lf_summed"), tile + (t + 1))
            a.activation(b["norms"][:, t % 2, :], b["norms"][:, t % 2, :], ACT.Sqrt).then_inc(k.sem("lf_lengths"), 1)

        def sequence(bt, last):
            tile = ll * TILES + bt * TPG
            for t in range(TPG):
                if t + 2 < TPG or not last:
                    keep(bt, tile, t + 2)
                if t + 1 < TPG or not last:
                    lengths(tile, t + 1)
                a.wait_ge(k.sem("lf_turned"), tile + (t + 1 + LEAD))
                for half, (dst, first) in enumerate((("qT", 0), ("kT", P))):
                    o = a.activation(b[dst][:, :, bass.ds(bt * SEQ + (t * P + first), P)],
                                     k.ps[:, 6 + half, :].rearrange("p (a b) -> p a b", a=PAIRS), ACT.Copy)
                o.then_inc(k.sem("lf_keys"), 1)

        keep(0, ll * TILES, 0)
        keep(0, ll * TILES, 1)
        lengths(ll * TILES, 0)
        sequences(a, sequence)
        a.wait_ge(k.sem("lf_rotated"), LEAD + (ll + 1) * TILES)

        use_table(k, a, ACT.Exp)

        def exps(bt, u):
            at, tile, t = ll * BATCH * HALVES + bt * HALVES, ll * TILES + bt * TPG, u // 2
            a.wait_ge(k.sem("lf_maxima"), at + (u + 1))
            if u % 2 == 0:
                a.wait_ge(k.sem("lf_out"), tile + (t - 1 + LEAD))
            if u > 1:
                a.wait_ge(k.sem("lf_probs_turned"), at + (u - 1))
            for h in range(4):
                o = a.activation(b["p"][:, u % 2, h, :], b["s"][:, u % 2, h, :], ACT.Exp, scale=-1.0,
                                 bias=b["negmax"][:, u % 2, h:h + 1],
                                 accum_out=b["sum"][:, t % 2, 4 * (u % 2) + h:4 * (u % 2) + h + 1])
            o.then_inc(k.sem("lf_probs"), 1)

        def sequence(bt, last):
            at, tile = ll * BATCH * HALVES + bt * HALVES, ll * TILES + bt * TPG

            def out_copy(t):
                a.wait_ge(k.sem("lf_out_turned"), tile + (t + 1))
                a.wait_ge(k.sem("lf_out_projected"), tile + (t - 1 + LEAD))
                a.activation(b["oT"][:, t % 2, :], k.ps[:, 7, :], ACT.Copy).then_inc(k.sem("lf_out_copied"), 1)

            for u in range(HALVES):
                if u + 1 < HALVES or not last:
                    exps(bt, u + 1)
                a.wait_ge(k.sem("lf_probs_turned"), at + (u + 1))
                a.wait_ge(k.sem("lf_values"), at + (u - 1 + LEAD))
                a.activation(b["pT"][:, u % 2, 0:3, :], k.ps[:, 4, 0:3 * P].rearrange("p (a b) -> p a b", a=3), ACT.Copy)\
                    .then_inc(k.sem("lf_probs_copied_act"), 1)
                if u % 2 == 0 and u:
                    out_copy(u // 2 - 1)
            out_copy(TPG - 1)

        exps(0, 0)
        sequences(a, sequence)

        a.wait_ge(k.sem("lf_added"), LEAD + (ll + 1) * TILES)
        norm_act(k, a, ln + 1 + layer)
        transpose_act(k, a, k.xt_calls[m] + 2 * layer + 1, k.xT, b["vec"][:, 0:1], b["vec"][:, 1:2])
        use_table(k, a, ACT.Gelu)
        with a.Fori(0, GROUPS // 2) as i:
            at = ll * GROUPS * CH + i * (2 * CH)
            a.wait_ge(k.sem("lf_hidden"), at + LEAD)
            for step in range(2 * CH):
                c = step % CH
                a.wait_ge(k.sem("lf_up"), at + (step + 1))
                if step >= 2:
                    a.wait_ge(k.sem("lf_hidden"), at + (step - 1 + LEAD))
                a.activation(b["ge"][:, step % 2, :], k.ps[:, 2 * (step % 2) + 1, :], ACT.Gelu,
                             bias=b["vec"][:, 2 + CH + c:3 + CH + c]).then_inc(k.sem("lf_gelu"), 1)


def local_dve(k, v, m, n, ln):
    b = local_layout(k)
    low = slice(0, DIM // 2)
    norm_dve(k, v, ln, k.x[:, :, :], b["y"])
    v.memset(k.xn[0:1, 0:TILES:TPG, DIM // 2:DIM], 0.0)
    v.drain()
    v.sem_inc(k.sem("lf_y_ready"), 1)
    v.tensor_copy(k.xn[:, :, low], b["y"][:, :, low]).then_inc(k.sem("lf_halves_joined"), 1)
    v.memset(b["early"], 0.0)
    v.memset(b["kT"][:, :, 0:P], 0.0)
    v.memset(b["v"][:, 0, :], 0.0).then_inc(k.sem("lf_cleared"), 1)
    v.wait_ge(k.sem("lf_tables"), 64 * (n + 1))
    for layer in range(LAYERS):
        ll = n * LAYERS + layer
        if layer:
            v.tensor_copy(k.xn[:, :, low], b["y"][:, :, low]).then_inc(k.sem("lf_halves_joined"), 1)
        v.wait_ge(k.sem("lf_weights"), 32 * (ll + 1))
        sc = b["scales"].unsqueeze(1)
        v.tensor_tensor(b["tc"], b["cos"], sc.broadcast_to([P, TPG, 2, HDL]), ALU.mult)
        for half in range(2):
            own, other = (slice(half * 32, half * 32 + 32), slice((1 - half) * 32, (1 - half) * 32 + 32))
            v.tensor_tensor(b["ts"][:, :, :, own], b["sin"][:, :, :, own],
                            b["scales"][:, :, other].unsqueeze(1).broadcast_to([P, TPG, 2, 32]), ALU.mult)
        v.wait_ge(k.sem("xT_ready"), (k.xt_calls[m] + 2 * layer + 1) * GROUPS)
        v.drain()

        def stage(bt, tile, t):
            v.wait_ge(k.sem("lf_projected"), tile + (t - 3 + LEAD if t > 1 else LEAD))
            v.tensor_copy(b["hs"][:, t % TPG, :], k.xT[:, bass.ds(bt * SEQ + t * P, P)]).then_inc(k.sem("lf_staged"), 1)

        def add_squares(tile, t):
            v.wait_ge(k.sem("lf_squares"), tile + (t + 1))
            v.tensor_reduce(b["norms"][:, t % 2, :], b["qsq"][:, t % 2, :].rearrange("p (h d) -> p h d", d=HDL), X_AXIS,
                            ALU.add).then_inc(k.sem("lf_summed"), 1)

        def rotate(tile, t):
            norms = b["norms"][:, t % 2, :]
            v.wait_ge(k.sem("lf_lengths"), tile + (t + 1))
            v.tensor_scalar(norms, norms, 1e-12, None, ALU.max)
            v.drain()
            v.reciprocal(norms, norms)
            v.drain()
            qk = b["qk"][:, t, :].rearrange("p (h d) -> p h d", d=HDL)
            v.tensor_tensor(qk, qk, bc(norms, HDL), ALU.mult)
            v.drain()
            qk, turned, swapped = (x.rearrange("p (a h d) -> p a h d", a=2, d=HDL)
                                   for x in (b["qk"][:, t, :], b["qr"][:, t % 2, :], b["swp"][:, t % 2, :]))
            v.wait_ge(k.sem("lf_turned"), tile + (t - 1 + LEAD))
            for half in range(2):
                own, other = (slice(half * 32, half * 32 + 32), slice((1 - half) * 32, (1 - half) * 32 + 32))
                v.tensor_tensor(swapped[:, :, :, own], qk[:, :, :, other],
                                b["ts"][:, t, :, own].unsqueeze(2).broadcast_to([P, 2, HEADSL, 32]), ALU.mult)
            v.tensor_tensor(turned, qk, b["tc"][:, t, :, :].unsqueeze(2).broadcast_to([P, 2, HEADSL, HDL]), ALU.mult)
            v.drain()
            v.sem_inc(k.sem("lf_rotated"), 1)

        def sequence(bt, last):
            tile = ll * TILES + bt * TPG
            for t in range(TPG):
                if t + 1 < TPG or not last:
                    add_squares(tile, t + 1)
                if not last:
                    stage(bt, tile, t + TPG)
                rotate(tile, t)

        for t in range(TPG):
            stage(0, ll * TILES, t)
        add_squares(ll * TILES, 0)
        sequences(v, sequence)
        v.wait_ge(k.sem("lf_keys"), LEAD + (ll + 1) * TILES)

        def queries(bt, t):
            for half in range(2):
                o = v.tensor_scalar(b["qm"][:, t % 2, :, :].rearrange("p (a h) c -> p a h c", h=2)[:, :, half, :],
                                    b["qT"][:, :, bass.ds(bt * SEQ + t * P, P)], b["half"][:, half:half + 1],
                                    QK_SCALE * math.sqrt(HDL), ALU.mult, ALU.mult)
            o.then_inc(k.sem("lf_queries_masked"), 1)

        def early(bt, t):
            src = b["v"].rearrange("p t d -> p (t d)")[WINDOW:P, bass.ds(bt * (TPG * INNER) + t * INNER, INNER)]
            v.tensor_copy(b["early"][WINDOW:P, t % 2, :, HDL:P], src.rearrange("p (a h d) -> p a h d", h=2, d=HDL)[:, :, 1, :])\
                .then_inc(k.sem("lf_early"), 1)

        def maxima(bt, u):
            at = ll * BATCH * HALVES + bt * HALVES
            v.wait_ge(k.sem("lf_probs"), at + (u - 1 + LEAD))
            hold(k, v, "lf_scores", at + (u + 1 + LEAD))
            for h in range(4):
                o = v.tensor_tensor_reduce(b["s"][:, u % 2, h, :],
                                           k.ps[:, 2 * (u % 2) + h // 2, h % 2 * SEEN:(h % 2 + 1) * SEEN],
                                           b["mask"][:, min(u % HALVES // 2, 1), h % 2, :], -1.0, 3.0e38, ALU.add, ALU.min,
                                           b["negmax"][:, u % 2, h:h + 1])
            o.then_inc(k.sem("lf_maxima"), 1)

        def sequence(bt, last):
            at, tile = ll * BATCH * HALVES + bt * HALVES, ll * TILES + bt * TPG

            def copy(u):
                v.wait_ge(k.sem("lf_values"), at + (u - 1 + LEAD))
                v.wait_ge(k.sem("lf_probs_turned"), at + (u + 1))
                v.tensor_copy(b["pT"][:, u % 2, 3:6, :], k.ps[:, 5, 0:3 * P].rearrange("p (a b) -> p a b", a=3))\
                    .then_inc(k.sem("lf_probs_copied_dve"), 1)

            def out(t):
                v.wait_ge(k.sem("lf_values"), at + (2 * t + 2 + LEAD))
                total = b["sum"][:, t % 2, :]
                v.reciprocal(total, total)
                v.drain()
                v.tensor_tensor(b["o"][:, t % 2, :].rearrange("p (h d) -> p h d", d=HDL),
                                k.ps[:, 6, :].rearrange("p (h d) -> p h d", d=HDL), bc(total, HDL), ALU.mult)\
                    .then_inc(k.sem("lf_out"), 1)

            def add(t):
                v.wait_ge(k.sem("lf_out_projected"), tile + (t + 1 + LEAD))
                yt = b["y"][:, bass.ds(bt * TPG + t, 1), :].rearrange("p a d -> p (a d)")
                v.tensor_tensor(yt, k.ps[:, 7, 0:P], yt, ALU.add)\
                    .then_inc(k.sem("lf_added"), 1)

            for u in range(HALVES):
                t = u // 2
                copy(u)
                if u + 2 < HALVES or not last:
                    maxima(bt, u + 2)
                if u % 2:
                    if t:
                        add(t - 1)
                    out(t)
                    if t + 2 < TPG or not last:
                        early(bt, t + 2)
                elif t + 2 < TPG or not last:
                    queries(bt, t + 2)
            add(TPG - 1)

        for t in range(2):
            queries(0, t)
            early(0, t)
        maxima(0, 0)
        maxima(0, 1)
        sequences(v, sequence)

        v.wait_ge(k.sem("lf_added"), LEAD + (ll + 1) * TILES)
        v.sem_inc(k.sem("lf_y_ready"), 1)
        v.tensor_copy(k.xn[:, :, low], b["y"][:, :, low]).then_inc(k.sem("lf_halves_joined"), 1)
        v.wait_ge(k.sem("lf_ffn_weights"), 80 * (ll + 1))
        v.wait_ge(k.sem("lf_shifted"), SHIFTS * (2 * ll + 2))
        norm_dve(k, v, ln + 1 + layer, k.xn[:, :, :], k.xn[:, :, :])
        v.tensor_tensor(b["y"], b["y"], b["b2"].unsqueeze(1).broadcast_to([P, TILES, P]), ALU.add)
        v.drain()
        with v.Fori(0, GROUPS // 2) as i:
            at = ll * GROUPS * CH + i * (2 * CH)
            group = ll * GROUPS + i * 2
            v.wait_ge(k.sem("lf_down"), group + LEAD)

            def add(g):
                v.wait_ge(k.sem("lf_down"), group + (g + 1 + LEAD))
                yg = b["y"][:, bass.ds(i * (2 * TPG) + g * TPG, TPG), :]
                v.tensor_tensor(yg, k.ps[:, 4 + g, :].rearrange("p (a b) -> p a b", a=TPG), yg, ALU.add)\
                    .then_inc(k.sem("lf_ffn_added"), 1)

            for step in range(2 * CH):
                g, c = divmod(step, CH)
                v.wait_ge(k.sem("lf_gelu"), at + (step + 1))
                v.scalar_tensor_tensor(b["hid"][:, g, c, :], k.ps[:, 2 * (step % 2), :], b["vec"][:, 2 + c:3 + c],
                                       b["ge"][:, step % 2, :], ALU.add, ALU.mult).then_inc(k.sem("lf_hidden"), 1)
            add(0)
            add(1)
        v.drain()
        if layer + 1 < LAYERS:
            v.memset(k.xn[0:1, 0:TILES:TPG, DIM // 2:DIM], 0.0)
            v.drain()
            v.sem_inc(k.sem("lf_y_ready"), 1)
            v.sem_inc(k.sem("lf_layer_done"), 1)
        else:
            v.scalar_tensor_tensor(k.x[:, :, :].rearrange("p t d -> p (t d)"), b["y"].rearrange("p t d -> p (t d)"), 0.5,
                                   k.x[:, :, :].rearrange("p t d -> p (t d)"), ALU.mult, ALU.add)
            v.drain()
            v.sem_inc(k.sem("lf_layer_done"), 1)
            v.sem_inc(k.sem("x_updated"), 1)


def lay_out_local(a, i):
    import numpy as _np

    c, f = _np.ascontiguousarray, _np.float32
    a["lf_wqkv"] = i["L1_ffn_wqkv"]
    a["lf_scales"] = c(_np.concatenate([i["L1_ffn_q_scale"], i["L1_ffn_k_scale"]], axis=1))
    a["lf_wo"] = c(i["L1_ffn_wo"].reshape(LAYERS, PAIRS, P, DIM).transpose(0, 2, 1, 3).reshape(LAYERS, P, PAIRS * DIM))
    w1 = _np.zeros((LAYERS, DIM, 2, CH * P), f)
    w1[:, :, :, :HID] = i["L1_ffn_w1"].reshape(LAYERS, DIM, 2, HID)
    a["lf_w1"] = w1.reshape(LAYERS, DIM, 2 * CH * P)
    w2 = _np.zeros((LAYERS, CH * P, DIM), f)
    w2[:, :HID] = i["L1_ffn_w2"]
    a["lf_w2"] = c(w2.reshape(LAYERS, CH, P, DIM).transpose(0, 2, 1, 3).reshape(LAYERS, P, CH * DIM))
    b1 = _np.zeros((LAYERS, 2, CH * P), f)
    b1[:, :, :HID] = i["L1_ffn_b1"].reshape(LAYERS, 2, HID)
    a["lf_vec"] = c(_np.concatenate([i["L1_ffn_ln_g"][:, :, None], i["L1_ffn_ln_b"][:, :, None],
                                     b1.reshape(LAYERS, 2 * CH, P).transpose(0, 2, 1)], axis=2))
    a["lf_b2"] = i["L1_ffn_b2"]
    own, earlier = _np.arange(P), _np.arange(-WINDOW, 0)
    q = _np.arange(P)[:, None, None]
    key = _np.stack([_np.concatenate([own, earlier]), _np.concatenate([earlier, own])])[None]
    seen = (key <= q) & (key >= q - WINDOW)
    a["lf_mask"] = c(_np.stack([_np.where(seen & (key >= 0), 0, -1e30), _np.where(seen, 0, -1e30)], axis=1).astype(f))
    half = _np.arange(0, HDL, 2, dtype=f)
    inv = (f(1.0) / f(10000.0) ** (half / f(HDL))).astype(f)
    t = _np.arange(SEQ, dtype=f)
    freqs = (t[:, None] * inv[None, :]).astype(_np.float64)
    base = ((half + 0.4 * HDL) / (1.4 * HDL)).astype(_np.float64)
    scale = base[None, :] ** ((t - SEQ // 2) / float(WINDOW // 2))[:, None]
    cos, sin = _np.cos(freqs), _np.sin(freqs)

    def table(x, lower):
        both = _np.stack([_np.concatenate([lower * x * z, x * z], axis=1) for z in (scale, 1.0 / scale)], axis=1)
        return c(both.reshape(TPG, P, 2, HDL).transpose(1, 0, 2, 3).astype(f))

    a["lf_cos"], a["lf_sin"] = table(cos, 1.0), table(sin, -1.0)

relu_moe = {"norms": 1, "transposes": 1, "gates": 1, "stores": 1, "backs": 1, "sync": relu_moe_sync, "tensor": relu_moe_pe,
            "scalar": relu_moe_act, "vector": relu_moe_dve}

swiglu_moe = {"norms": 3, "transposes": 3, "gates": 1, "stores": 0, "backs": 0, "sync": swiglu_sync,
              "tensor": swiglu_pe, "scalar": swiglu_act, "vector": swiglu_dve}
small_moe = {"norms": 1, "transposes": 1, "gates": 1, "stores": 1, "backs": 1, "sync": small_sync,
             "tensor": small_pe, "scalar": small_act, "vector": small_dve}


def attention_kind(c, norms):
    def bind(f):
        return lambda k, eng, m, n, ln: f(k, eng, m, n, ln, c)
    return {"norms": norms, "transposes": 1, "gates": 0, "backs": 0, "att_blocks": c.blocks, "flat": c.blocks == 1,
            "sync": bind(attention_sync), "tensor": bind(attention_pe), "scalar": bind(attention_act),
            "vector": bind(attention_dve)}


attn0, attn1, attn3 = attention_kind(A0, 1), attention_kind(A1, 2), attention_kind(A3, 1)
s4d = {"norms": 1, "transposes": 1, "gates": 0, "backs": 0, "sync": s4d_sync, "tensor": s4d_pe, "scalar": s4d_act,
       "vector": s4d_dve}
local_ffn = {"norms": 3, "transposes": 4, "gates": 0, "backs": 0, "sync": local_sync, "tensor": local_pe,
             "scalar": local_act, "vector": local_dve}



KINDS = {"ffn0": relu_moe, "attn0": attn0, "ffn1": local_ffn, "attn1": attn1, "ffn2": swiglu_moe, "attn2": s4d,
         "ffn3": small_moe, "attn3": attn3}
STAGES = ["ffn0", "attn0", "ffn0", "ffn1", "attn1", "ffn1", "ffn2", "attn2", "ffn2", "ffn3", "attn3", "ffn3"]


def build(nc, ins, out, stages=STAGES):
    with ExitStack() as ctx:
        k = Program(nc, ctx, ins)
        k.gates_dram = nc.dram_tensor("gates_dram", (32 * TILES, P), F32, kind="Internal").ap()
        k.toeplitz_dram = nc.dram_tensor("toeplitz_dram", (HEADS, P, SPAN), F32, kind="Internal").ap()
        k.rel_dram = nc.dram_tensor("rel_dram", (HEADS, 2 * SEQ), F32, kind="Internal").ap()
        k.ln_calls, k.xt_calls, k.gate_calls, k.back_calls, k.kind_calls = [], [], [], [], []
        k.att_calls, k.att_blocks, k.flat_calls, k.gate_stores = [], [], [], []
        lns = xts = gates = backs = atts = blocks = flats = stores = 0
        seen = {}
        for s in stages:
            kind = KINDS[s]
            k.ln_calls.append(lns), k.xt_calls.append(xts), k.gate_calls.append(gates), k.back_calls.append(backs)
            k.kind_calls.append(seen.get(s, 0))
            seen[s] = seen.get(s, 0) + 1
            lns += kind["norms"]
            xts += kind["transposes"]
            gates += kind["gates"]
            backs += kind["backs"]
            k.att_calls.append(atts), k.att_blocks.append(blocks), k.flat_calls.append(flats - seen[s] + 1)
            k.gate_stores.append(stores)
            stores += kind.get("stores", 0)
            atts += "att_blocks" in kind
            blocks += kind.get("att_blocks", 0)
            flats += bool(kind.get("flat"))
        x_in = ins["x"].rearrange("b (t p) d -> p (b t) d", p=P)
        x_out = out.rearrange("b (t p) d -> p (b t) d", p=P)
        block = ctx.enter_context(nc.Block())

        def run(which, eng):
            for name in LED.get(which, []):
                eng.sem_inc(k.sem(name), LEAD)
            for m, s in enumerate(stages):
                KINDS[s][which](k, eng, m, k.kind_calls[m], k.ln_calls[m])

        @block.sync
        def _(sp):
            sp.dma_start(k.x[:, :, :], x_in).then_inc(k.sem("x_loaded"), 16)
            sp.dma_start(k.ident[:, :], ins["ident"]).then_inc(k.sem("x_loaded"), 16)
            run("sync", sp)
            sp.wait_ge(k.sem("x_updated"), len(stages) + 1)
            sp.dma_start(x_out, k.x[:, :, :]).then_inc(k.sem("x_stored"), 16)
            sp.wait_ge(k.sem("x_stored"), 16)

        @block.vector
        def _(v):
            v.wait_ge(k.sem("x_loaded"), 32)
            v.tensor_copy(k.ln_a[:, :], k.x[:, :, 0]).then_inc(k.sem("x_updated"), 1)
            run("vector", v)

        @block.tensor
        def _(pe):
            pe.wait_ge(k.sem("x_updated"), 1)
            run("tensor", pe)

        @block.scalar
        def _(a):
            run("scalar", a)


def lay_out(i):
    import numpy as _np

    c = _np.ascontiguousarray
    f = _np.float32
    a = {"x": i["L0_attn_X"], "ident": _np.eye(P, dtype=f), "rank": _np.arange(32, 0, -1).astype(f)}
    a["l0_gate_w"] = c(i["L0_ffn_gate_w"].T)
    a["l0_b2"] = i["L0_ffn_b2"]
    a["l0_w"] = c(_np.concatenate([
        i["L0_ffn_w1"],
        i["L0_ffn_w2"].reshape(E0, C0, P, DIM).transpose(0, 2, 1, 3).reshape(E0, P, C0 * DIM),
        i["L0_ffn_b1"].reshape(E0, C0, P).transpose(0, 2, 1)], axis=2))
    for more in (lay_out_attention, lay_out_swiglu, lay_out_small, lay_out_local, lay_out_s4d):
        more(a, i)
    return a


def kernel(**inputs):
    import numpy as _np
    import concourse.bacc as _bacc
    from concourse import mybir as _mybir
    from concourse.bass_utils import run_bass_kernel_spmd as _run

    nc = _bacc.Bacc("TRN2", target_bir_lowering=False, num_devices=1)
    arrays, ins = {}, {}
    for name, a in lay_out({n: _np.asarray(v) for n, v in inputs.items()}).items():
        arrays[f"in_{name}"] = a
        ins[name] = nc.dram_tensor(f"in_{name}", a.shape, _mybir.dt.from_np(a.dtype), kind="ExternalInput").ap()
    out = nc.dram_tensor("out_x", (BATCH, SEQ, DIM), _mybir.dt.float32, kind="ExternalOutput").ap()
    build(nc, ins, out)
    return _run(nc, [arrays], core_ids=[0]).results[0]["out_x"]
```
